# Optimizing a Trainium2 kernel written in Bass

```python
import numpy as np
import jax
import jax.numpy as jnp

def _softmax(x, axis=-1):
    return jax.nn.softmax(x, axis=axis)

def _gelu(x):
    return jax.nn.gelu(x, approximate=True)

def _silu(x):
    return jax.nn.silu(x)

def _sigmoid(x):
    return jax.nn.sigmoid(x)

def _layernorm(x, axis=-1, eps=1e-05):
    m = jnp.mean(x, axis=axis, keepdims=True)
    v = jnp.var(x, axis=axis, keepdims=True)
    return (x - m) / jnp.sqrt(v + eps)

def _scatter_add(tgt, idx, src, axis=0):
    return tgt.at[idx].add(src)

def _segment_sum(src, seg, n):
    return jax.ops.segment_sum(src, seg, n)
kernel_name = 'mk_audio_tower_d4_tok_aud1d512_r4_2a2860'

def setup_inputs(seed: int=0):
    np.random.seed(seed)
    _w = jnp.asarray

    def _rec_inputs():
        import jax
        import jax.numpy as jnp
        _rk = jax.random.key(seed)
        x = 0.00021031 + 1.00007 * jax.random.normal(jax.random.fold_in(_rk, 1), (64, 4000), jnp.float32)
        return x
    x = _rec_inputs()

    def _L0_tok_setup():
        import jax, jax.numpy as jnp
        import numpy as np
        FRAME_LENGTH = 256
        B, T = (16, 524288)

        def _mdct_matrix(length):
            L2 = length
            Lh = L2 // 2
            n = jnp.arange(L2, dtype=jnp.float32) + 0.5
            k = jnp.pi / Lh * n[:Lh]
            n = n + Lh / 2
            z = jnp.sqrt(jnp.float32(2.0 / Lh * 2.0))
            return z * jnp.cos(n[:, None] * k[None, :])
        key = jax.random.key(seed)
        x = jax.random.normal(key, (B, T), dtype=jnp.float32)
        return {'x': x}
    _L0_tok_all = _L0_tok_setup()
    _L0_tok_in = {k: v for k, v in _L0_tok_all.items() if k in ()}
    del _L0_tok_all

    def _L0_attn_setup():
        import jax, jax.numpy as jnp
        import numpy as np
        from jax import lax
        B_, L_, D_ = (4, 128, 128)
        HID, H2 = (128, 64)
        NL, DST, DCV, DIN, DTR = (3, 16, 4, 256, 32)

        def _silu(x):
            return x * jax.nn.sigmoid(x)

        def _layernorm(x, g, b):
            m = x.mean(-1, keepdims=True)
            v = x.var(-1, keepdims=True)
            return (x - m) / jnp.sqrt(v + 1e-05) * g + b

        def _mamba(x, wi, cw, cb, xpw, dw, db, Alog, Dp, wo):
            Bsz, Ls, _ = x.shape
            xz = jnp.einsum('bld,ed->ble', x, wi)
            xin, z = jnp.split(xz, 2, axis=-1)
            xpad = jnp.pad(xin, ((0, 0), (DCV - 1, 0), (0, 0)))
            u = cb + sum((xpad[:, k:k + Ls, :] * cw[:, k] for k in range(DCV)))
            u = _silu(u)
            xdbl = jnp.einsum('blc,ec->ble', u, xpw)
            dt_in = xdbl[..., :DTR]
            Bc = xdbl[..., DTR:DTR + DST]
            Cc = xdbl[..., DTR + DST:]
            dt = jax.nn.softplus(jnp.einsum('blr,cr->blc', dt_in, dw) + db)
            A = -jnp.exp(Alog)

            def step(h, inp):
                dt_t, B_t, C_t, u_t = inp
                dA = jnp.exp(dt_t[..., None] * A)
                h = dA * h + (dt_t * u_t)[..., None] * B_t[:, None, :]
                y = jnp.einsum('bcn,bn->bc', h, C_t)
                return (h, y)
            h0 = jnp.zeros((Bsz, DIN, DST), x.dtype)
            _, ys = lax.scan(step, h0, (dt.transpose(1, 0, 2), Bc.transpose(1, 0, 2), Cc.transpose(1, 0, 2), u.transpose(1, 0, 2)))
            y = ys.transpose(1, 0, 2) + u * Dp
            y = y * _silu(z)
            return jnp.einsum('blc,dc->bld', y, wo)

        def _lstm_dir(x, wih, whh, bih, bhh, reverse):
            Bsz = x.shape[0]

            def step(carry, xt):
                h, c = carry
                g = xt @ wih.T + h @ whh.T + bih + bhh
                i, f, gg, o = jnp.split(g, 4, axis=-1)
                c = jax.nn.sigmoid(f) * c + jax.nn.sigmoid(i) * jnp.tanh(gg)
                h = jax.nn.sigmoid(o) * jnp.tanh(c)
                return ((h, c), h)
            init = (jnp.zeros((Bsz, H2), x.dtype), jnp.zeros((Bsz, H2), x.dtype))
            _, hs = lax.scan(step, init, x.transpose(1, 0, 2), reverse=reverse)
            return hs.transpose(1, 0, 2)
        key = jax.random.key(seed)
        ks = jax.random.split(key, 16)
        rn = lambda k, s, sc=0.02: jax.random.normal(k, s, jnp.float32) * sc
        inp = {}
        inp['x'] = jax.random.normal(ks[0], (B_, L_, D_), jnp.float32)
        inp['in_proj_w'] = rn(ks[1], (NL, 2 * DIN, D_))
        inp['conv_w'] = rn(ks[2], (NL, DIN, DCV), 0.2)
        inp['conv_b'] = jnp.zeros((NL, DIN), jnp.float32)
        inp['x_proj_w'] = rn(ks[3], (NL, DTR + 2 * DST, DIN))
        inp['dt_proj_w'] = rn(ks[4], (NL, DIN, DTR), 0.1)
        inp['dt_proj_b'] = jnp.full((NL, DIN), -4.0, jnp.float32)
        inp['A_log'] = jnp.log(jnp.broadcast_to(jnp.arange(1, DST + 1, dtype=jnp.float32), (NL, DIN, DST)))
        inp['D_param'] = jnp.ones((NL, DIN), jnp.float32)
        inp['out_proj_w'] = rn(ks[5], (NL, D_, DIN))
        inp['ln_g'] = jnp.ones((NL, D_), jnp.float32)
        inp['ln_b'] = jnp.zeros((NL, D_), jnp.float32)
        inp['lstm_w_ih'] = rn(ks[6], (2, 4 * H2, D_), 0.05)
        inp['lstm_w_hh'] = rn(ks[7], (2, 4 * H2, H2), 0.05)
        inp['lstm_b_ih'] = jnp.zeros((2, 4 * H2), jnp.float32)
        inp['lstm_b_hh'] = jnp.zeros((2, 4 * H2), jnp.float32)
        inp['fusion_w'] = rn(ks[8], (HID, D_ + HID), 0.02)
        inp['fusion_b'] = jnp.zeros((HID,), jnp.float32)
        return inp
    _L0_attn_all = _L0_attn_setup()
    _L0_attn_in = {k: v for k, v in _L0_attn_all.items() if k in ('in_proj_w', 'conv_w', 'conv_b', 'x_proj_w', 'dt_proj_w', 'dt_proj_b', 'A_log', 'D_param', 'out_proj_w', 'ln_g', 'ln_b', 'lstm_w_ih', 'lstm_w_hh', 'lstm_b_ih', 'lstm_b_hh', 'fusion_w', 'fusion_b')}
    del _L0_attn_all

    def _L0_ffn_setup():
        import jax, jax.numpy as jnp
        import numpy as np
        CAPACITY_FACTOR = 1.2
        key = jax.random.key(seed)
        k1, k2, k3 = jax.random.split(key, 3)
        B, S, D, E = (8, 1024, 128, 16)
        x = jax.random.normal(k1, (B, S, D), dtype=jnp.float32)
        switch_w = jax.random.normal(k2, (E, D), dtype=jnp.float32) * 0.02
        switch_b = jnp.zeros((E,), dtype=jnp.float32)
        expert_w = jax.random.normal(k3, (E, D, D), dtype=jnp.float32) * 0.02
        expert_b = jnp.zeros((E, D), dtype=jnp.float32)
        return {'x': x, 'switch_w': switch_w, 'switch_b': switch_b, 'expert_w': expert_w, 'expert_b': expert_b}
    _L0_ffn_all = _L0_ffn_setup()
    _L0_ffn_in = {k: v for k, v in _L0_ffn_all.items() if k in ('switch_w', 'switch_b', 'expert_w', 'expert_b')}
    del _L0_ffn_all

    def _L1_attn_setup():
        import jax, jax.numpy as jnp
        import numpy as np
        NUM_HEADS = 8
        EPS = 1e-12

        def _l2_normalize(t):
            sq = jnp.sum(t * t, axis=-1, keepdims=True)
            return t * jax.lax.rsqrt(jnp.maximum(sq, EPS))
        key = jax.random.key(seed)
        ks = jax.random.split(key, 4)
        B, N, C = (8, 1024, 128)
        x = jax.random.normal(ks[0], (B, N, C), dtype=jnp.float32)
        w_qkv = jax.random.normal(ks[1], (C, 3 * C), dtype=jnp.float32) * C ** (-0.5)
        b_qkv = jnp.zeros((3 * C,), dtype=jnp.float32)
        w_proj = jax.random.normal(ks[2], (C, C), dtype=jnp.float32) * C ** (-0.5)
        b_proj = jnp.zeros((C,), dtype=jnp.float32)
        return {'x': x, 'w_qkv': w_qkv, 'b_qkv': b_qkv, 'w_proj': w_proj, 'b_proj': b_proj}
    _L1_attn_all = _L1_attn_setup()
    _L1_attn_in = {k: v for k, v in _L1_attn_all.items() if k in ('w_qkv', 'b_qkv', 'w_proj', 'b_proj')}
    del _L1_attn_all

    def _L1_ffn_setup():
        import jax, jax.numpy as jnp
        import numpy as np
        D, E, DR, K, DFF, DSH = (128, 64, 64, 2, 512, 256)
        TEMP = 0.7
        SHARED_SCALE = 0.25
        EPS = 1e-05

        def _ln(x, g, b):
            m = jnp.mean(x, axis=-1, keepdims=True)
            v = jnp.mean(jnp.square(x - m), axis=-1, keepdims=True)
            return (x - m) * jax.lax.rsqrt(v + EPS) * g + b
        key = jax.random.key(seed)
        ks = jax.random.split(key, 16)
        s = 0.02
        return {'x': jax.random.normal(ks[0], (1, 128, D), dtype=jnp.float32), 'ln1_g': jnp.ones((D,), jnp.float32), 'ln1_b': jnp.zeros((D,), jnp.float32), 'Wr': jax.random.normal(ks[1], (D, DR), jnp.float32) * s, 'codebook': jax.random.normal(ks[2], (E, DR), jnp.float32), 'W1': jax.random.normal(ks[3], (E, D, DFF), jnp.float32) * s, 'b1': jnp.zeros((E, DFF), jnp.float32), 'W2': jax.random.normal(ks[4], (E, DFF, D), jnp.float32) * s, 'b2': jnp.zeros((E, D), jnp.float32), 'Ws1': jax.random.normal(ks[5], (D, DSH), jnp.float32) * s, 'bs1': jnp.zeros((DSH,), jnp.float32), 'Ws2': jax.random.normal(ks[6], (DSH, D), jnp.float32) * s, 'bs2': jnp.zeros((D,), jnp.float32), 'ffln_g': jnp.ones((D,), jnp.float32), 'ffln_b': jnp.zeros((D,), jnp.float32), 'Wf1': jax.random.normal(ks[7], (D, DFF), jnp.float32) * s, 'bf1': jnp.zeros((DFF,), jnp.float32), 'Wf2': jax.random.normal(ks[8], (DFF, D), jnp.float32) * s, 'bf2': jnp.zeros((D,), jnp.float32)}
    _L1_ffn_all = _L1_ffn_setup()
    _L1_ffn_in = {k: v for k, v in _L1_ffn_all.items() if k in ('ln1_g', 'ln1_b', 'Wr', 'codebook', 'W1', 'b1', 'W2', 'b2', 'Ws1', 'bs1', 'Ws2', 'bs2', 'ffln_g', 'ffln_b', 'Wf1', 'bf1', 'Wf2', 'bf2')}
    del _L1_ffn_all

    def _L2_attn_setup():
        import jax, jax.numpy as jnp
        import numpy as np
        D_MODEL = 128
        N = 64
        L_MAX = 512
        BATCH = 8
        DT = 0.1

        def _compute_kernel(L_param, P_left, P_right, B, C, log_dt):
            I = jnp.eye(N, dtype=L_param.dtype)
            L_mat = I * jnp.exp(L_param)[:, None, :]
            P = jnp.einsum('dnk,dkm->dnm', P_left, P_right)
            A = -L_mat + P
            dt = jnp.exp(log_dt)
            A = A * dt[..., None]
            Bd = B * dt
            M = I - A / 2
            dA = jnp.linalg.solve(M, I + A / 2)
            dB = jnp.linalg.solve(M, Bd[..., None])[..., 0]

            def step(state, _):
                k_t = jnp.einsum('dn,dn->d', C, state)
                new_state = jnp.einsum('dnm,dm->dn', dA, state)
                return (new_state, k_t)
            _, k = jax.lax.scan(step, dB, None, length=L_MAX)
            return k.T
        key = jax.random.key(seed)
        ks = jax.random.split(key, 6)
        x = jax.random.normal(ks[0], (BATCH, L_MAX, D_MODEL), dtype=jnp.float32)
        L_param = jnp.full((D_MODEL, N), 0.5, dtype=jnp.float32)
        P_left = 0.01 * jax.random.normal(ks[1], (D_MODEL, N, 2), dtype=jnp.float32)
        P_right = 0.01 * jax.random.normal(ks[2], (D_MODEL, 2, N), dtype=jnp.float32)
        B = jax.random.normal(ks[3], (D_MODEL, N), dtype=jnp.float32) / np.sqrt(N).astype(np.float32)
        C = jax.random.normal(ks[4], (D_MODEL, N), dtype=jnp.float32) / np.sqrt(N).astype(np.float32)
        D = jnp.ones((D_MODEL,), dtype=jnp.float32)
        log_dt = jnp.log(DT * jnp.ones((D_MODEL, 1), dtype=jnp.float32))
        return {'x': x, 'L_param': L_param, 'P_left': P_left, 'P_right': P_right, 'B': B, 'C': C, 'D': D, 'log_dt': log_dt}
    _L2_attn_all = _L2_attn_setup()
    _L2_attn_in = {k: v for k, v in _L2_attn_all.items() if k in ('L_param', 'P_left', 'P_right', 'B', 'C', 'D', 'log_dt')}
    del _L2_attn_all

    def _L2_ffn_setup():
        import jax, jax.numpy as jnp
        import numpy as np
        B, S, D, F, E = (4, 512, 128, 512, 8)
        key = jax.random.key(seed)
        k = jax.random.split(key, 5)
        x = jax.random.normal(k[0], (B, S, D), dtype=jnp.float32)
        Ws = jax.random.normal(k[1], (D, E), dtype=jnp.float32) * 0.02
        bs = jnp.zeros((E,), dtype=jnp.float32)
        W1 = jax.random.normal(k[2], (E, D, F), dtype=jnp.float32) * 0.02
        b1 = jnp.zeros((E, F), dtype=jnp.float32)
        W2 = jax.random.normal(k[3], (E, F, D), dtype=jnp.float32) * 0.02
        b2 = jnp.zeros((E, D), dtype=jnp.float32)
        return {'x': x, 'Ws': Ws, 'bs': bs, 'W1': W1, 'b1': b1, 'W2': W2, 'b2': b2}
    _L2_ffn_all = _L2_ffn_setup()
    _L2_ffn_in = {k: v for k, v in _L2_ffn_all.items() if k in ('Ws', 'bs', 'W1', 'b1', 'W2', 'b2')}
    del _L2_ffn_all

    def _L3_attn_setup():
        import jax, jax.numpy as jnp
        import numpy as np
        DIM = 128
        key = jax.random.key(seed)
        k1, k2, k3, k4 = jax.random.split(key, 4)
        B, N = (32, 256)
        embeddings = jax.random.normal(k1, (B, N, DIM), dtype=jnp.float32)
        bound = float(np.sqrt(6.0 / (2 * DIM)))
        Wq = jax.random.uniform(k2, (DIM, DIM), jnp.float32, -bound, bound)
        Wk = jax.random.uniform(k3, (DIM, DIM), jnp.float32, -bound, bound)
        Wv = jax.random.uniform(k4, (DIM, DIM), jnp.float32, -bound, bound)
        return {'embeddings': embeddings, 'Wq': Wq, 'Wk': Wk, 'Wv': Wv}
    _L3_attn_all = _L3_attn_setup()
    _L3_attn_in = {k: v for k, v in _L3_attn_all.items() if k in ('Wq', 'Wk', 'Wv')}
    del _L3_attn_all

    def _L3_ffn_setup():
        import jax, jax.numpy as jnp
        import numpy as np
        S, B, I, O, H, E, K = (128, 32, 128, 128, 128, 8, 2)

        def _expert(x_seq, Wi, Wh, b, Wo, bo):
            Bsz = x_seq.shape[1]
            Hd = Wh.shape[0]

            def step(carry, xt):
                h, c = carry
                gates = xt @ Wi + h @ Wh + b
                i_, f_, g_, o_ = jnp.split(gates, 4, axis=-1)
                c = jax.nn.sigmoid(f_) * c + jax.nn.sigmoid(i_) * jnp.tanh(g_)
                h = jax.nn.sigmoid(o_) * jnp.tanh(c)
                return ((h, c), h @ Wo + bo)
            init = (jnp.zeros((Bsz, Hd), x_seq.dtype), jnp.zeros((Bsz, Hd), x_seq.dtype))
            _, ys = jax.lax.scan(step, init, x_seq)
            return ys
        key = jax.random.key(seed)
        ks = jax.random.split(key, 6)
        s = 0.02
        return {'x': jax.random.normal(ks[0], (S, B, I), dtype=jnp.float32), 'router_w': jax.random.normal(ks[1], (I, E), dtype=jnp.float32) * s, 'router_b': jnp.zeros((E,), dtype=jnp.float32), 'Wi': jax.random.normal(ks[2], (E, I, 4 * H), dtype=jnp.float32) * s, 'Wh': jax.random.normal(ks[3], (E, H, 4 * H), dtype=jnp.float32) * s, 'b': jnp.zeros((E, 4 * H), dtype=jnp.float32), 'Wo': jax.random.normal(ks[4], (E, H, O), dtype=jnp.float32) * s, 'bo': jnp.zeros((E, O), dtype=jnp.float32)}
    _L3_ffn_all = _L3_ffn_setup()
    _L3_ffn_in = {k: v for k, v in _L3_ffn_all.items() if k in ('router_w', 'router_b', 'Wi', 'Wh', 'b', 'Wo', 'bo')}
    del _L3_ffn_all
    return {'x': x, 'L0_attn_in_proj_w': _L0_attn_in['in_proj_w'], 'L0_attn_conv_w': _L0_attn_in['conv_w'], 'L0_attn_conv_b': _L0_attn_in['conv_b'], 'L0_attn_x_proj_w': _L0_attn_in['x_proj_w'], 'L0_attn_dt_proj_w': _L0_attn_in['dt_proj_w'], 'L0_attn_dt_proj_b': _L0_attn_in['dt_proj_b'], 'L0_attn_A_log': _L0_attn_in['A_log'], 'L0_attn_D_param': _L0_attn_in['D_param'], 'L0_attn_out_proj_w': _L0_attn_in['out_proj_w'], 'L0_attn_ln_g': _L0_attn_in['ln_g'], 'L0_attn_ln_b': _L0_attn_in['ln_b'], 'L0_attn_lstm_w_ih': _L0_attn_in['lstm_w_ih'], 'L0_attn_lstm_w_hh': _L0_attn_in['lstm_w_hh'], 'L0_attn_lstm_b_ih': _L0_attn_in['lstm_b_ih'], 'L0_attn_lstm_b_hh': _L0_attn_in['lstm_b_hh'], 'L0_attn_fusion_w': _L0_attn_in['fusion_w'], 'L0_attn_fusion_b': _L0_attn_in['fusion_b'], 'L0_ffn_switch_w': _L0_ffn_in['switch_w'], 'L0_ffn_switch_b': _L0_ffn_in['switch_b'], 'L0_ffn_expert_w': _L0_ffn_in['expert_w'], 'L0_ffn_expert_b': _L0_ffn_in['expert_b'], 'L1_attn_w_qkv': _L1_attn_in['w_qkv'], 'L1_attn_b_qkv': _L1_attn_in['b_qkv'], 'L1_attn_w_proj': _L1_attn_in['w_proj'], 'L1_attn_b_proj': _L1_attn_in['b_proj'], 'L1_ffn_ln1_g': _L1_ffn_in['ln1_g'], 'L1_ffn_ln1_b': _L1_ffn_in['ln1_b'], 'L1_ffn_Wr': _L1_ffn_in['Wr'], 'L1_ffn_codebook': _L1_ffn_in['codebook'], 'L1_ffn_W1': _L1_ffn_in['W1'], 'L1_ffn_b1': _L1_ffn_in['b1'], 'L1_ffn_W2': _L1_ffn_in['W2'], 'L1_ffn_b2': _L1_ffn_in['b2'], 'L1_ffn_Ws1': _L1_ffn_in['Ws1'], 'L1_ffn_bs1': _L1_ffn_in['bs1'], 'L1_ffn_Ws2': _L1_ffn_in['Ws2'], 'L1_ffn_bs2': _L1_ffn_in['bs2'], 'L1_ffn_ffln_g': _L1_ffn_in['ffln_g'], 'L1_ffn_ffln_b': _L1_ffn_in['ffln_b'], 'L1_ffn_Wf1': _L1_ffn_in['Wf1'], 'L1_ffn_bf1': _L1_ffn_in['bf1'], 'L1_ffn_Wf2': _L1_ffn_in['Wf2'], 'L1_ffn_bf2': _L1_ffn_in['bf2'], 'L2_attn_L_param': _L2_attn_in['L_param'], 'L2_attn_P_left': _L2_attn_in['P_left'], 'L2_attn_P_right': _L2_attn_in['P_right'], 'L2_attn_B': _L2_attn_in['B'], 'L2_attn_C': _L2_attn_in['C'], 'L2_attn_D': _L2_attn_in['D'], 'L2_attn_log_dt': _L2_attn_in['log_dt'], 'L2_ffn_Ws': _L2_ffn_in['Ws'], 'L2_ffn_bs': _L2_ffn_in['bs'], 'L2_ffn_W1': _L2_ffn_in['W1'], 'L2_ffn_b1': _L2_ffn_in['b1'], 'L2_ffn_W2': _L2_ffn_in['W2'], 'L2_ffn_b2': _L2_ffn_in['b2'], 'L3_attn_Wq': _L3_attn_in['Wq'], 'L3_attn_Wk': _L3_attn_in['Wk'], 'L3_attn_Wv': _L3_attn_in['Wv'], 'L3_ffn_router_w': _L3_ffn_in['router_w'], 'L3_ffn_router_b': _L3_ffn_in['router_b'], 'L3_ffn_Wi': _L3_ffn_in['Wi'], 'L3_ffn_Wh': _L3_ffn_in['Wh'], 'L3_ffn_b': _L3_ffn_in['b'], 'L3_ffn_Wo': _L3_ffn_in['Wo'], 'L3_ffn_bo': _L3_ffn_in['bo']}

def reference(x, L0_attn_in_proj_w, L0_attn_conv_w, L0_attn_conv_b, L0_attn_x_proj_w, L0_attn_dt_proj_w, L0_attn_dt_proj_b, L0_attn_A_log, L0_attn_D_param, L0_attn_out_proj_w, L0_attn_ln_g, L0_attn_ln_b, L0_attn_lstm_w_ih, L0_attn_lstm_w_hh, L0_attn_lstm_b_ih, L0_attn_lstm_b_hh, L0_attn_fusion_w, L0_attn_fusion_b, L0_ffn_switch_w, L0_ffn_switch_b, L0_ffn_expert_w, L0_ffn_expert_b, L1_attn_w_qkv, L1_attn_b_qkv, L1_attn_w_proj, L1_attn_b_proj, L1_ffn_ln1_g, L1_ffn_ln1_b, L1_ffn_Wr, L1_ffn_codebook, L1_ffn_W1, L1_ffn_b1, L1_ffn_W2, L1_ffn_b2, L1_ffn_Ws1, L1_ffn_bs1, L1_ffn_Ws2, L1_ffn_bs2, L1_ffn_ffln_g, L1_ffn_ffln_b, L1_ffn_Wf1, L1_ffn_bf1, L1_ffn_Wf2, L1_ffn_bf2, L2_attn_L_param, L2_attn_P_left, L2_attn_P_right, L2_attn_B, L2_attn_C, L2_attn_D, L2_attn_log_dt, L2_ffn_Ws, L2_ffn_bs, L2_ffn_W1, L2_ffn_b1, L2_ffn_W2, L2_ffn_b2, L3_attn_Wq, L3_attn_Wk, L3_attn_Wv, L3_ffn_router_w, L3_ffn_router_b, L3_ffn_Wi, L3_ffn_Wh, L3_ffn_b, L3_ffn_Wo, L3_ffn_bo):
    import jax
    import jax.numpy as jnp

    def _L0_tok_ref(x):
        import jax, jax.numpy as jnp
        import numpy as np
        FRAME_LENGTH = 256
        B, T = (16, 524288)

        def _mdct_matrix(length):
            L2 = length
            Lh = L2 // 2
            n = jnp.arange(L2, dtype=jnp.float32) + 0.5
            k = jnp.pi / Lh * n[:Lh]
            n = n + Lh / 2
            z = jnp.sqrt(jnp.float32(2.0 / Lh * 2.0))
            return z * jnp.cos(n[:, None] * k[None, :])
        L = FRAME_LENGTH
        hop = L // 2
        xp = jnp.pad(x, ((0, 0), (L // 2, hop + (L - 1) // 2)))
        n_frames = (xp.shape[-1] - L) // hop + 1
        idx = jnp.arange(n_frames)[:, None] * hop + jnp.arange(L)[None, :]
        frames = xp[:, idx]
        w = jnp.sin(jnp.pi * (jnp.arange(L, dtype=jnp.float32) + 0.5) / L)
        Wm = _mdct_matrix(L)
        return jnp.einsum('bnl,lk->bnk', frames * w, Wm)

    def _L0_attn_ref(x, in_proj_w, conv_w, conv_b, x_proj_w, dt_proj_w, dt_proj_b, A_log, D_param, out_proj_w, ln_g, ln_b, lstm_w_ih, lstm_w_hh, lstm_b_ih, lstm_b_hh, fusion_w, fusion_b):
        import jax, jax.numpy as jnp
        import numpy as np
        from jax import lax
        B_, L_, D_ = (4, 128, 128)
        HID, H2 = (128, 64)
        NL, DST, DCV, DIN, DTR = (3, 16, 4, 256, 32)

        def _silu(x):
            return x * jax.nn.sigmoid(x)

        def _layernorm(x, g, b):
            m = x.mean(-1, keepdims=True)
            v = x.var(-1, keepdims=True)
            return (x - m) / jnp.sqrt(v + 1e-05) * g + b

        def _mamba(x, wi, cw, cb, xpw, dw, db, Alog, Dp, wo):
            Bsz, Ls, _ = x.shape
            xz = jnp.einsum('bld,ed->ble', x, wi)
            xin, z = jnp.split(xz, 2, axis=-1)
            xpad = jnp.pad(xin, ((0, 0), (DCV - 1, 0), (0, 0)))
            u = cb + sum((xpad[:, k:k + Ls, :] * cw[:, k] for k in range(DCV)))
            u = _silu(u)
            xdbl = jnp.einsum('blc,ec->ble', u, xpw)
            dt_in = xdbl[..., :DTR]
            Bc = xdbl[..., DTR:DTR + DST]
            Cc = xdbl[..., DTR + DST:]
            dt = jax.nn.softplus(jnp.einsum('blr,cr->blc', dt_in, dw) + db)
            A = -jnp.exp(Alog)

            def step(h, inp):
                dt_t, B_t, C_t, u_t = inp
                dA = jnp.exp(dt_t[..., None] * A)
                h = dA * h + (dt_t * u_t)[..., None] * B_t[:, None, :]
                y = jnp.einsum('bcn,bn->bc', h, C_t)
                return (h, y)
            h0 = jnp.zeros((Bsz, DIN, DST), x.dtype)
            _, ys = lax.scan(step, h0, (dt.transpose(1, 0, 2), Bc.transpose(1, 0, 2), Cc.transpose(1, 0, 2), u.transpose(1, 0, 2)))
            y = ys.transpose(1, 0, 2) + u * Dp
            y = y * _silu(z)
            return jnp.einsum('blc,dc->bld', y, wo)

        def _lstm_dir(x, wih, whh, bih, bhh, reverse):
            Bsz = x.shape[0]

            def step(carry, xt):
                h, c = carry
                g = xt @ wih.T + h @ whh.T + bih + bhh
                i, f, gg, o = jnp.split(g, 4, axis=-1)
                c = jax.nn.sigmoid(f) * c + jax.nn.sigmoid(i) * jnp.tanh(gg)
                h = jax.nn.sigmoid(o) * jnp.tanh(c)
                return ((h, c), h)
            init = (jnp.zeros((Bsz, H2), x.dtype), jnp.zeros((Bsz, H2), x.dtype))
            _, hs = lax.scan(step, init, x.transpose(1, 0, 2), reverse=reverse)
            return hs.transpose(1, 0, 2)
        m = x
        for i in range(NL):
            mo = _mamba(m, in_proj_w[i], conv_w[i], conv_b[i], x_proj_w[i], dt_proj_w[i], dt_proj_b[i], A_log[i], D_param[i], out_proj_w[i])
            m = _layernorm(m + mo, ln_g[i], ln_b[i])
        lf = _lstm_dir(x, lstm_w_ih[0], lstm_w_hh[0], lstm_b_ih[0], lstm_b_hh[0], False)
        lb = _lstm_dir(x, lstm_w_ih[1], lstm_w_hh[1], lstm_b_ih[1], lstm_b_hh[1], True)
        comb = jnp.concatenate([m, lf, lb], axis=-1)
        return comb @ fusion_w.T + fusion_b

    def _L0_ffn_ref(x, switch_w, switch_b, expert_w, expert_b):
        import jax, jax.numpy as jnp
        import numpy as np
        CAPACITY_FACTOR = 1.2
        B, S, D = x.shape
        E = switch_w.shape[0]
        N = B * S
        xf = x.reshape(N, D)
        logits = xf @ switch_w.T + switch_b
        probs = jax.nn.softmax(logits, axis=-1)
        route_probs = jnp.max(probs, axis=-1)
        routes = jnp.argmax(probs, axis=-1)
        oh = jax.nn.one_hot(routes, E, dtype=jnp.int32)
        pos = jnp.take_along_axis(jnp.cumsum(oh, axis=0), routes[:, None], axis=1)[:, 0] - 1
        capacity = int(CAPACITY_FACTOR * N / E)
        keep = pos < capacity
        buf = jnp.zeros((E, capacity, D), dtype=xf.dtype).at[routes, pos].set(xf)
        y = jnp.einsum('ecd,efd->ecf', buf, expert_w) + expert_b[:, None, :]
        gathered = y[routes, jnp.minimum(pos, capacity - 1)]
        out = jnp.where(keep[:, None], gathered, xf) * route_probs[:, None]
        return out.reshape(B, S, D)

    def _L1_attn_ref(x, w_qkv, b_qkv, w_proj, b_proj):
        import jax, jax.numpy as jnp
        import numpy as np
        NUM_HEADS = 8
        EPS = 1e-12

        def _l2_normalize(t):
            sq = jnp.sum(t * t, axis=-1, keepdims=True)
            return t * jax.lax.rsqrt(jnp.maximum(sq, EPS))
        B, N, C = x.shape
        h = NUM_HEADS
        d = C // h
        scale = d ** (-0.5)
        qkv = x @ w_qkv + b_qkv
        qkv = qkv.reshape(B, N, 3, h, d)
        qkv = jnp.transpose(qkv, (2, 0, 3, 1, 4))
        q, k, v = (qkv[0], qkv[1], qkv[2])
        q = _l2_normalize(q) * scale
        k = _l2_normalize(k)
        attn = jnp.einsum('bhnd,bhne->bhde', q, k)
        attn = jax.nn.softmax(attn, axis=-1)
        out = jnp.einsum('bhnd,bhde->bhne', v, attn)
        out = jnp.transpose(out, (0, 2, 1, 3)).reshape(B, N, C)
        out = out @ w_proj + b_proj
        return out

    def _L1_ffn_ref(x, ln1_g, ln1_b, Wr, codebook, W1, b1, W2, b2, Ws1, bs1, Ws2, bs2, ffln_g, ffln_b, Wf1, bf1, Wf2, bf2):
        import jax, jax.numpy as jnp
        import numpy as np
        D, E, DR, K, DFF, DSH = (128, 64, 64, 2, 512, 256)
        TEMP = 0.7
        SHARED_SCALE = 0.25
        EPS = 1e-05

        def _ln(x, g, b):
            m = jnp.mean(x, axis=-1, keepdims=True)
            v = jnp.mean(jnp.square(x - m), axis=-1, keepdims=True)
            return (x - m) * jax.lax.rsqrt(v + EPS) * g + b
        B, S, _ = x.shape
        T = B * S
        h = _ln(x, ln1_g, ln1_b).reshape(T, D)
        r = h @ Wr
        logits = r @ codebook.T / TEMP
        probs = jax.nn.softmax(logits, axis=-1)
        vals, idx = jax.lax.top_k(probs, K)
        w = vals / jnp.sum(vals, axis=-1, keepdims=True)
        combine = jnp.zeros((T, E), x.dtype).at[jnp.arange(T)[:, None], idx].set(w)
        eh = jax.nn.silu(jnp.einsum('td,edf->tef', h, W1) + b1)
        eo = jnp.einsum('tef,efd->ted', eh, W2) + b2
        moe = jnp.einsum('te,ted->td', combine, eo)
        shared = (jax.nn.silu(h @ Ws1 + bs1) @ Ws2 + bs2) * SHARED_SCALE
        hmoe = (moe + shared).reshape(B, S, D)
        f = _ln(hmoe, ffln_g, ffln_b)
        f = jax.nn.silu(f @ Wf1 + bf1) @ Wf2 + bf2
        return x + hmoe + f

    def _L2_attn_ref(x, L_param, P_left, P_right, B, C, D, log_dt):
        import jax, jax.numpy as jnp
        import numpy as np
        D_MODEL = 128
        N = 64
        L_MAX = 512
        BATCH = 8
        DT = 0.1

        def _compute_kernel(L_param, P_left, P_right, B, C, log_dt):
            I = jnp.eye(N, dtype=L_param.dtype)
            L_mat = I * jnp.exp(L_param)[:, None, :]
            P = jnp.einsum('dnk,dkm->dnm', P_left, P_right)
            A = -L_mat + P
            dt = jnp.exp(log_dt)
            A = A * dt[..., None]
            Bd = B * dt
            M = I - A / 2
            dA = jnp.linalg.solve(M, I + A / 2)
            dB = jnp.linalg.solve(M, Bd[..., None])[..., 0]

            def step(state, _):
                k_t = jnp.einsum('dn,dn->d', C, state)
                new_state = jnp.einsum('dnm,dm->dn', dA, state)
                return (new_state, k_t)
            _, k = jax.lax.scan(step, dB, None, length=L_MAX)
            return k.T
        batch, L, _ = x.shape
        xt = jnp.transpose(x, (0, 2, 1))
        kernel = _compute_kernel(L_param, P_left, P_right, B, C, log_dt)
        n_fft = 2 * L_MAX
        kf = jnp.fft.rfft(kernel, n=n_fft)
        xf = jnp.fft.rfft(xt, n=n_fft)
        y = jnp.fft.irfft(xf * kf, n=n_fft)[..., :L]
        y = y + D[None, :, None] * xt
        return jnp.transpose(y, (0, 2, 1))

    def _L2_ffn_ref(x, Ws, bs, W1, b1, W2, b2):
        import jax, jax.numpy as jnp
        import numpy as np
        B, S, D, F, E = (4, 512, 128, 512, 8)
        Bb, Ss, Dd = x.shape
        xt = x.reshape(-1, Dd)
        logits = xt @ Ws + bs
        probs = jax.nn.softmax(logits, axis=-1)
        prob_max = jnp.max(probs, axis=-1)
        routes = jnp.argmax(probs, axis=-1)
        onehot = jax.nn.one_hot(routes, W1.shape[0], dtype=xt.dtype)

        def expert_ffn(w1, bb1, w2, bb2):
            h = jax.nn.gelu(xt @ w1 + bb1, approximate=False)
            return h @ w2 + bb2
        y = jax.vmap(expert_ffn)(W1, b1, W2, b2)
        out = jnp.einsum('te,etd->td', onehot, y)
        out = out * prob_max[:, None]
        return out.reshape(Bb, Ss, Dd)

    def _L3_attn_ref(embeddings, Wq, Wk, Wv):
        import jax, jax.numpy as jnp
        import numpy as np
        DIM = 128
        q = jnp.einsum('bnd,ed->bne', embeddings, Wq)
        k = jnp.einsum('bnd,ed->bne', embeddings, Wk)
        v = jnp.einsum('bnd,ed->bne', embeddings, Wv)
        scale = jnp.sqrt(jnp.asarray(DIM, dtype=embeddings.dtype))
        attn = jnp.einsum('bqe,bke->bqk', q, k) / scale
        attn = jnp.where(attn == 0, jnp.asarray(1e-10, attn.dtype), attn)
        attn = jax.nn.softmax(attn, axis=-1)
        return jnp.einsum('bqk,bke->bqe', attn, v)

    def _L3_ffn_ref(x, router_w, router_b, Wi, Wh, b, Wo, bo):
        import jax, jax.numpy as jnp
        import numpy as np
        S, B, I, O, H, E, K = (128, 32, 128, 128, 128, 8, 2)

        def _expert(x_seq, Wi, Wh, b, Wo, bo):
            Bsz = x_seq.shape[1]
            Hd = Wh.shape[0]

            def step(carry, xt):
                h, c = carry
                gates = xt @ Wi + h @ Wh + b
                i_, f_, g_, o_ = jnp.split(gates, 4, axis=-1)
                c = jax.nn.sigmoid(f_) * c + jax.nn.sigmoid(i_) * jnp.tanh(g_)
                h = jax.nn.sigmoid(o_) * jnp.tanh(c)
                return ((h, c), h @ Wo + bo)
            init = (jnp.zeros((Bsz, Hd), x_seq.dtype), jnp.zeros((Bsz, Hd), x_seq.dtype))
            _, ys = jax.lax.scan(step, init, x_seq)
            return ys
        S_, B_, I_ = x.shape
        N = S_ * B_
        flat_x = x.reshape(N, I_)
        logits = flat_x @ router_w + router_b
        top_vals, top_idx = jax.lax.top_k(logits, K)
        rw = jax.nn.softmax(top_vals, axis=1)
        mask = (top_idx.T[:, None, :] == jnp.arange(E)[None, :, None]).astype(x.dtype)
        expert_x = (mask[..., None] * flat_x[None, None]).reshape(K, E, S_, B_, I_)
        run_e = jax.vmap(_expert, in_axes=(0, 0, 0, 0, 0, 0))
        run_ke = jax.vmap(run_e, in_axes=(0, None, None, None, None, None))
        out = run_ke(expert_x, Wi, Wh, b, Wo, bo)
        out = out.reshape(K, E, N, -1)
        y = jnp.einsum('ken,nk,keno->no', mask, rw, out)
        return y.reshape(S_, B_, -1)
    h = _L0_tok_ref(x)
    h = h + _L0_attn_ref(_layernorm(h, axis=-1), L0_attn_in_proj_w, L0_attn_conv_w, L0_attn_conv_b, L0_attn_x_proj_w, L0_attn_dt_proj_w, L0_attn_dt_proj_b, L0_attn_A_log, L0_attn_D_param, L0_attn_out_proj_w, L0_attn_ln_g, L0_attn_ln_b, L0_attn_lstm_w_ih, L0_attn_lstm_w_hh, L0_attn_lstm_b_ih, L0_attn_lstm_b_hh, L0_attn_fusion_w, L0_attn_fusion_b)
    h = h + _L0_ffn_ref(_layernorm(h, axis=-1), L0_ffn_switch_w, L0_ffn_switch_b, L0_ffn_expert_w, L0_ffn_expert_b)
    h = h + _L1_attn_ref(_layernorm(h, axis=-1), L1_attn_w_qkv, L1_attn_b_qkv, L1_attn_w_proj, L1_attn_b_proj)
    h = h + _L1_ffn_ref(_layernorm(h, axis=-1), L1_ffn_ln1_g, L1_ffn_ln1_b, L1_ffn_Wr, L1_ffn_codebook, L1_ffn_W1, L1_ffn_b1, L1_ffn_W2, L1_ffn_b2, L1_ffn_Ws1, L1_ffn_bs1, L1_ffn_Ws2, L1_ffn_bs2, L1_ffn_ffln_g, L1_ffn_ffln_b, L1_ffn_Wf1, L1_ffn_bf1, L1_ffn_Wf2, L1_ffn_bf2)
    h = h + _L2_attn_ref(_layernorm(h, axis=-1), L2_attn_L_param, L2_attn_P_left, L2_attn_P_right, L2_attn_B, L2_attn_C, L2_attn_D, L2_attn_log_dt)
    h = h + _L2_ffn_ref(_layernorm(h, axis=-1), L2_ffn_Ws, L2_ffn_bs, L2_ffn_W1, L2_ffn_b1, L2_ffn_W2, L2_ffn_b2)
    h = h + _L3_attn_ref(_layernorm(h, axis=-1), L3_attn_Wq, L3_attn_Wk, L3_attn_Wv)
    h = h + _L3_ffn_ref(_layernorm(h, axis=-1), L3_ffn_router_w, L3_ffn_router_b, L3_ffn_Wi, L3_ffn_Wh, L3_ffn_b, L3_ffn_Wo, L3_ffn_bo)
    return h

_drawn_inputs = setup_inputs


def setup_inputs(seed=0):
    import zlib

    import numpy as np

    out = dict(_drawn_inputs(seed))
    spreads = {'L0_attn_conv_b': (0.0, 0.8),
     'L0_attn_dt_proj_b': (-4.0, 0.6),
     'L0_attn_D_param': (1.0, 0.6),
     'L0_attn_ln_g': (1.0, 0.2),
     'L0_attn_ln_b': (0.0, 0.1),
     'L0_attn_lstm_b_ih': (0.0, 0.8),
     'L0_attn_lstm_b_hh': (0.0, 0.8),
     'L0_attn_fusion_b': (0.0, 0.1),
     'L0_ffn_switch_b': (0.0, 0.36),
     'L0_ffn_expert_b': (0.0, 0.8),
     'L1_attn_b_qkv': (0.0, 0.541),
     'L1_attn_b_proj': (0.0, 0.1),
     'L1_ffn_ln1_g': (1.0, 0.6),
     'L1_ffn_ln1_b': (0.0, 0.433),
     'L1_ffn_b1': (0.0, 0.8),
     'L1_ffn_b2': (0.0, 0.1),
     'L1_ffn_bs1': (0.0, 0.8),
     'L1_ffn_bs2': (0.0, 0.66),
     'L1_ffn_ffln_g': (1.0, 0.6),
     'L1_ffn_ffln_b': (0.0, 0.8),
     'L1_ffn_bf1': (0.0, 0.767),
     'L1_ffn_bf2': (0.0, 0.1),
     'L2_attn_L_param': (0.5, 0.6),
     'L2_attn_D': (1.0, 0.2),
     'L2_attn_log_dt': (-2.3025851249694824, 0.6),
     'L2_ffn_bs': (0.0, 0.8),
     'L2_ffn_b1': (0.0, 0.8),
     'L2_ffn_b2': (0.0, 0.8),
     'L3_ffn_router_b': (0.0, 0.612),
     'L3_ffn_b': (0.0, 0.8),
     'L3_ffn_bo': (0.0, 0.386)}
    factors = {'L0_attn_in_proj_w': 8.0,
     'L0_attn_conv_w': 8.0,
     'L0_attn_x_proj_w': 8.0,
     'L0_attn_dt_proj_w': 8.0,
     'L0_attn_A_log': 8.0,
     'L0_attn_out_proj_w': 8.0,
     'L0_attn_lstm_w_hh': 8.0,
     'L0_ffn_switch_w': 2.686,
     'L0_ffn_expert_w': 3.49,
     'L1_ffn_W1': 2.849,
     'L1_ffn_Ws1': 8.0,
     'L1_ffn_Ws2': 8.0,
     'L2_attn_P_left': 8.0,
     'L2_attn_P_right': 8.0,
     'L2_attn_B': 8.0,
     'L2_attn_C': 8.0,
     'L2_ffn_Ws': 8.0,
     'L2_ffn_W1': 8.0,
     'L2_ffn_W2': 8.0,
     'L3_ffn_router_w': 3.18,
     'L3_ffn_Wi': 8.0,
     'L3_ffn_Wh': 8.0,
     'L3_ffn_Wo': 8.0}
    for name, (base, spread) in spreads.items():
        noise = np.random.default_rng([zlib.crc32(name.encode()), seed]).standard_normal(out[name].shape)
        drawn = base * np.exp(spread * noise) if base else spread * noise
        out[name] = jnp.asarray(drawn.astype(out[name].dtype))
    for name, factor in factors.items():
        out[name] = (out[name] * factor).astype(out[name].dtype)
    return out
```

```python
import concourse.bass as bass
from concourse import mybir
from contextlib import ExitStack, contextmanager
import numpy as np

F32 = mybir.dt.float32
BF16 = mybir.dt.bfloat16
F16 = mybir.dt.float16
I32 = mybir.dt.int32
ALU = mybir.AluOpType
ACT = mybir.ActivationFunctionType
AX = mybir.AxisListType

NB = 64
S = 33
D = 128
NT = NB * S
CH = NT // 4
HB = CH // 2
NCH = 4
BANK = 512
EPS = 1e-5
TT = 96
NTT = NT // TT
ds = bass.ds


class Chain:

    def __init__(self, eng, sem):
        self.eng, self.sem, self.n, self.at = eng, sem, 0, None

    def __call__(self, ins):
        ins.then_inc(self.sem, 1)
        self.n += 1
        self.eng.wait_ge(self.sem, self.n if self.at is None else self.at + self.n)

    @contextmanager
    def loop(self, count, per):
        start = self.n
        with self.eng.Fori(0, count) as i:
            self.at = i * per
            yield i
            assert self.n - start == per, (self.n - start, per)
        self.at = None
        self.n = start + count * per


class Hold:

    def __init__(self, eng, passed):
        self.eng, self.passed = eng, passed

    def __call__(self, sem, value):
        self.eng.wait_ge(sem, value)
        self.eng.sem_inc(self.passed, 1)


def unique(nc, name):
    return f"{name}_{nc.next_id()}"


def sbuf(nc, ctx, name, shape, dt=F32):
    return ctx.enter_context(nc.sbuf_tensor(unique(nc, name), shape, dt))


def psum(nc, ctx, name, shape, dt=F32):
    return ctx.enter_context(nc.psum_tensor(unique(nc, name), shape, dt))


@contextmanager
def stage(nc, names):
    with ExitStack() as ctx:
        sems = [ctx.enter_context(nc.semaphore(unique(nc, n))) for n in names.split()]
        yield sems
        for s in sems:
            nc.gpsimd.sem_clear(s)
        nc.all_engine_barrier()


class Counted:

    def __init__(self, sem):
        self.sem, self.n = sem, 0

    def add(self, n):
        self.n += n
        return self.n


def halves(ap):
    return ap.rearrange("p (h n) -> p h n", h=2)


def layernorm(nc, cst, src, dst, gain=None, shift=None):
    with ExitStack() as ctx:
        mean_ps = psum(nc, ctx, "mean_ps", [128, 2, 2, BANK], F32)
        var_ps = psum(nc, ctx, "var_ps", [128, 2, 2, BANK], F32)
        sq = sbuf(nc, ctx, "sq", [128, 2, CH], F32)
        rstd = sbuf(nc, ctx, "rstd", [128, 2, CH], F32)
        (mean_ready, centered, squared, var_ready, logged, rstd_ready, scaled, shifted) = ctx.enter_context(
            stage(nc, "mean_ready centered squared var_ready logged rstd_ready scaled shifted"))
        block = ctx.enter_context(nc.Block())

        def part(t, c):
            return t[:, c * CH:(c + 1) * CH]

        @block.tensor
        def _(pe):
            def mean(c):
                if c >= 2:
                    pe.wait_ge(centered, c - 1)
                for h in range(2):
                    last = nc.tensor.matmul(mean_ps[:, c % 2, h, 0:HB], cst["avg"], halves(part(src, c))[:, h, :],
                                            start=True, stop=True)
                last.then_inc(mean_ready, 1)

            def var(c):
                pe.wait_ge(squared, c + 1)
                if c >= 2:
                    pe.wait_ge(logged, c - 1)
                for h in range(2):
                    last = nc.tensor.matmul(var_ps[:, c % 2, h, 0:HB], cst["avg"], halves(sq[:, c % 2, :])[:, h, :],
                                            start=True, stop=True)
                last.then_inc(var_ready, 1)

            mean(0)
            for c in range(NCH):
                if c + 1 < NCH:
                    mean(c + 1)
                var(c)

        @block.vector
        def _(dve):
            def center(c):
                dve.wait_ge(mean_ready, c + 1)
                nc.vector.tensor_tensor(halves(part(dst, c)), halves(part(src, c)), mean_ps[:, c % 2, :, 0:HB],
                                        ALU.subtract).then_inc(centered, 1)

            def scale(c):
                dve.wait_ge(rstd_ready, c + 1)
                dve.wait_ge(centered, c + 1)
                d = part(dst, c)
                if gain is None:
                    nc.vector.tensor_tensor(d, d, rstd[:, c % 2, :], ALU.mult).then_inc(scaled, 1)
                else:
                    nc.vector.scalar_tensor_tensor(out=d, in0=d, scalar=gain, in1=rstd[:, c % 2, :], op0=ALU.mult,
                                                   op1=ALU.mult).then_inc(scaled, 1)
                    dve.wait_ge(scaled, c + 1)
                    nc.vector.tensor_scalar(d, d, shift, None, ALU.add).then_inc(shifted, 1)

            center(0)
            for c in range(NCH):
                if c + 1 < NCH:
                    center(c + 1)
                scale(c)

        @block.scalar
        def _(act):
            def square(c):
                act.wait_ge(centered, c + 1)
                if c >= 2:
                    act.wait_ge(var_ready, c - 1)
                nc.scalar.activation(sq[:, c % 2, :], part(dst, c), ACT.Square).then_inc(squared, 1)

            nc.scalar.preload_act_table_set("natural_log_exp_and_others")
            square(0)
            for c in range(NCH):
                if c + 1 < NCH:
                    square(c + 1)
                act.wait_ge(var_ready, c + 1)
                if c >= 2:
                    act.wait_ge(scaled, c - 1)
                r = rstd[:, c % 2, :]
                nc.scalar.activation(halves(r), var_ps[:, c % 2, :, 0:HB], ACT.Ln, bias=cst["eps"]).then_inc(logged, 1)
                act.wait_ge(logged, c + 1)
                nc.scalar.activation(r, r, ACT.Exp, scale=-0.5).then_inc(rstd_ready, 1)


def tokenize(nc, cst, frames_dram, hT):
    with ExitStack() as ctx:
        blocks = sbuf(nc, ctx, "blocks", [128, NB, S + 1], F32)
        ps = psum(nc, ctx, "ps", [128, 2, 2, BANK], F32)
        (loaded, framed, kept) = ctx.enter_context(stage(nc, "loaded framed kept"))
        block = ctx.enter_context(nc.Block())

        @block.sync
        def _(sp):
            sp.dma_start(blocks[:, :, :], frames_dram.rearrange("p (b s) -> p b s", b=NB)).then_inc(loaded, 16)

        @block.tensor
        def _(pe):
            pe.wait_ge(loaded, 16)
            for c in range(NCH):
                if c >= 2:
                    pe.wait_ge(kept, c - 1)
                for h in range(2):
                    b0 = 16 * c + 8 * h
                    for k in range(2):
                        last = nc.tensor.matmul(ps[:, c % 2, h, 0:HB], cst["mdct"][:, k, :],
                                                blocks[:, b0:b0 + 8, k:k + S], start=(k == 0), stop=(k == 1))
                last.then_inc(framed, 1)

        @block.vector
        def _(dve):
            for c in range(NCH):
                dve.wait_ge(framed, c + 1)
                nc.vector.tensor_copy(halves(hT[:, c * CH:(c + 1) * CH]), ps[:, c % 2, :, 0:HB]).then_inc(kept, 1)


NL, DST, DCV, DIN, DTR, H2 = 3, 16, 4, 256, 32, 64
MW = {}
_at = 0
for _name, _width in (("wi", 2 * DIN), ("cw", 2 * DCV), ("cb", 2), ("xp", 2 * 128), ("dw", DIN), ("db", 2),
                      ("alog", 2 * DST), ("dp", 2), ("wo", 2 * D), ("g", 1), ("b", 1)):
    MW[_name] = (_at, _width)
    _at += _width
MWID = _at


def mamba_layer(nc, cst, layer, w_dram, m):
    with ExitStack() as ctx:
        def sb(name, shape, dt=F32):
            return sbuf(nc, ctx, name, shape, dt)

        w = sb("w", [128, MWID])
        u = sb("u", [128, 2, NT])
        sz = sb("sz", [128, 2, NT])
        dt = sb("dt", [128, 2, NT])
        du = sb("du", [128, 2, NT])
        xd = sb("xd", [128, NT])
        bc = sb("bc", [128, NT + CH], BF16)
        negA = sb("negA", [128, 2 * DST])

        def W(name, a=0, n=None):
            at, width = MW[name]
            return w[:, at + a:at + (width if n is None else a + n)]

        def chunk(t, half, c):
            return t[:, half, ds(c * CH, CH)]

        with ExitStack() as c1:
            px = psum(nc, c1, "px", [128, 2, 2, BANK], F32)
            pz = psum(nc, c1, "pz", [128, 2, 2, BANK], F32)
            (w_loaded, x_ready, z_ready, tap0, conv, u_ready, z_done, xd_ready, xd_done, pe_passed, act_passed) = c1.enter_context(
                stage(nc, "w_loaded x_ready z_ready tap0 conv u_ready z_done xd_ready xd_done pe_passed act_passed"))
            block = c1.enter_context(nc.Block())

            @block.sync
            def _(sp):
                sp.dma_start(w[:, :], w_dram[ds(layer, 1), :, :].rearrange("o p n -> p (o n)")).then_inc(w_loaded, 16)

            @block.tensor
            def _(pe):
                hold = Hold(pe, pe_passed)
                pe.wait_ge(w_loaded, 16)
                with pe.Fori(0, NCH) as c:
                    hold(xd_done, c)
                    for half in range(2):
                        for k in range(2):
                            last = nc.tensor.matmul(px[:, half, k, 0:HB], W("wi", half * 128, 128),
                                                    m[:, ds(c * CH + k * HB, HB)], start=True, stop=True)
                    last.then_inc(x_ready, 1)
                    hold(z_done, c)
                    for half in range(2):
                        for k in range(2):
                            last = nc.tensor.matmul(pz[:, half, k, 0:HB], W("wi", DIN + half * 128, 128),
                                                    m[:, ds(c * CH + k * HB, HB)], start=True, stop=True)
                    last.then_inc(z_ready, 1)
                    hold(u_ready, c + 1)
                    for k in range(2):
                        for half in range(2):
                            last = nc.tensor.matmul(px[:, 0, k, 0:HB], W("xp", half * 128, 128),
                                                    u[:, half, ds(c * CH + k * HB, HB)], start=(half == 0), stop=(half == 1))
                    last.then_inc(xd_ready, 1)

            @block.scalar
            def _(act):
                hold = Hold(act, act_passed)
                nc.scalar.preload_act_table_set("silu_and_others")
                act.wait_ge(w_loaded, 16)
                with act.Fori(0, NCH) as c:
                    hold(x_ready, c + 1)
                    for half in range(2):
                        last = nc.scalar.activation(halves(chunk(u, half, c)), px[:, half, :, 0:HB], ACT.Identity,
                                                    scale=W("cw", half * DCV + DCV - 1, 1), bias=W("cb", half, 1))
                    last.then_inc(tap0, 1)
                    hold(z_ready, c + 1)
                    for half in range(2):
                        last = nc.scalar.activation(halves(chunk(sz, half, c)), pz[:, half, :, 0:HB], ACT.Silu)
                    last.then_inc(z_done, 1)
                    hold(conv, 3 * c + 3)
                    last = nc.scalar.activation(u[:, :, ds(c * CH, CH)], u[:, :, ds(c * CH, CH)], ACT.Silu)
                    last.then_inc(u_ready, 1)
                    hold(xd_ready, c + 1)
                    nc.scalar.activation(halves(xd[:, ds(c * CH, CH)]), px[:, 0, :, 0:HB], ACT.Copy).then_inc(xd_done, 1)

            @block.vector
            def _(dve):
                with dve.Fori(0, NCH) as c:
                    dve.wait_ge(tap0, c + 1)
                    for j in range(1, DCV):
                        if j > 1:
                            dve.wait_ge(conv, 3 * c + (j - 1))
                        for half in range(2):
                            for k in range(2):
                                o = u[:, half, ds(c * CH + k * HB, HB)].rearrange("p (b s) -> p b s", s=S)[:, :, j:S]
                                x = px[:, half, k, 0:HB].rearrange("p (b s) -> p b s", s=S)[:, :, 0:S - j]
                                last = nc.vector.scalar_tensor_tensor(
                                    out=o, in0=x, scalar=W("cw", half * DCV + DCV - 1 - j, 1), in1=o,
                                    op0=ALU.mult, op1=ALU.add)
                        last.then_inc(conv, 1)

        with ExitStack() as c1:
            pd = psum(nc, c1, "pd", [128, 2, 2, BANK], F32)
            pe_ = psum(nc, c1, "pe", [128, 2, 2, BANK], F32)
            ser = sbuf(nc, c1, "ser", [128, 2, CH], F32)
            small = sbuf(nc, c1, "small", [128, 2, CH], mybir.dt.int8)
            soft = sbuf(nc, c1, "soft", [128, 2, 2, CH], F32)
            left = sbuf(nc, c1, "left", [128, CH])
            high = sbuf(nc, c1, "high", [128, CH], BF16)
            (d_ready, ac, x_done, soft_ready, dt_done, dc, pc) = c1.enter_context(
                stage(nc, "d_ready act_chain x_done soft_ready dt_done dve_chain pool_chain"))
            block = c1.enter_context(nc.Block())

            @block.gpsimd
            def _(pool):
                link = Chain(pool, pc)
                g = nc.gpsimd
                link(g.memset(bc[:, :], 0.0))
                for c in range(NCH):
                    at = slice(c * CH, (c + 1) * CH)
                    link(g.tensor_copy(high[:, :], xd[:, at]))
                    link(g.tensor_copy(bc[32:64, at], high[32:64, :]))
                    link(g.tensor_tensor(left[:, :], xd[:, at], high[:, :], ALU.subtract))
                    link(g.tensor_copy(high[:, :], left[:, :]))
                    link(g.tensor_copy(bc[64:96, at], high[64:96, :]))
                    link(g.tensor_tensor(bc[96:128, at], left[96:128, :], high[96:128, :], ALU.subtract))

            @block.tensor
            def _(pe):
                for c in range(NCH):
                    if c >= 1:
                        pe.wait_ge(x_done, c)
                    for half in range(2):
                        for k in range(2):
                            a = c * CH + k * HB
                            last = nc.tensor.matmul(pd[:, half, k, 0:HB], W("dw", half * 128, 128)[0:DTR, :],
                                                    xd[0:DTR, a:a + HB], start=True, stop=True)
                    last.then_inc(d_ready, 1)

            @block.scalar
            def _(act):
                link = Chain(act, ac)
                nc.scalar.preload_act_table_set("natural_log_exp_and_others")
                link(nc.scalar.activation(negA[:, :], W("alog"), ACT.Exp))
                link(nc.scalar.activation(negA[:, :], negA[:, :], ACT.Copy, scale=-1.0))
                for c in range(NCH):
                    act.wait_ge(x_done, c + 1)
                    if c >= 1:
                        act.wait_ge(dt_done, c)
                    s = soft[:, c % 2, :, :]
                    link(nc.scalar.activation(s, dt[:, :, c * CH:(c + 1) * CH], ACT.Abs))
                    e = pe_[:, :, :, 0:HB]
                    s4 = s.rearrange("p a (h n) -> p a h n", h=2)
                    link(nc.scalar.activation(e, s4, ACT.Exp, scale=-1.0))
                    nc.scalar.activation(s4, e, ACT.Ln, bias=1.0).then_inc(soft_ready, 1)

            @block.vector
            def _(dve):
                link = Chain(dve, dc)

                def biased(c):
                    dve.wait_ge(d_ready, c + 1)
                    for half in range(2):
                        last = nc.vector.tensor_scalar(halves(dt[:, half, c * CH:(c + 1) * CH]),
                                                       pd[:, half, :, 0:HB], W("db", half, 1), None, ALU.add)
                    last.then_inc(x_done, 1)

                biased(0)
                for c in range(NCH):
                    if c + 1 < NCH:
                        biased(c + 1)
                    dve.wait_ge(soft_ready, c + 1)
                    dve.wait_ge(x_done, c + 1)
                    for half in range(2):
                        e = pe_[:, half, :, 0:HB]
                        nc.vector.tensor_scalar(halves(small[:, half, :]), e, 1.0 / 32, None, ALU.is_lt)
                        last = nc.vector.tensor_scalar(halves(ser[:, half, :]), e, -0.25, None, ALU.mult)
                    link(last)
                    for a in (1.0 / 3, -0.5, 1.0):
                        for half in range(2):
                            t, e = halves(ser[:, half, :]), pe_[:, half, :, 0:HB]
                            last = nc.vector.scalar_tensor_tensor(out=e if a == 1.0 else t, in0=t, scalar=a, in1=e,
                                                                  op0=ALU.add, op1=ALU.mult)
                        link(last)
                    soft_c = soft[:, c % 2, :, :].rearrange("p a (h n) -> p a h n", h=2)
                    link(nc.vector.copy_predicated(soft_c, small[:, :, :].rearrange("p a (h n) -> p a h n", h=2),
                                                   pe_[:, :, :, 0:HB]))
                    d = dt[:, :, c * CH:(c + 1) * CH]
                    link(nc.vector.scalar_tensor_tensor(out=d, in0=d, scalar=0.0, in1=soft[:, c % 2, :, :],
                                                        op0=ALU.max, op1=ALU.add))
                    nc.vector.tensor_tensor(du[:, :, c * CH:(c + 1) * CH], d, u[:, :, c * CH:(c + 1) * CH],
                                            ALU.mult).then_inc(dt_done, 1)

        with ExitStack() as c1:
            pb = psum(nc, c1, "pb", [128, 2, BANK], F32)
            pcc = psum(nc, c1, "pcc", [128, 2, BANK], F32)
            py = psum(nc, c1, "py", [128, 2, 2, BANK], F32)
            Bs = sbuf(nc, c1, "Bs", [128, 4, CH], F32)
            dA = sbuf(nc, c1, "dA", [128, 2, 2, CH], F32)
            dBu = sbuf(nc, c1, "dBu", [128, 2, 2, CH], F32)
            hst = sbuf(nc, c1, "hst", [128, 4, 2 * CH], F32)
            hC = sbuf(nc, c1, "hC", [128, 2, 2, CH], F32)
            (z0, b_ready, b_kept, dBu_ready, c_ready, dA_ready, h_ready, c_used, y_added, y_skip, y_done, pe_passed,
             act_passed, pool_passed) = c1.enter_context(
                stage(nc, "dA_zeroed b_ready b_kept dBu_ready c_ready dA_ready h_ready c_used y_added y_skip y_done "
                          "pe_passed act_passed pool_passed"))
            block = c1.enter_context(nc.Block())

            @block.gpsimd
            def _(pool):
                hold = Hold(pool, pool_passed)
                nc.gpsimd.memset(dA[:, :, :, :], 0.0).then_inc(z0, 1)
                with pool.Fori(0, NCH) as c:
                    for n in range(DST):
                        i = c * DST + n
                        hold(b_kept, i + 2)
                        hold(h_ready, i + 1)
                        nc.gpsimd.tensor_tensor(dBu[:, n % 2, :, :], du[:, :, ds(c * CH, CH)],
                                                Bs[:, n % 4, :].unsqueeze(1).broadcast_to([128, 2, CH]),
                                                ALU.mult).then_inc(dBu_ready, 1)

            @block.tensor
            def _(pe):
                hold = Hold(pe, pe_passed)

                def spread(c, r, o, done):
                    for k in range(2):
                        last = nc.tensor.matmul(o[:, k, 0:HB], cst["row"][:, r, :], bc[:, ds(c * CH + k * HB, HB)],
                                                start=True, stop=True)
                    last.then_inc(done, 1)

                pe.sem_inc(y_added, 2)
                for n in range(3):
                    pe.wait_ge(b_kept, n + 1)
                    spread(0, n, pb, b_ready)
                with pe.Fori(0, NCH) as c:
                    def add(n):
                        for half in range(2):
                            for k in range(2):
                                last = nc.tensor.matmul(py[:, half, k, 0:HB], cst["ident"],
                                                        hC[:, n % 2, half, k * HB:(k + 1) * HB],
                                                        start=(n == 0), stop=(n == DST - 1))
                        last.then_inc(y_added, 1)

                    for n in range(DST):
                        i = c * DST + n
                        hold(b_kept, i + 4)
                        spread(c + (n + 3) // DST, (n + 3) % DST, pb, b_ready)
                        hold(c_used, i + 1)
                        spread(c, DST + n, pcc, c_ready)
                        if n == 1:
                            pe.wait_ge(y_skip, c + 1)
                        if n >= 1:
                            add(n - 1)
                    pe.wait_ge(c_used, c * DST + (DST + 1))
                    add(DST - 1)

            @block.scalar
            def _(act):
                hold = Hold(act, act_passed)

                def keep(k, step):
                    act.wait_ge(b_ready, step)
                    nc.scalar.activation(halves(Bs[:, k, :]), pb[:, :, 0:HB], ACT.Copy).then_inc(b_kept, 1)

                act.sem_inc(b_kept, 1)
                act.wait_ge(z0, 1)
                keep(0, 1)
                keep(1, 2)
                with act.Fori(0, NCH) as c:
                    for n in range(DST):
                        i = c * DST + n
                        hold(h_ready, i + 1)
                        for half in range(2):
                            o = dA[:, n % 2, half, :].rearrange("p (b s) -> p b s", s=S)[:, :, 1:S]
                            x = chunk(dt, half, c).rearrange("p (b s) -> p b s", s=S)[:, :, 1:S]
                            last = nc.scalar.activation(o, x, ACT.Exp, scale=negA[:, half * DST + n:half * DST + n + 1])
                        last.then_inc(dA_ready, 1)
                        keep((n + 2) % 4, i + 3)

            @block.vector
            def _(dve):
                dve.sem_inc(h_ready, 2)
                dve.sem_inc(c_used, 1)
                dve.sem_inc(y_skip, 1)
                with dve.Fori(0, NCH) as c:
                    def weigh(n):
                        i = c * DST + n
                        dve.wait_ge(h_ready, i + 3)
                        dve.wait_ge(c_ready, i + 1)
                        dve.wait_ge(y_added, i + 1)
                        nc.vector.tensor_tensor(
                            hC[:, n % 2, :, :].rearrange("p a (h n) -> p a h n", h=2),
                            hst[:, n % 4, :].rearrange("p (a h n) -> p a h n", a=2, h=2),
                            pcc[:, :, 0:HB].unsqueeze(1).broadcast_to([128, 2, 2, HB]), ALU.mult).then_inc(c_used, 1)

                    for n in range(DST):
                        i = c * DST + n
                        dve.wait_ge(dBu_ready, i + 1)
                        dve.wait_ge(dA_ready, i + 1)
                        nc.vector.tensor_tensor_scan(hst[:, n % 4, :], dA[:, n % 2, :, :].rearrange("p a n -> p (a n)"),
                                                     dBu[:, n % 2, :, :].rearrange("p a n -> p (a n)"), 0.0, ALU.mult,
                                                     ALU.add).then_inc(h_ready, 1)
                        if n >= 1:
                            weigh(n - 1)
                    weigh(DST - 1)
                    dve.wait_ge(y_added, c * DST + (DST + 2))
                    for half in range(2):
                        uc = halves(chunk(u, half, c))
                        last = nc.vector.scalar_tensor_tensor(out=uc, in0=uc, scalar=W("dp", half, 1),
                                                              in1=py[:, half, :, 0:HB], op0=ALU.mult, op1=ALU.add)
                    last.then_inc(y_skip, 1)
                    dve.wait_ge(y_skip, c + 2)
                    uc = u[:, :, ds(c * CH, CH)]
                    nc.vector.tensor_tensor(uc, uc, sz[:, :, ds(c * CH, CH)], ALU.mult).then_inc(y_done, 1)

        with ExitStack() as c1:
            po = psum(nc, c1, "po", [128, 2, 2, BANK], F32)
            (o_ready, o_added) = c1.enter_context(stage(nc, "o_ready o_added"))
            block = c1.enter_context(nc.Block())

            @block.tensor
            def _(pe):
                for c in range(NCH):
                    if c >= 2:
                        pe.wait_ge(o_added, c - 1)
                    for k in range(2):
                        for half in range(2):
                            a = c * CH + k * HB
                            last = nc.tensor.matmul(po[:, c % 2, k, 0:HB], W("wo", half * D, D), u[:, half, a:a + HB],
                                                    start=(half == 0), stop=(half == 1))
                    last.then_inc(o_ready, 1)

            @block.vector
            def _(dve):
                for c in range(NCH):
                    dve.wait_ge(o_ready, c + 1)
                    mc = halves(m[:, c * CH:(c + 1) * CH])
                    nc.vector.tensor_tensor(mc, mc, po[:, c % 2, :, 0:HB], ALU.add).then_inc(o_added, 1)
        layernorm(nc, cst, m, m, W("g"), W("b"))


def lstm_fusion(nc, cst, w_dram, x, m, hT):
    with ExitStack() as ctx:
        def sb(name, shape, dt=F32):
            return sbuf(nc, ctx, name, shape, dt)

        wih = sb("wih", [128, 2, 4, 2 * H2])
        whh = sb("whh", [128, 4, 2, H2])
        bias = sb("bias", [128, 4])
        bias2 = sb("bias2", [128, 4])
        fw = sb("fw", [128, 3, D])
        fb = sb("fb", [128, 1])
        hist = sb("hist", [128, S, NB])
        zero = sb("zero", [128, NB])
        gates = sb("gates", [128, 4, NB])
        cs = sb("cs", [128, NB])
        t1 = sb("t1", [128, NB])
        t2 = sb("t2", [128, NB])
        tc = sb("tc", [128, NB])
        pg = psum(nc, ctx, "pg", [128, 2, BANK], F32)
        pf = psum(nc, ctx, "pf", [128, 5, BANK], F32)
        (w_loaded, whh_loaded, whh_zeroed, ready, g_ready, g_used, t_ready, ac, dc, c_ready, tc_ready, h_ready, f_ready, pe_passed) = ctx.enter_context(
            stage(nc, "w_loaded whh_loaded whh_zeroed ready g_ready g_used t_ready act_chain dve_chain c_ready tc_ready h_ready f_ready pe_passed"))
        block = ctx.enter_context(nc.Block())
        wih_d, whh_d, b_d, fw_d, fb_d = w_dram

        @block.sync
        def _(sp):
            for dst, src in ((wih[:, :, :, :], wih_d), (bias[:, :], b_d[0]), (bias2[:, :], b_d[1]),
                             (fw[:, :, :], fw_d), (fb[:, :], fb_d)):
                sp.dma_start(dst, src).then_inc(w_loaded, 16)
            sp.wait_ge(whh_zeroed, 1)
            for d in range(2):
                sp.dma_start(whh[d * H2:(d + 1) * H2, :, d, :], whh_d[d]).then_inc(whh_loaded, 16)

        @block.gpsimd
        def _(pool):
            nc.gpsimd.memset(whh[:, :, :, :], 0.0).then_inc(whh_zeroed, 1)

        @block.tensor
        def _(pe):
            hold = Hold(pe, pe_passed)
            pe.wait_ge(w_loaded, 80)
            pe.wait_ge(whh_loaded, 32)
            pe.wait_ge(ready, 1)
            xs = x[:, :].rearrange("p (b s) -> p s b", s=S)

            def gate(g, rhs_f, rhs_b, h, slot, last_h):
                o = pg[:, slot, g * NB:(g + 1) * NB]
                nc.tensor.matmul(o, whh[:, g, :, :].rearrange("p d h -> p (d h)"), h, start=True, stop=False)
                nc.tensor.matmul(o, wih[:, 0, g, :], rhs_f, start=False, stop=False)
                return nc.tensor.matmul(o, wih[:, 1, g, :], rhs_b, start=False, stop=True)

            for g in range(4):
                last = gate(g, xs[:, 0, :], xs[:, S - 1, :], zero[:, :], 0, None)
            last.then_inc(g_ready, 1)
            with pe.Fori(1, S) as t:
                pe.wait_ge(h_ready, t)
                for g in range(4):
                    last = gate(g, xs[:, ds(t, 1), :].rearrange("p o b -> p (o b)"),
                                xs[:, ds(S - 1 - t, 1), :].rearrange("p o b -> p (o b)"),
                                hist[:, ds(t - 1, 1), :].rearrange("p o b -> p (o b)"), 0, None)
                last.then_inc(g_ready, 1)
            pe.wait_ge(h_ready, S)
            ms = m[:, :].rearrange("p (b s) -> p s b", s=S)
            for s in range(S):
                o = pf[:, s // 8, (s % 8) * NB:(s % 8 + 1) * NB]
                nc.tensor.matmul(o, fw[:, 0, :], ms[:, s, :], start=True, stop=False)
                nc.tensor.matmul(o, fw[:, 1, :], hist[:, s, :], start=False, stop=False)
                last = nc.tensor.matmul(o, fw[:, 2, :], hist[:, S - 1 - s, :], start=False, stop=True)
            last.then_inc(f_ready, 1)

        @block.scalar
        def _(act):
            nc.scalar.preload_act_table_set("sigmoid_and_others")
            act.wait_ge(ready, 1)
            with act.Fori(0, S) as t:
                act.wait_ge(g_ready, t + 1)
                for g, f in enumerate((ACT.Sigmoid, ACT.Sigmoid, ACT.Tanh, ACT.Sigmoid)):
                    last = nc.scalar.activation(gates[:, g, :], pg[:, 0, g * NB:(g + 1) * NB], f, bias=bias[:, g:g + 1])
                last.then_inc(t_ready, 1)
                act.wait_ge(c_ready, t + 1)
                nc.scalar.activation(tc[:, :], cs[:, :], ACT.Tanh).then_inc(tc_ready, 1)

        @block.vector
        def _(dve):
            link = Chain(dve, dc)
            dve.wait_ge(w_loaded, 80)
            link(nc.vector.memset(zero[:, :], 0.0))
            link(nc.vector.memset(cs[:, :], 0.0))
            nc.vector.tensor_tensor(bias[:, :], bias[:, :], bias2[:, :], ALU.add).then_inc(ready, 1)
            with link.loop(S, 2) as t:
                dve.wait_ge(t_ready, t + 1)
                link(nc.vector.tensor_tensor(t1[:, :], gates[:, 1, :], cs[:, :], ALU.mult))
                link(nc.vector.tensor_tensor(t2[:, :], gates[:, 0, :], gates[:, 2, :], ALU.mult))
                nc.vector.tensor_tensor(cs[:, :], t1[:, :], t2[:, :], ALU.add).then_inc(c_ready, 1)
                dve.wait_ge(tc_ready, t + 1)
                nc.vector.tensor_tensor(hist[:, ds(t, 1), :].rearrange("p o b -> p (o b)"), gates[:, 3, :], tc[:, :],
                                        ALU.mult).then_inc(h_ready, 1)
            dve.wait_ge(f_ready, 1)
            hs = hT[:, :].rearrange("p (b s) -> p s b", s=S)
            for q in range(5):
                n = min(8, S - 8 * q)
                o = hs[:, 8 * q:8 * q + n, :]
                nc.vector.scalar_tensor_tensor(out=o, in0=pf[:, q, 0:n * NB].rearrange("p (s b) -> p s b", b=NB),
                                               scalar=fb[:, :], in1=o, op0=ALU.add, op1=ALU.add)


def load(nc, *pairs):
    with ExitStack() as ctx:
        (loaded,) = ctx.enter_context(stage(nc, "loaded"))
        block = ctx.enter_context(nc.Block())

        @block.sync
        def _(sp):
            for dst, src in pairs:
                sp.dma_start(dst, src).then_inc(loaded, 16)
            sp.wait_ge(loaded, 16 * len(pairs))


def project_features(nc, x, out, w, bias, rows=D, residual=False):
    with ExitStack() as ctx:
        ps = psum(nc, ctx, "ps", [128, 2, 2, BANK], F32)
        (multiplied, kept) = ctx.enter_context(stage(nc, "multiplied kept"))
        block = ctx.enter_context(nc.Block())

        @block.tensor
        def _(pe):
            for c in range(NCH):
                if c >= 2:
                    pe.wait_ge(kept, c - 1)
                for k in range(2):
                    a = c * CH + k * HB
                    last = nc.tensor.matmul(ps[0:rows, c % 2, k, 0:HB], w, x[:, a:a + HB], start=True, stop=True)
                last.then_inc(multiplied, 1)

        if residual:
            @block.vector
            def _(dve):
                for c in range(NCH):
                    dve.wait_ge(multiplied, c + 1)
                    o = halves(out[:, c * CH:(c + 1) * CH])
                    nc.vector.scalar_tensor_tensor(out=o, in0=ps[0:rows, c % 2, :, 0:HB], scalar=bias, in1=o,
                                                   op0=ALU.add, op1=ALU.add).then_inc(kept, 1)
        else:
            @block.scalar
            def _(act):
                for c in range(NCH):
                    act.wait_ge(multiplied, c + 1)
                    o = halves(out[:, c * CH:(c + 1) * CH])
                    if bias is None:
                        nc.scalar.activation(o, ps[0:rows, c % 2, :, 0:HB], ACT.Copy).then_inc(kept, 1)
                    else:
                        nc.scalar.activation(o, ps[0:rows, c % 2, :, 0:HB], ACT.Identity, bias=bias).then_inc(kept, 1)


def project_tokens(nc, x, T, w, out, bias):
    K, n = w.shape
    with ExitStack() as ctx:
        xt = sbuf(nc, ctx, "xt", [K, 2, T], F32)
        ps = psum(nc, ctx, "ps", [128, 2, BANK], F32)
        (st0, st1, mu0, mu1, kp0, kp1, act_passed, dve_passed) = ctx.enter_context(
            stage(nc, "staged0 staged1 multiplied0 multiplied1 kept0 kept1 act_passed dve_passed"))
        staged, multiplied, kept = (st0, st1), (mu0, mu1), (kp0, kp1)
        block = ctx.enter_context(nc.Block())

        @block.scalar
        def _(act):
            hold = Hold(act, act_passed)
            with act.Fori(0, NT // T // 2) as i:
                for j in range(2):
                    hold(multiplied[j], i)
                    nc.scalar.activation(xt[:, j, :], x[0:K, ds((2 * i + j) * T, T)], ACT.Copy).then_inc(staged[j], 1)

        @block.tensor
        def _(pe):
            with pe.Fori(0, NT // T // 2) as i:
                for j in range(2):
                    pe.wait_ge(kept[j], i)
                    pe.wait_ge(staged[j], i + 1)
                    nc.tensor.matmul(ps[0:T, j, 0:n], xt[:, j, :], w, start=True, stop=True).then_inc(multiplied[j], 1)

        @block.vector
        def _(dve):
            hold = Hold(dve, dve_passed)
            with dve.Fori(0, NT // T // 2) as i:
                for j in range(2):
                    hold(multiplied[j], i + 1)
                    o = out[:, ds(2 * i + j, 1), :].rearrange("p o n -> p (o n)")
                    if bias is None:
                        nc.vector.tensor_copy(o, ps[0:T, j, 0:n]).then_inc(kept[j], 1)
                    else:
                        nc.vector.tensor_tensor(o, ps[0:T, j, 0:n], bias, ALU.add).then_inc(kept[j], 1)


AT = 2 * S
NAT = NT // AT
G = 4
NH, HD = 8, 16


def channel_attention(nc, cst, a, x, hT):
    with ExitStack() as ctx:
        def sb(name, shape, dt=F32):
            return sbuf(nc, ctx, name, shape, dt)

        w = sb("w", [128, 4 * D])
        bqk = sb("bqk", [AT, 2 * D])
        cols = sb("cols", [128, 2])
        hmask = sb("hmask", [128, D])
        smask = sb("smask", [AT, 2])
        qk = sb("qk", [AT, NAT, 2 * D])
        vT = sb("vT", [128, NT])
        oT = sb("oT", [128, NT])
        load(nc, (w[:, :], a["ca_w"]), (bqk[:, :], a["ca_bqk"]), (cols[:, :], a["ca_b"]),
             (hmask[:, :], a["c_headmask"]), (smask[:, :], a["c_seqmask"]))
        project_tokens(nc, x, AT, w[:, 0:2 * D], qk, bqk[:, :])
        project_features(nc, x, vT, w[:, 2 * D:3 * D], cols[:, 0:1])
        with ExitStack() as c1:
            NG = NAT * 2 * NH
            sq = sbuf(nc, c1, "sq", [AT, NAT, 2 * D])
            r = sbuf(nc, c1, "r", [AT, NG])
            (squared, summed, ac, r_ready, dc) = c1.enter_context(stage(nc, "squared summed act_chain r_ready dve_chain"))
            block = c1.enter_context(nc.Block())

            @block.scalar
            def _(act):
                link = Chain(act, ac)
                nc.scalar.activation(sq[:, :, :], qk[:, :, :], ACT.Square).then_inc(squared, 1)
                act.wait_ge(summed, 1)
                link(nc.scalar.activation(r[:, :], r[:, :], ACT.Ln))
                nc.scalar.activation(r[:, :], r[:, :], ACT.Exp, scale=-0.5).then_inc(r_ready, 1)

            @block.vector
            def _(dve):
                link = Chain(dve, dc)
                dve.wait_ge(squared, 1)
                link(nc.vector.tensor_reduce(r[:, :], sq[:, :, :].rearrange("p t (g d) -> p (t g) d", d=HD), AX.X, ALU.add))
                nc.vector.tensor_scalar(r[:, :], r[:, :], 1e-12, None, ALU.max).then_inc(summed, 1)
                dve.wait_ge(r_ready, 1)
                q = r[:, :].rearrange("p (t h) -> p t h", h=2 * NH)[:, :, 0:NH]
                link(nc.vector.tensor_scalar(q, q, HD ** -0.5, None, ALU.mult))
                g = qk[:, :, :].rearrange("p t (g d) -> p (t g) d", d=HD)
                link(nc.vector.tensor_tensor(g, g, r[:, :].unsqueeze(2).broadcast_to([AT, NG, HD]), ALU.mult))
        with ExitStack() as c1:
            q = sbuf(nc, c1, "q", [AT, G, D])
            kx = sbuf(nc, c1, "kx", [AT, G, 2, D])
            sc = sbuf(nc, c1, "sc", [128, 2 * G, D])
            mx = sbuf(nc, c1, "mx", [128, 2 * G])
            sm = sbuf(nc, c1, "sm", [128, 2 * G])
            ps = psum(nc, c1, "ps", [128, 2 * G, D])
            po = psum(nc, c1, "po", [128, BANK])
            (q_staged, kx_ready, scored, centered, exped, a_ready, out_ready, out_kept, dc, act_passed, dve_passed, pe_passed) = c1.enter_context(
                stage(nc, "q_staged kx_ready scored centered exped a_ready out_ready out_kept dve_chain act_passed dve_passed pe_passed"))
            block = c1.enter_context(nc.Block())

            @block.scalar
            def _(act):
                hold = Hold(act, act_passed)
                with act.Fori(0, NAT // G) as i:
                    hold(scored, i)
                    nc.scalar.activation(q[:, :, :], qk[:, ds(i * G, G), 0:D], ACT.Copy).then_inc(q_staged, 1)
                    act.wait_ge(centered, i + 1)
                    nc.scalar.activation(sc[:, :, :], sc[:, :, :], ACT.Exp).then_inc(exped, 1)
                    hold(out_ready, i + 1)
                    nc.scalar.activation(oT[:, ds(i * G * AT, G * AT)], po[:, 0:G * AT], ACT.Copy).then_inc(out_kept, 1)

            @block.tensor
            def _(pe):
                hold = Hold(pe, pe_passed)
                with pe.Fori(0, NAT // G) as i:
                    pe.wait_ge(q_staged, i + 1)
                    pe.wait_ge(kx_ready, i + 1)
                    for t in range(G):
                        last = nc.tensor.matmul(ps[:, 2 * t:2 * t + 2, :], q[:, t, :], kx[:, t, :, :],
                                                start=True, stop=True)
                    last.then_inc(scored, 1)
                    hold(a_ready, i + 1)
                    pe.wait_ge(out_kept, i)
                    for s in range(2 * G):
                        last = nc.tensor.matmul(po[:, s * S:(s + 1) * S], sc[:, s, :], vT[:, ds((i * 2 * G + s) * S, S)],
                                                start=True, stop=True)
                    last.then_inc(out_ready, 1)

            @block.vector
            def _(dve):
                hold = Hold(dve, dve_passed)
                link = Chain(dve, dc)
                with link.loop(NAT // G, 6) as i:
                    hold(scored, i)
                    for s in range(2):
                        last = nc.vector.tensor_scalar(kx[:, :, s, :], qk[:, ds(i * G, G), D:2 * D], smask[:, s:s + 1], None, ALU.mult)
                    last.then_inc(kx_ready, 1)
                    hold(scored, i + 1)
                    dve.wait_ge(out_ready, i)
                    link(nc.vector.tensor_tensor(sc[:, :, :], ps[:, :, :], hmask[:, :].unsqueeze(1).broadcast_to([128, 2 * G, D]), ALU.add))
                    link(nc.vector.tensor_reduce(mx[:, :], sc[:, :, :], AX.X, ALU.max))
                    nc.vector.tensor_tensor(sc[:, :, :], sc[:, :, :], mx[:, :].unsqueeze(2).broadcast_to([128, 2 * G, D]),
                                            ALU.subtract).then_inc(centered, 1)
                    dve.wait_ge(exped, i + 1)
                    link(nc.vector.tensor_reduce(sm[:, :], sc[:, :, :], AX.X, ALU.add))
                    link(nc.vector.reciprocal(sm[:, :], sm[:, :]))
                    link(nc.vector.tensor_tensor(sc[:, :, :], sc[:, :, :], sm[:, :].unsqueeze(2).broadcast_to([128, 2 * G, D]), ALU.mult))
                    nc.vector.tensor_copy(mx[:, 0:1], sm[:, 0:1]).then_inc(a_ready, 1)
                    link(nc.vector.tensor_copy(mx[:, 1:2], sm[:, 1:2]))
        project_features(nc, oT, hT, w[:, 3 * D:4 * D], cols[:, 1:2], residual=True)


def frame_attention(nc, cst, a, x, hT):
    with ExitStack() as ctx:
        def sb(name, shape, dt=F32):
            return sbuf(nc, ctx, name, shape, dt)

        w = sb("w", [128, 3 * D])
        bmask = sb("bmask", [AT, AT])
        qT = sb("qT", [128, NT])
        kT = sb("kT", [128, NT])
        v = sb("v", [AT, NAT, D])
        load(nc, (w[:, :], a["fa_w"]), (bmask[:, :], a["c_blockmask"]))
        project_features(nc, x, qT, w[:, 0:D], None)
        project_features(nc, x, kT, w[:, D:2 * D], None)
        project_tokens(nc, x, AT, w[:, 2 * D:3 * D], v, None)
        with ExitStack() as c1:
            q = sbuf(nc, c1, "q", [128, G, AT])
            vs = sbuf(nc, c1, "vs", [AT, G, D])
            sc = sbuf(nc, c1, "sc", [AT, G, AT])
            zr = sbuf(nc, c1, "zr", [AT, G, AT])
            pT = sbuf(nc, c1, "pT", [AT, G, AT])
            mx = sbuf(nc, c1, "mx", [AT, G])
            sm = sbuf(nc, c1, "sm", [AT, G])
            ps = psum(nc, c1, "ps", [AT, BANK])
            pt = psum(nc, c1, "pt", [AT, BANK])
            po = psum(nc, c1, "po", [128, BANK])
            (staged, scored, centered, exped, p_ready, turned, pT_ready, out_ready, out_added, dc, act_passed, pe_passed) = c1.enter_context(
                stage(nc, "staged scored centered exped p_ready turned pT_ready out_ready out_added dve_chain act_passed pe_passed"))
            block = c1.enter_context(nc.Block())

            def tiles(t):
                return t[:, 0:G * AT].rearrange("p (g n) -> p g n", g=G)

            @block.scalar
            def _(act):
                hold = Hold(act, act_passed)
                with act.Fori(0, NAT // G) as i:
                    hold(out_ready, i)
                    nc.scalar.activation(vs[:, :, :], v[:, ds(i * G, G), :], ACT.Copy)
                    nc.scalar.activation(q[:, :, :].rearrange("p g n -> p (g n)"), qT[:, ds(i * G * AT, G * AT)],
                                         ACT.Copy).then_inc(staged, 1)
                    act.wait_ge(centered, i + 1)
                    nc.scalar.activation(sc[:, :, :], sc[:, :, :], ACT.Exp).then_inc(exped, 1)
                    act.wait_ge(turned, i + 1)
                    nc.scalar.activation(pT[:, :, :], tiles(pt), ACT.Copy).then_inc(pT_ready, 1)

            @block.tensor
            def _(pe):
                hold = Hold(pe, pe_passed)
                with pe.Fori(0, NAT // G) as i:
                    hold(staged, i + 1)
                    for t in range(G):
                        last = nc.tensor.matmul(ps[:, t * AT:(t + 1) * AT], q[:, t, :], kT[:, ds((i * G + t) * AT, AT)],
                                                start=True, stop=True)
                    last.then_inc(scored, 1)
                    pe.wait_ge(p_ready, i + 1)
                    for t in range(G):
                        last = nc.tensor.transpose(pt[:, t * AT:(t + 1) * AT], sc[:, t, :], cst["ident"][0:AT, 0:AT])
                    last.then_inc(turned, 1)
                    pe.wait_ge(pT_ready, i + 1)
                    pe.wait_ge(out_added, i)
                    for t in range(G):
                        last = nc.tensor.matmul(po[:, t * AT:(t + 1) * AT], vs[:, t, :], pT[:, t, :], start=True, stop=True)
                    last.then_inc(out_ready, 1)

            @block.vector
            def _(dve):
                link = Chain(dve, dc)
                with link.loop(NAT // G, 7) as i:
                    dve.wait_ge(scored, i + 1)
                    dve.wait_ge(turned, i)
                    link(nc.vector.tensor_scalar(sc[:, :, :], tiles(ps), D ** -0.5, None, ALU.mult))
                    link(nc.vector.tensor_scalar(zr[:, :, :], sc[:, :, :], 0.0, 1e-10, ALU.is_equal, ALU.mult))
                    link(nc.vector.tensor_tensor(sc[:, :, :], sc[:, :, :], zr[:, :, :], ALU.add))
                    link(nc.vector.tensor_tensor(sc[:, :, :], sc[:, :, :], bmask[:, :].unsqueeze(1).broadcast_to([AT, G, AT]), ALU.add))
                    link(nc.vector.tensor_reduce(mx[:, :], sc[:, :, :], AX.X, ALU.max))
                    nc.vector.tensor_tensor(sc[:, :, :], sc[:, :, :], mx[:, :].unsqueeze(2).broadcast_to([AT, G, AT]),
                                            ALU.subtract).then_inc(centered, 1)
                    dve.wait_ge(exped, i + 1)
                    link(nc.vector.tensor_reduce(sm[:, :], sc[:, :, :], AX.X, ALU.add))
                    link(nc.vector.reciprocal(sm[:, :], sm[:, :]))
                    nc.vector.tensor_tensor(sc[:, :, :], sc[:, :, :], sm[:, :].unsqueeze(2).broadcast_to([AT, G, AT]),
                                            ALU.mult).then_inc(p_ready, 1)
                    dve.wait_ge(out_ready, i + 1)
                    o = hT[:, ds(i * G * AT, G * AT)]
                    nc.vector.tensor_tensor(o, po[:, 0:G * AT], o, ALU.add).then_inc(out_added, 1)


NST = 64


def state_space(nc, cst, a, x, hT):
    with ExitStack() as ctx:
        def sb(name, shape, dt=F32):
            return sbuf(nc, ctx, name, shape, dt)

        p = sb("p", [128, 7 * NST + 2])
        fc = sb("fc", [128, 3, NST])
        e = sb("e", [128, 2, NST])
        e2 = sb("e2", [128, 2, NST])
        di = sb("di", [128, NST])
        qd = sb("qd", [128, NST])
        st = sb("st", [128, 2, NST])
        bd = sb("bd", [128, NST])
        prod = sb("prod", [128, 4, NST])
        g = sb("g", [128, 4])
        kc = sb("kc", [128, 4])
        t1 = sb("t1", [128, 2])
        dt = sb("dt", [128, 1])
        dots = sb("dots", [128, S, 3])
        xp = sb("xp", [128, NB, 2 * S - 1])
        diag = sb("diag", [128, 2, 128])
        py = psum(nc, ctx, "py", [128, 8, BANK])
        load(nc, (p[:, :], a["ss_w"]))
        L, Pl, Pr = p[:, 0:NST], p[:, NST:3 * NST].rearrange("p (k n) -> p k n", k=2), p[:, 3 * NST:5 * NST].rearrange("p (k n) -> p k n", k=2)
        B, C = p[:, 5 * NST:6 * NST], p[:, 6 * NST:7 * NST]
        log_dt, Dp = p[:, 7 * NST:7 * NST + 1], p[:, 7 * NST + 1:7 * NST + 2]
        with ExitStack() as c1:
            (ac, exped, dc, padded, taps) = c1.enter_context(stage(nc, "act_chain exped dve_chain padded taps"))
            block = c1.enter_context(nc.Block())

            @block.scalar
            def _(act):
                nc.scalar.activation(dt[:, :], log_dt, ACT.Exp)
                nc.scalar.activation(L, L, ACT.Exp).then_inc(exped, 1)

            @block.gpsimd
            def _(pool):
                nc.gpsimd.memset(xp[:, :, 0:S - 1], 0.0).then_inc(padded, 1)
                nc.gpsimd.tensor_copy(xp[:, :, S - 1:2 * S - 1], x[:, :].rearrange("p (b s) -> p b s", s=S)).then_inc(padded, 1)

            @block.vector
            def _(dve):
                link = Chain(dve, dc)
                v = nc.vector
                dve.wait_ge(exped, 1)
                b2 = [128, 2, NST]
                link(v.tensor_scalar(di[:, :], L, dt[:, :], 0.5, ALU.mult, ALU.mult))
                link(v.tensor_scalar(di[:, :], di[:, :], 1.0, None, ALU.add))
                link(v.reciprocal(di[:, :], di[:, :]))
                link(v.tensor_scalar(Pl, Pl, dt[:, :], 0.5, ALU.mult, ALU.mult))
                link(v.tensor_tensor(e2[:, :, :], Pl, di[:, :].unsqueeze(1).broadcast_to(b2), ALU.mult))
                link(v.tensor_tensor(fc[:, 0:2, :], Pr, di[:, :].unsqueeze(1).broadcast_to(b2), ALU.mult))
                link(v.tensor_copy(fc[:, 2, :], C))
                for i in range(2):
                    link(v.tensor_tensor(prod[:, 2 * i:2 * i + 2, :], fc[:, i:i + 1, :].broadcast_to(b2), Pl, ALU.mult))
                link(v.tensor_reduce(g[:, :], prod[:, :, :], AX.X, ALU.add))
                link(v.tensor_scalar(kc[:, 0:1], g[:, 3:4], -1.0, 1.0, ALU.mult, ALU.add))
                link(v.tensor_scalar(kc[:, 3:4], g[:, 0:1], -1.0, 1.0, ALU.mult, ALU.add))
                link(v.tensor_copy(kc[:, 1:3], g[:, 1:3]))
                link(v.tensor_tensor(t1[:, 0:1], kc[:, 0:1], kc[:, 3:4], ALU.mult))
                link(v.tensor_tensor(t1[:, 1:2], kc[:, 1:2], kc[:, 2:3], ALU.mult))
                link(v.tensor_tensor(t1[:, 0:1], t1[:, 0:1], t1[:, 1:2], ALU.subtract))
                link(v.reciprocal(t1[:, 0:1], t1[:, 0:1]))
                link(v.tensor_scalar(kc[:, :], kc[:, :], t1[:, 0:1], None, ALU.mult))
                for j in range(2):
                    link(v.tensor_scalar(e[:, j, :], e2[:, 0, :], kc[:, j:j + 1], None, ALU.mult))
                    link(v.scalar_tensor_tensor(out=e[:, j, :], in0=e2[:, 1, :], scalar=kc[:, 2 + j:3 + j], in1=e[:, j, :],
                                                op0=ALU.mult, op1=ALU.add))

                def dot(s, out):
                    link(v.tensor_tensor(prod[:, 0:3, :], fc[:, :, :], s.unsqueeze(1).broadcast_to([128, 3, NST]), ALU.mult))
                    link(v.tensor_reduce(out, prod[:, 0:3, :], AX.X, ALU.add))

                link(v.tensor_scalar(bd[:, :], B, dt[:, :], None, ALU.mult))
                dot(bd[:, :], kc[:, 0:3])
                link(v.tensor_tensor(st[:, 0, :], bd[:, :], di[:, :], ALU.mult))
                for j in range(2):
                    link(v.scalar_tensor_tensor(out=st[:, 0, :], in0=e[:, j, :], scalar=kc[:, j:j + 1], in1=st[:, 0, :],
                                                op0=ALU.mult, op1=ALU.add))
                link(v.tensor_scalar(qd[:, :], di[:, :], 2.0, -1.0, ALU.mult, ALU.add))
                link(v.tensor_scalar(e[:, :, :], e[:, :, :], 2.0, None, ALU.mult))
                with link.loop(S, 5) as t:
                    d = dots[:, ds(t, 1), :].rearrange("p o n -> p (o n)")
                    dot(st[:, 0, :], d)
                    link(v.tensor_tensor(st[:, 0, :], st[:, 0, :], qd[:, :], ALU.mult))
                    for j in range(2):
                        link(v.scalar_tensor_tensor(out=st[:, 0, :], in0=e[:, j, :], scalar=d[:, j:j + 1], in1=st[:, 0, :],
                                                    op0=ALU.mult, op1=ALU.add))
                link(v.tensor_tensor(dots[:, 0, 2:3], dots[:, 0, 2:3], Dp, ALU.add))
        with ExitStack() as c1:
            (d0, d1, u0, u1, summed, dc) = c1.enter_context(stage(nc, "diag_ready0 diag_ready1 diag_used0 diag_used1 summed dve_chain"))
            diag_ready, diag_used = (d0, d1), (u0, u1)
            block = c1.enter_context(nc.Block())

            @block.vector
            def _(dve):
                def build(j, i, t):
                    dve.wait_ge(diag_used[j], i)
                    nc.vector.tensor_scalar(diag[:, j, :], cst["ident"], t.rearrange("p o n -> p (o n)"), None,
                                            ALU.mult).then_inc(diag_ready[j], 1)

                with dve.Fori(0, (S - 1) // 2) as i:
                    for j in range(2):
                        build(j, i, dots[:, ds(2 * i + j, 1), 2:3])
                build(0, (S - 1) // 2, dots[:, S - 1:S, 2:3])
                dve.wait_ge(summed, 1)
                for q in range(8):
                    o = hT[:, q * HB:(q + 1) * HB]
                    nc.vector.tensor_tensor(o, py[:, q, 0:HB], o, ALU.add)

            @block.tensor
            def _(pe):
                def tap(j, i, t, first, final):
                    pe.wait_ge(diag_ready[j], i + 1)
                    for q in range(8):
                        at = ds(S - 1 - t, S) if not isinstance(t, int) else slice(S - 1 - t, 2 * S - 1 - t)
                        last = nc.tensor.matmul(py[:, q, 0:HB], diag[:, j, :], xp[:, 8 * q:8 * q + 8, at],
                                                start=first, stop=final)
                    return last

                tap(0, 0, 0, True, False).then_inc(diag_used[0], 1)
                tap(1, 0, 1, False, False).then_inc(diag_used[1], 1)
                with pe.Fori(1, (S - 1) // 2) as i:
                    for j in range(2):
                        tap(j, i, 2 * i + j, False, False).then_inc(diag_used[j], 1)
                tap(0, (S - 1) // 2, S - 1, False, True).then_inc(summed, 1)


BIG = 1024.0


def route(nc, a, l, E, K, oh, gate, prob):
    with ExitStack() as ctx:
        iota = sbuf(nc, ctx, "iota", [TT, E])
        cand = sbuf(nc, ctx, "cand", [TT, NTT, E])
        left = sbuf(nc, ctx, "left", [TT, NTT, E])
        mx = sbuf(nc, ctx, "mx", [TT, 2, NTT])
        first = sbuf(nc, ctx, "first", [TT, NTT])
        load(nc, (iota[:, :], a["c_iota"][0:TT, 0:E]))
        (dc, ready, exped) = ctx.enter_context(stage(nc, "dve_chain ready exped"))
        block = ctx.enter_context(nc.Block())
        full = [TT, NTT, E]

        def over(t):
            return t.unsqueeze(2).broadcast_to(full)

        @block.vector
        def _(dve):
            link = Chain(dve, dc)
            v = nc.vector
            io = iota[:, :].unsqueeze(1).broadcast_to(full)
            src = l
            for k in range(K):
                link(v.tensor_reduce(mx[:, k, :], src[:, :, :], AX.X, ALU.max))
                link(v.tensor_tensor(cand[:, :, :], src[:, :, :], over(mx[:, k, :]), ALU.is_equal))
                link(v.tensor_scalar(cand[:, :, :], cand[:, :, :], -BIG, BIG, ALU.mult, ALU.add))
                link(v.tensor_tensor(cand[:, :, :], cand[:, :, :], io, ALU.add))
                link(v.tensor_reduce(first[:, :], cand[:, :, :], AX.X, ALU.min))
                link(v.tensor_tensor(oh[k][:, :, :], io, over(first[:, :]), ALU.is_equal))
                if k + 1 < K:
                    link(v.tensor_scalar(left[:, :, :], oh[k][:, :, :], -1e30, None, ALU.mult))
                    link(v.tensor_tensor(left[:, :, :], left[:, :, :], l[:, :, :], ALU.add))
                    src = left
            if prob:
                v.tensor_tensor(cand[:, :, :], l[:, :, :], over(mx[:, 0, :]), ALU.subtract).then_inc(ready, 1)
                dve.wait_ge(exped, 1)
                link(v.tensor_reduce(first[:, :], cand[:, :, :], AX.X, ALU.add))
                link(v.reciprocal(gate[0][:, :], first[:, :]))
            else:
                v.tensor_tensor(gate[1][:, :], mx[:, 1, :], mx[:, 0, :], ALU.subtract).then_inc(ready, 1)
                dve.wait_ge(exped, 1)
                link(v.tensor_scalar(first[:, :], gate[1][:, :], 1.0, None, ALU.add))
                link(v.reciprocal(gate[0][:, :], first[:, :]))
                link(v.tensor_tensor(gate[1][:, :], gate[1][:, :], gate[0][:, :], ALU.mult))

        @block.scalar
        def _(act):
            act.wait_ge(ready, 1)
            t = cand[:, :, :] if prob else gate[1][:, :]
            nc.scalar.activation(t, t, ACT.Exp).then_inc(exped, 1)


def token_rows(nc, cst, x, out):
    with ExitStack() as ctx:
        xt = sbuf(nc, ctx, "xt", [D, 2, TT])
        ps = psum(nc, ctx, "ps", [TT, 2, BANK])
        (st0, st1, t0, t1, kp0, kp1, act_passed, dve_passed) = ctx.enter_context(
            stage(nc, "staged0 staged1 turned0 turned1 kept0 kept1 act_passed dve_passed"))
        staged, turned, kept = (st0, st1), (t0, t1), (kp0, kp1)
        block = ctx.enter_context(nc.Block())

        @block.scalar
        def _(act):
            hold = Hold(act, act_passed)
            with act.Fori(0, NTT // 2) as i:
                for j in range(2):
                    hold(turned[j], i)
                    nc.scalar.activation(xt[:, j, :], x[:, ds((2 * i + j) * TT, TT)], ACT.Copy).then_inc(staged[j], 1)

        @block.tensor
        def _(pe):
            with pe.Fori(0, NTT // 2) as i:
                for j in range(2):
                    pe.wait_ge(kept[j], i)
                    pe.wait_ge(staged[j], i + 1)
                    nc.tensor.transpose(ps[:, j, 0:D], xt[:, j, :], cst["ident"]).then_inc(turned[j], 1)

        @block.vector
        def _(dve):
            hold = Hold(dve, dve_passed)
            with dve.Fori(0, NTT // 2) as i:
                for j in range(2):
                    hold(turned[j], i + 1)
                    nc.vector.tensor_copy(out[:, ds(2 * i + j, 1), :].rearrange("p o n -> p (o n)"), ps[:, j, 0:D]).then_inc(kept[j], 1)


ST = 128


def mixture(nc, cst, a, key, x, logits, out, E, K, F, act_fn, prob, capacity=None):
    NTILE = (K * NT + E * (ST - 1)) // ST
    NTILE += NTILE % 2
    NSLOT = NTILE * ST
    W1, W2, B1 = (F, F, F // 128) if F else (D, 0, 0)
    WE = W1 + W2 + B1
    FC = F // 128
    w_dram, b_dram = a[key + "_w"], a[key + "_b"]
    xs = nc.dram_tensor(unique(nc, "slots_in"), [NSLOT, D], F32, kind="Internal").ap()
    ys = nc.dram_tensor(unique(nc, "slots_out"), [NSLOT, D], F32, kind="Internal").ap()
    with ExitStack() as ctx:
        def sb(name, shape, dt=F32):
            return sbuf(nc, ctx, name, shape, dt)

        oh = [sb(f"oh{k}", [TT, NTT, E]) for k in range(K)]
        gate = [sb(f"gate{k}", [TT, NTT]) for k in range(K)]
        keepg = sb("keepg", [TT, 2, NTT])
        slot = [sb(f"slot{k}", [TT, NTT], I32) for k in range(K)]
        eid = sb("eid", [1, NTILE], I32)
        rows = sb("rows", [TT, NTT, D])
        route(nc, a, logits, E, K, oh, gate, prob)
        token_rows(nc, cst, x, rows)

        with ExitStack() as c1:
            NBK = -(-NTT * E // BANK)
            comb = sbuf(nc, c1, "comb", [TT, NTT * E])
            rank = sbuf(nc, c1, "rank", [TT, NTT, E])
            tot = sbuf(nc, c1, "tot", [TT, E, NTT])
            keep_t = sbuf(nc, c1, "keep_t", [TT, E, NTT])
            incl = sbuf(nc, c1, "incl", [TT, E, NTT])
            tri = sbuf(nc, c1, "tri", [TT, TT])
            ones = sbuf(nc, c1, "ones", [TT, TT])
            tf = sbuf(nc, c1, "tf", [TT, 4, E])
            ti = sbuf(nc, c1, "ti", [TT, E], I32)
            it = sbuf(nc, c1, "it", [1, NTILE])
            cmp = sbuf(nc, c1, "cmp", [1, NTILE, E])
            ef = sbuf(nc, c1, "ef", [1, NTILE])
            sf = sbuf(nc, c1, "sf", [TT, NTT])
            pr = psum(nc, c1, "pr", [TT, NBK * BANK])
            pt = psum(nc, c1, "pt", [TT, NBK * BANK])
            load(nc, (tri[:, :], a["c_tri"]), (keep_t[:, :, :], a["c_carry"][:, 0:E * NTT].rearrange("p (e t) -> p e t", e=E)),
                 (it[:, :], a["c_iota"][0:1, 0:NTILE]))
            (dc, combined, counted) = c1.enter_context(stage(nc, "dve_chain combined counted"))
            block = c1.enter_context(nc.Block())

            @block.tensor
            def _(pe):
                pe.wait_ge(combined, 1)
                for lhs, o in ((tri, pr), (ones, pt)):
                    for q in range(NBK):
                        n = min(BANK, NTT * E - q * BANK)
                        last = nc.tensor.matmul(o[:, q * BANK:q * BANK + n], lhs[:, :], comb[:, q * BANK:q * BANK + n],
                                                start=True, stop=True)
                last.then_inc(counted, 1)

            @block.vector
            def _(dve):
                link = Chain(dve, dc)
                v = nc.vector
                cb = comb[:, :].rearrange("p (t e) -> p t e", e=E)
                link(v.memset(ones[:, :], 1.0))
                if K == 2:
                    v.tensor_tensor(cb, oh[0][:, :, :], oh[1][:, :, :], ALU.add).then_inc(combined, 1)
                else:
                    v.tensor_copy(cb, oh[0][:, :, :]).then_inc(combined, 1)
                dve.wait_ge(counted, 1)
                link(v.tensor_copy(tot[:, :, :], pt[:, 0:NTT * E].rearrange("p (t e) -> p e t", e=E)))
                flat = "p e t -> p (e t)"
                link(v.tensor_tensor_scan(incl[:, :, :].rearrange(flat), keep_t[:, :, :].rearrange(flat),
                                          tot[:, :, :].rearrange(flat), 0.0, ALU.mult, ALU.add))
                link(v.tensor_tensor(tot[:, :, :], incl[:, :, :], tot[:, :, :], ALU.subtract))
                link(v.tensor_tensor(rank[:, :, :], pr[:, 0:NTT * E].rearrange("p (t e) -> p t e", e=E),
                                     tot[:, :, :].rearrange("p e t -> p t e"), ALU.add))
                n_e = incl[:, :, NTT - 1]
                link(v.tensor_scalar(ti[:, :], n_e, float(ST - 1), None, ALU.add))
                link(v.tensor_scalar(ti[:, :], ti[:, :], ST.bit_length() - 1, None, ALU.logical_shift_right))
                link(v.tensor_copy(tf[:, 0, :], ti[:, :]))
                link(v.memset(tf[:, 1, :], 1.0))
                link(v.tensor_tensor_scan(tf[:, 2, :], tf[:, 1, :], tf[:, 0, :], 0.0, ALU.mult, ALU.add))
                link(v.tensor_tensor(tf[:, 3, :], tf[:, 2, :], tf[:, 0, :], ALU.subtract))
                if capacity is not None:
                    link(v.tensor_tensor(cb, rank[:, :, :], oh[0][:, :, :], ALU.mult))
                    link(v.tensor_reduce(sf[:, :], cb, AX.X, ALU.add))
                    link(v.tensor_scalar(sf[:, :], sf[:, :], float(capacity), None, ALU.is_le))
                    link(v.tensor_tensor(keepg[:, 0, :], sf[:, :], gate[0][:, :], ALU.mult))
                    link(v.tensor_tensor(keepg[:, 1, :], gate[0][:, :], keepg[:, 0, :], ALU.subtract))
                link(v.tensor_scalar(tf[:, 1, :], tf[:, 3, :], float(ST), -1.0, ALU.mult, ALU.add))
                link(v.tensor_tensor(rank[:, :, :], rank[:, :, :], tf[:, 1:2, :].broadcast_to([TT, NTT, E]), ALU.add))
                for k in range(K):
                    link(v.tensor_tensor(cb, rank[:, :, :], oh[k][:, :, :], ALU.mult))
                    link(v.tensor_reduce(sf[:, :], cb, AX.X, ALU.add))
                    link(v.tensor_copy(slot[k][:, :], sf[:, :]))
                link(v.tensor_tensor(cmp[:, :, :], tf[0:1, 2:3, :].broadcast_to([1, NTILE, E]),
                                     it[:, :].unsqueeze(2).broadcast_to([1, NTILE, E]), ALU.is_le))
                link(v.tensor_reduce(ef[:, :], cmp[:, :, :], AX.X, ALU.add))
                link(v.tensor_scalar(ef[:, :], ef[:, :], float(E - 1), None, ALU.min))
                link(v.tensor_copy(eid[:, :], ef[:, :]))

        with ExitStack() as c1:
            zero = sbuf(nc, c1, "zero", [128, NTILE // 2 * D])
            (zeroed, cleared) = c1.enter_context(stage(nc, "zeroed cleared"))
            scattered, all_scattered = cst["scattered"].sem, cst["scattered"].add(16 * K * NTT)
            block = c1.enter_context(nc.Block())

            @block.vector
            def _(dve):
                nc.vector.memset(zero[:, :], 0.0).then_inc(zeroed, 1)

            @block.sync
            def _(sp):
                sp.wait_ge(zeroed, 1)
                for h in range(2):
                    sp.dma_start(xs[h * (NSLOT // 2):(h + 1) * (NSLOT // 2), :].rearrange("(p r) d -> p (r d)", p=128),
                                 zero[:, :]).then_inc(cleared, 16)

            @block.gpsimd
            def _(pool):
                pool.wait_ge(cleared, 32)
                for k in range(K):
                    for t in range(NTT):
                        pool.indirect_dma_start(xs, bass.IndirectOffsetOnAxis(ap=slot[k][:, t:t + 1], axis=0),
                                                rows[:, t, :], None).then_inc(scattered, 16)
                pool.wait_ge(scattered, all_scattered)

        with ExitStack() as c1:
            wb = sbuf(nc, c1, "wb", [128, 2, WE])
            bb = sbuf(nc, c1, "bb", [1, 2, D])
            xi = sbuf(nc, c1, "xi", [ST, 2, D])
            xT = sbuf(nc, c1, "xT", [D, 2, ST])
            eh = sbuf(nc, c1, "eh", [128, 2, max(FC, 1), ST])
            yo = sbuf(nc, c1, "yo", [ST, 2, D])
            one = sbuf(nc, c1, "one", [1, ST])
            px = psum(nc, c1, "px", [D, 2, BANK])
            ph = psum(nc, c1, "ph", [128, 2, BANK])
            po = psum(nc, c1, "po", [ST, 2, BANK])
            names = "w_loaded x_loaded turned xT_ready up h_ready down y_ready stored"
            pairs = c1.enter_context(stage(nc, " ".join(f"{n}{j}" for n in names.split() for j in range(2)) + " one_ready sp_passed"))
            (w_loaded, x_loaded, turned, xT_ready, up, h_ready, down, y_ready, stored) = [pairs[2 * i:2 * i + 2] for i in range(9)]
            one_ready, sp_passed = pairs[18:]
            block = c1.enter_context(nc.Block())

            @block.sync
            def _(sp):
                hold = Hold(sp, sp_passed)
                with sp.Fori(0, NTILE // 2) as i:
                    for j in range(2):
                        e = sp.value_load(eid[0:1, ds(2 * i + j, 1)], min_val=0, max_val=E - 1)
                        hold(down[j], i)
                        sp.dma_start(xi[:, j, :], xs[ds((2 * i + j) * ST, ST), :]).then_inc(x_loaded[j], 16)
                        sp.dma_start(wb[:, j, :], w_dram[ds(e, 1), :, :].rearrange("o p n -> p (o n)")).then_inc(w_loaded[j], 16)
                        sp.dma_start(bb[:, j, :], b_dram[ds(e, 1), :]).then_inc(w_loaded[j], 16)

            @block.tensor
            def _(pe):
                pe.wait_ge(one_ready, 1)
                with pe.Fori(0, NTILE // 2) as i:
                    for j in range(2):
                        pe.wait_ge(x_loaded[j], 16 * (i + 1))
                        nc.tensor.transpose(px[:, j, 0:ST], xi[:, j, :], cst["ident"]).then_inc(turned[j], 1)
                        pe.wait_ge(xT_ready[j], i + 1)
                        pe.wait_ge(w_loaded[j], 32 * (i + 1))
                        if F:
                            for f in range(FC):
                                last = nc.tensor.matmul(ph[:, j, f * ST:(f + 1) * ST], wb[:, j, f * 128:(f + 1) * 128],
                                                        xT[:, j, :], start=True, stop=True)
                            last.then_inc(up[j], 1)
                    for j in range(2):
                        pe.wait_ge(y_ready[j], i)
                        if F:
                            pe.wait_ge(h_ready[j], i + 1)
                            for f in range(FC):
                                nc.tensor.matmul(po[:, j, 0:D], eh[:, j, f, :], wb[:, j, F + f * D:F + (f + 1) * D],
                                                 start=(f == 0), stop=False)
                        else:
                            nc.tensor.matmul(po[:, j, 0:D], xT[:, j, :], wb[:, j, 0:D], start=True, stop=False)
                        nc.tensor.matmul(po[:, j, 0:D], one[:, :], bb[:, j, :], start=False, stop=True).then_inc(down[j], 1)

            @block.vector
            def _(dve):
                nc.vector.memset(one[:, :], 1.0).then_inc(one_ready, 1)
                with dve.Fori(0, NTILE // 2) as i:
                    for j in range(2):
                        dve.wait_ge(turned[j], i + 1)
                        dve.wait_ge(down[j], i)
                        nc.vector.tensor_copy(xT[:, j, :], px[:, j, 0:ST]).then_inc(xT_ready[j], 1)
                    for j in range(2):
                        dve.wait_ge(down[j], i + 1)
                        dve.wait_ge(stored[j], 16 * i)
                        nc.vector.tensor_copy(yo[:, j, :], po[:, j, 0:D]).then_inc(y_ready[j], 1)

            @block.scalar
            def _(act):
                if F:
                    nc.scalar.preload_act_table_set("silu_and_others" if act_fn == ACT.Silu else "gelu_and_others")
                with act.Fori(0, NTILE // 2) as i:
                    if F:
                        for j in range(2):
                            act.wait_ge(up[j], i + 1)
                            for f in range(FC):
                                last = nc.scalar.activation(eh[:, j, f, :], ph[:, j, f * ST:(f + 1) * ST], act_fn,
                                                            bias=wb[:, j, W1 + W2 + f:W1 + W2 + f + 1])
                            last.then_inc(h_ready[j], 1)
                    for j in range(2):
                        act.wait_ge(y_ready[j], i + 1)
                        act.dma_start(ys[ds((2 * i + j) * ST, ST), :], yo[:, j, :]).then_inc(stored[j], 16)
                for j in range(2):
                    act.wait_ge(stored[j], 16 * (NTILE // 2))

        with ExitStack() as c1:
            gk = [sbuf(nc, c1, f"g{k}", [TT, NTT, D]) for k in range(K)]
            pt = psum(nc, c1, "pt", [D, 2, BANK])
            gathered = [(g.sem, g.add(16 * K)) for g in cst["gathered"]]
            (weighed, turned, added, dc) = c1.enter_context(stage(nc, "weighed turned added dve_chain"))
            block = c1.enter_context(nc.Block())

            @block.gpsimd
            def _(pool):
                for t in range(NTT):
                    for k in range(K):
                        pool.indirect_dma_start(gk[k][:, t, :], None, ys,
                                                bass.IndirectOffsetOnAxis(ap=slot[k][:, t:t + 1], axis=0)).then_inc(gathered[t][0], 16)

            @block.vector
            def _(dve):
                link = Chain(dve, dc)
                v = nc.vector

                def weigh(t):
                    dve.wait_ge(*gathered[t])
                    r = gk[0][:, t, :]
                    if capacity is not None:
                        link(v.tensor_scalar(r, r, keepg[:, 0, t:t + 1], None, ALU.mult))
                        v.scalar_tensor_tensor(out=r, in0=rows[:, t, :], scalar=keepg[:, 1, t:t + 1], in1=r,
                                               op0=ALU.mult, op1=ALU.add).then_inc(weighed, 1)
                    elif K == 1:
                        v.tensor_scalar(r, r, gate[0][:, t:t + 1], None, ALU.mult).then_inc(weighed, 1)
                    else:
                        link(v.tensor_scalar(r, r, gate[0][:, t:t + 1], None, ALU.mult))
                        v.scalar_tensor_tensor(out=r, in0=gk[1][:, t, :], scalar=gate[1][:, t:t + 1], in1=r,
                                               op0=ALU.mult, op1=ALU.add).then_inc(weighed, 1)

                def add(t):
                    dve.wait_ge(turned, t + 1)
                    o = out[:, t * TT:(t + 1) * TT]
                    v.tensor_tensor(o, pt[:, t % 2, 0:TT], o, ALU.add).then_inc(added, 1)

                weigh(0)
                for t in range(NTT):
                    if t + 1 < NTT:
                        weigh(t + 1)
                    add(t)

            @block.tensor
            def _(pe):
                for t in range(NTT):
                    if t >= 2:
                        pe.wait_ge(added, t - 1)
                    pe.wait_ge(weighed, t + 1)
                    nc.tensor.transpose(pt[:, t % 2, 0:TT], gk[0][:, t, :], cst["ident"][0:TT, 0:TT]).then_inc(turned, 1)


def switch_ffn(nc, cst, a, x, hT):
    E = 16
    with ExitStack() as ctx:
        w = sbuf(nc, ctx, "w", [128, E])
        b = sbuf(nc, ctx, "b", [TT, E])
        l = sbuf(nc, ctx, "l", [TT, NTT, E])
        load(nc, (w[:, :], a["sw_r"]), (b[:, :], a["sw_rb"]))
        project_tokens(nc, x, TT, w[:, :], l, b[:, :])
        mixture(nc, cst, a, "sw", x, l, hT, E, 1, 0, None, True, capacity=int(1.2 * NT / E))


def gelu_ffn(nc, cst, a, x, hT):
    E = 8
    with ExitStack() as ctx:
        w = sbuf(nc, ctx, "w", [128, E])
        b = sbuf(nc, ctx, "b", [TT, E])
        l = sbuf(nc, ctx, "l", [TT, NTT, E])
        load(nc, (w[:, :], a["gf_r"]), (b[:, :], a["gf_rb"]))
        project_tokens(nc, x, TT, w[:, :], l, b[:, :])
        mixture(nc, cst, a, "gf", x, l, hT, E, 1, 512, ACT.Gelu, True)


def two_layer(nc, x, w1, b1, w2, b2, out, F, add):
    FC = F // 128
    with ExitStack() as ctx:
        hid = sbuf(nc, ctx, "hid", [128, 2, FC, HB])
        ph = psum(nc, ctx, "ph", [128, FC, BANK])
        po = psum(nc, ctx, "po", [128, 2, BANK])
        (up, h_ready, down, kept) = ctx.enter_context(stage(nc, "up h_ready down kept"))
        block = ctx.enter_context(nc.Block())
        n = 2 * NCH

        @block.tensor
        def _(pe):
            def second(c):
                pe.wait_ge(h_ready, c + 1)
                if c >= 2:
                    pe.wait_ge(kept, c - 1)
                for f in range(FC):
                    last = nc.tensor.matmul(po[:, c % 2, 0:HB], w2[:, f * D:(f + 1) * D], hid[:, c % 2, f, :],
                                            start=(f == 0), stop=(f == FC - 1))
                last.then_inc(down, 1)

            for c in range(n):
                if c >= 1:
                    pe.wait_ge(h_ready, c)
                for f in range(FC):
                    last = nc.tensor.matmul(ph[:, f, 0:HB], w1[:, f * 128:(f + 1) * 128], x[:, c * HB:(c + 1) * HB],
                                            start=True, stop=True)
                last.then_inc(up, 1)
                if c >= 1:
                    second(c - 1)
            second(n - 1)

        @block.scalar
        def _(act):
            nc.scalar.preload_act_table_set("silu_and_others")
            for c in range(n):
                act.wait_ge(up, c + 1)
                if c >= 2:
                    act.wait_ge(down, c - 1)
                for f in range(FC):
                    last = nc.scalar.activation(hid[:, c % 2, f, :], ph[:, f, 0:HB], ACT.Silu, bias=b1[:, f:f + 1])
                last.then_inc(h_ready, 1)

        @block.vector
        def _(dve):
            for c in range(n):
                dve.wait_ge(down, c + 1)
                o = out[:, c * HB:(c + 1) * HB]
                if add:
                    nc.vector.scalar_tensor_tensor(out=o, in0=po[:, c % 2, 0:HB], scalar=b2, in1=o,
                                                   op0=ALU.add, op1=ALU.add).then_inc(kept, 1)
                else:
                    nc.vector.tensor_scalar(o, po[:, c % 2, 0:HB], b2, SHARED_SCALE, ALU.add, ALU.mult).then_inc(kept, 1)


SHARED_SCALE = 0.25
TEMP = 0.7


def silu_ffn(nc, cst, a, x, hT):
    E, DR, DFF, DSH = 64, 64, 512, 256
    with ExitStack() as ctx:
        c = sbuf(nc, ctx, "c", [128, 12])
        moe = sbuf(nc, ctx, "moe", [128, NT])
        h = sbuf(nc, ctx, "h", [128, NT])
        load(nc, (c[:, :], a["sf_cols"]))
        layernorm(nc, cst, x, h, c[:, 0:1], c[:, 1:2])
        with ExitStack() as c1:
            w = sbuf(nc, c1, "w", [128, 2 * DSH])
            load(nc, (w[:, :], a["sf_ws"]))
            two_layer(nc, h, w[:, 0:DSH], c[:, 4:6], w[:, DSH:2 * DSH], c[:, 6:7], moe, DSH, False)
        with ExitStack() as c1:
            w = sbuf(nc, c1, "w", [128, DR])
            cb = sbuf(nc, c1, "cb", [DR, E])
            r = sbuf(nc, c1, "r", [DR, NT])
            l = sbuf(nc, c1, "l", [TT, NTT, E])
            load(nc, (w[:, :], a["sf_wr"]), (cb[:, :], a["sf_code"]))
            project_features(nc, h, r, w[:, :], None, rows=DR)
            project_tokens(nc, r, TT, cb[:, :], l, None)
            with ExitStack() as c2:
                (scaled,) = c2.enter_context(stage(nc, "scaled"))
                block = c2.enter_context(nc.Block())

                @block.vector
                def _(dve):
                    nc.vector.tensor_scalar(l[:, :, :], l[:, :, :], 1.0 / TEMP, None, ALU.mult).then_inc(scaled, 1)
            mixture(nc, cst, a, "sf", h, l, moe, E, 2, DFF, ACT.Silu, False)
        layernorm(nc, cst, moe, h, c[:, 2:3], c[:, 3:4])
        with ExitStack() as c1:
            w = sbuf(nc, c1, "w", [128, 2 * DFF])
            load(nc, (w[:, :], a["sf_wf"]))
            two_layer(nc, h, w[:, 0:DFF], c[:, 7:11], w[:, DFF:2 * DFF], c[:, 11:12], hT, DFF, True)
        with ExitStack() as c1:
            (dc,) = c1.enter_context(stage(nc, "dve_chain"))
            block = c1.enter_context(nc.Block())

            @block.vector
            def _(dve):
                link = Chain(dve, dc)
                link(nc.vector.tensor_tensor(hT[:, :], hT[:, :], moe[:, :], ALU.add))
                link(nc.vector.tensor_tensor(hT[:, :], hT[:, :], x[:, :], ALU.add))



LE, LK, TS, BT = 8, 2, NB, S
EK = LE * LK
HE = LE // 2
CB = LK * BT
PERB = BANK // CB
GO = (0, 1, 3, 2)


def lstm_experts(nc, cst, a, x, hT):
    with ExitStack() as ctx:
        def sb(name, shape, dt=F32):
            return sbuf(nc, ctx, name, shape, dt)

        mb = sb("mb", [128, EK, NT], F16)
        rwb = sb("rwb", [128, LK, NT])
        wT = sb("wT", [EK, NT])
        bsp = sb("bsp", [3 * LE, 4 * D], BF16)
        bsel = sb("bsel", [3 * LE, LE, CB], BF16)
        bo = sb("bo", [EK, D])
        wo = sb("wo", [128, LE, D])
        wi = sb("wi", [128, 2, LE, 4 * D], F16)
        wh = sb("wh", [128, 2, LE, 4 * D], F16)
        xs = sb("xs", [128, 2, NT], F16)
        scale = sb("scale", [128, 2])
        with ExitStack() as c1:
            w = sbuf(nc, c1, "w", [128, LE])
            b = sbuf(nc, c1, "b", [TT, LE])
            l = sbuf(nc, c1, "l", [TT, NTT, LE])
            oh = [sbuf(nc, c1, f"oh{k}", [TT, NTT, LE]) for k in range(LK)]
            gate = [sbuf(nc, c1, f"gate{k}", [TT, NTT]) for k in range(LK)]
            load(nc, (w[:, :], a["le_r"]), (b[:, :], a["le_rb"]), (bo[:, :], a["le_bo"]),
                 (wo[:, :, :], a["le_wo"].rearrange("p (e n) -> p e n", e=LE)))
            project_tokens(nc, x, TT, w[:, :], l, b[:, :])
            route(nc, a, l, LE, LK, oh, gate, False)
            expand_routes(nc, cst, a, oh, gate, mb, rwb, wT)
        split_weights(nc, cst, a, x, xs, wi, wh, scale)
        split_bias(nc, a, bsp, bsel, scale)
        UN = 4
        HC = HE * CB
        xm = sb("xm", [128, 2, 2, EK, BT], F16)
        z = sb("z", [128, 2, 5, HC])
        prod = sb("prod", [128, 2, 2, HC])
        tc = sb("tc", [128, 2, HC])
        h = sb("h", [128, 2, HC])
        hs = sb("hs", [128, 2, 2, HC], F16)
        hm = sb("hm", [128, 2, HE, LK, BT])
        hw = sb("hw", [128, UN, EK, BT])
        pg = [psum(nc, ctx, f"pg{q}", [128, 3, BANK]) for q in range(2)]
        py = psum(nc, ctx, "py", [128, BANK])
        names = "gates_ready activated c_ready tc_ready h_ready high_ready parts_ready hw_ready"
        s16 = ctx.enter_context(stage(nc, " ".join(f"{n}{q}" for n in names.split() for q in range(2))))
        gates_ready, activated, c_ready, tc_ready, h_ready, high_ready, parts_ready, hw_ready = [s16[2 * i:2 * i + 2] for i in range(8)]
        (cleared, x_ready, y_ready, y_added, dc, pc, pe_passed, dve_passed, pool_passed) = ctx.enter_context(
            stage(nc, "cleared x_ready y_ready y_added dve_chain pool_chain pe_passed dve_passed pool_passed"))
        block = ctx.enter_context(nc.Block())
        IT = TS // UN

        def tokens(t, n=1):
            return ds(t * BT, n * BT)

        def col(g, e):
            m = g * HE + e
            return m // PERB, (m % PERB) * CB

        @block.tensor
        def _(pe):
            hold = Hold(pe, pe_passed)
            pe.wait_ge(cleared, 1)

            def gates(q, t, j):
                p = pg[q]
                pe.wait_ge(activated[q], t)
                pe.wait_ge(x_ready, t + 1)
                seen = set()
                for g in range(4):
                    e = 0
                    while e < HE:
                        bank, c = col(g, e)
                        n = 1
                        while e + n < HE and col(g, e + n)[0] == bank:
                            n += 1
                        nc.tensor.matmul(p[:, bank, c:c + n * CB], bsp[:, GO[g] * D:(GO[g] + 1) * D],
                                         bsel[:, q * HE + e:q * HE + e + n, :].rearrange("p e c -> p (e c)"),
                                         start=bank not in seen, stop=False, skip_group_check=True)
                        seen.add(bank)
                        e += n
                for u in range(2):
                    if u:
                        pe.wait_ge(parts_ready[q], t)
                    for g in range(4):
                        for e in range(HE):
                            bank, c = col(g, e)
                            ee = q * HE + e
                            if u:
                                rhs = [hs[:, q, part, e * CB:(e + 1) * CB] for part in range(2)]
                            else:
                                rhs = [xm[:, j % 2, part, ee * LK:(ee + 1) * LK, :].rearrange("p k b -> p (k b)") for part in range(2)]
                            for wp, rp in ((0, 0), (0, 1), (1, 0)):
                                last = nc.tensor.matmul(p[:, bank, c:c + CB], (wh if u else wi)[:, wp, ee, GO[g] * D:(GO[g] + 1) * D],
                                                        rhs[rp], start=False, stop=u == 1 and wp == 1, skip_group_check=True)
                last.then_inc(gates_ready[q], 1)

            def output(i):
                for q in range(2):
                    hold(hw_ready[q], UN * i + UN)
                hold(y_added, i)
                for m in range(EK):
                    nc.tensor.matmul(py[:, 0:UN * BT], wo[:, m // LK, :], hw[:, :, m, :], start=(m == 0), stop=False)
                nc.tensor.matmul(py[:, 0:UN * BT], bo[:, :], wT[:, tokens(UN * i, UN)], start=False, stop=True).then_inc(y_ready, 1)

            def body(i, first):
                for j in range(UN):
                    t = UN * i + j
                    gates(0, t, j)
                    if j == 0 and not first:
                        output(i - 1)
                    gates(1, t, j)

            body(0, True)
            with pe.Fori(1, IT) as i:
                body(i, False)
            output(IT - 1)

        @block.scalar
        def _(act):
            def body(i):
                for j in range(UN):
                    t = UN * i + j
                    for q in range(2):
                        act.wait_ge(gates_ready[q], t + 1)
                        flat = z[:, q, :, :].rearrange("p g n -> p (g n)")
                        for f, lo, hi in ((ACT.Sigmoid, 0, 3 * HE), (ACT.Tanh, 3 * HE, 4 * HE)):
                            while lo < hi:
                                bank = lo // PERB
                                n = min(hi, (bank + 1) * PERB) - lo
                                c = (lo % PERB) * CB
                                last = nc.scalar.activation(flat[:, lo * CB:(lo + n) * CB], pg[q][:, bank, c:c + n * CB], f,
                                                            scale=scale[:, 1:2])
                                lo += n
                        last.then_inc(activated[q], 1)
                        act.wait_ge(c_ready[q], t + 1)
                        nc.scalar.activation(tc[:, q, :], z[:, q, 4, :], ACT.Tanh).then_inc(tc_ready[q], 1)
                        act.wait_ge(h_ready[q], t + 1)
                        nc.scalar.activation(hs[:, q, 0, :], h[:, q, :], ACT.Copy).then_inc(high_ready[q], 1)

            nc.scalar.preload_act_table_set("sigmoid_and_others")
            with act.Fori(0, IT) as i:
                body(i)

        @block.vector
        def _(dve):
            link = Chain(dve, dc)
            hold = Hold(dve, dve_passed)
            v = nc.vector
            v.memset(hs[:, :, :, :], 0.0)
            v.memset(z[:, :, 4, :], 0.0).then_inc(cleared, 1)

            def add(i):
                hold(y_ready, i + 1)
                o = hT[:, tokens(UN * i, UN)]
                v.tensor_tensor(o, py[:, 0:UN * BT], o, ALU.add).then_inc(y_added, 1)

            def body(i, first):
                for j in range(UN):
                    t = UN * i + j
                    for q in range(2):
                        dve.wait_ge(activated[q], t + 1)
                        link(v.tensor_tensor(prod[:, q, :, :], z[:, q, 0:2, :], z[:, q, 3:5, :], ALU.mult))
                        v.tensor_tensor(z[:, q, 4, :], prod[:, q, 0, :], prod[:, q, 1, :], ALU.add).then_inc(c_ready[q], 1)
                        dve.wait_ge(tc_ready[q], t + 1)
                        dve.wait_ge(hw_ready[q], t)
                        v.tensor_tensor(h[:, q, :], z[:, q, 2, :], tc[:, q, :], ALU.mult).then_inc(h_ready[q], 1)
                        dve.wait_ge(high_ready[q], t + 1)
                        v.tensor_tensor(hs[:, q, 1, :], h[:, q, :], hs[:, q, 0, :], ALU.subtract).then_inc(parts_ready[q], 1)
                    if j == 1 and not first:
                        add(i - 1)

            dve.wait_ge(cleared, 1)
            body(0, True)
            with link.loop(IT - 1, 2 * UN) as i:
                body(i + 1, False)
            add(IT - 1)

        @block.gpsimd
        def _(pool):
            link = Chain(pool, pc)
            hold = Hold(pool, pool_passed)
            g = nc.gpsimd

            def mask_x(t, j):
                for part in range(2):
                    last = g.tensor_tensor(xm[:, j % 2, part, :, :], xs[:, part, tokens(t)].unsqueeze(1).broadcast_to([128, EK, BT]),
                                           mb[:, :, tokens(t)], ALU.mult)
                last.then_inc(x_ready, 1)

            def weigh(t, j, i):
                for q in range(2):
                    hold(h_ready[q], t + 1)
                    if j == 0:
                        hold(y_ready, i)
                    hold(hw_ready[q], t)
                    link(g.tensor_tensor(hm[:, q, :, :, :].rearrange("p e k b -> p (e k) b"),
                                         h[:, q, :].rearrange("p (m b) -> p m b", b=BT),
                                         mb[:, q * HE * LK:(q + 1) * HE * LK, tokens(t)], ALU.mult))
                    pool.sem_inc(pool_passed, 1)
                    g.tensor_tensor(hw[:, j, q * HE * LK:(q + 1) * HE * LK, :].rearrange("p (e k) b -> p e k b", k=LK),
                                    hm[:, q, :, :, :], rwb[:, :, tokens(t)].unsqueeze(1).broadcast_to([128, HE, LK, BT]),
                                    ALU.mult).then_inc(hw_ready[q], 1)

            mask_x(0, 0)
            mask_x(1, 1)
            with link.loop(IT - 1, 2 * UN) as i:
                for j in range(UN):
                    weigh(UN * i + j, j, i)
                    mask_x(UN * i + j + 2, j)
            for j in range(UN):
                weigh(TS - UN + j, j, IT - 1)
                if j + 2 < UN:
                    mask_x(TS - UN + j + 2, j)


def split_weights(nc, cst, a, x, xs, wi, wh, scale):
    with ExitStack() as ctx:
        wf = [sbuf(nc, ctx, f"wf{k}", [128, LE * 4 * D]) for k in range(2)]
        mx = sbuf(nc, ctx, "mx", [128, 3])
        row = sbuf(nc, ctx, "row", [1, 130])
        k = sbuf(nc, ctx, "k", [128, 3], I32)
        kf = sbuf(nc, ctx, "kf", [128, 3])
        ps = psum(nc, ctx, "ps", [128, BANK])
        pb = psum(nc, ctx, "pb", [128, BANK])
        (wl0, wl1, ones_set, reduced, turned, largest, spread, dc, scale_ready, highs, xhigh) = ctx.enter_context(
            stage(nc, "w_loaded0 w_loaded1 ones_set reduced turned largest spread dve_chain scale_ready highs x_high"))
        block = ctx.enter_context(nc.Block())

        @block.sync
        def _(sp):
            sp.dma_start(wf[0][:, :], a["le_wi"]).then_inc(wl0, 16)
            sp.dma_start(wf[1][:, :], a["le_wh"]).then_inc(wl1, 16)

        @block.tensor
        def _(pe):
            pe.wait_ge(reduced, 1)
            nc.tensor.transpose(ps[0:1, 0:128], mx[:, 2:3], cst["ident"]).then_inc(turned, 1)
            pe.wait_ge(largest, 1)
            nc.tensor.matmul(pb[:, 0:1], row[0:1, 2:130], row[0:1, 0:1], start=True, stop=True).then_inc(spread, 1)

        @block.scalar
        def _(act):
            act.wait_ge(xhigh, 1)
            for n in range(2):
                act.wait_ge(scale_ready, 1 + n)
                w = (wi, wh)[n]
                nc.scalar.activation(w[:, 0, :, :].rearrange("p e n -> p (e n)"), wf[n][:, :], ACT.Copy).then_inc(highs, 1)

        @block.vector
        def _(dve):
            link = Chain(dve, dc)
            v = nc.vector
            v.tensor_copy(xs[:, 0, :], x[:, :]).then_inc(xhigh, 1)
            dve.wait_ge(xhigh, 1)
            link(v.tensor_tensor(xs[:, 1, :], x[:, :], xs[:, 0, :], ALU.subtract))
            link(v.memset(row[:, :], 1.0))
            for n in range(2):
                dve.wait_ge((wl0, wl1)[n], 16)
                link(v.tensor_reduce(mx[:, n:n + 1], wf[n][:, :], AX.X, ALU.max, apply_absolute_value=True))
            v.tensor_tensor(mx[:, 2:3], mx[:, 0:1], mx[:, 1:2], ALU.max).then_inc(reduced, 1)
            dve.wait_ge(turned, 1)
            v.tensor_reduce(row[:, 0:1], ps[0:1, 0:128], AX.X, ALU.max).then_inc(largest, 1)
            dve.wait_ge(spread, 1)
            link(v.tensor_scalar(kf[:, 0:1], pb[:, 0:1], 2.0 ** -60, None, ALU.max))
            link(v.tensor_scalar(k[:, 0:1], kf[:, 0:1].bitcast(I32), 23, None, ALU.logical_shift_right))
            link(v.tensor_scalar(k[:, 1:2], k[:, 0:1], -1.0, 127.0 + 127.0 + 13.0, ALU.mult, ALU.add))
            link(v.tensor_scalar(k[:, 2:3], k[:, 0:1], -13.0, None, ALU.add))
            link(v.tensor_scalar(scale[:, :].bitcast(I32), k[:, 1:3], 23, None, ALU.logical_shift_left))
            for n in range(2):
                v.tensor_scalar(wf[n][:, :], wf[n][:, :], scale[:, 0:1], None, ALU.mult).then_inc(scale_ready, 1)
            for n in range(2):
                dve.wait_ge(highs, n + 1)
                w = (wi, wh)[n]
                link(v.tensor_tensor(w[:, 1, :, :].rearrange("p e n -> p (e n)"), wf[n][:, :],
                                     w[:, 0, :, :].rearrange("p e n -> p (e n)"), ALU.subtract))


def expand_routes(nc, cst, a, oh, gate, mb, rwb, wT):
    with ExitStack() as ctx:
        ek = sbuf(nc, ctx, "ek", [TT, NTT, 2 * EK + LK])
        mT = sbuf(nc, ctx, "mT", [EK, NT], BF16)
        gT = sbuf(nc, ctx, "gT", [LK, NT])
        sel = sbuf(nc, ctx, "sel", [EK, EK, 128])
        selb = sbuf(nc, ctx, "selb", [EK, EK, 128], BF16)
        pt = psum(nc, ctx, "pt", [EK, 2, BANK])
        pbc = psum(nc, ctx, "pbc", [128, 2, 2, BANK])
        load(nc, (sel[:, :, :], a["c_sel"].rearrange("p (e n) -> p e n", e=EK)))
        (placed, turned, kept, spread, read_a, read_b, dc) = ctx.enter_context(
            stage(nc, "placed turned kept spread spread_kept_act spread_kept_dve dve_chain"))
        block = ctx.enter_context(nc.Block())
        PB = BANK // TT
        parts = [(0, EK, mT), (EK, EK, wT), (2 * EK, LK, gT)]
        groups = [(p, q) for p in range(3) for q in range(-(-NTT // PB))]

        @block.vector
        def _(dve):
            link = Chain(dve, dc)
            v = nc.vector
            link(v.tensor_copy(selb[:, :, :], sel[:, :, :]))
            for k in range(LK):
                m = ek[:, :, 0:EK].rearrange("p t (e k) -> p t e k", k=LK)[:, :, :, k]
                w = ek[:, :, EK:2 * EK].rearrange("p t (e k) -> p t e k", k=LK)[:, :, :, k]
                v.tensor_copy(m, oh[k][:, :, :])
                v.tensor_copy(ek[:, :, 2 * EK + k], gate[k][:, :])
                link(v.tensor_tensor(w, oh[k][:, :, :], gate[k][:, :].unsqueeze(2).broadcast_to([TT, NTT, LE]), ALU.mult))
            v.tensor_copy(ek[0:1, 0, 0:1], ek[0:1, 0, 0:1]).then_inc(placed, 1)
            for n, (p, q) in enumerate(groups):
                at, rows, dst = parts[p]
                dve.wait_ge(turned, n + 1)
                m = min(PB, NTT - q * PB) * TT
                v.tensor_copy(dst[:, q * PB * TT:q * PB * TT + m], pt[0:rows, n % 2, 0:m]).then_inc(kept, 1)
            for n in range(1, (EK + LK) * NCH, 2):
                dve.wait_ge(spread, n + 1)
                r, c = n // NCH, n % NCH
                o = mb[:, r, c * CH:(c + 1) * CH] if r < EK else rwb[:, r - EK, c * CH:(c + 1) * CH]
                v.tensor_copy(halves(o), pbc[:, n % 2, :, 0:HB]).then_inc(read_b, 1)

        @block.scalar
        def _(act):
            for n in range(0, (EK + LK) * NCH, 2):
                act.wait_ge(spread, n + 1)
                r, c = n // NCH, n % NCH
                o = mb[:, r, c * CH:(c + 1) * CH] if r < EK else rwb[:, r - EK, c * CH:(c + 1) * CH]
                nc.scalar.activation(halves(o), pbc[:, n % 2, :, 0:HB], ACT.Copy).then_inc(read_a, 1)

        @block.tensor
        def _(pe):
            pe.wait_ge(placed, 1)
            for n, (p, q) in enumerate(groups):
                at, rows, dst = parts[p]
                if n >= 2:
                    pe.wait_ge(kept, n - 1)
                for t in range(q * PB, min(NTT, (q + 1) * PB)):
                    last = nc.tensor.transpose(pt[0:rows, n % 2, (t - q * PB) * TT:(t - q * PB + 1) * TT],
                                               ek[:, t, at:at + rows], cst["ident"][0:TT, 0:TT])
                last.then_inc(turned, 1)
            pe.wait_ge(kept, len(groups))
            for n in range((EK + LK) * NCH):
                r, c = n // NCH, n % NCH
                if n >= 2:
                    pe.wait_ge((read_a, read_b)[n % 2], n // 2)
                for k in range(2):
                    a0 = c * CH + k * HB
                    if r < EK:
                        last = nc.tensor.matmul(pbc[:, n % 2, k, 0:HB], selb[:, r, :], mT[:, a0:a0 + HB], start=True, stop=True)
                    else:
                        last = nc.tensor.matmul(pbc[:, n % 2, k, 0:HB], sel[0:LK, r - EK, :], gT[:, a0:a0 + HB], start=True, stop=True)
                last.then_inc(spread, 1)


def split_bias(nc, a, bsp, bsel, scale):
    with ExitStack() as ctx:
        P = 3 * LE
        b = sbuf(nc, ctx, "b", [P, 4 * D])
        r = sbuf(nc, ctx, "r", [P, 4 * D])
        part = sbuf(nc, ctx, "part", [P, 3, 4 * D], BF16)
        pick = sbuf(nc, ctx, "pick", [P, 3])
        bs = sbuf(nc, ctx, "bs", [P, LE])
        load(nc, (b[:, :], a["le_b"]), (pick[:, :], a["c_part"]), (bs[:, :], a["c_expert"]))
        (dc,) = ctx.enter_context(stage(nc, "dve_chain"))
        block = ctx.enter_context(nc.Block())

        @block.vector
        def _(dve):
            link = Chain(dve, dc)
            v = nc.vector
            link(v.tensor_scalar(b[:, :], b[:, :], scale[0:P, 0:1], None, ALU.mult))
            link(v.tensor_copy(part[:, 0, :], b[:, :]))
            link(v.tensor_tensor(r[:, :], b[:, :], part[:, 0, :], ALU.subtract))
            link(v.tensor_copy(part[:, 1, :], r[:, :]))
            link(v.tensor_tensor(r[:, :], r[:, :], part[:, 1, :], ALU.subtract))
            link(v.tensor_copy(part[:, 2, :], r[:, :]))
            link(v.tensor_scalar(bsp[:, :], part[:, 0, :], pick[:, 0:1], None, ALU.mult))
            for k in range(1, 3):
                link(v.scalar_tensor_tensor(out=bsp[:, :], in0=part[:, k, :], scalar=pick[:, k:k + 1], in1=bsp[:, :],
                                            op0=ALU.mult, op1=ALU.add))
            link(v.tensor_copy(bsel[:, :, :], bs[:, :].unsqueeze(2).broadcast_to([P, LE, CB])))


def masks():
    c = {}
    h = np.full((128, 128), -1e30, np.float32)
    for i in range(NH):
        h[HD * i:HD * i + HD, HD * i:HD * i + HD] = 0
    c["headmask"] = h
    s = np.zeros((AT, 2), np.float32)
    s[0:S, 0] = 1
    s[S:, 1] = 1
    c["seqmask"] = s
    b = np.full((AT, AT), -1e30, np.float32)
    b[0:S, 0:S] = 0
    b[S:, S:] = 0
    c["blockmask"] = b
    c["iota"] = np.tile(np.arange(128, dtype=np.float32)[None], (TT, 1))
    c["tri"] = np.triu(np.ones((TT, TT), np.float32))
    carry = np.ones((64, NTT), np.float32)
    carry[:, 0] = 0
    c["carry"] = np.tile(carry.reshape(1, -1), (TT, 1))
    sel = np.zeros((EK, EK, 128), np.float32)
    for i in range(EK):
        sel[i, i] = 1
    c["sel"] = sel.reshape(EK, -1)
    part, expert = np.zeros((3 * LE, 3), np.float32), np.zeros((3 * LE, LE), np.float32)
    for i in range(3 * LE):
        part[i, i // LE] = 1
        expert[i, i % LE] = 1
    c["part"], c["expert"] = part, expert
    return c


def rest(nc, ctx, cst, a, want, load_const, hT, xn):
    if want(2):
        layernorm(nc, cst, hT, xn)
        switch_ffn(nc, cst, a, xn, hT)
    if want(3):
        layernorm(nc, cst, hT, xn)
        channel_attention(nc, cst, a, xn, hT)
    if want(4):
        layernorm(nc, cst, hT, xn)
        silu_ffn(nc, cst, a, xn, hT)
    if want(5):
        layernorm(nc, cst, hT, xn)
        state_space(nc, cst, a, xn, hT)
    if want(6):
        layernorm(nc, cst, hT, xn)
        gelu_ffn(nc, cst, a, xn, hT)
    if want(7):
        layernorm(nc, cst, hT, xn)
        frame_attention(nc, cst, a, xn, hT)
    if want(8):
        layernorm(nc, cst, hT, xn)
        lstm_experts(nc, cst, a, xn, hT)


def lay_out_rest(I, f):
    f["ca_w"] = np.concatenate([I["L1_attn_w_qkv"], I["L1_attn_w_proj"]], 1)
    f["ca_bqk"] = np.tile(I["L1_attn_b_qkv"][None, 0:2 * D], (AT, 1))
    f["ca_b"] = np.stack([I["L1_attn_b_qkv"][2 * D:], I["L1_attn_b_proj"]], 1)
    f["fa_w"] = np.concatenate([I["L3_attn_W" + c].T for c in "qkv"], 1)
    f["ss_w"] = np.concatenate([I["L2_attn_L_param"], I["L2_attn_P_left"].transpose(0, 2, 1).reshape(D, -1),
                                I["L2_attn_P_right"].reshape(D, -1), I["L2_attn_B"], I["L2_attn_C"],
                                I["L2_attn_log_dt"], I["L2_attn_D"][:, None]], 1)
    f["sw_r"] = I["L0_ffn_switch_w"].T
    f["sw_rb"] = np.tile(I["L0_ffn_switch_b"][None], (TT, 1))
    f["sw_w"] = I["L0_ffn_expert_w"].transpose(0, 2, 1)
    f["sw_b"] = I["L0_ffn_expert_b"]

    def experts(w1, b1, w2):
        E, _, F = w1.shape
        return np.concatenate([w1, w2.reshape(E, F // 128, 128, D).transpose(0, 2, 1, 3).reshape(E, 128, -1),
                               b1.reshape(E, F // 128, 128).transpose(0, 2, 1)], 2)

    g = lambda n: I["L2_ffn_" + n]
    f["gf_r"], f["gf_rb"] = g("Ws"), np.tile(g("bs")[None], (TT, 1))
    f["gf_w"], f["gf_b"] = experts(g("W1"), g("b1"), g("W2")), g("b2")
    g = lambda n: I["L1_ffn_" + n]
    f["sf_w"], f["sf_b"] = experts(g("W1"), g("b1"), g("W2")), g("b2")
    f["sf_cols"] = np.concatenate([g("ln1_g")[:, None], g("ln1_b")[:, None], g("ffln_g")[:, None], g("ffln_b")[:, None],
                                   g("bs1").reshape(2, 128).T, g("bs2")[:, None], g("bf1").reshape(4, 128).T, g("bf2")[:, None]], 1)
    f["sf_ws"] = np.concatenate([g("Ws1"), g("Ws2").reshape(2, 128, D).transpose(1, 0, 2).reshape(128, -1)], 1)
    f["sf_wf"] = np.concatenate([g("Wf1"), g("Wf2").reshape(4, 128, D).transpose(1, 0, 2).reshape(128, -1)], 1)
    f["sf_wr"], f["sf_code"] = g("Wr"), g("codebook").T
    g = lambda n: I["L3_ffn_" + n]
    f["le_r"], f["le_rb"] = g("router_w"), np.tile(g("router_b")[None], (TT, 1))
    for n in ("Wi", "Wh", "Wo"):
        f["le_" + n.lower()] = g(n).transpose(1, 0, 2).reshape(128, -1)
    f["le_b"] = np.tile(g("b"), (3, 1))
    f["le_bo"] = np.repeat(g("bo"), LK, 0)
    f.update({"c_" + k: v for k, v in masks().items()})


def mdct_constant():
    L = 2 * D
    n = np.arange(L, dtype=np.float32) + np.float32(0.5)
    k = np.float32(np.pi / D) * n[:D]
    z = np.sqrt(np.float32(2.0 / D * 2.0))
    wm = z * np.cos((n + np.float32(D / 2))[:, None] * k[None, :]).astype(np.float32)
    win = np.sin(np.float32(np.pi) * n / np.float32(L)).astype(np.float32)
    return np.ascontiguousarray((win[:, None] * wm).astype(np.float32).reshape(2, D, D).transpose(1, 0, 2))


def constants():
    c = {}
    c["ident"] = np.eye(128, dtype=np.float32)
    c["avg"] = np.full((128, 128), 1.0 / 128, np.float32)
    c["mdct"] = mdct_constant().reshape(128, 256)
    c["row"] = np.concatenate([np.zeros((32, 32)), np.tile(np.eye(32), (3, 1))]).astype(np.float32)
    c["eps"] = np.full((128, 1), EPS, np.float32)
    return c


def build(nc, a, first=0, last=8, dbg=None):
    with ExitStack() as ctx:
        hT = sbuf(nc, ctx, "hT", [128, NT], F32)
        xn = sbuf(nc, ctx, "xn", [128, NT], F32)
        cst, dims = {}, {"mdct": "p (k n) -> p k n"}
        with ExitStack() as c1:
            tiles = {}
            for name in ("ident", "avg", "eps"):
                tiles[name] = sbuf(nc, ctx, name, list(a["c_" + name].shape))
                cst[name] = tiles[name][:, :]
            (loaded,) = c1.enter_context(stage(nc, "constants_loaded"))
            block = c1.enter_context(nc.Block())

            @block.sync
            def _(sp):
                n = 0
                for name, t in tiles.items():
                    sp.dma_start(t[:, :], a["c_" + name]).then_inc(loaded, 16)
                    n += 16
                if first > 0:
                    sp.dma_start(hT[:, :], a["h_in"]).then_inc(loaded, 16)
                    n += 16
                sp.wait_ge(loaded, n)

        def load_const(c1, name):
            t = sbuf(nc, c1, name, list(a["c_" + name].shape))
            with ExitStack() as c2:
                (loaded,) = c2.enter_context(stage(nc, "constants_loaded"))
                block = c2.enter_context(nc.Block())

                @block.sync
                def _(sp):
                    sp.dma_start(t[:, :], a["c_" + name]).then_inc(loaded, 16)
                    sp.wait_ge(loaded, 16)
            return t

        cst["gathered"] = [Counted(ctx.enter_context(nc.semaphore(f"gathered{t}"))) for t in range(NTT)]
        cst["scattered"] = Counted(ctx.enter_context(nc.semaphore("scattered")))

        def want(k):
            return first <= k <= last

        if want(0):
            with ExitStack() as c1:
                t = load_const(c1, "mdct")
                cst["mdct"] = t[:, :].rearrange("p (k n) -> p k n", k=2)
                tokenize(nc, cst, a["frames"], hT)
        if want(1):
            with ExitStack() as c1:
                m = sbuf(nc, c1, "m", [128, NT], F32)
                layernorm(nc, cst, hT, xn)
                with ExitStack() as c2:
                    (copied,) = c2.enter_context(stage(nc, "copied"))
                    block = c2.enter_context(nc.Block())

                    @block.vector
                    def _(dve):
                        nc.vector.tensor_copy(m[:, :], xn[:, :]).then_inc(copied, 1)
                with ExitStack() as c2:
                    row = sbuf(nc, c2, "row", [128, 32, 128], BF16)
                    t = load_const(c2, "row")
                    with ExitStack() as c3:
                        (widened,) = c3.enter_context(stage(nc, "widened"))
                        block = c3.enter_context(nc.Block())

                        @block.vector
                        def _(dve):
                            nc.vector.tensor_copy(row[:, :, :], t[:, :].unsqueeze(2).broadcast_to([128, 32, 128])).then_inc(widened, 1)
                    cst["row"] = row
                    with nc.Fori(0, NL) as layer:
                        mamba_layer(nc, cst, layer, a["mamba_w"], m)
                lstm_fusion(nc, cst, (a["lstm_ih"].rearrange("p (d g n) -> p d g n", d=2, g=4),
                                      a["lstm_hh"].rearrange("d p (g n) -> d p g n", g=4),
                                      a["lstm_b"], a["fus_w"].rearrange("p (k n) -> p k n", k=3), a["fus_b"]), xn, m, hT)
        rest(nc, ctx, cst, a, want, load_const, hT, xn)
        with ExitStack() as c1:
            (stored,) = c1.enter_context(stage(nc, "stored"))
            block = c1.enter_context(nc.Block())

            @block.sync
            def _(sp):
                sp.dma_start(a["out"], hT[:, :]).then_inc(stored, 16)
                sp.wait_ge(stored, 16)


def lay_out(inp):
    I = {k: np.asarray(v) for k, v in inp.items()}
    f = {}
    x = np.zeros((NB, (S + 1) * D), np.float32)
    x[:, D:D + I["x"].shape[1]] = I["x"]
    f["frames"] = x.reshape(NB, S + 1, D).transpose(2, 0, 1).reshape(D, NB * (S + 1))
    w = np.zeros((NL, 128, MWID), np.float32)

    def put(name, v):
        at, width = MW[name]
        w[:, 0:v.shape[1], at:at + width] = v
    g = lambda n: I["L0_attn_" + n]
    put("wi", g("in_proj_w").transpose(0, 2, 1))
    put("cw", g("conv_w").reshape(NL, 2, 128, DCV).transpose(0, 2, 1, 3).reshape(NL, 128, -1))
    put("cb", g("conv_b").reshape(NL, 2, 128).transpose(0, 2, 1))
    xp = g("x_proj_w")
    xp = np.concatenate([xp[:, 0:DTR]] + [xp[:, DTR:]] * 3, 1)
    put("xp", xp.reshape(NL, 128, 2, 128).transpose(0, 3, 2, 1).reshape(NL, 128, -1))
    put("dw", g("dt_proj_w").transpose(0, 2, 1))
    put("db", g("dt_proj_b").reshape(NL, 2, 128).transpose(0, 2, 1))
    put("alog", g("A_log").reshape(NL, 2, 128, DST).transpose(0, 2, 1, 3).reshape(NL, 128, -1))
    put("dp", g("D_param").reshape(NL, 2, 128).transpose(0, 2, 1))
    put("wo", g("out_proj_w").reshape(NL, D, 2, 128).transpose(0, 3, 2, 1).reshape(NL, 128, -1))
    put("g", g("ln_g")[:, :, None])
    put("b", g("ln_b")[:, :, None])
    f["mamba_w"] = w
    ih = np.zeros((D, 2, 4, 2, H2), np.float32)
    for d in range(2):
        ih[:, d, :, d, :] = g("lstm_w_ih")[d].T.reshape(D, 4, H2)
    f["lstm_ih"] = ih.reshape(D, -1)
    f["lstm_hh"] = g("lstm_w_hh").transpose(0, 2, 1)
    b = [g(n).reshape(2, 4, H2).transpose(0, 2, 1).reshape(128, 4) for n in ("lstm_b_ih", "lstm_b_hh")]
    f["lstm_b"] = np.stack(b)
    fw = np.zeros((128, 3, D), np.float32)
    fw[:, 0] = g("fusion_w").T[0:128]
    fw[0:H2, 1] = g("fusion_w").T[128:128 + H2]
    fw[H2:128, 2] = g("fusion_w").T[128 + H2:256]
    f["fus_w"] = fw.reshape(128, 3 * D)
    f["fus_b"] = g("fusion_b")[:, None]
    lay_out_rest(I, f)
    f.update({"c_" + k: v for k, v in constants().items()})
    return {k: np.ascontiguousarray(v) for k, v in f.items()}


def kernel(**inputs):
    import concourse.bacc as bacc
    from concourse.bass_utils import run_bass_kernel_spmd

    nc = bacc.Bacc("TRN2", target_bir_lowering=False, num_devices=1)
    arrays = lay_out(inputs)
    args = {k: nc.dram_tensor(k, list(v.shape), mybir.dt.from_np(v.dtype), kind="ExternalInput").ap()
            for k, v in arrays.items()}
    args["out"] = nc.dram_tensor("out", [128, NT], F32, kind="ExternalOutput").ap()
    build(nc, args)
    r = run_bass_kernel_spmd(nc, [arrays], core_ids=[0])
    return r.results[0]["out"].reshape(D, NB, S).transpose(1, 2, 0)
```

```python
import concourse.bass as bass
from concourse import mybir
from contextlib import ExitStack, contextmanager
import numpy as np

F32 = mybir.dt.float32
BF16 = mybir.dt.bfloat16
F16 = mybir.dt.float16
I32 = mybir.dt.int32
ALU = mybir.AluOpType
ACT = mybir.ActivationFunctionType
AX = mybir.AxisListType

NB = 64
S = 33
D = 128
NT = NB * S
CH = NT // 4
HB = CH // 2
NCH = 4
BANK = 512
EPS = 1e-5
TT = 96
NTT = NT // TT
ds = bass.ds


class Chain:

    def __init__(self, eng, sem):
        self.eng, self.sem, self.n, self.at = eng, sem, 0, None

    def __call__(self, ins):
        ins.then_inc(self.sem, 1)
        self.n += 1
        self.eng.wait_ge(self.sem, self.n if self.at is None else self.at + self.n)

    @contextmanager
    def loop(self, count, per):
        start = self.n
        with self.eng.Fori(0, count) as i:
            self.at = i * per
            yield i
            assert self.n - start == per, (self.n - start, per)
        self.at = None
        self.n = start + count * per


class Hold:

    def __init__(self, eng, passed):
        self.eng, self.passed = eng, passed

    def __call__(self, sem, value):
        self.eng.wait_ge(sem, value)
        self.eng.sem_inc(self.passed, 1)


def unique(nc, name):
    return f"{name}_{nc.next_id()}"


def sbuf(nc, ctx, name, shape, dt=F32):
    return ctx.enter_context(nc.sbuf_tensor(unique(nc, name), shape, dt))


def psum(nc, ctx, name, shape, dt=F32):
    return ctx.enter_context(nc.psum_tensor(unique(nc, name), shape, dt))


@contextmanager
def stage(nc, names):
    with ExitStack() as ctx:
        sems = [ctx.enter_context(nc.semaphore(unique(nc, n))) for n in names.split()]
        yield sems
        for s in sems:
            nc.gpsimd.sem_clear(s)
        nc.all_engine_barrier()


class Counted:

    def __init__(self, sem):
        self.sem, self.n = sem, 0

    def add(self, n):
        self.n += n
        return self.n


def halves(ap):
    return ap.rearrange("p (h n) -> p h n", h=2)


def layernorm(nc, cst, src, dst, gain=None, shift=None):
    with ExitStack() as ctx:
        mean_ps = psum(nc, ctx, "mean_ps", [128, 2, 2, BANK], F32)
        var_ps = psum(nc, ctx, "var_ps", [128, 2, 2, BANK], F32)
        sq = sbuf(nc, ctx, "sq", [128, 2, CH], F32)
        rstd = sbuf(nc, ctx, "rstd", [128, 2, CH], F32)
        (mean_ready, centered, squared, var_ready, logged, rstd_ready, scaled, shifted) = ctx.enter_context(
            stage(nc, "mean_ready centered squared var_ready logged rstd_ready scaled shifted"))
        block = ctx.enter_context(nc.Block())

        def part(t, c):
            return t[:, c * CH:(c + 1) * CH]

        @block.tensor
        def _(pe):
            def mean(c):
                if c >= 2:
                    pe.wait_ge(centered, c - 1)
                for h in range(2):
                    last = nc.tensor.matmul(mean_ps[:, c % 2, h, 0:HB], cst["avg"], halves(part(src, c))[:, h, :],
                                            start=True, stop=True)
                last.then_inc(mean_ready, 1)

            def var(c):
                pe.wait_ge(squared, c + 1)
                if c >= 2:
                    pe.wait_ge(logged, c - 1)
                for h in range(2):
                    last = nc.tensor.matmul(var_ps[:, c % 2, h, 0:HB], cst["avg"], halves(sq[:, c % 2, :])[:, h, :],
                                            start=True, stop=True)
                last.then_inc(var_ready, 1)

            mean(0)
            for c in range(NCH):
                if c + 1 < NCH:
                    mean(c + 1)
                var(c)

        @block.vector
        def _(dve):
            def center(c):
                dve.wait_ge(mean_ready, c + 1)
                nc.vector.tensor_tensor(halves(part(dst, c)), halves(part(src, c)), mean_ps[:, c % 2, :, 0:HB],
                                        ALU.subtract).then_inc(centered, 1)

            def scale(c):
                dve.wait_ge(rstd_ready, c + 1)
                dve.wait_ge(centered, c + 1)
                d = part(dst, c)
                if gain is None:
                    nc.vector.tensor_tensor(d, d, rstd[:, c % 2, :], ALU.mult).then_inc(scaled, 1)
                else:
                    nc.vector.scalar_tensor_tensor(out=d, in0=d, scalar=gain, in1=rstd[:, c % 2, :], op0=ALU.mult,
                                                   op1=ALU.mult).then_inc(scaled, 1)
                    dve.wait_ge(scaled, c + 1)
                    nc.vector.tensor_scalar(d, d, shift, None, ALU.add).then_inc(shifted, 1)

            center(0)
            for c in range(NCH):
                if c + 1 < NCH:
                    center(c + 1)
                scale(c)

        @block.scalar
        def _(act):
            def square(c):
                act.wait_ge(centered, c + 1)
                if c >= 2:
                    act.wait_ge(var_ready, c - 1)
                nc.scalar.activation(sq[:, c % 2, :], part(dst, c), ACT.Square).then_inc(squared, 1)

            nc.scalar.preload_act_table_set("natural_log_exp_and_others")
            square(0)
            for c in range(NCH):
                if c + 1 < NCH:
                    square(c + 1)
                act.wait_ge(var_ready, c + 1)
                if c >= 2:
                    act.wait_ge(scaled, c - 1)
                r = rstd[:, c % 2, :]
                nc.scalar.activation(halves(r), var_ps[:, c % 2, :, 0:HB], ACT.Ln, bias=cst["eps"]).then_inc(logged, 1)
                act.wait_ge(logged, c + 1)
                nc.scalar.activation(r, r, ACT.Exp, scale=-0.5).then_inc(rstd_ready, 1)


def tokenize(nc, cst, frames_dram, hT):
    with ExitStack() as ctx:
        blocks = sbuf(nc, ctx, "blocks", [128, NB, S + 1], F32)
        ps = psum(nc, ctx, "ps", [128, 2, 2, BANK], F32)
        (loaded, framed, kept) = ctx.enter_context(stage(nc, "loaded framed kept"))
        block = ctx.enter_context(nc.Block())

        @block.sync
        def _(sp):
            sp.dma_start(blocks[:, :, :], frames_dram.rearrange("p (b s) -> p b s", b=NB)).then_inc(loaded, 16)

        @block.tensor
        def _(pe):
            pe.wait_ge(loaded, 16)
            for c in range(NCH):
                if c >= 2:
                    pe.wait_ge(kept, c - 1)
                for h in range(2):
                    b0 = 16 * c + 8 * h
                    for k in range(2):
                        last = nc.tensor.matmul(ps[:, c % 2, h, 0:HB], cst["mdct"][:, k, :],
                                                blocks[:, b0:b0 + 8, k:k + S], start=(k == 0), stop=(k == 1))
                last.then_inc(framed, 1)

        @block.vector
        def _(dve):
            for c in range(NCH):
                dve.wait_ge(framed, c + 1)
                nc.vector.tensor_copy(halves(hT[:, c * CH:(c + 1) * CH]), ps[:, c % 2, :, 0:HB]).then_inc(kept, 1)


NL, DST, DCV, DIN, DTR, H2 = 3, 16, 4, 256, 32, 64
MW = {}
_at = 0
for _name, _width in (("wi", 2 * DIN), ("cw", 2 * DCV), ("cb", 2), ("xp", 2 * 128), ("dw", DIN), ("db", 2),
                      ("alog", 2 * DST), ("dp", 2), ("wo", 2 * D), ("g", 1), ("b", 1)):
    MW[_name] = (_at, _width)
    _at += _width
MWID = _at


def mamba_layer(nc, cst, layer, w_dram, m):
    with ExitStack() as ctx:
        def sb(name, shape, dt=F32):
            return sbuf(nc, ctx, name, shape, dt)

        w = sb("w", [128, MWID])
        u = sb("u", [128, 2, NT])
        sz = sb("sz", [128, 2, NT])
        dt = sb("dt", [128, 2, NT])
        du = sb("du", [128, 2, NT])
        xd = sb("xd", [128, NT])
        bc = sb("bc", [128, NT + CH], BF16)
        negA = sb("negA", [128, 2 * DST])

        def W(name, a=0, n=None):
            at, width = MW[name]
            return w[:, at + a:at + (width if n is None else a + n)]

        def chunk(t, half, c):
            return t[:, half, ds(c * CH, CH)]

        with ExitStack() as c1:
            px = psum(nc, c1, "px", [128, 2, 2, BANK], F32)
            pz = psum(nc, c1, "pz", [128, 2, BANK], F32)
            pxd = psum(nc, c1, "pxd", [128, 2, BANK], F32)
            left = sbuf(nc, c1, "left", [128, CH])
            high = sbuf(nc, c1, "high", [128, CH], BF16)
            (w_loaded, x_ready, z_ready, tap0, conv, u_ready, z_done, xd_ready, xd_done, pc) = c1.enter_context(
                stage(nc, "w_loaded x_ready z_ready tap0 conv u_ready z_done xd_ready xd_done pool_chain"))
            block = c1.enter_context(nc.Block())

            def cols(c, k):
                return slice(c * CH + k * HB, c * CH + (k + 1) * HB)

            @block.sync
            def _(sp):
                sp.dma_start(w[:, :], w_dram[ds(layer, 1), :, :].rearrange("o p n -> p (o n)")).then_inc(w_loaded, 16)

            @block.tensor
            def _(pe):
                def x(c):
                    if c >= 1:
                        pe.wait_ge(conv, (DCV - 1) * c)
                    for half in range(2):
                        for k in range(2):
                            last = nc.tensor.matmul(px[:, half, k, 0:HB], W("wi", half * 128, 128), m[:, cols(c, k)],
                                                    start=True, stop=True)
                    last.then_inc(x_ready, 1)

                pe.wait_ge(w_loaded, 16)
                x(0)
                for c in range(NCH):
                    for half in range(2):
                        if c + half >= 1:
                            pe.wait_ge(z_done, 2 * c + half)
                        for k in range(2):
                            last = nc.tensor.matmul(pz[:, k, 0:HB], W("wi", DIN + half * 128, 128), m[:, cols(c, k)],
                                                    start=True, stop=True)
                        last.then_inc(z_ready, 1)
                    if c + 1 < NCH:
                        x(c + 1)
                    pe.wait_ge(u_ready, c + 1)
                    if c >= 1:
                        pe.wait_ge(xd_done, c)
                    for k in range(2):
                        for half in range(2):
                            last = nc.tensor.matmul(pxd[:, k, 0:HB], W("xp", half * 128, 128), u[:, half, cols(c, k)],
                                                    start=(half == 0), stop=(half == 1))
                    last.then_inc(xd_ready, 1)

            @block.scalar
            def _(act):
                nc.scalar.preload_act_table_set("silu_and_others")
                for c in range(NCH):
                    act.wait_ge(x_ready, c + 1)
                    for half in range(2):
                        last = nc.scalar.activation(halves(chunk(u, half, c)), px[:, half, :, 0:HB], ACT.Identity,
                                                    scale=W("cw", half * DCV + DCV - 1, 1), bias=W("cb", half, 1))
                    last.then_inc(tap0, 1)
                    for half in range(2):
                        act.wait_ge(z_ready, 2 * c + half + 1)
                        nc.scalar.activation(halves(chunk(sz, half, c)), pz[:, :, 0:HB], ACT.Silu).then_inc(z_done, 1)
                    if c >= 1:
                        act.wait_ge(xd_ready, c)
                        nc.scalar.activation(halves(xd[:, (c - 1) * CH:c * CH]), pxd[:, :, 0:HB], ACT.Copy).then_inc(xd_done, 1)
                    act.wait_ge(conv, (DCV - 1) * (c + 1))
                    uc = u[:, :, c * CH:(c + 1) * CH]
                    nc.scalar.activation(uc, uc, ACT.Silu).then_inc(u_ready, 1)
                act.wait_ge(xd_ready, NCH)
                nc.scalar.activation(halves(xd[:, (NCH - 1) * CH:]), pxd[:, :, 0:HB], ACT.Copy).then_inc(xd_done, 1)

            @block.vector
            def _(dve):
                for c in range(NCH):
                    dve.wait_ge(tap0, c + 1)
                    for j in range(1, DCV):
                        if j > 1:
                            dve.wait_ge(conv, (DCV - 1) * c + (j - 1))
                        for half in range(2):
                            for k in range(2):
                                o = u[:, half, cols(c, k)].rearrange("p (b s) -> p b s", s=S)[:, :, j:S]
                                x = px[:, half, k, 0:HB].rearrange("p (b s) -> p b s", s=S)[:, :, 0:S - j]
                                last = nc.vector.scalar_tensor_tensor(
                                    out=o, in0=x, scalar=W("cw", half * DCV + DCV - 1 - j, 1), in1=o,
                                    op0=ALU.mult, op1=ALU.add)
                        last.then_inc(conv, 1)

            @block.gpsimd
            def _(pool):
                link = Chain(pool, pc)
                g = nc.gpsimd
                link(g.memset(bc[:, :], 0.0))
                for c in range(NCH):
                    at = slice(c * CH, (c + 1) * CH)
                    pool.wait_ge(xd_done, c + 1)
                    link(g.tensor_copy(high[:, :], xd[:, at]))
                    link(g.tensor_copy(bc[32:64, at], high[32:64, :]))
                    link(g.tensor_tensor(left[:, :], xd[:, at], high[:, :], ALU.subtract))
                    link(g.tensor_copy(high[:, :], left[:, :]))
                    link(g.tensor_copy(bc[64:96, at], high[64:96, :]))
                    link(g.tensor_tensor(bc[96:128, at], left[96:128, :], high[96:128, :], ALU.subtract))

        with ExitStack() as c1:
            pd = psum(nc, c1, "pd", [128, 2, 2, 2, BANK], F32)
            e = sbuf(nc, c1, "e", [128, 2, 2, CH], F32)
            ser = sbuf(nc, c1, "ser", [128, 2, 2, CH], F32)
            small = sbuf(nc, c1, "small", [128, 2, 2, CH], mybir.dt.int8)
            ln = sbuf(nc, c1, "ln", [128, 2, 2, CH], F32)
            (d_ready, ac, x_read, kept, e_ready, ser_ready, ln_ready, marked, dt_done, dc, du_done) = c1.enter_context(
                stage(nc, "d_ready act_chain x_read max_kept e_ready ser_ready ln_ready marked dt_done dve_chain du_done"))
            block = c1.enter_context(nc.Block())

            @block.tensor
            def _(pe):
                for c in range(NCH):
                    if c >= 2:
                        pe.wait_ge(kept, c - 1)
                    for half in range(2):
                        for k in range(2):
                            a = c * CH + k * HB
                            last = nc.tensor.matmul(pd[:, c % 2, half, k, 0:HB], W("dw", half * 128, 128)[0:DTR, :],
                                                    xd[0:DTR, a:a + HB], start=True, stop=True)
                    last.then_inc(d_ready, 1)

            @block.scalar
            def _(act):
                link = Chain(act, ac)
                nc.scalar.preload_act_table_set("natural_log_exp_and_others")
                link(nc.scalar.activation(negA[:, :], W("alog"), ACT.Exp))
                link(nc.scalar.activation(negA[:, :], negA[:, :], ACT.Copy, scale=-1.0))
                for c in range(NCH):
                    act.wait_ge(d_ready, c + 1)
                    if c >= 2:
                        act.wait_ge(dt_done, c - 1)
                    ec = e[:, c % 2, :, :]
                    for half in range(2):
                        last = nc.scalar.activation(halves(ec[:, half, :]), pd[:, c % 2, half, :, 0:HB], ACT.Abs,
                                                    bias=W("db", half, 1))
                    last.then_inc(x_read, 1)
                    act.wait_ge(x_read, c + 1)
                    nc.scalar.activation(ec, ec, ACT.Exp, scale=-1.0).then_inc(e_ready, 1)
                    act.wait_ge(e_ready, c + 1)
                    nc.scalar.activation(ser[:, c % 2, :, :], ec, ACT.Copy, scale=-0.25).then_inc(ser_ready, 1)
                    nc.scalar.activation(ln[:, c % 2, :, :], ec, ACT.Ln, bias=1.0).then_inc(ln_ready, 1)

            @block.vector
            def _(dve):
                link = Chain(dve, dc)
                v = nc.vector
                for c in range(NCH):
                    d = dt[:, :, c * CH:(c + 1) * CH]
                    dve.wait_ge(x_read, c + 1)
                    for half in range(2):
                        last = v.tensor_scalar(halves(d[:, half, :]), pd[:, c % 2, half, :, 0:HB], W("db", half, 1), 0.0,
                                               ALU.add, ALU.max)
                    last.then_inc(kept, 1)
                    dve.wait_ge(ser_ready, c + 1)
                    t = ser[:, c % 2, :, :]
                    for k in (1.0 / 3, -0.5, 1.0):
                        link(v.scalar_tensor_tensor(out=t, in0=t, scalar=k, in1=e[:, c % 2, :, :], op0=ALU.add, op1=ALU.mult))
                    dve.wait_ge(ln_ready, c + 1)
                    dve.wait_ge(marked, c + 1)
                    link(v.copy_predicated(ln[:, c % 2, :, :], small[:, c % 2, :, :], t))
                    dve.wait_ge(kept, c + 1)
                    v.tensor_tensor(d, d, ln[:, c % 2, :, :], ALU.add).then_inc(dt_done, 1)

            @block.gpsimd
            def _(pool):
                def mark(c):
                    pool.wait_ge(e_ready, c + 1)
                    nc.gpsimd.tensor_scalar(small[:, c % 2, :, :], e[:, c % 2, :, :], 1.0 / 32, None,
                                            ALU.is_lt).then_inc(marked, 1)

                mark(0)
                for c in range(NCH):
                    if c + 1 < NCH:
                        mark(c + 1)
                    pool.wait_ge(dt_done, c + 1)
                    at = slice(c * CH, (c + 1) * CH)
                    nc.gpsimd.tensor_tensor(du[:, :, at], dt[:, :, at], u[:, :, at], ALU.mult).then_inc(du_done, 1)

        with ExitStack() as c1:
            pb = psum(nc, c1, "pb", [128, 2, BANK], F32)
            pcc = psum(nc, c1, "pcc", [128, 2, BANK], F32)
            py = psum(nc, c1, "py", [128, 2, 2, BANK], F32)
            Bs = sbuf(nc, c1, "Bs", [128, 4, CH], F32)
            dA = sbuf(nc, c1, "dA", [128, 2, 2, CH], F32)
            dBu = sbuf(nc, c1, "dBu", [128, 2, 2, CH], F32)
            hst = sbuf(nc, c1, "hst", [128, 4, 2 * CH], F32)
            hC = sbuf(nc, c1, "hC", [128, 2, 2, CH], F32)
            (z0, b_ready, b_kept, dBu_ready, c_ready, dA_ready, h_ready, c_used, y_added, y_skip, y_done, pe_passed,
             act_passed, pool_passed) = c1.enter_context(
                stage(nc, "dA_zeroed b_ready b_kept dBu_ready c_ready dA_ready h_ready c_used y_added y_skip y_done "
                          "pe_passed act_passed pool_passed"))
            block = c1.enter_context(nc.Block())

            @block.gpsimd
            def _(pool):
                hold = Hold(pool, pool_passed)
                nc.gpsimd.memset(dA[:, :, :, :], 0.0).then_inc(z0, 1)
                with pool.Fori(0, NCH) as c:
                    for n in range(DST):
                        i = c * DST + n
                        hold(b_kept, i + 2)
                        hold(h_ready, i + 1)
                        nc.gpsimd.tensor_tensor(dBu[:, n % 2, :, :], du[:, :, ds(c * CH, CH)],
                                                Bs[:, n % 4, :].unsqueeze(1).broadcast_to([128, 2, CH]),
                                                ALU.mult).then_inc(dBu_ready, 1)

            @block.tensor
            def _(pe):
                hold = Hold(pe, pe_passed)

                def spread(c, r, o, done):
                    for k in range(2):
                        last = nc.tensor.matmul(o[:, k, 0:HB], cst["row"][:, r, :], bc[:, ds(c * CH + k * HB, HB)],
                                                start=True, stop=True)
                    last.then_inc(done, 1)

                pe.sem_inc(y_added, 2)
                for n in range(3):
                    pe.wait_ge(b_kept, n + 1)
                    spread(0, n, pb, b_ready)
                with pe.Fori(0, NCH) as c:
                    def add(n):
                        for half in range(2):
                            for k in range(2):
                                last = nc.tensor.matmul(py[:, half, k, 0:HB], cst["ident"],
                                                        hC[:, n % 2, half, k * HB:(k + 1) * HB],
                                                        start=(n == 0), stop=(n == DST - 1))
                        last.then_inc(y_added, 1)

                    for n in range(DST):
                        i = c * DST + n
                        hold(b_kept, i + 4)
                        spread(c + (n + 3) // DST, (n + 3) % DST, pb, b_ready)
                        hold(c_used, i + 1)
                        spread(c, DST + n, pcc, c_ready)
                        if n == 1:
                            pe.wait_ge(y_skip, c + 1)
                        if n >= 1:
                            add(n - 1)
                    pe.wait_ge(c_used, c * DST + (DST + 1))
                    add(DST - 1)

            @block.scalar
            def _(act):
                hold = Hold(act, act_passed)

                def keep(k, step):
                    act.wait_ge(b_ready, step)
                    nc.scalar.activation(halves(Bs[:, k, :]), pb[:, :, 0:HB], ACT.Copy).then_inc(b_kept, 1)

                act.sem_inc(b_kept, 1)
                act.wait_ge(z0, 1)
                keep(0, 1)
                keep(1, 2)
                with act.Fori(0, NCH) as c:
                    for n in range(DST):
                        i = c * DST + n
                        hold(h_ready, i + 1)
                        for half in range(2):
                            o = dA[:, n % 2, half, :].rearrange("p (b s) -> p b s", s=S)[:, :, 1:S]
                            x = chunk(dt, half, c).rearrange("p (b s) -> p b s", s=S)[:, :, 1:S]
                            last = nc.scalar.activation(o, x, ACT.Exp, scale=negA[:, half * DST + n:half * DST + n + 1])
                        last.then_inc(dA_ready, 1)
                        keep((n + 2) % 4, i + 3)

            @block.vector
            def _(dve):
                dve.sem_inc(h_ready, 2)
                dve.sem_inc(c_used, 1)
                dve.sem_inc(y_skip, 1)
                with dve.Fori(0, NCH) as c:
                    def weigh(n):
                        i = c * DST + n
                        dve.wait_ge(h_ready, i + 3)
                        dve.wait_ge(c_ready, i + 1)
                        dve.wait_ge(y_added, i + 1)
                        nc.vector.tensor_tensor(
                            hC[:, n % 2, :, :].rearrange("p a (h n) -> p a h n", h=2),
                            hst[:, n % 4, :].rearrange("p (a h n) -> p a h n", a=2, h=2),
                            pcc[:, :, 0:HB].unsqueeze(1).broadcast_to([128, 2, 2, HB]), ALU.mult).then_inc(c_used, 1)

                    for n in range(DST):
                        i = c * DST + n
                        dve.wait_ge(dBu_ready, i + 1)
                        dve.wait_ge(dA_ready, i + 1)
                        nc.vector.tensor_tensor_scan(hst[:, n % 4, :], dA[:, n % 2, :, :].rearrange("p a n -> p (a n)"),
                                                     dBu[:, n % 2, :, :].rearrange("p a n -> p (a n)"), 0.0, ALU.mult,
                                                     ALU.add).then_inc(h_ready, 1)
                        if n >= 1:
                            weigh(n - 1)
                    weigh(DST - 1)
                    dve.wait_ge(y_added, c * DST + (DST + 2))
                    for half in range(2):
                        uc = halves(chunk(u, half, c))
                        last = nc.vector.scalar_tensor_tensor(out=uc, in0=uc, scalar=W("dp", half, 1),
                                                              in1=py[:, half, :, 0:HB], op0=ALU.mult, op1=ALU.add)
                    last.then_inc(y_skip, 1)
                    dve.wait_ge(y_skip, c + 2)
                    uc = u[:, :, ds(c * CH, CH)]
                    nc.vector.tensor_tensor(uc, uc, sz[:, :, ds(c * CH, CH)], ALU.mult).then_inc(y_done, 1)

        with ExitStack() as c1:
            po = psum(nc, c1, "po", [128, 2, 2, BANK], F32)
            (o_ready, o_added) = c1.enter_context(stage(nc, "o_ready o_added"))
            block = c1.enter_context(nc.Block())

            @block.tensor
            def _(pe):
                for c in range(NCH):
                    if c >= 2:
                        pe.wait_ge(o_added, c - 1)
                    for k in range(2):
                        for half in range(2):
                            a = c * CH + k * HB
                            last = nc.tensor.matmul(po[:, c % 2, k, 0:HB], W("wo", half * D, D), u[:, half, a:a + HB],
                                                    start=(half == 0), stop=(half == 1))
                    last.then_inc(o_ready, 1)

            @block.vector
            def _(dve):
                for c in range(NCH):
                    dve.wait_ge(o_ready, c + 1)
                    mc = halves(m[:, c * CH:(c + 1) * CH])
                    nc.vector.tensor_tensor(mc, mc, po[:, c % 2, :, 0:HB], ALU.add).then_inc(o_added, 1)
        layernorm(nc, cst, m, m, W("g"), W("b"))


def lstm_fusion(nc, cst, w_dram, x, m, hT):
    with ExitStack() as ctx:
        def sb(name, shape, dt=F32):
            return sbuf(nc, ctx, name, shape, dt)

        GP = NB + 32
        wih = sb("wih", [128, 4, 2 * H2])
        whh = sb("whh", [128, 4, 2, H2])
        bias = sb("bias", [128, 4])
        bias2 = sb("bias2", [128, 4])
        fw = sb("fw", [128, 3, D])
        fb = sb("fb", [128, 1])
        gx = sb("gx", [128, S, 4, GP])
        hist = sb("hist", [128, (S + 1) * NB + 32])
        z = sb("z", [128, 5, NB])
        prod = sb("prod", [128, 2, NB])
        tc = sb("tc", [128, NB])
        wih_d, whh_d, b_d, fw_d, fb_d = w_dram
        FG = BANK // NB
        NFG = -(-S // FG)
        with ExitStack() as c1:
            pi = psum(nc, c1, "pi", [128, 2, 4, BANK])
            (w_loaded, whh_loaded, zeroed, biased, multiplied, placed) = c1.enter_context(
                stage(nc, "w_loaded whh_loaded zeroed biased multiplied placed"))
            block = c1.enter_context(nc.Block())

            @block.sync
            def _(sp):
                for dst, src in ((wih[:, :, :], wih_d), (bias[:, :], b_d[0]), (bias2[:, :], b_d[1]),
                                 (fw[:, :, :], fw_d), (fb[:, :], fb_d)):
                    sp.dma_start(dst, src).then_inc(w_loaded, 16)
                sp.wait_ge(zeroed, 1)
                for d in range(2):
                    sp.dma_start(whh[d * H2:(d + 1) * H2, :, d, :], whh_d[d]).then_inc(whh_loaded, 16)
                sp.wait_ge(whh_loaded, 32)

            @block.gpsimd
            def _(pool):
                nc.gpsimd.memset(whh[:, :, :, :], 0.0).then_inc(zeroed, 1)
                nc.gpsimd.memset(gx[:, :, :, NB:GP], 0.0)
                nc.gpsimd.memset(hist[:, :], 0.0)
                nc.gpsimd.memset(z[:, 4, :], 0.0).then_inc(zeroed, 1)

            @block.tensor
            def _(pe):
                pe.wait_ge(w_loaded, 80)
                xs = x[:, :].rearrange("p (b s) -> p s b", s=S)
                for q in range(NFG):
                    if q >= 2:
                        pe.wait_ge(placed, q - 1)
                    n = min(FG, S - q * FG)
                    for g in range(4):
                        last = nc.tensor.matmul(pi[:, q % 2, g, 0:n * NB], wih[:, g, :], xs[:, q * FG:q * FG + n, :],
                                                start=True, stop=True)
                    last.then_inc(multiplied, 1)

            @block.vector
            def _(dve):
                v = nc.vector
                dve.wait_ge(w_loaded, 80)
                v.tensor_tensor(bias[:, :], bias[:, :], bias2[:, :], ALU.add).then_inc(biased, 1)
                dve.wait_ge(biased, 1)
                for q in range(NFG):
                    dve.wait_ge(multiplied, q + 1)
                    n = min(FG, S - q * FG)
                    for g in range(4):
                        v.tensor_scalar(gx[0:H2, q * FG:q * FG + n, g, 0:NB],
                                        pi[0:H2, q % 2, g, 0:n * NB].rearrange("p (s b) -> p s b", b=NB),
                                        bias[0:H2, g:g + 1], None, ALU.add)
                    for s in range(n):
                        last = v.tensor_tensor(gx[H2:128, S - 1 - (q * FG + s), :, 0:NB],
                                               pi[H2:128, q % 2, :, s * NB:(s + 1) * NB],
                                               bias[H2:128, :].unsqueeze(2).broadcast_to([H2, 4, NB]), ALU.add)
                    last.then_inc(placed, 1)

        pg = psum(nc, ctx, "pg", [128, 2, BANK], F32)
        pf = psum(nc, ctx, "pf", [128, NFG, BANK], F32)
        (g_ready, t_ready, dc, c_ready, tc_ready, h_ready, f_ready) = ctx.enter_context(
            stage(nc, "g_ready t_ready dve_chain c_ready tc_ready h_ready f_ready"))
        block = ctx.enter_context(nc.Block())

        @block.tensor
        def _(pe):
            ms = m[:, :].rearrange("p (b s) -> p s b", s=S)

            def from_x(t, j):
                nc.tensor.matmul(pg[:, j, 0:4 * GP], cst["ident"], gx[:, ds(t, 1), :, :].rearrange("p o g b -> p (o g b)"),
                                 start=True, stop=False, skip_group_check=True)

            def from_h(t, j):
                for g in range(4):
                    last = nc.tensor.matmul(pg[:, j, g * GP:(g + 1) * GP], whh[:, g, :, :].rearrange("p d h -> p (d h)"),
                                            hist[:, ds(t * NB, GP)], start=False, stop=True, skip_group_check=True)
                last.then_inc(g_ready, 1)

            from_x(0, 0)
            from_h(0, 0)
            for q in range(NFG):
                n = min(FG, S - q * FG)
                nc.tensor.matmul(pf[:, q, 0:n * NB], fw[:, 0, :], ms[:, q * FG:q * FG + n, :], start=True, stop=False,
                                 skip_group_check=True)
            with pe.Fori(0, (S - 1) // 2) as i:
                for j in range(2):
                    t = 2 * i + j + 1
                    from_x(t, (j + 1) % 2)
                    pe.wait_ge(h_ready, t)
                    from_h(t, (j + 1) % 2)
            pe.wait_ge(h_ready, S)
            for q in range(NFG):
                n = min(FG, S - q * FG)
                nc.tensor.matmul(pf[:, q, 0:n * NB], fw[:, 1, :], hist[:, (q * FG + 1) * NB:(q * FG + 1 + n) * NB],
                                 start=False, stop=False, skip_group_check=True)
            for s in range(S):
                last = nc.tensor.matmul(pf[:, s // FG, (s % FG) * NB:(s % FG + 1) * NB], fw[:, 2, :],
                                        hist[:, (S - s) * NB:(S - s + 1) * NB], start=False, stop=True,
                                        skip_group_check=True)
            last.then_inc(f_ready, 1)

        @block.scalar
        def _(act):
            nc.scalar.preload_act_table_set("sigmoid_and_others")

            def step(t, j):
                act.wait_ge(g_ready, t + 1)
                p = pg[:, j, 0:4 * GP].rearrange("p (g b) -> p g b", b=GP)
                nc.scalar.activation(z[:, 0:3, :], p[:, 0:3, 0:NB], ACT.Sigmoid)
                nc.scalar.activation(z[:, 3, :], p[:, 3, 0:NB], ACT.Tanh).then_inc(t_ready, 1)
                act.wait_ge(c_ready, t + 1)
                nc.scalar.activation(tc[:, :], z[:, 4, :], ACT.Tanh).then_inc(tc_ready, 1)

            step(0, 0)
            with act.Fori(0, (S - 1) // 2) as i:
                for j in range(2):
                    step(2 * i + j + 1, (j + 1) % 2)

        @block.vector
        def _(dve):
            link = Chain(dve, dc)
            with link.loop(S, 1) as t:
                dve.wait_ge(t_ready, t + 1)
                link(nc.vector.tensor_tensor(prod[:, :, :], z[:, 0:2, :], z[:, 3:5, :], ALU.mult))
                nc.vector.tensor_tensor(z[:, 4, :], prod[:, 0, :], prod[:, 1, :], ALU.add).then_inc(c_ready, 1)
                dve.wait_ge(tc_ready, t + 1)
                nc.vector.tensor_tensor(hist[:, ds((t + 1) * NB, NB)], z[:, 2, :], tc[:, :], ALU.mult).then_inc(h_ready, 1)
            dve.wait_ge(f_ready, 1)
            hs = hT[:, :].rearrange("p (b s) -> p s b", s=S)
            for q in range(NFG):
                n = min(FG, S - FG * q)
                o = hs[:, FG * q:FG * q + n, :]
                nc.vector.scalar_tensor_tensor(out=o, in0=pf[:, q, 0:n * NB].rearrange("p (s b) -> p s b", b=NB),
                                               scalar=fb[:, :], in1=o, op0=ALU.add, op1=ALU.add)


def load(nc, *pairs):
    with ExitStack() as ctx:
        (loaded,) = ctx.enter_context(stage(nc, "loaded"))
        block = ctx.enter_context(nc.Block())

        @block.sync
        def _(sp):
            for dst, src in pairs:
                sp.dma_start(dst, src).then_inc(loaded, 16)
            sp.wait_ge(loaded, 16 * len(pairs))


def project_features(nc, x, out, w, bias, rows=D, residual=False):
    with ExitStack() as ctx:
        ps = psum(nc, ctx, "ps", [128, 2, 2, BANK], F32)
        (multiplied, kept) = ctx.enter_context(stage(nc, "multiplied kept"))
        block = ctx.enter_context(nc.Block())

        @block.tensor
        def _(pe):
            for c in range(NCH):
                if c >= 2:
                    pe.wait_ge(kept, c - 1)
                for k in range(2):
                    a = c * CH + k * HB
                    last = nc.tensor.matmul(ps[0:rows, c % 2, k, 0:HB], w, x[:, a:a + HB], start=True, stop=True)
                last.then_inc(multiplied, 1)

        if residual:
            @block.vector
            def _(dve):
                for c in range(NCH):
                    dve.wait_ge(multiplied, c + 1)
                    o = halves(out[:, c * CH:(c + 1) * CH])
                    nc.vector.scalar_tensor_tensor(out=o, in0=ps[0:rows, c % 2, :, 0:HB], scalar=bias, in1=o,
                                                   op0=ALU.add, op1=ALU.add).then_inc(kept, 1)
        else:
            @block.scalar
            def _(act):
                for c in range(NCH):
                    act.wait_ge(multiplied, c + 1)
                    o = halves(out[:, c * CH:(c + 1) * CH])
                    if bias is None:
                        nc.scalar.activation(o, ps[0:rows, c % 2, :, 0:HB], ACT.Copy).then_inc(kept, 1)
                    else:
                        nc.scalar.activation(o, ps[0:rows, c % 2, :, 0:HB], ACT.Identity, bias=bias).then_inc(kept, 1)


def project_tokens(nc, x, T, w, out, bias):
    K, n = w.shape
    with ExitStack() as ctx:
        xt = sbuf(nc, ctx, "xt", [K, 2, T], F32)
        ps = psum(nc, ctx, "ps", [128, 2, BANK], F32)
        (st0, st1, mu0, mu1, kp0, kp1, act_passed, dve_passed) = ctx.enter_context(
            stage(nc, "staged0 staged1 multiplied0 multiplied1 kept0 kept1 act_passed dve_passed"))
        staged, multiplied, kept = (st0, st1), (mu0, mu1), (kp0, kp1)
        block = ctx.enter_context(nc.Block())

        @block.scalar
        def _(act):
            hold = Hold(act, act_passed)
            with act.Fori(0, NT // T // 2) as i:
                for j in range(2):
                    hold(multiplied[j], i)
                    nc.scalar.activation(xt[:, j, :], x[0:K, ds((2 * i + j) * T, T)], ACT.Copy).then_inc(staged[j], 1)

        @block.tensor
        def _(pe):
            with pe.Fori(0, NT // T // 2) as i:
                for j in range(2):
                    pe.wait_ge(kept[j], i)
                    pe.wait_ge(staged[j], i + 1)
                    nc.tensor.matmul(ps[0:T, j, 0:n], xt[:, j, :], w, start=True, stop=True).then_inc(multiplied[j], 1)

        @block.vector
        def _(dve):
            hold = Hold(dve, dve_passed)
            with dve.Fori(0, NT // T // 2) as i:
                for j in range(2):
                    hold(multiplied[j], i + 1)
                    o = out[:, ds(2 * i + j, 1), :].rearrange("p o n -> p (o n)")
                    if bias is None:
                        nc.vector.tensor_copy(o, ps[0:T, j, 0:n]).then_inc(kept[j], 1)
                    else:
                        nc.vector.tensor_tensor(o, ps[0:T, j, 0:n], bias, ALU.add).then_inc(kept[j], 1)


AT = 2 * S
NAT = NT // AT
G = 4
NH, HD = 8, 16


def channel_attention(nc, cst, a, x, hT):
    with ExitStack() as ctx:
        def sb(name, shape, dt=F32):
            return sbuf(nc, ctx, name, shape, dt)

        w = sb("w", [128, 4 * D])
        bqk = sb("bqk", [AT, 2 * D])
        cols = sb("cols", [128, 2])
        hmask = sb("hmask", [128, D])
        smask = sb("smask", [AT, 2])
        qk = sb("qk", [AT, NAT, 2 * D])
        vT = sb("vT", [128, NT])
        oT = sb("oT", [128, NT])
        load(nc, (w[:, :], a["ca_w"]), (bqk[:, :], a["ca_bqk"]), (cols[:, :], a["ca_b"]),
             (hmask[:, :], a["c_headmask"]), (smask[:, :], a["c_seqmask"]))
        project_tokens(nc, x, AT, w[:, 0:2 * D], qk, bqk[:, :])
        project_features(nc, x, vT, w[:, 2 * D:3 * D], cols[:, 0:1])
        with ExitStack() as c1:
            NG = NAT * 2 * NH
            sq = sbuf(nc, c1, "sq", [AT, NAT, 2 * D])
            r = sbuf(nc, c1, "r", [AT, NG])
            (squared, summed, ac, r_ready, dc) = c1.enter_context(stage(nc, "squared summed act_chain r_ready dve_chain"))
            block = c1.enter_context(nc.Block())

            @block.scalar
            def _(act):
                link = Chain(act, ac)
                nc.scalar.activation(sq[:, :, :], qk[:, :, :], ACT.Square).then_inc(squared, 1)
                act.wait_ge(summed, 1)
                link(nc.scalar.activation(r[:, :], r[:, :], ACT.Ln))
                nc.scalar.activation(r[:, :], r[:, :], ACT.Exp, scale=-0.5).then_inc(r_ready, 1)

            @block.vector
            def _(dve):
                link = Chain(dve, dc)
                dve.wait_ge(squared, 1)
                link(nc.vector.tensor_reduce(r[:, :], sq[:, :, :].rearrange("p t (g d) -> p (t g) d", d=HD), AX.X, ALU.add))
                nc.vector.tensor_scalar(r[:, :], r[:, :], 1e-12, None, ALU.max).then_inc(summed, 1)
                dve.wait_ge(r_ready, 1)
                q = r[:, :].rearrange("p (t h) -> p t h", h=2 * NH)[:, :, 0:NH]
                link(nc.vector.tensor_scalar(q, q, HD ** -0.5, None, ALU.mult))
                g = qk[:, :, :].rearrange("p t (g d) -> p (t g) d", d=HD)
                link(nc.vector.tensor_tensor(g, g, r[:, :].unsqueeze(2).broadcast_to([AT, NG, HD]), ALU.mult))
        with ExitStack() as c1:
            q = sbuf(nc, c1, "q", [AT, G, D])
            kx = sbuf(nc, c1, "kx", [AT, G, 2, D])
            sc = sbuf(nc, c1, "sc", [128, 2 * G, D])
            mx = sbuf(nc, c1, "mx", [128, 2 * G])
            sm = sbuf(nc, c1, "sm", [128, 2 * G])
            ps = psum(nc, c1, "ps", [128, 2 * G, D])
            po = psum(nc, c1, "po", [128, BANK])
            (q_staged, kx_ready, scored, centered, exped, a_ready, out_ready, out_kept, dc, act_passed, dve_passed, pe_passed) = c1.enter_context(
                stage(nc, "q_staged kx_ready scored centered exped a_ready out_ready out_kept dve_chain act_passed dve_passed pe_passed"))
            block = c1.enter_context(nc.Block())

            @block.scalar
            def _(act):
                hold = Hold(act, act_passed)
                with act.Fori(0, NAT // G) as i:
                    hold(scored, i)
                    nc.scalar.activation(q[:, :, :], qk[:, ds(i * G, G), 0:D], ACT.Copy).then_inc(q_staged, 1)
                    act.wait_ge(centered, i + 1)
                    nc.scalar.activation(sc[:, :, :], sc[:, :, :], ACT.Exp).then_inc(exped, 1)
                    hold(out_ready, i + 1)
                    nc.scalar.activation(oT[:, ds(i * G * AT, G * AT)], po[:, 0:G * AT], ACT.Copy).then_inc(out_kept, 1)

            @block.tensor
            def _(pe):
                hold = Hold(pe, pe_passed)
                with pe.Fori(0, NAT // G) as i:
                    pe.wait_ge(q_staged, i + 1)
                    pe.wait_ge(kx_ready, i + 1)
                    for t in range(G):
                        last = nc.tensor.matmul(ps[:, 2 * t:2 * t + 2, :], q[:, t, :], kx[:, t, :, :],
                                                start=True, stop=True)
                    last.then_inc(scored, 1)
                    hold(a_ready, i + 1)
                    pe.wait_ge(out_kept, i)
                    for s in range(2 * G):
                        last = nc.tensor.matmul(po[:, s * S:(s + 1) * S], sc[:, s, :], vT[:, ds((i * 2 * G + s) * S, S)],
                                                start=True, stop=True)
                    last.then_inc(out_ready, 1)

            @block.vector
            def _(dve):
                hold = Hold(dve, dve_passed)
                link = Chain(dve, dc)
                with link.loop(NAT // G, 6) as i:
                    hold(scored, i)
                    for s in range(2):
                        last = nc.vector.tensor_scalar(kx[:, :, s, :], qk[:, ds(i * G, G), D:2 * D], smask[:, s:s + 1], None, ALU.mult)
                    last.then_inc(kx_ready, 1)
                    hold(scored, i + 1)
                    dve.wait_ge(out_ready, i)
                    link(nc.vector.tensor_tensor(sc[:, :, :], ps[:, :, :], hmask[:, :].unsqueeze(1).broadcast_to([128, 2 * G, D]), ALU.add))
                    link(nc.vector.tensor_reduce(mx[:, :], sc[:, :, :], AX.X, ALU.max))
                    nc.vector.tensor_tensor(sc[:, :, :], sc[:, :, :], mx[:, :].unsqueeze(2).broadcast_to([128, 2 * G, D]),
                                            ALU.subtract).then_inc(centered, 1)
                    dve.wait_ge(exped, i + 1)
                    link(nc.vector.tensor_reduce(sm[:, :], sc[:, :, :], AX.X, ALU.add))
                    link(nc.vector.reciprocal(sm[:, :], sm[:, :]))
                    link(nc.vector.tensor_tensor(sc[:, :, :], sc[:, :, :], sm[:, :].unsqueeze(2).broadcast_to([128, 2 * G, D]), ALU.mult))
                    nc.vector.tensor_copy(mx[:, 0:1], sm[:, 0:1]).then_inc(a_ready, 1)
                    link(nc.vector.tensor_copy(mx[:, 1:2], sm[:, 1:2]))
        project_features(nc, oT, hT, w[:, 3 * D:4 * D], cols[:, 1:2], residual=True)


def frame_attention(nc, cst, a, x, hT):
    with ExitStack() as ctx:
        def sb(name, shape, dt=F32):
            return sbuf(nc, ctx, name, shape, dt)

        w = sb("w", [128, 3 * D])
        bmask = sb("bmask", [AT, AT])
        qT = sb("qT", [128, NT])
        kT = sb("kT", [128, NT])
        v = sb("v", [AT, NAT, D])
        load(nc, (w[:, :], a["fa_w"]), (bmask[:, :], a["c_blockmask"]))
        project_features(nc, x, qT, w[:, 0:D], None)
        project_features(nc, x, kT, w[:, D:2 * D], None)
        project_tokens(nc, x, AT, w[:, 2 * D:3 * D], v, None)
        with ExitStack() as c1:
            q = sbuf(nc, c1, "q", [128, G, AT])
            vs = sbuf(nc, c1, "vs", [AT, G, D])
            sc = sbuf(nc, c1, "sc", [AT, G, AT])
            zr = sbuf(nc, c1, "zr", [AT, G, AT])
            pT = sbuf(nc, c1, "pT", [AT, G, AT])
            mx = sbuf(nc, c1, "mx", [AT, G])
            sm = sbuf(nc, c1, "sm", [AT, G])
            ps = psum(nc, c1, "ps", [AT, BANK])
            pt = psum(nc, c1, "pt", [AT, BANK])
            po = psum(nc, c1, "po", [128, BANK])
            (staged, scored, centered, exped, p_ready, turned, pT_ready, out_ready, out_added, dc, act_passed, pe_passed) = c1.enter_context(
                stage(nc, "staged scored centered exped p_ready turned pT_ready out_ready out_added dve_chain act_passed pe_passed"))
            block = c1.enter_context(nc.Block())

            def tiles(t):
                return t[:, 0:G * AT].rearrange("p (g n) -> p g n", g=G)

            @block.scalar
            def _(act):
                hold = Hold(act, act_passed)
                with act.Fori(0, NAT // G) as i:
                    hold(out_ready, i)
                    nc.scalar.activation(vs[:, :, :], v[:, ds(i * G, G), :], ACT.Copy)
                    nc.scalar.activation(q[:, :, :].rearrange("p g n -> p (g n)"), qT[:, ds(i * G * AT, G * AT)],
                                         ACT.Copy).then_inc(staged, 1)
                    act.wait_ge(centered, i + 1)
                    nc.scalar.activation(sc[:, :, :], sc[:, :, :], ACT.Exp).then_inc(exped, 1)
                    act.wait_ge(turned, i + 1)
                    nc.scalar.activation(pT[:, :, :], tiles(pt), ACT.Copy).then_inc(pT_ready, 1)

            @block.tensor
            def _(pe):
                hold = Hold(pe, pe_passed)
                with pe.Fori(0, NAT // G) as i:
                    hold(staged, i + 1)
                    for t in range(G):
                        last = nc.tensor.matmul(ps[:, t * AT:(t + 1) * AT], q[:, t, :], kT[:, ds((i * G + t) * AT, AT)],
                                                start=True, stop=True)
                    last.then_inc(scored, 1)
                    pe.wait_ge(p_ready, i + 1)
                    for t in range(G):
                        last = nc.tensor.transpose(pt[:, t * AT:(t + 1) * AT], sc[:, t, :], cst["ident"][0:AT, 0:AT])
                    last.then_inc(turned, 1)
                    pe.wait_ge(pT_ready, i + 1)
                    pe.wait_ge(out_added, i)
                    for t in range(G):
                        last = nc.tensor.matmul(po[:, t * AT:(t + 1) * AT], vs[:, t, :], pT[:, t, :], start=True, stop=True)
                    last.then_inc(out_ready, 1)

            @block.vector
            def _(dve):
                link = Chain(dve, dc)
                with link.loop(NAT // G, 7) as i:
                    dve.wait_ge(scored, i + 1)
                    dve.wait_ge(turned, i)
                    link(nc.vector.tensor_scalar(sc[:, :, :], tiles(ps), D ** -0.5, None, ALU.mult))
                    link(nc.vector.tensor_scalar(zr[:, :, :], sc[:, :, :], 0.0, 1e-10, ALU.is_equal, ALU.mult))
                    link(nc.vector.tensor_tensor(sc[:, :, :], sc[:, :, :], zr[:, :, :], ALU.add))
                    link(nc.vector.tensor_tensor(sc[:, :, :], sc[:, :, :], bmask[:, :].unsqueeze(1).broadcast_to([AT, G, AT]), ALU.add))
                    link(nc.vector.tensor_reduce(mx[:, :], sc[:, :, :], AX.X, ALU.max))
                    nc.vector.tensor_tensor(sc[:, :, :], sc[:, :, :], mx[:, :].unsqueeze(2).broadcast_to([AT, G, AT]),
                                            ALU.subtract).then_inc(centered, 1)
                    dve.wait_ge(exped, i + 1)
                    link(nc.vector.tensor_reduce(sm[:, :], sc[:, :, :], AX.X, ALU.add))
                    link(nc.vector.reciprocal(sm[:, :], sm[:, :]))
                    nc.vector.tensor_tensor(sc[:, :, :], sc[:, :, :], sm[:, :].unsqueeze(2).broadcast_to([AT, G, AT]),
                                            ALU.mult).then_inc(p_ready, 1)
                    dve.wait_ge(out_ready, i + 1)
                    o = hT[:, ds(i * G * AT, G * AT)]
                    nc.vector.tensor_tensor(o, po[:, 0:G * AT], o, ALU.add).then_inc(out_added, 1)


NST = 64


def state_space(nc, cst, a, x, hT):
    with ExitStack() as ctx:
        def sb(name, shape, dt=F32):
            return sbuf(nc, ctx, name, shape, dt)

        p = sb("p", [128, 7 * NST + 2])
        fc = sb("fc", [128, 3, NST])
        e = sb("e", [128, 2, NST])
        e2 = sb("e2", [128, 2, NST])
        di = sb("di", [128, NST])
        qd = sb("qd", [128, NST])
        st = sb("st", [128, 2, NST])
        bd = sb("bd", [128, NST])
        prod = sb("prod", [128, 4, NST])
        g = sb("g", [128, 4])
        kc = sb("kc", [128, 4])
        t1 = sb("t1", [128, 2])
        dt = sb("dt", [128, 1])
        dots = sb("dots", [128, S, 3])
        xp = sb("xp", [128, NB, 2 * S - 1])
        diag = sb("diag", [128, 2, 128])
        py = psum(nc, ctx, "py", [128, 8, BANK])
        load(nc, (p[:, :], a["ss_w"]))
        L, Pl, Pr = p[:, 0:NST], p[:, NST:3 * NST].rearrange("p (k n) -> p k n", k=2), p[:, 3 * NST:5 * NST].rearrange("p (k n) -> p k n", k=2)
        B, C = p[:, 5 * NST:6 * NST], p[:, 6 * NST:7 * NST]
        log_dt, Dp = p[:, 7 * NST:7 * NST + 1], p[:, 7 * NST + 1:7 * NST + 2]
        with ExitStack() as c1:
            (ac, exped, dc, padded, taps) = c1.enter_context(stage(nc, "act_chain exped dve_chain padded taps"))
            block = c1.enter_context(nc.Block())

            @block.scalar
            def _(act):
                nc.scalar.activation(dt[:, :], log_dt, ACT.Exp)
                nc.scalar.activation(L, L, ACT.Exp).then_inc(exped, 1)

            @block.gpsimd
            def _(pool):
                nc.gpsimd.memset(xp[:, :, 0:S - 1], 0.0).then_inc(padded, 1)
                nc.gpsimd.tensor_copy(xp[:, :, S - 1:2 * S - 1], x[:, :].rearrange("p (b s) -> p b s", s=S)).then_inc(padded, 1)

            @block.vector
            def _(dve):
                link = Chain(dve, dc)
                v = nc.vector
                dve.wait_ge(exped, 1)
                b2 = [128, 2, NST]
                link(v.tensor_scalar(di[:, :], L, dt[:, :], 0.5, ALU.mult, ALU.mult))
                link(v.tensor_scalar(di[:, :], di[:, :], 1.0, None, ALU.add))
                link(v.reciprocal(di[:, :], di[:, :]))
                link(v.tensor_scalar(Pl, Pl, dt[:, :], 0.5, ALU.mult, ALU.mult))
                link(v.tensor_tensor(e2[:, :, :], Pl, di[:, :].unsqueeze(1).broadcast_to(b2), ALU.mult))
                link(v.tensor_tensor(fc[:, 0:2, :], Pr, di[:, :].unsqueeze(1).broadcast_to(b2), ALU.mult))
                link(v.tensor_copy(fc[:, 2, :], C))
                for i in range(2):
                    link(v.tensor_tensor(prod[:, 2 * i:2 * i + 2, :], fc[:, i:i + 1, :].broadcast_to(b2), Pl, ALU.mult))
                link(v.tensor_reduce(g[:, :], prod[:, :, :], AX.X, ALU.add))
                link(v.tensor_scalar(kc[:, 0:1], g[:, 3:4], -1.0, 1.0, ALU.mult, ALU.add))
                link(v.tensor_scalar(kc[:, 3:4], g[:, 0:1], -1.0, 1.0, ALU.mult, ALU.add))
                link(v.tensor_copy(kc[:, 1:3], g[:, 1:3]))
                link(v.tensor_tensor(t1[:, 0:1], kc[:, 0:1], kc[:, 3:4], ALU.mult))
                link(v.tensor_tensor(t1[:, 1:2], kc[:, 1:2], kc[:, 2:3], ALU.mult))
                link(v.tensor_tensor(t1[:, 0:1], t1[:, 0:1], t1[:, 1:2], ALU.subtract))
                link(v.reciprocal(t1[:, 0:1], t1[:, 0:1]))
                link(v.tensor_scalar(kc[:, :], kc[:, :], t1[:, 0:1], None, ALU.mult))
                for j in range(2):
                    link(v.tensor_scalar(e[:, j, :], e2[:, 0, :], kc[:, j:j + 1], None, ALU.mult))
                    link(v.scalar_tensor_tensor(out=e[:, j, :], in0=e2[:, 1, :], scalar=kc[:, 2 + j:3 + j], in1=e[:, j, :],
                                                op0=ALU.mult, op1=ALU.add))

                def dot(s, out):
                    link(v.tensor_tensor(prod[:, 0:3, :], fc[:, :, :], s.unsqueeze(1).broadcast_to([128, 3, NST]), ALU.mult))
                    link(v.tensor_reduce(out, prod[:, 0:3, :], AX.X, ALU.add))

                link(v.tensor_scalar(bd[:, :], B, dt[:, :], None, ALU.mult))
                dot(bd[:, :], kc[:, 0:3])
                link(v.tensor_tensor(st[:, 0, :], bd[:, :], di[:, :], ALU.mult))
                for j in range(2):
                    link(v.scalar_tensor_tensor(out=st[:, 0, :], in0=e[:, j, :], scalar=kc[:, j:j + 1], in1=st[:, 0, :],
                                                op0=ALU.mult, op1=ALU.add))
                link(v.tensor_scalar(qd[:, :], di[:, :], 2.0, -1.0, ALU.mult, ALU.add))
                link(v.tensor_scalar(e[:, :, :], e[:, :, :], 2.0, None, ALU.mult))
                with link.loop(S, 5) as t:
                    d = dots[:, ds(t, 1), :].rearrange("p o n -> p (o n)")
                    dot(st[:, 0, :], d)
                    link(v.tensor_tensor(st[:, 0, :], st[:, 0, :], qd[:, :], ALU.mult))
                    for j in range(2):
                        link(v.scalar_tensor_tensor(out=st[:, 0, :], in0=e[:, j, :], scalar=d[:, j:j + 1], in1=st[:, 0, :],
                                                    op0=ALU.mult, op1=ALU.add))
                link(v.tensor_tensor(dots[:, 0, 2:3], dots[:, 0, 2:3], Dp, ALU.add))
        with ExitStack() as c1:
            (d0, d1, u0, u1, summed, dc) = c1.enter_context(stage(nc, "diag_ready0 diag_ready1 diag_used0 diag_used1 summed dve_chain"))
            diag_ready, diag_used = (d0, d1), (u0, u1)
            block = c1.enter_context(nc.Block())

            @block.vector
            def _(dve):
                def build(j, i, t):
                    dve.wait_ge(diag_used[j], i)
                    nc.vector.tensor_scalar(diag[:, j, :], cst["ident"], t.rearrange("p o n -> p (o n)"), None,
                                            ALU.mult).then_inc(diag_ready[j], 1)

                with dve.Fori(0, (S - 1) // 2) as i:
                    for j in range(2):
                        build(j, i, dots[:, ds(2 * i + j, 1), 2:3])
                build(0, (S - 1) // 2, dots[:, S - 1:S, 2:3])
                dve.wait_ge(summed, 1)
                for q in range(8):
                    o = hT[:, q * HB:(q + 1) * HB]
                    nc.vector.tensor_tensor(o, py[:, q, 0:HB], o, ALU.add)

            @block.tensor
            def _(pe):
                def tap(j, i, t, first, final):
                    pe.wait_ge(diag_ready[j], i + 1)
                    for q in range(8):
                        at = ds(S - 1 - t, S) if not isinstance(t, int) else slice(S - 1 - t, 2 * S - 1 - t)
                        last = nc.tensor.matmul(py[:, q, 0:HB], diag[:, j, :], xp[:, 8 * q:8 * q + 8, at],
                                                start=first, stop=final)
                    return last

                tap(0, 0, 0, True, False).then_inc(diag_used[0], 1)
                tap(1, 0, 1, False, False).then_inc(diag_used[1], 1)
                with pe.Fori(1, (S - 1) // 2) as i:
                    for j in range(2):
                        tap(j, i, 2 * i + j, False, False).then_inc(diag_used[j], 1)
                tap(0, (S - 1) // 2, S - 1, False, True).then_inc(summed, 1)


BIG = 1024.0


def route(nc, a, l, E, K, oh, gate, prob):
    with ExitStack() as ctx:
        iota = sbuf(nc, ctx, "iota", [TT, E])
        cand = sbuf(nc, ctx, "cand", [TT, NTT, E])
        left = sbuf(nc, ctx, "left", [TT, NTT, E])
        mx = sbuf(nc, ctx, "mx", [TT, 2, NTT])
        first = sbuf(nc, ctx, "first", [TT, NTT])
        load(nc, (iota[:, :], a["c_iota"][0:TT, 0:E]))
        (dc, ready, exped) = ctx.enter_context(stage(nc, "dve_chain ready exped"))
        block = ctx.enter_context(nc.Block())
        full = [TT, NTT, E]

        def over(t):
            return t.unsqueeze(2).broadcast_to(full)

        @block.vector
        def _(dve):
            link = Chain(dve, dc)
            v = nc.vector
            io = iota[:, :].unsqueeze(1).broadcast_to(full)
            src = l
            for k in range(K):
                link(v.tensor_reduce(mx[:, k, :], src[:, :, :], AX.X, ALU.max))
                link(v.tensor_tensor(cand[:, :, :], src[:, :, :], over(mx[:, k, :]), ALU.is_equal))
                link(v.tensor_scalar(cand[:, :, :], cand[:, :, :], -BIG, BIG, ALU.mult, ALU.add))
                link(v.tensor_tensor(cand[:, :, :], cand[:, :, :], io, ALU.add))
                link(v.tensor_reduce(first[:, :], cand[:, :, :], AX.X, ALU.min))
                link(v.tensor_tensor(oh[k][:, :, :], io, over(first[:, :]), ALU.is_equal))
                if k + 1 < K:
                    link(v.tensor_scalar(left[:, :, :], oh[k][:, :, :], -1e30, None, ALU.mult))
                    link(v.tensor_tensor(left[:, :, :], left[:, :, :], l[:, :, :], ALU.add))
                    src = left
            if prob:
                v.tensor_tensor(cand[:, :, :], l[:, :, :], over(mx[:, 0, :]), ALU.subtract).then_inc(ready, 1)
                dve.wait_ge(exped, 1)
                link(v.tensor_reduce(first[:, :], cand[:, :, :], AX.X, ALU.add))
                link(v.reciprocal(gate[0][:, :], first[:, :]))
            else:
                v.tensor_tensor(gate[1][:, :], mx[:, 1, :], mx[:, 0, :], ALU.subtract).then_inc(ready, 1)
                dve.wait_ge(exped, 1)
                link(v.tensor_scalar(first[:, :], gate[1][:, :], 1.0, None, ALU.add))
                link(v.reciprocal(gate[0][:, :], first[:, :]))
                link(v.tensor_tensor(gate[1][:, :], gate[1][:, :], gate[0][:, :], ALU.mult))

        @block.scalar
        def _(act):
            act.wait_ge(ready, 1)
            t = cand[:, :, :] if prob else gate[1][:, :]
            nc.scalar.activation(t, t, ACT.Exp).then_inc(exped, 1)


def token_rows(nc, cst, x, out):
    with ExitStack() as ctx:
        xt = sbuf(nc, ctx, "xt", [D, 2, TT])
        ps = psum(nc, ctx, "ps", [TT, 2, BANK])
        (st0, st1, t0, t1, kp0, kp1, act_passed, dve_passed) = ctx.enter_context(
            stage(nc, "staged0 staged1 turned0 turned1 kept0 kept1 act_passed dve_passed"))
        staged, turned, kept = (st0, st1), (t0, t1), (kp0, kp1)
        block = ctx.enter_context(nc.Block())

        @block.scalar
        def _(act):
            hold = Hold(act, act_passed)
            with act.Fori(0, NTT // 2) as i:
                for j in range(2):
                    hold(turned[j], i)
                    nc.scalar.activation(xt[:, j, :], x[:, ds((2 * i + j) * TT, TT)], ACT.Copy).then_inc(staged[j], 1)

        @block.tensor
        def _(pe):
            with pe.Fori(0, NTT // 2) as i:
                for j in range(2):
                    pe.wait_ge(kept[j], i)
                    pe.wait_ge(staged[j], i + 1)
                    nc.tensor.transpose(ps[:, j, 0:D], xt[:, j, :], cst["ident"]).then_inc(turned[j], 1)

        @block.vector
        def _(dve):
            hold = Hold(dve, dve_passed)
            with dve.Fori(0, NTT // 2) as i:
                for j in range(2):
                    hold(turned[j], i + 1)
                    nc.vector.tensor_copy(out[:, ds(2 * i + j, 1), :].rearrange("p o n -> p (o n)"), ps[:, j, 0:D]).then_inc(kept[j], 1)


ST = 128


def mixture(nc, cst, a, key, x, logits, out, E, K, F, act_fn, prob, capacity=None):
    NTILE = (K * NT + E * (ST - 1)) // ST
    UN = 4
    NTILE = -(-NTILE // UN) * UN
    NSLOT = NTILE * ST
    W1, W2, B1 = (F, F, F // 128) if F else (D, 0, 0)
    WE = W1 + W2 + B1
    FC = F // 128
    w_dram, b_dram = a[key + "_w"], a[key + "_b"]
    xs = nc.dram_tensor(unique(nc, "slots_in"), [NSLOT, D], F32, kind="Internal").ap()
    ys = nc.dram_tensor(unique(nc, "slots_out"), [NSLOT, D], F32, kind="Internal").ap()
    with ExitStack() as ctx:
        def sb(name, shape, dt=F32):
            return sbuf(nc, ctx, name, shape, dt)

        oh = [sb(f"oh{k}", [TT, NTT, E]) for k in range(K)]
        gate = [sb(f"gate{k}", [TT, NTT]) for k in range(K)]
        keepg = sb("keepg", [TT, 2, NTT])
        slot = [sb(f"slot{k}", [TT, NTT], I32) for k in range(K)]
        eid = sb("eid", [1, NTILE], I32)
        rows = sb("rows", [TT, NTT, D])
        zero = sb("zero", [128, D])
        (zeroed, cleared) = ctx.enter_context(stage(nc, "zeroed cleared"))
        with nc.Block() as block:
            @block.vector
            def _(dve):
                nc.vector.memset(zero[:, :], 0.0).then_inc(zeroed, 1)

            @block.sync
            def _(sp):
                sp.wait_ge(zeroed, 1)
                sp.dma_start(xs.rearrange("(p r) d -> p r d", p=128),
                             zero[:, :].unsqueeze(1).broadcast_to([128, NTILE, D])).then_inc(cleared, 16)
        route(nc, a, logits, E, K, oh, gate, prob)
        token_rows(nc, cst, x, rows)

        with ExitStack() as c1:
            NBK = -(-NTT * E // BANK)
            comb = sbuf(nc, c1, "comb", [TT, NTT * E])
            rank = sbuf(nc, c1, "rank", [TT, NTT, E])
            tot = sbuf(nc, c1, "tot", [TT, E, NTT])
            keep_t = sbuf(nc, c1, "keep_t", [TT, E, NTT])
            incl = sbuf(nc, c1, "incl", [TT, E, NTT])
            tri = sbuf(nc, c1, "tri", [TT, TT])
            ones = sbuf(nc, c1, "ones", [TT, TT])
            tf = sbuf(nc, c1, "tf", [TT, 4, E])
            ti = sbuf(nc, c1, "ti", [TT, E], I32)
            it = sbuf(nc, c1, "it", [1, NTILE])
            cmp = sbuf(nc, c1, "cmp", [1, NTILE, E])
            ef = sbuf(nc, c1, "ef", [1, NTILE])
            sf = sbuf(nc, c1, "sf", [TT, NTT])
            pr = psum(nc, c1, "pr", [TT, NBK * BANK])
            pt = psum(nc, c1, "pt", [TT, NBK * BANK])
            load(nc, (tri[:, :], a["c_tri"]), (keep_t[:, :, :], a["c_carry"][:, 0:E * NTT].rearrange("p (e t) -> p e t", e=E)),
                 (it[:, :], a["c_iota"][0:1, 0:NTILE]))
            (dc, combined, counted) = c1.enter_context(stage(nc, "dve_chain combined counted"))
            block = c1.enter_context(nc.Block())

            @block.tensor
            def _(pe):
                pe.wait_ge(combined, 1)
                for lhs, o in ((tri, pr), (ones, pt)):
                    for q in range(NBK):
                        n = min(BANK, NTT * E - q * BANK)
                        last = nc.tensor.matmul(o[:, q * BANK:q * BANK + n], lhs[:, :], comb[:, q * BANK:q * BANK + n],
                                                start=True, stop=True)
                last.then_inc(counted, 1)

            @block.vector
            def _(dve):
                link = Chain(dve, dc)
                v = nc.vector
                cb = comb[:, :].rearrange("p (t e) -> p t e", e=E)
                link(v.memset(ones[:, :], 1.0))
                if K == 2:
                    v.tensor_tensor(cb, oh[0][:, :, :], oh[1][:, :, :], ALU.add).then_inc(combined, 1)
                else:
                    v.tensor_copy(cb, oh[0][:, :, :]).then_inc(combined, 1)
                dve.wait_ge(counted, 1)
                link(v.tensor_copy(tot[:, :, :], pt[:, 0:NTT * E].rearrange("p (t e) -> p e t", e=E)))
                flat = "p e t -> p (e t)"
                link(v.tensor_tensor_scan(incl[:, :, :].rearrange(flat), keep_t[:, :, :].rearrange(flat),
                                          tot[:, :, :].rearrange(flat), 0.0, ALU.mult, ALU.add))
                link(v.tensor_tensor(tot[:, :, :], incl[:, :, :], tot[:, :, :], ALU.subtract))
                link(v.tensor_tensor(rank[:, :, :], pr[:, 0:NTT * E].rearrange("p (t e) -> p t e", e=E),
                                     tot[:, :, :].rearrange("p e t -> p t e"), ALU.add))
                n_e = incl[:, :, NTT - 1]
                link(v.tensor_scalar(ti[:, :], n_e, float(ST - 1), None, ALU.add))
                link(v.tensor_scalar(ti[:, :], ti[:, :], ST.bit_length() - 1, None, ALU.logical_shift_right))
                link(v.tensor_copy(tf[:, 0, :], ti[:, :]))
                link(v.memset(tf[:, 1, :], 1.0))
                link(v.tensor_tensor_scan(tf[:, 2, :], tf[:, 1, :], tf[:, 0, :], 0.0, ALU.mult, ALU.add))
                link(v.tensor_tensor(tf[:, 3, :], tf[:, 2, :], tf[:, 0, :], ALU.subtract))
                if capacity is not None:
                    link(v.tensor_tensor(cb, rank[:, :, :], oh[0][:, :, :], ALU.mult))
                    link(v.tensor_reduce(sf[:, :], cb, AX.X, ALU.add))
                    link(v.tensor_scalar(sf[:, :], sf[:, :], float(capacity), None, ALU.is_le))
                    link(v.tensor_tensor(keepg[:, 0, :], sf[:, :], gate[0][:, :], ALU.mult))
                    link(v.tensor_tensor(keepg[:, 1, :], gate[0][:, :], keepg[:, 0, :], ALU.subtract))
                link(v.tensor_scalar(tf[:, 1, :], tf[:, 3, :], float(ST), -1.0, ALU.mult, ALU.add))
                link(v.tensor_tensor(rank[:, :, :], rank[:, :, :], tf[:, 1:2, :].broadcast_to([TT, NTT, E]), ALU.add))
                for k in range(K):
                    link(v.tensor_tensor(cb, rank[:, :, :], oh[k][:, :, :], ALU.mult))
                    link(v.tensor_reduce(sf[:, :], cb, AX.X, ALU.add))
                    link(v.tensor_copy(slot[k][:, :], sf[:, :]))
                link(v.tensor_tensor(cmp[:, :, :], tf[0:1, 2:3, :].broadcast_to([1, NTILE, E]),
                                     it[:, :].unsqueeze(2).broadcast_to([1, NTILE, E]), ALU.is_le))
                link(v.tensor_reduce(ef[:, :], cmp[:, :, :], AX.X, ALU.add))
                link(v.tensor_scalar(ef[:, :], ef[:, :], float(E - 1), None, ALU.min))
                link(v.tensor_copy(eid[:, :], ef[:, :]))

        with ExitStack() as c1:
            scattered, all_scattered = cst["scattered"].sem, cst["scattered"].add(16 * K * NTT)
            block = c1.enter_context(nc.Block())

            @block.gpsimd
            def _(pool):
                pool.wait_ge(cleared, 16)
                for k in range(K):
                    for t in range(NTT):
                        pool.indirect_dma_start(xs, bass.IndirectOffsetOnAxis(ap=slot[k][:, t:t + 1], axis=0),
                                                rows[:, t, :], None).then_inc(scattered, 16)
                pool.wait_ge(scattered, all_scattered)

        with ExitStack() as c1:
            IT = NTILE // UN
            wb = sbuf(nc, c1, "wb", [128, UN, WE])
            bb = sbuf(nc, c1, "bb", [1, UN, D])
            xi = sbuf(nc, c1, "xi", [ST, UN, D])
            xT = sbuf(nc, c1, "xT", [D, UN, ST])
            eh = sbuf(nc, c1, "eh", [128, 2, max(FC, 1), ST])
            yo = sbuf(nc, c1, "yo", [ST, UN, D])
            one = sbuf(nc, c1, "one", [1, ST])
            px = psum(nc, c1, "px", [D, 2, BANK])
            ph = psum(nc, c1, "ph", [128, 2, BANK])
            po = psum(nc, c1, "po", [ST, 2, BANK])
            (one_ready, turned, xT_ready, up, h_ready, down, y_ready, sp_passed) = c1.enter_context(
                stage(nc, "one_ready turned xT_ready up h_ready down y_ready sp_passed"))
            per_buffer = c1.enter_context(stage(nc, " ".join(f"{n}{j}" for n in ("w_loaded", "x_loaded", "stored") for j in range(UN))))
            w_loaded, x_loaded, stored = [per_buffer[UN * k:UN * k + UN] for k in range(3)]
            FREE = UN
            block = c1.enter_context(nc.Block())

            def unrolled(eng, body):
                with eng.Fori(0, IT - 1) as i:
                    for j in range(UN):
                        body(i, j, False)
                for j in range(UN):
                    body(IT - 1, j, True)

            @block.sync
            def _(sp):
                hold = Hold(sp, sp_passed)
                with sp.Fori(0, IT) as i:
                    for j in range(UN):
                        e = sp.value_load(eid[0:1, ds(UN * i + j, 1)], min_val=0, max_val=E - 1)
                        hold(down, UN * i + j + 1)
                        sp.dma_start(xi[:, j, :], xs[ds((UN * i + j) * ST, ST), :]).then_inc(x_loaded[j], 16)
                        sp.dma_start(wb[:, j, :], w_dram[ds(e, 1), :, :].rearrange("o p n -> p (o n)")).then_inc(w_loaded[j], 16)
                        sp.dma_start(bb[:, j, :], b_dram[ds(e, 1), :]).then_inc(w_loaded[j], 16)

            @block.tensor
            def _(pe):
                pe.sem_inc(down, FREE)
                pe.wait_ge(one_ready, 1)

                def turn(i, j):
                    i, j = i + j // UN, j % UN
                    pe.wait_ge(x_loaded[j], 16 * (i + 1))
                    nc.tensor.transpose(px[:, j % 2, 0:ST], xi[:, j, :], cst["ident"]).then_inc(turned, 1)

                def first_layer(i, j):
                    pe.wait_ge(xT_ready, UN * i + j + 1)
                    i, j = i + j // UN, j % UN
                    pe.wait_ge(w_loaded[j], 32 * (i + 1))
                    for f in range(FC):
                        last = nc.tensor.matmul(ph[:, j % 2, f * ST:(f + 1) * ST], wb[:, j, f * 128:(f + 1) * 128],
                                                xT[:, j, :], start=True, stop=True)
                    last.then_inc(up, 1)

                def second_layer(i, j):
                    t = UN * i + j
                    pe.wait_ge(y_ready, t + 1)
                    if F:
                        pe.wait_ge(h_ready, t + 1)
                        for f in range(FC):
                            nc.tensor.matmul(po[:, j % 2, 0:D], eh[:, j % 2, f, :], wb[:, j, F + f * D:F + (f + 1) * D],
                                             start=(f == 0), stop=False)
                    else:
                        pe.wait_ge(w_loaded[j], 32 * (i + 1))
                        nc.tensor.matmul(po[:, j % 2, 0:D], xT[:, j, :], wb[:, j, 0:D], start=True, stop=False)
                    nc.tensor.matmul(po[:, j % 2, 0:D], one[:, :], bb[:, j, :], start=False, stop=True).then_inc(down, 1)

                turn(0, 0)
                turn(0, 1)
                if F:
                    first_layer(0, 0)

                def body(i, j, last):
                    if not last or j + 2 < UN:
                        pe.wait_ge(xT_ready, UN * i + j + 1)
                        turn(i, j + 2)
                    elif not F:
                        pe.wait_ge(xT_ready, UN * i + j + 1)
                    if F and (not last or j + 1 < UN):
                        first_layer(i, j + 1)
                    second_layer(i, j)

                unrolled(pe, body)

            @block.vector
            def _(dve):
                def turn(i, j):
                    t = UN * i + j
                    dve.wait_ge(turned, t + 1)
                    dve.wait_ge(down, t + 1)
                    nc.vector.tensor_copy(xT[:, j % UN, :], px[:, j % 2, 0:ST]).then_inc(xT_ready, 1)

                dve.sem_inc(y_ready, 2)
                nc.vector.memset(one[:, :], 1.0).then_inc(one_ready, 1)
                turn(0, 0)
                turn(0, 1)

                def body(i, j, last):
                    if not last or j + 2 < UN:
                        turn(i, j + 2)
                    dve.wait_ge(down, UN * i + j + 1 + FREE)
                    dve.wait_ge(stored[j], 16 * i)
                    nc.vector.tensor_copy(yo[:, j, :], po[:, j % 2, 0:D]).then_inc(y_ready, 1)

                unrolled(dve, body)

            @block.scalar
            def _(act):
                def hidden(i, j):
                    t = UN * i + j
                    act.wait_ge(up, t + 1)
                    act.wait_ge(down, t + FREE - 1)
                    j = j % UN
                    for f in range(FC):
                        last = nc.scalar.activation(eh[:, j % 2, f, :], ph[:, j % 2, f * ST:(f + 1) * ST], act_fn,
                                                    bias=wb[:, j, W1 + W2 + f:W1 + W2 + f + 1])
                    last.then_inc(h_ready, 1)

                if F:
                    nc.scalar.preload_act_table_set("silu_and_others" if act_fn == ACT.Silu else "gelu_and_others")
                    hidden(0, 0)

                def body(i, j, last):
                    if F and (not last or j + 1 < UN):
                        hidden(i, j + 1)
                    act.wait_ge(y_ready, UN * i + j + 3)
                    act.dma_start(ys[ds((UN * i + j) * ST, ST), :], yo[:, j, :]).then_inc(stored[j], 16)

                unrolled(act, body)
                for j in range(UN):
                    act.wait_ge(stored[j], 16 * IT)

        with ExitStack() as c1:
            gk = [sbuf(nc, c1, f"g{k}", [TT, NTT, D]) for k in range(K)]
            pt = psum(nc, c1, "pt", [D, 2, BANK])
            gathered = [(g.sem, g.add(16 * K)) for g in cst["gathered"]]
            (weighed, turned, added, dc) = c1.enter_context(stage(nc, "weighed turned added dve_chain"))
            block = c1.enter_context(nc.Block())

            @block.gpsimd
            def _(pool):
                for t in range(NTT):
                    for k in range(K):
                        pool.indirect_dma_start(gk[k][:, t, :], None, ys,
                                                bass.IndirectOffsetOnAxis(ap=slot[k][:, t:t + 1], axis=0)).then_inc(gathered[t][0], 16)

            @block.vector
            def _(dve):
                link = Chain(dve, dc)
                v = nc.vector

                def weigh(t):
                    dve.wait_ge(*gathered[t])
                    r = gk[0][:, t, :]
                    if capacity is not None:
                        link(v.tensor_scalar(r, r, keepg[:, 0, t:t + 1], None, ALU.mult))
                        v.scalar_tensor_tensor(out=r, in0=rows[:, t, :], scalar=keepg[:, 1, t:t + 1], in1=r,
                                               op0=ALU.mult, op1=ALU.add).then_inc(weighed, 1)
                    elif K == 1:
                        v.tensor_scalar(r, r, gate[0][:, t:t + 1], None, ALU.mult).then_inc(weighed, 1)
                    else:
                        link(v.tensor_scalar(r, r, gate[0][:, t:t + 1], None, ALU.mult))
                        v.scalar_tensor_tensor(out=r, in0=gk[1][:, t, :], scalar=gate[1][:, t:t + 1], in1=r,
                                               op0=ALU.mult, op1=ALU.add).then_inc(weighed, 1)

                def add(t):
                    dve.wait_ge(turned, t + 1)
                    o = out[:, t * TT:(t + 1) * TT]
                    v.tensor_tensor(o, pt[:, t % 2, 0:TT], o, ALU.add).then_inc(added, 1)

                weigh(0)
                for t in range(NTT):
                    if t + 1 < NTT:
                        weigh(t + 1)
                    add(t)

            @block.tensor
            def _(pe):
                for t in range(NTT):
                    if t >= 2:
                        pe.wait_ge(added, t - 1)
                    pe.wait_ge(weighed, t + 1)
                    nc.tensor.transpose(pt[:, t % 2, 0:TT], gk[0][:, t, :], cst["ident"][0:TT, 0:TT]).then_inc(turned, 1)


def switch_ffn(nc, cst, a, x, hT):
    E = 16
    with ExitStack() as ctx:
        w = sbuf(nc, ctx, "w", [128, E])
        b = sbuf(nc, ctx, "b", [TT, E])
        l = sbuf(nc, ctx, "l", [TT, NTT, E])
        load(nc, (w[:, :], a["sw_r"]), (b[:, :], a["sw_rb"]))
        project_tokens(nc, x, TT, w[:, :], l, b[:, :])
        mixture(nc, cst, a, "sw", x, l, hT, E, 1, 0, None, True, capacity=int(1.2 * NT / E))


def gelu_ffn(nc, cst, a, x, hT):
    E = 8
    with ExitStack() as ctx:
        w = sbuf(nc, ctx, "w", [128, E])
        b = sbuf(nc, ctx, "b", [TT, E])
        l = sbuf(nc, ctx, "l", [TT, NTT, E])
        load(nc, (w[:, :], a["gf_r"]), (b[:, :], a["gf_rb"]))
        project_tokens(nc, x, TT, w[:, :], l, b[:, :])
        mixture(nc, cst, a, "gf", x, l, hT, E, 1, 512, ACT.Gelu, True)


def two_layer(nc, x, w1, b1, w2, b2, out, F, add):
    FC = F // 128
    with ExitStack() as ctx:
        hid = sbuf(nc, ctx, "hid", [128, 2, FC, HB])
        ph = psum(nc, ctx, "ph", [128, FC, BANK])
        po = psum(nc, ctx, "po", [128, 2, BANK])
        (up, h_ready, down, kept) = ctx.enter_context(stage(nc, "up h_ready down kept"))
        block = ctx.enter_context(nc.Block())
        n = 2 * NCH

        @block.tensor
        def _(pe):
            def second(c):
                pe.wait_ge(h_ready, c + 1)
                if c >= 2:
                    pe.wait_ge(kept, c - 1)
                for f in range(FC):
                    last = nc.tensor.matmul(po[:, c % 2, 0:HB], w2[:, f * D:(f + 1) * D], hid[:, c % 2, f, :],
                                            start=(f == 0), stop=(f == FC - 1))
                last.then_inc(down, 1)

            for c in range(n):
                if c >= 1:
                    pe.wait_ge(h_ready, c)
                for f in range(FC):
                    last = nc.tensor.matmul(ph[:, f, 0:HB], w1[:, f * 128:(f + 1) * 128], x[:, c * HB:(c + 1) * HB],
                                            start=True, stop=True)
                last.then_inc(up, 1)
                if c >= 1:
                    second(c - 1)
            second(n - 1)

        @block.scalar
        def _(act):
            nc.scalar.preload_act_table_set("silu_and_others")
            for c in range(n):
                act.wait_ge(up, c + 1)
                if c >= 2:
                    act.wait_ge(down, c - 1)
                for f in range(FC):
                    last = nc.scalar.activation(hid[:, c % 2, f, :], ph[:, f, 0:HB], ACT.Silu, bias=b1[:, f:f + 1])
                last.then_inc(h_ready, 1)

        @block.vector
        def _(dve):
            for c in range(n):
                dve.wait_ge(down, c + 1)
                o = out[:, c * HB:(c + 1) * HB]
                if add:
                    nc.vector.scalar_tensor_tensor(out=o, in0=po[:, c % 2, 0:HB], scalar=b2, in1=o,
                                                   op0=ALU.add, op1=ALU.add).then_inc(kept, 1)
                else:
                    nc.vector.tensor_scalar(o, po[:, c % 2, 0:HB], b2, SHARED_SCALE, ALU.add, ALU.mult).then_inc(kept, 1)


SHARED_SCALE = 0.25
TEMP = 0.7


def silu_ffn(nc, cst, a, x, hT):
    E, DR, DFF, DSH = 64, 64, 512, 256
    with ExitStack() as ctx:
        c = sbuf(nc, ctx, "c", [128, 12])
        moe = sbuf(nc, ctx, "moe", [128, NT])
        h = sbuf(nc, ctx, "h", [128, NT])
        load(nc, (c[:, :], a["sf_cols"]))
        layernorm(nc, cst, x, h, c[:, 0:1], c[:, 1:2])
        with ExitStack() as c1:
            w = sbuf(nc, c1, "w", [128, 2 * DSH])
            load(nc, (w[:, :], a["sf_ws"]))
            two_layer(nc, h, w[:, 0:DSH], c[:, 4:6], w[:, DSH:2 * DSH], c[:, 6:7], moe, DSH, False)
        with ExitStack() as c1:
            w = sbuf(nc, c1, "w", [128, DR])
            cb = sbuf(nc, c1, "cb", [DR, E])
            r = sbuf(nc, c1, "r", [DR, NT])
            l = sbuf(nc, c1, "l", [TT, NTT, E])
            load(nc, (w[:, :], a["sf_wr"]), (cb[:, :], a["sf_code"]))
            project_features(nc, h, r, w[:, :], None, rows=DR)
            project_tokens(nc, r, TT, cb[:, :], l, None)
            with ExitStack() as c2:
                (scaled,) = c2.enter_context(stage(nc, "scaled"))
                block = c2.enter_context(nc.Block())

                @block.vector
                def _(dve):
                    nc.vector.tensor_scalar(l[:, :, :], l[:, :, :], 1.0 / TEMP, None, ALU.mult).then_inc(scaled, 1)
            mixture(nc, cst, a, "sf", h, l, moe, E, 2, DFF, ACT.Silu, False)
        layernorm(nc, cst, moe, h, c[:, 2:3], c[:, 3:4])
        with ExitStack() as c1:
            w = sbuf(nc, c1, "w", [128, 2 * DFF])
            load(nc, (w[:, :], a["sf_wf"]))
            two_layer(nc, h, w[:, 0:DFF], c[:, 7:11], w[:, DFF:2 * DFF], c[:, 11:12], hT, DFF, True)
        with ExitStack() as c1:
            (dc,) = c1.enter_context(stage(nc, "dve_chain"))
            block = c1.enter_context(nc.Block())

            @block.vector
            def _(dve):
                link = Chain(dve, dc)
                link(nc.vector.tensor_tensor(hT[:, :], hT[:, :], moe[:, :], ALU.add))
                link(nc.vector.tensor_tensor(hT[:, :], hT[:, :], x[:, :], ALU.add))



LE, LK, TS, BT = 8, 2, NB, S
EK = LE * LK
HE = LE // 2
CB = LK * BT
PERB = BANK // CB
GO = (0, 1, 3, 2)


def lstm_experts(nc, cst, a, x, hT):
    with ExitStack() as ctx:
        def sb(name, shape, dt=F32):
            return sbuf(nc, ctx, name, shape, dt)

        mb = sb("mb", [128, EK, NT], F16)
        rwb = sb("rwb", [128, LK, NT])
        wT = sb("wT", [EK, NT])
        bsp = sb("bsp", [3 * LE, 4 * D], BF16)
        bsel = sb("bsel", [3 * LE, LE, CB], BF16)
        bo = sb("bo", [EK, D])
        wo = sb("wo", [128, LE, D])
        wi = sb("wi", [128, 2, LE, 4 * D], F16)
        wh = sb("wh", [128, 2, LE, 4 * D], F16)
        xs = sb("xs", [128, 2, NT], F16)
        scale = sb("scale", [128, 2])
        with ExitStack() as c1:
            w = sbuf(nc, c1, "w", [128, LE])
            b = sbuf(nc, c1, "b", [TT, LE])
            l = sbuf(nc, c1, "l", [TT, NTT, LE])
            oh = [sbuf(nc, c1, f"oh{k}", [TT, NTT, LE]) for k in range(LK)]
            gate = [sbuf(nc, c1, f"gate{k}", [TT, NTT]) for k in range(LK)]
            load(nc, (w[:, :], a["le_r"]), (b[:, :], a["le_rb"]), (bo[:, :], a["le_bo"]),
                 (wo[:, :, :], a["le_wo"].rearrange("p (e n) -> p e n", e=LE)))
            project_tokens(nc, x, TT, w[:, :], l, b[:, :])
            route(nc, a, l, LE, LK, oh, gate, False)
            expand_routes(nc, cst, a, oh, gate, mb, rwb, wT)
        split_weights(nc, cst, a, x, xs, wi, wh, scale)
        split_bias(nc, a, bsp, bsel, scale)
        UN = 4
        HC = HE * CB
        xm = sb("xm", [128, 2, 2, EK, BT], F16)
        z = sb("z", [128, 2, 5, HC])
        prod = sb("prod", [128, 2, 2, HC])
        tc = sb("tc", [128, 2, HC])
        h = sb("h", [128, 2, HC])
        hs = sb("hs", [128, 2, 2, HC], F16)
        hm = sb("hm", [128, 2, HE, LK, BT])
        hw = sb("hw", [128, UN, EK, BT])
        pg = [psum(nc, ctx, f"pg{q}", [128, 3, BANK]) for q in range(2)]
        py = psum(nc, ctx, "py", [128, BANK])
        names = "gates_ready activated c_ready tc_ready h_ready high_ready parts_ready hw_ready"
        s16 = ctx.enter_context(stage(nc, " ".join(f"{n}{q}" for n in names.split() for q in range(2))))
        gates_ready, activated, c_ready, tc_ready, h_ready, high_ready, parts_ready, hw_ready = [s16[2 * i:2 * i + 2] for i in range(8)]
        (cleared, x_ready, y_ready, y_added, dc, pc, pe_passed, dve_passed, pool_passed) = ctx.enter_context(
            stage(nc, "cleared x_ready y_ready y_added dve_chain pool_chain pe_passed dve_passed pool_passed"))
        block = ctx.enter_context(nc.Block())
        IT = TS // UN

        def tokens(t, n=1):
            return ds(t * BT, n * BT)

        def col(g, e):
            m = g * HE + e
            return m // PERB, (m % PERB) * CB

        @block.tensor
        def _(pe):
            hold = Hold(pe, pe_passed)
            pe.wait_ge(cleared, 1)

            def gates(q, t, j):
                p = pg[q]
                pe.wait_ge(activated[q], t)
                pe.wait_ge(x_ready, t + 1)
                seen = set()
                for g in range(4):
                    e = 0
                    while e < HE:
                        bank, c = col(g, e)
                        n = 1
                        while e + n < HE and col(g, e + n)[0] == bank:
                            n += 1
                        nc.tensor.matmul(p[:, bank, c:c + n * CB], bsp[:, GO[g] * D:(GO[g] + 1) * D],
                                         bsel[:, q * HE + e:q * HE + e + n, :].rearrange("p e c -> p (e c)"),
                                         start=bank not in seen, stop=False, skip_group_check=True)
                        seen.add(bank)
                        e += n
                for u in range(2):
                    if u:
                        pe.wait_ge(parts_ready[q], t)
                    for g in range(4):
                        for e in range(HE):
                            bank, c = col(g, e)
                            ee = q * HE + e
                            if u:
                                rhs = [hs[:, q, part, e * CB:(e + 1) * CB] for part in range(2)]
                            else:
                                rhs = [xm[:, j % 2, part, ee * LK:(ee + 1) * LK, :].rearrange("p k b -> p (k b)") for part in range(2)]
                            for wp, rp in ((0, 0), (0, 1), (1, 0)):
                                last = nc.tensor.matmul(p[:, bank, c:c + CB], (wh if u else wi)[:, wp, ee, GO[g] * D:(GO[g] + 1) * D],
                                                        rhs[rp], start=False, stop=u == 1 and wp == 1, skip_group_check=True)
                last.then_inc(gates_ready[q], 1)

            def output(i):
                for q in range(2):
                    hold(hw_ready[q], UN * i + UN)
                hold(y_added, i)
                for m in range(EK):
                    nc.tensor.matmul(py[:, 0:UN * BT], wo[:, m // LK, :], hw[:, :, m, :], start=(m == 0), stop=False)
                nc.tensor.matmul(py[:, 0:UN * BT], bo[:, :], wT[:, tokens(UN * i, UN)], start=False, stop=True).then_inc(y_ready, 1)

            def body(i, first):
                for j in range(UN):
                    t = UN * i + j
                    gates(0, t, j)
                    if j == 0 and not first:
                        output(i - 1)
                    gates(1, t, j)

            body(0, True)
            with pe.Fori(1, IT) as i:
                body(i, False)
            output(IT - 1)

        @block.scalar
        def _(act):
            def body(i):
                for j in range(UN):
                    t = UN * i + j
                    for q in range(2):
                        act.wait_ge(gates_ready[q], t + 1)
                        flat = z[:, q, :, :].rearrange("p g n -> p (g n)")
                        for f, lo, hi in ((ACT.Sigmoid, 0, 3 * HE), (ACT.Tanh, 3 * HE, 4 * HE)):
                            while lo < hi:
                                bank = lo // PERB
                                n = min(hi, (bank + 1) * PERB) - lo
                                c = (lo % PERB) * CB
                                last = nc.scalar.activation(flat[:, lo * CB:(lo + n) * CB], pg[q][:, bank, c:c + n * CB], f,
                                                            scale=scale[:, 1:2])
                                lo += n
                        last.then_inc(activated[q], 1)
                        act.wait_ge(c_ready[q], t + 1)
                        nc.scalar.activation(tc[:, q, :], z[:, q, 4, :], ACT.Tanh).then_inc(tc_ready[q], 1)

            nc.scalar.preload_act_table_set("sigmoid_and_others")
            with act.Fori(0, IT) as i:
                body(i)

        @block.vector
        def _(dve):
            link = Chain(dve, dc)
            hold = Hold(dve, dve_passed)
            v = nc.vector
            v.memset(hs[:, :, :, :], 0.0)
            v.memset(z[:, :, 4, :], 0.0).then_inc(cleared, 1)

            def add(i):
                hold(y_ready, i + 1)
                o = hT[:, tokens(UN * i, UN)]
                v.tensor_tensor(o, py[:, 0:UN * BT], o, ALU.add).then_inc(y_added, 1)

            def body(i, first):
                for j in range(UN):
                    t = UN * i + j
                    for q in range(2):
                        dve.wait_ge(activated[q], t + 1)
                        link(v.tensor_tensor(prod[:, q, :, :], z[:, q, 0:2, :], z[:, q, 3:5, :], ALU.mult))
                        v.tensor_tensor(z[:, q, 4, :], prod[:, q, 0, :], prod[:, q, 1, :], ALU.add).then_inc(c_ready[q], 1)
                        dve.wait_ge(tc_ready[q], t + 1)
                        dve.wait_ge(hw_ready[q], t)
                        v.tensor_tensor(h[:, q, :], z[:, q, 2, :], tc[:, q, :], ALU.mult).then_inc(h_ready[q], 1)
                        v.tensor_tensor(hs[:, q, 0, :], z[:, q, 2, :], tc[:, q, :], ALU.mult).then_inc(high_ready[q], 1)
                        dve.wait_ge(high_ready[q], t + 1)
                        v.tensor_tensor(hs[:, q, 1, :], h[:, q, :], hs[:, q, 0, :], ALU.subtract).then_inc(parts_ready[q], 1)
                    if j == 1 and not first:
                        add(i - 1)

            dve.wait_ge(cleared, 1)
            body(0, True)
            with link.loop(IT - 1, 2 * UN) as i:
                body(i + 1, False)
            add(IT - 1)

        @block.gpsimd
        def _(pool):
            link = Chain(pool, pc)
            hold = Hold(pool, pool_passed)
            g = nc.gpsimd

            def mask_x(t, j):
                for part in range(2):
                    last = g.tensor_tensor(xm[:, j % 2, part, :, :], xs[:, part, tokens(t)].unsqueeze(1).broadcast_to([128, EK, BT]),
                                           mb[:, :, tokens(t)], ALU.mult)
                last.then_inc(x_ready, 1)

            def weigh(t, j, i):
                for q in range(2):
                    hold(h_ready[q], t + 1)
                    if j == 0:
                        hold(y_ready, i)
                    hold(hw_ready[q], t)
                    link(g.tensor_tensor(hm[:, q, :, :, :].rearrange("p e k b -> p (e k) b"),
                                         h[:, q, :].rearrange("p (m b) -> p m b", b=BT),
                                         mb[:, q * HE * LK:(q + 1) * HE * LK, tokens(t)], ALU.mult))
                    pool.sem_inc(pool_passed, 1)
                    g.tensor_tensor(hw[:, j, q * HE * LK:(q + 1) * HE * LK, :].rearrange("p (e k) b -> p e k b", k=LK),
                                    hm[:, q, :, :, :], rwb[:, :, tokens(t)].unsqueeze(1).broadcast_to([128, HE, LK, BT]),
                                    ALU.mult).then_inc(hw_ready[q], 1)

            mask_x(0, 0)
            mask_x(1, 1)
            with link.loop(IT - 1, 2 * UN) as i:
                for j in range(UN):
                    weigh(UN * i + j, j, i)
                    mask_x(UN * i + j + 2, j)
            for j in range(UN):
                weigh(TS - UN + j, j, IT - 1)
                if j + 2 < UN:
                    mask_x(TS - UN + j + 2, j)


def split_weights(nc, cst, a, x, xs, wi, wh, scale):
    with ExitStack() as ctx:
        wf = [sbuf(nc, ctx, f"wf{k}", [128, LE * 4 * D]) for k in range(2)]
        mx = sbuf(nc, ctx, "mx", [128, 3])
        row = sbuf(nc, ctx, "row", [1, 130])
        k = sbuf(nc, ctx, "k", [128, 3], I32)
        kf = sbuf(nc, ctx, "kf", [128, 3])
        ps = psum(nc, ctx, "ps", [128, BANK])
        pb = psum(nc, ctx, "pb", [128, BANK])
        (wl0, wl1, ones_set, reduced, turned, largest, spread, dc, scale_ready, highs, xhigh) = ctx.enter_context(
            stage(nc, "w_loaded0 w_loaded1 ones_set reduced turned largest spread dve_chain scale_ready highs x_high"))
        block = ctx.enter_context(nc.Block())

        @block.sync
        def _(sp):
            sp.dma_start(wf[0][:, :], a["le_wi"]).then_inc(wl0, 16)
            sp.dma_start(wf[1][:, :], a["le_wh"]).then_inc(wl1, 16)

        @block.tensor
        def _(pe):
            pe.wait_ge(reduced, 1)
            nc.tensor.transpose(ps[0:1, 0:128], mx[:, 2:3], cst["ident"]).then_inc(turned, 1)
            pe.wait_ge(largest, 1)
            nc.tensor.matmul(pb[:, 0:1], row[0:1, 2:130], row[0:1, 0:1], start=True, stop=True).then_inc(spread, 1)

        @block.scalar
        def _(act):
            act.wait_ge(xhigh, 1)
            for n in range(2):
                act.wait_ge(scale_ready, 1 + n)
                w = (wi, wh)[n]
                nc.scalar.activation(w[:, 0, :, :].rearrange("p e n -> p (e n)"), wf[n][:, :], ACT.Copy).then_inc(highs, 1)

        @block.vector
        def _(dve):
            link = Chain(dve, dc)
            v = nc.vector
            v.tensor_copy(xs[:, 0, :], x[:, :]).then_inc(xhigh, 1)
            dve.wait_ge(xhigh, 1)
            link(v.tensor_tensor(xs[:, 1, :], x[:, :], xs[:, 0, :], ALU.subtract))
            link(v.memset(row[:, :], 1.0))
            for n in range(2):
                dve.wait_ge((wl0, wl1)[n], 16)
                link(v.tensor_reduce(mx[:, n:n + 1], wf[n][:, :], AX.X, ALU.max, apply_absolute_value=True))
            v.tensor_tensor(mx[:, 2:3], mx[:, 0:1], mx[:, 1:2], ALU.max).then_inc(reduced, 1)
            dve.wait_ge(turned, 1)
            v.tensor_reduce(row[:, 0:1], ps[0:1, 0:128], AX.X, ALU.max).then_inc(largest, 1)
            dve.wait_ge(spread, 1)
            link(v.tensor_scalar(kf[:, 0:1], pb[:, 0:1], 2.0 ** -60, None, ALU.max))
            link(v.tensor_scalar(k[:, 0:1], kf[:, 0:1].bitcast(I32), 23, None, ALU.logical_shift_right))
            link(v.tensor_scalar(k[:, 1:2], k[:, 0:1], -1.0, 127.0 + 127.0 + 13.0, ALU.mult, ALU.add))
            link(v.tensor_scalar(k[:, 2:3], k[:, 0:1], -13.0, None, ALU.add))
            link(v.tensor_scalar(scale[:, :].bitcast(I32), k[:, 1:3], 23, None, ALU.logical_shift_left))
            for n in range(2):
                v.tensor_scalar(wf[n][:, :], wf[n][:, :], scale[:, 0:1], None, ALU.mult).then_inc(scale_ready, 1)
            for n in range(2):
                dve.wait_ge(highs, n + 1)
                w = (wi, wh)[n]
                link(v.tensor_tensor(w[:, 1, :, :].rearrange("p e n -> p (e n)"), wf[n][:, :],
                                     w[:, 0, :, :].rearrange("p e n -> p (e n)"), ALU.subtract))


def expand_routes(nc, cst, a, oh, gate, mb, rwb, wT):
    with ExitStack() as ctx:
        ek = sbuf(nc, ctx, "ek", [TT, NTT, 2 * EK + LK])
        mT = sbuf(nc, ctx, "mT", [EK, NT], BF16)
        gT = sbuf(nc, ctx, "gT", [LK, NT])
        sel = sbuf(nc, ctx, "sel", [EK, EK, 128])
        selb = sbuf(nc, ctx, "selb", [EK, EK, 128], BF16)
        pt = psum(nc, ctx, "pt", [EK, 2, BANK])
        pbc = psum(nc, ctx, "pbc", [128, 2, 2, BANK])
        load(nc, (sel[:, :, :], a["c_sel"].rearrange("p (e n) -> p e n", e=EK)))
        (placed, turned, kept, spread, read_a, read_b, dc) = ctx.enter_context(
            stage(nc, "placed turned kept spread spread_kept_act spread_kept_dve dve_chain"))
        block = ctx.enter_context(nc.Block())
        PB = BANK // TT
        parts = [(0, EK, mT), (EK, EK, wT), (2 * EK, LK, gT)]
        groups = [(p, q) for p in range(3) for q in range(-(-NTT // PB))]

        @block.vector
        def _(dve):
            link = Chain(dve, dc)
            v = nc.vector
            link(v.tensor_copy(selb[:, :, :], sel[:, :, :]))
            for k in range(LK):
                m = ek[:, :, 0:EK].rearrange("p t (e k) -> p t e k", k=LK)[:, :, :, k]
                w = ek[:, :, EK:2 * EK].rearrange("p t (e k) -> p t e k", k=LK)[:, :, :, k]
                v.tensor_copy(m, oh[k][:, :, :])
                v.tensor_copy(ek[:, :, 2 * EK + k], gate[k][:, :])
                link(v.tensor_tensor(w, oh[k][:, :, :], gate[k][:, :].unsqueeze(2).broadcast_to([TT, NTT, LE]), ALU.mult))
            v.tensor_copy(ek[0:1, 0, 0:1], ek[0:1, 0, 0:1]).then_inc(placed, 1)
            for n, (p, q) in enumerate(groups):
                at, rows, dst = parts[p]
                dve.wait_ge(turned, n + 1)
                m = min(PB, NTT - q * PB) * TT
                v.tensor_copy(dst[:, q * PB * TT:q * PB * TT + m], pt[0:rows, n % 2, 0:m]).then_inc(kept, 1)
            for n in range(1, (EK + LK) * NCH, 2):
                dve.wait_ge(spread, n + 1)
                r, c = n // NCH, n % NCH
                o = mb[:, r, c * CH:(c + 1) * CH] if r < EK else rwb[:, r - EK, c * CH:(c + 1) * CH]
                v.tensor_copy(halves(o), pbc[:, n % 2, :, 0:HB]).then_inc(read_b, 1)

        @block.scalar
        def _(act):
            for n in range(0, (EK + LK) * NCH, 2):
                act.wait_ge(spread, n + 1)
                r, c = n // NCH, n % NCH
                o = mb[:, r, c * CH:(c + 1) * CH] if r < EK else rwb[:, r - EK, c * CH:(c + 1) * CH]
                nc.scalar.activation(halves(o), pbc[:, n % 2, :, 0:HB], ACT.Copy).then_inc(read_a, 1)

        @block.tensor
        def _(pe):
            pe.wait_ge(placed, 1)
            for n, (p, q) in enumerate(groups):
                at, rows, dst = parts[p]
                if n >= 2:
                    pe.wait_ge(kept, n - 1)
                for t in range(q * PB, min(NTT, (q + 1) * PB)):
                    last = nc.tensor.transpose(pt[0:rows, n % 2, (t - q * PB) * TT:(t - q * PB + 1) * TT],
                                               ek[:, t, at:at + rows], cst["ident"][0:TT, 0:TT])
                last.then_inc(turned, 1)
            pe.wait_ge(kept, len(groups))
            for n in range((EK + LK) * NCH):
                r, c = n // NCH, n % NCH
                if n >= 2:
                    pe.wait_ge((read_a, read_b)[n % 2], n // 2)
                for k in range(2):
                    a0 = c * CH + k * HB
                    if r < EK:
                        last = nc.tensor.matmul(pbc[:, n % 2, k, 0:HB], selb[:, r, :], mT[:, a0:a0 + HB], start=True, stop=True)
                    else:
                        last = nc.tensor.matmul(pbc[:, n % 2, k, 0:HB], sel[0:LK, r - EK, :], gT[:, a0:a0 + HB], start=True, stop=True)
                last.then_inc(spread, 1)


def split_bias(nc, a, bsp, bsel, scale):
    with ExitStack() as ctx:
        P = 3 * LE
        b = sbuf(nc, ctx, "b", [P, 4 * D])
        r = sbuf(nc, ctx, "r", [P, 4 * D])
        part = sbuf(nc, ctx, "part", [P, 3, 4 * D], BF16)
        pick = sbuf(nc, ctx, "pick", [P, 3])
        bs = sbuf(nc, ctx, "bs", [P, LE])
        load(nc, (b[:, :], a["le_b"]), (pick[:, :], a["c_part"]), (bs[:, :], a["c_expert"]))
        (dc,) = ctx.enter_context(stage(nc, "dve_chain"))
        block = ctx.enter_context(nc.Block())

        @block.vector
        def _(dve):
            link = Chain(dve, dc)
            v = nc.vector
            link(v.tensor_scalar(b[:, :], b[:, :], scale[0:P, 0:1], None, ALU.mult))
            link(v.tensor_copy(part[:, 0, :], b[:, :]))
            link(v.tensor_tensor(r[:, :], b[:, :], part[:, 0, :], ALU.subtract))
            link(v.tensor_copy(part[:, 1, :], r[:, :]))
            link(v.tensor_tensor(r[:, :], r[:, :], part[:, 1, :], ALU.subtract))
            link(v.tensor_copy(part[:, 2, :], r[:, :]))
            link(v.tensor_scalar(bsp[:, :], part[:, 0, :], pick[:, 0:1], None, ALU.mult))
            for k in range(1, 3):
                link(v.scalar_tensor_tensor(out=bsp[:, :], in0=part[:, k, :], scalar=pick[:, k:k + 1], in1=bsp[:, :],
                                            op0=ALU.mult, op1=ALU.add))
            link(v.tensor_copy(bsel[:, :, :], bs[:, :].unsqueeze(2).broadcast_to([P, LE, CB])))


def masks():
    c = {}
    h = np.full((128, 128), -1e30, np.float32)
    for i in range(NH):
        h[HD * i:HD * i + HD, HD * i:HD * i + HD] = 0
    c["headmask"] = h
    s = np.zeros((AT, 2), np.float32)
    s[0:S, 0] = 1
    s[S:, 1] = 1
    c["seqmask"] = s
    b = np.full((AT, AT), -1e30, np.float32)
    b[0:S, 0:S] = 0
    b[S:, S:] = 0
    c["blockmask"] = b
    c["iota"] = np.tile(np.arange(128, dtype=np.float32)[None], (TT, 1))
    c["tri"] = np.triu(np.ones((TT, TT), np.float32))
    carry = np.ones((64, NTT), np.float32)
    carry[:, 0] = 0
    c["carry"] = np.tile(carry.reshape(1, -1), (TT, 1))
    sel = np.zeros((EK, EK, 128), np.float32)
    for i in range(EK):
        sel[i, i] = 1
    c["sel"] = sel.reshape(EK, -1)
    part, expert = np.zeros((3 * LE, 3), np.float32), np.zeros((3 * LE, LE), np.float32)
    for i in range(3 * LE):
        part[i, i // LE] = 1
        expert[i, i % LE] = 1
    c["part"], c["expert"] = part, expert
    return c


def rest(nc, ctx, cst, a, want, load_const, hT, xn):
    if want(2):
        layernorm(nc, cst, hT, xn)
        switch_ffn(nc, cst, a, xn, hT)
    if want(3):
        layernorm(nc, cst, hT, xn)
        channel_attention(nc, cst, a, xn, hT)
    if want(4):
        layernorm(nc, cst, hT, xn)
        silu_ffn(nc, cst, a, xn, hT)
    if want(5):
        layernorm(nc, cst, hT, xn)
        state_space(nc, cst, a, xn, hT)
    if want(6):
        layernorm(nc, cst, hT, xn)
        gelu_ffn(nc, cst, a, xn, hT)
    if want(7):
        layernorm(nc, cst, hT, xn)
        frame_attention(nc, cst, a, xn, hT)
    if want(8):
        layernorm(nc, cst, hT, xn)
        lstm_experts(nc, cst, a, xn, hT)


def lay_out_rest(I, f):
    f["ca_w"] = np.concatenate([I["L1_attn_w_qkv"], I["L1_attn_w_proj"]], 1)
    f["ca_bqk"] = np.tile(I["L1_attn_b_qkv"][None, 0:2 * D], (AT, 1))
    f["ca_b"] = np.stack([I["L1_attn_b_qkv"][2 * D:], I["L1_attn_b_proj"]], 1)
    f["fa_w"] = np.concatenate([I["L3_attn_W" + c].T for c in "qkv"], 1)
    f["ss_w"] = np.concatenate([I["L2_attn_L_param"], I["L2_attn_P_left"].transpose(0, 2, 1).reshape(D, -1),
                                I["L2_attn_P_right"].reshape(D, -1), I["L2_attn_B"], I["L2_attn_C"],
                                I["L2_attn_log_dt"], I["L2_attn_D"][:, None]], 1)
    f["sw_r"] = I["L0_ffn_switch_w"].T
    f["sw_rb"] = np.tile(I["L0_ffn_switch_b"][None], (TT, 1))
    f["sw_w"] = I["L0_ffn_expert_w"].transpose(0, 2, 1)
    f["sw_b"] = I["L0_ffn_expert_b"]

    def experts(w1, b1, w2):
        E, _, F = w1.shape
        return np.concatenate([w1, w2.reshape(E, F // 128, 128, D).transpose(0, 2, 1, 3).reshape(E, 128, -1),
                               b1.reshape(E, F // 128, 128).transpose(0, 2, 1)], 2)

    g = lambda n: I["L2_ffn_" + n]
    f["gf_r"], f["gf_rb"] = g("Ws"), np.tile(g("bs")[None], (TT, 1))
    f["gf_w"], f["gf_b"] = experts(g("W1"), g("b1"), g("W2")), g("b2")
    g = lambda n: I["L1_ffn_" + n]
    f["sf_w"], f["sf_b"] = experts(g("W1"), g("b1"), g("W2")), g("b2")
    f["sf_cols"] = np.concatenate([g("ln1_g")[:, None], g("ln1_b")[:, None], g("ffln_g")[:, None], g("ffln_b")[:, None],
                                   g("bs1").reshape(2, 128).T, g("bs2")[:, None], g("bf1").reshape(4, 128).T, g("bf2")[:, None]], 1)
    f["sf_ws"] = np.concatenate([g("Ws1"), g("Ws2").reshape(2, 128, D).transpose(1, 0, 2).reshape(128, -1)], 1)
    f["sf_wf"] = np.concatenate([g("Wf1"), g("Wf2").reshape(4, 128, D).transpose(1, 0, 2).reshape(128, -1)], 1)
    f["sf_wr"], f["sf_code"] = g("Wr"), g("codebook").T
    g = lambda n: I["L3_ffn_" + n]
    f["le_r"], f["le_rb"] = g("router_w"), np.tile(g("router_b")[None], (TT, 1))
    for n in ("Wi", "Wh", "Wo"):
        f["le_" + n.lower()] = g(n).transpose(1, 0, 2).reshape(128, -1)
    f["le_b"] = np.tile(g("b"), (3, 1))
    f["le_bo"] = np.repeat(g("bo"), LK, 0)
    f.update({"c_" + k: v for k, v in masks().items()})


def mdct_constant():
    L = 2 * D
    n = np.arange(L, dtype=np.float32) + np.float32(0.5)
    k = np.float32(np.pi / D) * n[:D]
    z = np.sqrt(np.float32(2.0 / D * 2.0))
    wm = z * np.cos((n + np.float32(D / 2))[:, None] * k[None, :]).astype(np.float32)
    win = np.sin(np.float32(np.pi) * n / np.float32(L)).astype(np.float32)
    return np.ascontiguousarray((win[:, None] * wm).astype(np.float32).reshape(2, D, D).transpose(1, 0, 2))


def constants():
    c = {}
    c["ident"] = np.eye(128, dtype=np.float32)
    c["avg"] = np.full((128, 128), 1.0 / 128, np.float32)
    c["mdct"] = mdct_constant().reshape(128, 256)
    c["row"] = np.concatenate([np.zeros((32, 32)), np.tile(np.eye(32), (3, 1))]).astype(np.float32)
    c["eps"] = np.full((128, 1), EPS, np.float32)
    return c


def build(nc, a, first=0, last=8, dbg=None):
    with ExitStack() as ctx:
        hT = sbuf(nc, ctx, "hT", [128, NT], F32)
        xn = sbuf(nc, ctx, "xn", [128, NT], F32)
        cst, dims = {}, {"mdct": "p (k n) -> p k n"}
        with ExitStack() as c1:
            tiles = {}
            for name in ("ident", "avg", "eps"):
                tiles[name] = sbuf(nc, ctx, name, list(a["c_" + name].shape))
                cst[name] = tiles[name][:, :]
            (loaded,) = c1.enter_context(stage(nc, "constants_loaded"))
            block = c1.enter_context(nc.Block())

            @block.sync
            def _(sp):
                n = 0
                for name, t in tiles.items():
                    sp.dma_start(t[:, :], a["c_" + name]).then_inc(loaded, 16)
                    n += 16
                if first > 0:
                    sp.dma_start(hT[:, :], a["h_in"]).then_inc(loaded, 16)
                    n += 16
                sp.wait_ge(loaded, n)

        def load_const(c1, name):
            t = sbuf(nc, c1, name, list(a["c_" + name].shape))
            with ExitStack() as c2:
                (loaded,) = c2.enter_context(stage(nc, "constants_loaded"))
                block = c2.enter_context(nc.Block())

                @block.sync
                def _(sp):
                    sp.dma_start(t[:, :], a["c_" + name]).then_inc(loaded, 16)
                    sp.wait_ge(loaded, 16)
            return t

        cst["gathered"] = [Counted(ctx.enter_context(nc.semaphore(f"gathered{t}"))) for t in range(NTT)]
        cst["scattered"] = Counted(ctx.enter_context(nc.semaphore("scattered")))

        def want(k):
            return first <= k <= last

        if want(0):
            with ExitStack() as c1:
                t = load_const(c1, "mdct")
                cst["mdct"] = t[:, :].rearrange("p (k n) -> p k n", k=2)
                tokenize(nc, cst, a["frames"], hT)
        if want(1):
            with ExitStack() as c1:
                m = sbuf(nc, c1, "m", [128, NT], F32)
                layernorm(nc, cst, hT, xn)
                with ExitStack() as c2:
                    (copied,) = c2.enter_context(stage(nc, "copied"))
                    block = c2.enter_context(nc.Block())

                    @block.vector
                    def _(dve):
                        nc.vector.tensor_copy(m[:, :], xn[:, :]).then_inc(copied, 1)
                with ExitStack() as c2:
                    row = sbuf(nc, c2, "row", [128, 32, 128], BF16)
                    t = load_const(c2, "row")
                    with ExitStack() as c3:
                        (widened,) = c3.enter_context(stage(nc, "widened"))
                        block = c3.enter_context(nc.Block())

                        @block.vector
                        def _(dve):
                            nc.vector.tensor_copy(row[:, :, :], t[:, :].unsqueeze(2).broadcast_to([128, 32, 128])).then_inc(widened, 1)
                    cst["row"] = row
                    with nc.Fori(0, NL) as layer:
                        mamba_layer(nc, cst, layer, a["mamba_w"], m)
                lstm_fusion(nc, cst, (a["lstm_ih"].rearrange("p (g n) -> p g n", g=4),
                                      a["lstm_hh"].rearrange("d p (g n) -> d p g n", g=4),
                                      a["lstm_b"], a["fus_w"].rearrange("p (k n) -> p k n", k=3), a["fus_b"]), xn, m, hT)
        rest(nc, ctx, cst, a, want, load_const, hT, xn)
        with ExitStack() as c1:
            (stored,) = c1.enter_context(stage(nc, "stored"))
            block = c1.enter_context(nc.Block())

            @block.sync
            def _(sp):
                sp.dma_start(a["out"], hT[:, :]).then_inc(stored, 16)
                sp.wait_ge(stored, 16)


def lay_out(inp):
    I = {k: np.asarray(v) for k, v in inp.items()}
    f = {}
    x = np.zeros((NB, (S + 1) * D), np.float32)
    x[:, D:D + I["x"].shape[1]] = I["x"]
    f["frames"] = x.reshape(NB, S + 1, D).transpose(2, 0, 1).reshape(D, NB * (S + 1))
    w = np.zeros((NL, 128, MWID), np.float32)

    def put(name, v):
        at, width = MW[name]
        w[:, 0:v.shape[1], at:at + width] = v
    g = lambda n: I["L0_attn_" + n]
    put("wi", g("in_proj_w").transpose(0, 2, 1))
    put("cw", g("conv_w").reshape(NL, 2, 128, DCV).transpose(0, 2, 1, 3).reshape(NL, 128, -1))
    put("cb", g("conv_b").reshape(NL, 2, 128).transpose(0, 2, 1))
    xp = g("x_proj_w")
    xp = np.concatenate([xp[:, 0:DTR]] + [xp[:, DTR:]] * 3, 1)
    put("xp", xp.reshape(NL, 128, 2, 128).transpose(0, 3, 2, 1).reshape(NL, 128, -1))
    put("dw", g("dt_proj_w").transpose(0, 2, 1))
    put("db", g("dt_proj_b").reshape(NL, 2, 128).transpose(0, 2, 1))
    put("alog", g("A_log").reshape(NL, 2, 128, DST).transpose(0, 2, 1, 3).reshape(NL, 128, -1))
    put("dp", g("D_param").reshape(NL, 2, 128).transpose(0, 2, 1))
    put("wo", g("out_proj_w").reshape(NL, D, 2, 128).transpose(0, 3, 2, 1).reshape(NL, 128, -1))
    put("g", g("ln_g")[:, :, None])
    put("b", g("ln_b")[:, :, None])
    f["mamba_w"] = w
    order = [0, 1, 3, 2]
    f["lstm_ih"] = g("lstm_w_ih").reshape(2, 4, H2, D)[:, order].transpose(3, 1, 0, 2).reshape(D, -1)
    f["lstm_hh"] = g("lstm_w_hh").reshape(2, 4, H2, H2)[:, order].transpose(0, 3, 1, 2).reshape(2, H2, -1)
    b = [g(n).reshape(2, 4, H2)[:, order].transpose(0, 2, 1).reshape(128, 4) for n in ("lstm_b_ih", "lstm_b_hh")]
    f["lstm_b"] = np.stack(b)
    fw = np.zeros((128, 3, D), np.float32)
    fw[:, 0] = g("fusion_w").T[0:128]
    fw[0:H2, 1] = g("fusion_w").T[128:128 + H2]
    fw[H2:128, 2] = g("fusion_w").T[128 + H2:256]
    f["fus_w"] = fw.reshape(128, 3 * D)
    f["fus_b"] = g("fusion_b")[:, None]
    lay_out_rest(I, f)
    f.update({"c_" + k: v for k, v in constants().items()})
    return {k: np.ascontiguousarray(v) for k, v in f.items()}


def kernel(**inputs):
    import concourse.bacc as bacc
    from concourse.bass_utils import run_bass_kernel_spmd

    nc = bacc.Bacc("TRN2", target_bir_lowering=False, num_devices=1)
    arrays = lay_out(inputs)
    args = {k: nc.dram_tensor(k, list(v.shape), mybir.dt.from_np(v.dtype), kind="ExternalInput").ap()
            for k, v in arrays.items()}
    args["out"] = nc.dram_tensor("out", [128, NT], F32, kind="ExternalOutput").ap()
    build(nc, args)
    r = run_bass_kernel_spmd(nc, [arrays], core_ids=[0])
    return r.results[0]["out"].reshape(D, NB, S).transpose(1, 2, 0)
```

```python
import concourse.bass as bass
from concourse import mybir
from contextlib import ExitStack, contextmanager
import numpy as np

F32 = mybir.dt.float32
BF16 = mybir.dt.bfloat16
F16 = mybir.dt.float16
I32 = mybir.dt.int32
ALU = mybir.AluOpType
ACT = mybir.ActivationFunctionType
AX = mybir.AxisListType

NB = 64
S = 33
D = 128
NT = NB * S
CH = NT // 4
HB = CH // 2
NCH = 4
BANK = 512
EPS = 1e-5
TT = 96
NTT = NT // TT
ds = bass.ds


class Chain:

    def __init__(self, eng, sem):
        self.eng, self.sem, self.n, self.at = eng, sem, 0, None

    def __call__(self, ins):
        ins.then_inc(self.sem, 1)
        self.n += 1
        self.eng.wait_ge(self.sem, self.n if self.at is None else self.at + self.n)

    @contextmanager
    def loop(self, count, per):
        start = self.n
        with self.eng.Fori(0, count) as i:
            self.at = i * per
            yield i
            assert self.n - start == per, (self.n - start, per)
        self.at = None
        self.n = start + count * per


class Hold:

    def __init__(self, eng, passed):
        self.eng, self.passed = eng, passed

    def __call__(self, sem, value):
        self.eng.wait_ge(sem, value)
        self.eng.sem_inc(self.passed, 1)


def free(eng, *sems):
    for s in sems:
        eng.sem_inc(s, 1)


def unique(nc, name):
    return f"{name}_{nc.next_id()}"


def sbuf(nc, ctx, name, shape, dt=F32):
    return ctx.enter_context(nc.sbuf_tensor(unique(nc, name), shape, dt))


def psum(nc, ctx, name, shape, dt=F32):
    return ctx.enter_context(nc.psum_tensor(unique(nc, name), shape, dt))


@contextmanager
def stage(nc, names):
    with ExitStack() as ctx:
        sems = [ctx.enter_context(nc.semaphore(unique(nc, n))) for n in names.split()]
        yield sems
        for s in sems:
            nc.gpsimd.sem_clear(s)
        nc.all_engine_barrier()


class Counted:

    def __init__(self, sem):
        self.sem, self.n = sem, 0

    def add(self, n):
        self.n += n
        return self.n


def halves(ap):
    return ap.rearrange("p (h n) -> p h n", h=2)


def layernorm(nc, cst, src, dst, gain=None, shift=None):
    with ExitStack() as ctx:
        mean_ps = psum(nc, ctx, "mean_ps", [128, 2, 2, BANK], F32)
        var_ps = psum(nc, ctx, "var_ps", [128, 2, 2, BANK], F32)
        sq = sbuf(nc, ctx, "sq", [128, 2, CH], F32)
        rstd = sbuf(nc, ctx, "rstd", [128, 2, CH], F32)
        (mean_ready, centered, squared, var_ready, logged, rstd_ready, scaled, shifted) = ctx.enter_context(
            stage(nc, "mean_ready centered squared var_ready logged rstd_ready scaled shifted"))
        block = ctx.enter_context(nc.Block())

        def part(t, c):
            return t[:, c * CH:(c + 1) * CH]

        @block.tensor
        def _(pe):
            def mean(c):
                if c >= 2:
                    pe.wait_ge(centered, c - 1)
                for h in range(2):
                    last = nc.tensor.matmul(mean_ps[:, c % 2, h, 0:HB], cst["avg"], halves(part(src, c))[:, h, :],
                                            start=True, stop=True)
                last.then_inc(mean_ready, 1)

            def var(c):
                pe.wait_ge(squared, c + 1)
                if c >= 2:
                    pe.wait_ge(logged, c - 1)
                for h in range(2):
                    last = nc.tensor.matmul(var_ps[:, c % 2, h, 0:HB], cst["avg"], halves(sq[:, c % 2, :])[:, h, :],
                                            start=True, stop=True)
                last.then_inc(var_ready, 1)

            mean(0)
            for c in range(NCH):
                if c + 1 < NCH:
                    mean(c + 1)
                var(c)

        @block.vector
        def _(dve):
            def center(c):
                dve.wait_ge(mean_ready, c + 1)
                nc.vector.tensor_tensor(halves(part(dst, c)), halves(part(src, c)), mean_ps[:, c % 2, :, 0:HB],
                                        ALU.subtract).then_inc(centered, 1)

            def scale(c):
                dve.wait_ge(rstd_ready, c + 1)
                dve.wait_ge(centered, c + 1)
                d = part(dst, c)
                if gain is None:
                    nc.vector.tensor_tensor(d, d, rstd[:, c % 2, :], ALU.mult).then_inc(scaled, 1)
                else:
                    nc.vector.scalar_tensor_tensor(out=d, in0=d, scalar=gain, in1=rstd[:, c % 2, :], op0=ALU.mult,
                                                   op1=ALU.mult).then_inc(scaled, 1)
                    dve.wait_ge(scaled, c + 1)
                    nc.vector.tensor_scalar(d, d, shift, None, ALU.add).then_inc(shifted, 1)

            center(0)
            for c in range(NCH):
                if c + 1 < NCH:
                    center(c + 1)
                scale(c)

        @block.scalar
        def _(act):
            def square(c):
                act.wait_ge(centered, c + 1)
                if c >= 2:
                    act.wait_ge(var_ready, c - 1)
                nc.scalar.activation(sq[:, c % 2, :], part(dst, c), ACT.Square).then_inc(squared, 1)

            nc.scalar.preload_act_table_set("natural_log_exp_and_others")
            square(0)
            for c in range(NCH):
                if c + 1 < NCH:
                    square(c + 1)
                act.wait_ge(var_ready, c + 1)
                if c >= 2:
                    act.wait_ge(scaled, c - 1)
                r = rstd[:, c % 2, :]
                nc.scalar.activation(halves(r), var_ps[:, c % 2, :, 0:HB], ACT.Ln, bias=cst["eps"]).then_inc(logged, 1)
                act.wait_ge(logged, c + 1)
                nc.scalar.activation(r, r, ACT.Exp, scale=-0.5).then_inc(rstd_ready, 1)


def tokenize(nc, cst, frames_dram, hT):
    with ExitStack() as ctx:
        blocks = sbuf(nc, ctx, "blocks", [128, NB, S + 1], F32)
        ps = psum(nc, ctx, "ps", [128, 2, 2, BANK], F32)
        (loaded, framed, kept) = ctx.enter_context(stage(nc, "loaded framed kept"))
        block = ctx.enter_context(nc.Block())

        @block.sync
        def _(sp):
            sp.dma_start(blocks[:, :, :], frames_dram.rearrange("p (b s) -> p b s", b=NB)).then_inc(loaded, 16)

        @block.tensor
        def _(pe):
            pe.wait_ge(loaded, 16)
            for c in range(NCH):
                if c >= 2:
                    pe.wait_ge(kept, c - 1)
                for h in range(2):
                    b0 = 16 * c + 8 * h
                    for k in range(2):
                        last = nc.tensor.matmul(ps[:, c % 2, h, 0:HB], cst["mdct"][:, k, :],
                                                blocks[:, b0:b0 + 8, k:k + S], start=(k == 0), stop=(k == 1))
                last.then_inc(framed, 1)

        @block.vector
        def _(dve):
            for c in range(NCH):
                dve.wait_ge(framed, c + 1)
                nc.vector.tensor_copy(halves(hT[:, c * CH:(c + 1) * CH]), ps[:, c % 2, :, 0:HB]).then_inc(kept, 1)


NL, DST, DCV, DIN, DTR, H2 = 3, 16, 4, 256, 32, 64
MW = {}
_at = 0
for _name, _width in (("wi", 2 * DIN), ("cw", 2 * DCV), ("cb", 2), ("xp", 2 * 128), ("dw", DIN), ("db", 2),
                      ("alog", 2 * DST), ("dp", 2), ("wo", 2 * D), ("g", 1), ("b", 1)):
    MW[_name] = (_at, _width)
    _at += _width
MWID = _at


def mamba_layer(nc, cst, layer, w_dram, m):
    with ExitStack() as ctx:
        def sb(name, shape, dt=F32):
            return sbuf(nc, ctx, name, shape, dt)

        w = sb("w", [128, MWID])
        u = sb("u", [128, 2, NT])
        sz = sb("sz", [128, 2, NT])
        dt = sb("dt", [128, 2, NT])
        du = sb("du", [128, 2, NT])
        xd = sb("xd", [128, NT])
        bc = sb("bc", [128, NT + CH], BF16)
        negA = sb("negA", [128, 2 * DST])

        def W(name, a=0, n=None):
            at, width = MW[name]
            return w[:, at + a:at + (width if n is None else a + n)]

        def chunk(t, half, c):
            return t[:, half, ds(c * CH, CH)]

        with ExitStack() as c1:
            px = psum(nc, c1, "px", [128, 2, 2, BANK], F32)
            pz = psum(nc, c1, "pz", [128, 2, BANK], F32)
            pxd = psum(nc, c1, "pxd", [128, 2, BANK], F32)
            left = sbuf(nc, c1, "left", [128, CH])
            high = sbuf(nc, c1, "high", [128, CH], BF16)
            (w_loaded, x_ready, z_ready, tap0, conv, u_ready, z_done, xd_ready, xd_done, bc_zeroed, dc) = c1.enter_context(
                stage(nc, "w_loaded x_ready z_ready tap0 conv u_ready z_done xd_ready xd_done bc_zeroed dve_chain"))
            block = c1.enter_context(nc.Block())

            def cols(c, k):
                return slice(c * CH + k * HB, c * CH + (k + 1) * HB)

            @block.sync
            def _(sp):
                sp.dma_start(w[:, :], w_dram[ds(layer, 1), :, :].rearrange("o p n -> p (o n)")).then_inc(w_loaded, 16)

            @block.tensor
            def _(pe):
                def x(c):
                    if c >= 1:
                        pe.wait_ge(conv, (DCV - 1) * c)
                    for half in range(2):
                        for k in range(2):
                            last = nc.tensor.matmul(px[:, half, k, 0:HB], W("wi", half * 128, 128), m[:, cols(c, k)],
                                                    start=True, stop=True)
                    last.then_inc(x_ready, 1)

                pe.wait_ge(w_loaded, 16)
                x(0)
                for c in range(NCH):
                    for half in range(2):
                        if c + half >= 1:
                            pe.wait_ge(z_done, 2 * c + half)
                        for k in range(2):
                            last = nc.tensor.matmul(pz[:, k, 0:HB], W("wi", DIN + half * 128, 128), m[:, cols(c, k)],
                                                    start=True, stop=True)
                        last.then_inc(z_ready, 1)
                    if c + 1 < NCH:
                        x(c + 1)
                    pe.wait_ge(u_ready, c + 1)
                    if c >= 1:
                        pe.wait_ge(xd_done, c)
                    for k in range(2):
                        for half in range(2):
                            last = nc.tensor.matmul(pxd[:, k, 0:HB], W("xp", half * 128, 128), u[:, half, cols(c, k)],
                                                    start=(half == 0), stop=(half == 1))
                    last.then_inc(xd_ready, 1)

            @block.scalar
            def _(act):
                nc.scalar.preload_act_table_set("silu_and_others")
                for c in range(NCH):
                    act.wait_ge(x_ready, c + 1)
                    for half in range(2):
                        last = nc.scalar.activation(halves(chunk(u, half, c)), px[:, half, :, 0:HB], ACT.Identity,
                                                    scale=W("cw", half * DCV + DCV - 1, 1), bias=W("cb", half, 1))
                    last.then_inc(tap0, 1)
                    for half in range(2):
                        act.wait_ge(z_ready, 2 * c + half + 1)
                        nc.scalar.activation(halves(chunk(sz, half, c)), pz[:, :, 0:HB], ACT.Silu).then_inc(z_done, 1)
                    if c >= 1:
                        act.wait_ge(xd_ready, c)
                        nc.scalar.activation(halves(xd[:, (c - 1) * CH:c * CH]), pxd[:, :, 0:HB], ACT.Copy).then_inc(xd_done, 1)
                    act.wait_ge(conv, (DCV - 1) * (c + 1))
                    uc = u[:, :, c * CH:(c + 1) * CH]
                    nc.scalar.activation(uc, uc, ACT.Silu).then_inc(u_ready, 1)
                act.wait_ge(xd_ready, NCH)
                nc.scalar.activation(halves(xd[:, (NCH - 1) * CH:]), pxd[:, :, 0:HB], ACT.Copy).then_inc(xd_done, 1)

            @block.vector
            def _(dve):
                link = Chain(dve, dc)
                v = nc.vector

                def split(c):
                    at = slice(c * CH, (c + 1) * CH)
                    dve.wait_ge(xd_done, c + 1)
                    link(v.tensor_copy(high[:, :], xd[:, at]))
                    v.tensor_copy(bc[32:64, at], high[32:64, :])
                    link(v.tensor_tensor(left[:, :], xd[:, at], high[:, :], ALU.subtract))
                    link(v.tensor_copy(high[:, :], left[:, :]))
                    v.tensor_copy(bc[64:96, at], high[64:96, :])
                    link(v.tensor_tensor(bc[96:128, at], left[96:128, :], high[96:128, :], ALU.subtract))

                dve.wait_ge(bc_zeroed, 1)
                for c in range(NCH):
                    dve.wait_ge(tap0, c + 1)
                    for j in range(1, DCV):
                        if j > 1:
                            dve.wait_ge(conv, (DCV - 1) * c + (j - 1))
                        for half in range(2):
                            for k in range(2):
                                o = u[:, half, cols(c, k)].rearrange("p (b s) -> p b s", s=S)[:, :, j:S]
                                x = px[:, half, k, 0:HB].rearrange("p (b s) -> p b s", s=S)[:, :, 0:S - j]
                                last = nc.vector.scalar_tensor_tensor(
                                    out=o, in0=x, scalar=W("cw", half * DCV + DCV - 1 - j, 1), in1=o,
                                    op0=ALU.mult, op1=ALU.add)
                        last.then_inc(conv, 1)
                    if c >= 1:
                        split(c - 1)
                split(NCH - 1)

            @block.gpsimd
            def _(pool):
                nc.gpsimd.memset(bc[:, :], 0.0).then_inc(bc_zeroed, 1)

        with ExitStack() as c1:
            pd = psum(nc, c1, "pd", [128, 2, 2, 2, BANK], F32)
            e = sbuf(nc, c1, "e", [128, 2, 2, CH], F32)
            ser = sbuf(nc, c1, "ser", [128, 2, 2, CH], F32)
            small = sbuf(nc, c1, "small", [128, 2, 2, CH], mybir.dt.int8)
            ln = sbuf(nc, c1, "ln", [128, 2, 2, CH], F32)
            (d_ready, ac, x_read, kept, e_ready, ser_ready, ln_ready, marked, dt_done, dc, du_done) = c1.enter_context(
                stage(nc, "d_ready act_chain x_read max_kept e_ready ser_ready ln_ready marked dt_done dve_chain du_done"))
            block = c1.enter_context(nc.Block())

            @block.tensor
            def _(pe):
                for c in range(NCH):
                    if c >= 2:
                        pe.wait_ge(kept, c - 1)
                    for half in range(2):
                        for k in range(2):
                            a = c * CH + k * HB
                            last = nc.tensor.matmul(pd[:, c % 2, half, k, 0:HB], W("dw", half * 128, 128)[0:DTR, :],
                                                    xd[0:DTR, a:a + HB], start=True, stop=True)
                    last.then_inc(d_ready, 1)

            @block.scalar
            def _(act):
                link = Chain(act, ac)
                nc.scalar.preload_act_table_set("natural_log_exp_and_others")
                link(nc.scalar.activation(negA[:, :], W("alog"), ACT.Exp))
                link(nc.scalar.activation(negA[:, :], negA[:, :], ACT.Copy, scale=-1.0))
                for c in range(NCH):
                    act.wait_ge(d_ready, c + 1)
                    if c >= 2:
                        act.wait_ge(dt_done, c - 1)
                    ec = e[:, c % 2, :, :]
                    for half in range(2):
                        last = nc.scalar.activation(halves(ec[:, half, :]), pd[:, c % 2, half, :, 0:HB], ACT.Abs,
                                                    bias=W("db", half, 1))
                    last.then_inc(x_read, 1)
                    act.wait_ge(x_read, c + 1)
                    nc.scalar.activation(ec, ec, ACT.Exp, scale=-1.0).then_inc(e_ready, 1)
                    act.wait_ge(e_ready, c + 1)
                    nc.scalar.activation(ser[:, c % 2, :, :], ec, ACT.Copy, scale=-0.25).then_inc(ser_ready, 1)
                    nc.scalar.activation(ln[:, c % 2, :, :], ec, ACT.Ln, bias=1.0).then_inc(ln_ready, 1)

            @block.vector
            def _(dve):
                link = Chain(dve, dc)
                v = nc.vector
                for c in range(NCH):
                    d = dt[:, :, c * CH:(c + 1) * CH]
                    dve.wait_ge(x_read, c + 1)
                    for half in range(2):
                        last = v.tensor_scalar(halves(d[:, half, :]), pd[:, c % 2, half, :, 0:HB], W("db", half, 1), 0.0,
                                               ALU.add, ALU.max)
                    last.then_inc(kept, 1)
                    dve.wait_ge(ser_ready, c + 1)
                    t = ser[:, c % 2, :, :]
                    for k in (1.0 / 3, -0.5, 1.0):
                        link(v.scalar_tensor_tensor(out=t, in0=t, scalar=k, in1=e[:, c % 2, :, :], op0=ALU.add, op1=ALU.mult))
                    dve.wait_ge(ln_ready, c + 1)
                    dve.wait_ge(marked, c + 1)
                    link(v.copy_predicated(ln[:, c % 2, :, :], small[:, c % 2, :, :], t))
                    dve.wait_ge(kept, c + 1)
                    v.tensor_tensor(d, d, ln[:, c % 2, :, :], ALU.add).then_inc(dt_done, 1)

            @block.gpsimd
            def _(pool):
                def mark(c):
                    pool.wait_ge(e_ready, c + 1)
                    nc.gpsimd.tensor_scalar(small[:, c % 2, :, :], e[:, c % 2, :, :], 1.0 / 32, None,
                                            ALU.is_lt).then_inc(marked, 1)

                mark(0)
                for c in range(NCH):
                    if c + 1 < NCH:
                        mark(c + 1)
                    pool.wait_ge(dt_done, c + 1)
                    at = slice(c * CH, (c + 1) * CH)
                    nc.gpsimd.tensor_tensor(du[:, :, at], dt[:, :, at], u[:, :, at], ALU.mult).then_inc(du_done, 1)

        with ExitStack() as c1:
            pb = psum(nc, c1, "pb", [128, 2, BANK], F32)
            pcc = psum(nc, c1, "pcc", [128, 2, BANK], F32)
            py = psum(nc, c1, "py", [128, 2, 2, BANK], F32)
            Bs = sbuf(nc, c1, "Bs", [128, 4, CH], F32)
            dA = sbuf(nc, c1, "dA", [128, 2, 2, CH], F32)
            dBu = sbuf(nc, c1, "dBu", [128, 2, 2, CH], F32)
            hst = sbuf(nc, c1, "hst", [128, 4, 2 * CH], F32)
            hC = sbuf(nc, c1, "hC", [128, 2, 2, CH], F32)
            (z0, b_ready, b_kept, dBu_ready, c_ready, dA_ready, h_ready, c_used, y_added, y_skip, y_done, pe_passed,
             act_passed, pool_passed) = c1.enter_context(
                stage(nc, "dA_zeroed b_ready b_kept dBu_ready c_ready dA_ready h_ready c_used y_added y_skip y_done "
                          "pe_passed act_passed pool_passed"))
            block = c1.enter_context(nc.Block())

            @block.gpsimd
            def _(pool):
                hold = Hold(pool, pool_passed)
                nc.gpsimd.memset(dA[:, :, :, :], 0.0).then_inc(z0, 1)
                with pool.Fori(0, NCH) as c:
                    for n in range(DST):
                        i = c * DST + n
                        hold(b_kept, i + 2)
                        hold(h_ready, i + 1)
                        nc.gpsimd.tensor_tensor(dBu[:, n % 2, :, :], du[:, :, ds(c * CH, CH)],
                                                Bs[:, n % 4, :].unsqueeze(1).broadcast_to([128, 2, CH]),
                                                ALU.mult).then_inc(dBu_ready, 1)

            @block.tensor
            def _(pe):
                hold = Hold(pe, pe_passed)

                def spread(c, r, o, done):
                    for k in range(2):
                        last = nc.tensor.matmul(o[:, k, 0:HB], cst["row"][:, r, :], bc[:, ds(c * CH + k * HB, HB)],
                                                start=True, stop=True)
                    last.then_inc(done, 1)

                pe.sem_inc(y_added, 2)
                for n in range(3):
                    pe.wait_ge(b_kept, n + 1)
                    spread(0, n, pb, b_ready)
                with pe.Fori(0, NCH) as c:
                    def add(n):
                        for half in range(2):
                            for k in range(2):
                                last = nc.tensor.matmul(py[:, half, k, 0:HB], cst["ident"],
                                                        hC[:, n % 2, half, k * HB:(k + 1) * HB],
                                                        start=(n == 0), stop=(n == DST - 1))
                        last.then_inc(y_added, 1)

                    for n in range(DST):
                        i = c * DST + n
                        hold(b_kept, i + 4)
                        spread(c + (n + 3) // DST, (n + 3) % DST, pb, b_ready)
                        hold(c_used, i + 1)
                        spread(c, DST + n, pcc, c_ready)
                        if n == 1:
                            pe.wait_ge(y_skip, c + 1)
                        if n >= 1:
                            add(n - 1)
                    pe.wait_ge(c_used, c * DST + (DST + 1))
                    add(DST - 1)

            @block.scalar
            def _(act):
                hold = Hold(act, act_passed)

                def keep(k, step):
                    act.wait_ge(b_ready, step)
                    nc.scalar.activation(halves(Bs[:, k, :]), pb[:, :, 0:HB], ACT.Copy).then_inc(b_kept, 1)

                act.sem_inc(b_kept, 1)
                act.wait_ge(z0, 1)
                keep(0, 1)
                keep(1, 2)
                with act.Fori(0, NCH) as c:
                    for n in range(DST):
                        i = c * DST + n
                        hold(h_ready, i + 1)
                        for half in range(2):
                            o = dA[:, n % 2, half, :].rearrange("p (b s) -> p b s", s=S)[:, :, 1:S]
                            x = chunk(dt, half, c).rearrange("p (b s) -> p b s", s=S)[:, :, 1:S]
                            last = nc.scalar.activation(o, x, ACT.Exp, scale=negA[:, half * DST + n:half * DST + n + 1])
                        last.then_inc(dA_ready, 1)
                        keep((n + 2) % 4, i + 3)

            @block.vector
            def _(dve):
                dve.sem_inc(h_ready, 2)
                dve.sem_inc(c_used, 1)
                dve.sem_inc(y_skip, 1)

                def scan(c, n):
                    i = c * DST + n
                    dve.wait_ge(dBu_ready, i + 1)
                    dve.wait_ge(dA_ready, i + 1)
                    nc.vector.tensor_tensor_scan(hst[:, n % 4, :], dA[:, n % 2, :, :].rearrange("p a n -> p (a n)"),
                                                 dBu[:, n % 2, :, :].rearrange("p a n -> p (a n)"), 0.0, ALU.mult,
                                                 ALU.add).then_inc(h_ready, 1)

                def weigh(c, n):
                    i = c * DST + n
                    dve.wait_ge(h_ready, i + 3)
                    dve.wait_ge(c_ready, i + 1)
                    dve.wait_ge(y_added, i + 1)
                    nc.vector.tensor_tensor(
                        hC[:, n % 2, :, :].rearrange("p a (h n) -> p a h n", h=2),
                        hst[:, n % 4, :].rearrange("p (a h n) -> p a h n", a=2, h=2),
                        pcc[:, :, 0:HB].unsqueeze(1).broadcast_to([128, 2, 2, HB]), ALU.mult).then_inc(c_used, 1)

                def body(c, last):
                    weigh(c, 0)
                    for n in range(2, DST):
                        scan(c, n)
                        weigh(c, n - 1)
                    if not last:
                        scan(c, DST)
                    weigh(c, DST - 1)
                    if not last:
                        scan(c, DST + 1)
                    dve.wait_ge(y_added, c * DST + (DST + 2))
                    for half in range(2):
                        uc = halves(chunk(u, half, c))
                        ins = nc.vector.scalar_tensor_tensor(out=uc, in0=uc, scalar=W("dp", half, 1),
                                                             in1=py[:, half, :, 0:HB], op0=ALU.mult, op1=ALU.add)
                    ins.then_inc(y_skip, 1)
                    dve.wait_ge(y_skip, c + 2)
                    uc = u[:, :, ds(c * CH, CH)]
                    nc.vector.tensor_tensor(uc, uc, sz[:, :, ds(c * CH, CH)], ALU.mult).then_inc(y_done, 1)

                scan(0, 0)
                scan(0, 1)
                with dve.Fori(0, NCH - 1) as c:
                    body(c, False)
                body(NCH - 1, True)

        with ExitStack() as c1:
            po = psum(nc, c1, "po", [128, 2, 2, BANK], F32)
            (o_ready, o_added) = c1.enter_context(stage(nc, "o_ready o_added"))
            block = c1.enter_context(nc.Block())

            @block.tensor
            def _(pe):
                for c in range(NCH):
                    if c >= 2:
                        pe.wait_ge(o_added, c - 1)
                    for k in range(2):
                        for half in range(2):
                            a = c * CH + k * HB
                            last = nc.tensor.matmul(po[:, c % 2, k, 0:HB], W("wo", half * D, D), u[:, half, a:a + HB],
                                                    start=(half == 0), stop=(half == 1))
                    last.then_inc(o_ready, 1)

            @block.vector
            def _(dve):
                for c in range(NCH):
                    dve.wait_ge(o_ready, c + 1)
                    mc = halves(m[:, c * CH:(c + 1) * CH])
                    nc.vector.tensor_tensor(mc, mc, po[:, c % 2, :, 0:HB], ALU.add).then_inc(o_added, 1)
        layernorm(nc, cst, m, m, W("g"), W("b"))


def lstm_fusion(nc, cst, w_dram, x, m, hT):
    with ExitStack() as ctx:
        def sb(name, shape, dt=F32):
            return sbuf(nc, ctx, name, shape, dt)

        GP = NB + 32
        wih = sb("wih", [128, 4, 2 * H2])
        whh = sb("whh", [128, 4, 2, H2])
        bias = sb("bias", [128, 4])
        bias2 = sb("bias2", [128, 4])
        fw = sb("fw", [128, 3, D])
        fb = sb("fb", [128, 1])
        gx = sb("gx", [128, S, 4, GP])
        hist = sb("hist", [128, (S + 1) * NB + 32])
        z = sb("z", [128, 5, NB])
        prod = sb("prod", [128, 2, NB])
        tc = sb("tc", [128, NB])
        wih_d, whh_d, b_d, fw_d, fb_d = w_dram
        FG = BANK // NB
        NFG = -(-S // FG)
        with ExitStack() as c1:
            pi = psum(nc, c1, "pi", [128, 2, 4, BANK])
            (w_loaded, whh_loaded, zeroed, biased, multiplied, placed) = c1.enter_context(
                stage(nc, "w_loaded whh_loaded zeroed biased multiplied placed"))
            block = c1.enter_context(nc.Block())

            @block.sync
            def _(sp):
                for dst, src in ((wih[:, :, :], wih_d), (bias[:, :], b_d[0]), (bias2[:, :], b_d[1]),
                                 (fw[:, :, :], fw_d), (fb[:, :], fb_d)):
                    sp.dma_start(dst, src).then_inc(w_loaded, 16)
                sp.wait_ge(zeroed, 1)
                for d in range(2):
                    sp.dma_start(whh[d * H2:(d + 1) * H2, :, d, :], whh_d[d]).then_inc(whh_loaded, 16)
                sp.wait_ge(whh_loaded, 32)

            @block.gpsimd
            def _(pool):
                nc.gpsimd.memset(whh[:, :, :, :], 0.0).then_inc(zeroed, 1)
                nc.gpsimd.memset(gx[:, :, :, NB:GP], 0.0)
                nc.gpsimd.memset(hist[:, :], 0.0)
                nc.gpsimd.memset(z[:, 4, :], 0.0).then_inc(zeroed, 1)

            @block.tensor
            def _(pe):
                pe.wait_ge(w_loaded, 80)
                xs = x[:, :].rearrange("p (b s) -> p s b", s=S)
                for q in range(NFG):
                    if q >= 2:
                        pe.wait_ge(placed, q - 1)
                    n = min(FG, S - q * FG)
                    for g in range(4):
                        last = nc.tensor.matmul(pi[:, q % 2, g, 0:n * NB], wih[:, g, :], xs[:, q * FG:q * FG + n, :],
                                                start=True, stop=True)
                    last.then_inc(multiplied, 1)

            @block.vector
            def _(dve):
                v = nc.vector
                dve.wait_ge(w_loaded, 80)
                v.tensor_tensor(bias[:, :], bias[:, :], bias2[:, :], ALU.add).then_inc(biased, 1)
                dve.wait_ge(biased, 1)
                for q in range(NFG):
                    dve.wait_ge(multiplied, q + 1)
                    n = min(FG, S - q * FG)
                    for g in range(4):
                        v.tensor_scalar(gx[0:H2, q * FG:q * FG + n, g, 0:NB],
                                        pi[0:H2, q % 2, g, 0:n * NB].rearrange("p (s b) -> p s b", b=NB),
                                        bias[0:H2, g:g + 1], None, ALU.add)
                    for s in range(n):
                        last = v.tensor_tensor(gx[H2:128, S - 1 - (q * FG + s), :, 0:NB],
                                               pi[H2:128, q % 2, :, s * NB:(s + 1) * NB],
                                               bias[H2:128, :].unsqueeze(2).broadcast_to([H2, 4, NB]), ALU.add)
                    last.then_inc(placed, 1)

        pg = psum(nc, ctx, "pg", [128, 2, BANK], F32)
        pf = psum(nc, ctx, "pf", [128, NFG, BANK], F32)
        (g_ready, t_ready, dc, c_ready, tc_ready, h_ready, f_ready) = ctx.enter_context(
            stage(nc, "g_ready t_ready dve_chain c_ready tc_ready h_ready f_ready"))
        block = ctx.enter_context(nc.Block())

        @block.tensor
        def _(pe):
            ms = m[:, :].rearrange("p (b s) -> p s b", s=S)

            def from_x(t, j):
                nc.tensor.matmul(pg[:, j, 0:4 * GP], cst["ident"], gx[:, ds(t, 1), :, :].rearrange("p o g b -> p (o g b)"),
                                 start=True, stop=False, skip_group_check=True)

            def from_h(t, j):
                for g in range(4):
                    last = nc.tensor.matmul(pg[:, j, g * GP:(g + 1) * GP], whh[:, g, :, :].rearrange("p d h -> p (d h)"),
                                            hist[:, ds(t * NB, GP)], start=False, stop=True, skip_group_check=True)
                last.then_inc(g_ready, 1)

            from_x(0, 0)
            from_h(0, 0)
            for q in range(NFG):
                n = min(FG, S - q * FG)
                nc.tensor.matmul(pf[:, q, 0:n * NB], fw[:, 0, :], ms[:, q * FG:q * FG + n, :], start=True, stop=False,
                                 skip_group_check=True)
            with pe.Fori(0, (S - 1) // 2) as i:
                for j in range(2):
                    t = 2 * i + j + 1
                    from_x(t, (j + 1) % 2)
                    pe.wait_ge(h_ready, t)
                    from_h(t, (j + 1) % 2)
            pe.wait_ge(h_ready, S)
            for q in range(NFG):
                n = min(FG, S - q * FG)
                nc.tensor.matmul(pf[:, q, 0:n * NB], fw[:, 1, :], hist[:, (q * FG + 1) * NB:(q * FG + 1 + n) * NB],
                                 start=False, stop=False, skip_group_check=True)
            for s in range(S):
                last = nc.tensor.matmul(pf[:, s // FG, (s % FG) * NB:(s % FG + 1) * NB], fw[:, 2, :],
                                        hist[:, (S - s) * NB:(S - s + 1) * NB], start=False, stop=True,
                                        skip_group_check=True)
            last.then_inc(f_ready, 1)

        @block.scalar
        def _(act):
            nc.scalar.preload_act_table_set("sigmoid_and_others")

            def step(t, j):
                act.wait_ge(g_ready, t + 1)
                p = pg[:, j, 0:4 * GP].rearrange("p (g b) -> p g b", b=GP)
                nc.scalar.activation(z[:, 0:3, :], p[:, 0:3, 0:NB], ACT.Sigmoid)
                nc.scalar.activation(z[:, 3, :], p[:, 3, 0:NB], ACT.Tanh).then_inc(t_ready, 1)
                act.wait_ge(c_ready, t + 1)
                nc.scalar.activation(tc[:, :], z[:, 4, :], ACT.Tanh).then_inc(tc_ready, 1)

            step(0, 0)
            with act.Fori(0, (S - 1) // 2) as i:
                for j in range(2):
                    step(2 * i + j + 1, (j + 1) % 2)

        @block.vector
        def _(dve):
            link = Chain(dve, dc)
            with link.loop(S, 1) as t:
                dve.wait_ge(t_ready, t + 1)
                link(nc.vector.tensor_tensor(prod[:, :, :], z[:, 0:2, :], z[:, 3:5, :], ALU.mult))
                nc.vector.tensor_tensor(z[:, 4, :], prod[:, 0, :], prod[:, 1, :], ALU.add).then_inc(c_ready, 1)
                dve.wait_ge(tc_ready, t + 1)
                nc.vector.tensor_tensor(hist[:, ds((t + 1) * NB, NB)], z[:, 2, :], tc[:, :], ALU.mult).then_inc(h_ready, 1)
            dve.wait_ge(f_ready, 1)
            hs = hT[:, :].rearrange("p (b s) -> p s b", s=S)
            for q in range(NFG):
                n = min(FG, S - FG * q)
                o = hs[:, FG * q:FG * q + n, :]
                nc.vector.scalar_tensor_tensor(out=o, in0=pf[:, q, 0:n * NB].rearrange("p (s b) -> p s b", b=NB),
                                               scalar=fb[:, :], in1=o, op0=ALU.add, op1=ALU.add)


def load(nc, *pairs):
    with ExitStack() as ctx:
        (loaded,) = ctx.enter_context(stage(nc, "loaded"))
        block = ctx.enter_context(nc.Block())

        @block.sync
        def _(sp):
            for dst, src in pairs:
                sp.dma_start(dst, src).then_inc(loaded, 16)
            sp.wait_ge(loaded, 16 * len(pairs))


def project_features(nc, x, out, w, bias, rows=D, residual=False):
    with ExitStack() as ctx:
        ps = psum(nc, ctx, "ps", [128, 2, 2, BANK], F32)
        (multiplied, kept) = ctx.enter_context(stage(nc, "multiplied kept"))
        block = ctx.enter_context(nc.Block())

        @block.tensor
        def _(pe):
            for c in range(NCH):
                if c >= 2:
                    pe.wait_ge(kept, c - 1)
                for k in range(2):
                    a = c * CH + k * HB
                    last = nc.tensor.matmul(ps[0:rows, c % 2, k, 0:HB], w, x[:, a:a + HB], start=True, stop=True)
                last.then_inc(multiplied, 1)

        if residual:
            @block.vector
            def _(dve):
                for c in range(NCH):
                    dve.wait_ge(multiplied, c + 1)
                    o = halves(out[:, c * CH:(c + 1) * CH])
                    nc.vector.scalar_tensor_tensor(out=o, in0=ps[0:rows, c % 2, :, 0:HB], scalar=bias, in1=o,
                                                   op0=ALU.add, op1=ALU.add).then_inc(kept, 1)
        else:
            @block.scalar
            def _(act):
                for c in range(NCH):
                    act.wait_ge(multiplied, c + 1)
                    o = halves(out[:, c * CH:(c + 1) * CH])
                    if bias is None:
                        nc.scalar.activation(o, ps[0:rows, c % 2, :, 0:HB], ACT.Copy).then_inc(kept, 1)
                    else:
                        nc.scalar.activation(o, ps[0:rows, c % 2, :, 0:HB], ACT.Identity, bias=bias).then_inc(kept, 1)


def project_tokens(nc, x, T, w, out, bias):
    K, n = w.shape
    with ExitStack() as ctx:
        xt = sbuf(nc, ctx, "xt", [K, 2, T], F32)
        ps = psum(nc, ctx, "ps", [128, 2, BANK], F32)
        (st0, st1, mu0, mu1, kp0, kp1, act_passed, dve_passed) = ctx.enter_context(
            stage(nc, "staged0 staged1 multiplied0 multiplied1 kept0 kept1 act_passed dve_passed"))
        staged, multiplied, kept = (st0, st1), (mu0, mu1), (kp0, kp1)
        block = ctx.enter_context(nc.Block())

        @block.scalar
        def _(act):
            hold = Hold(act, act_passed)
            with act.Fori(0, NT // T // 2) as i:
                for j in range(2):
                    hold(multiplied[j], i + 1)
                    nc.scalar.activation(xt[:, j, :], x[0:K, ds((2 * i + j) * T, T)], ACT.Copy).then_inc(staged[j], 1)

        @block.tensor
        def _(pe):
            free(pe, *multiplied)
            with pe.Fori(0, NT // T // 2) as i:
                for j in range(2):
                    pe.wait_ge(kept[j], i + 1)
                    pe.wait_ge(staged[j], i + 1)
                    nc.tensor.matmul(ps[0:T, j, 0:n], xt[:, j, :], w, start=True, stop=True).then_inc(multiplied[j], 1)

        @block.vector
        def _(dve):
            hold = Hold(dve, dve_passed)
            free(dve, *kept)
            with dve.Fori(0, NT // T // 2) as i:
                for j in range(2):
                    hold(multiplied[j], i + 2)
                    o = out[:, ds(2 * i + j, 1), :].rearrange("p o n -> p (o n)")
                    if bias is None:
                        nc.vector.tensor_copy(o, ps[0:T, j, 0:n]).then_inc(kept[j], 1)
                    else:
                        nc.vector.tensor_tensor(o, ps[0:T, j, 0:n], bias, ALU.add).then_inc(kept[j], 1)


AT = 2 * S
NAT = NT // AT
G = 8
GB = 4
NH, HD = 8, 16


def channel_attention(nc, cst, a, x, hT):
    with ExitStack() as ctx:
        def sb(name, shape, dt=F32):
            return sbuf(nc, ctx, name, shape, dt)

        w = sb("w", [128, 4 * D])
        bqk = sb("bqk", [AT, 2 * D])
        cols = sb("cols", [128, 2])
        hmask = sb("hmask", [128, D])
        smask = sb("smask", [AT, 2])
        qk = sb("qk", [AT, NAT, 2 * D])
        vT = sb("vT", [128, NT])
        oT = sb("oT", [128, NT])
        load(nc, (w[:, :], a["ca_w"]), (bqk[:, :], a["ca_bqk"]), (cols[:, :], a["ca_b"]),
             (hmask[:, :], a["c_headmask"]), (smask[:, :], a["c_seqmask"]))
        project_tokens(nc, x, AT, w[:, 0:2 * D], qk, bqk[:, :])
        project_features(nc, x, vT, w[:, 2 * D:3 * D], cols[:, 0:1])
        with ExitStack() as c1:
            NG = NAT * 2 * NH
            sq = sbuf(nc, c1, "sq", [AT, NAT, 2 * D])
            r = sbuf(nc, c1, "r", [AT, NG])
            (squared, summed, ac, r_ready, dc) = c1.enter_context(stage(nc, "squared summed act_chain r_ready dve_chain"))
            block = c1.enter_context(nc.Block())

            @block.scalar
            def _(act):
                link = Chain(act, ac)
                nc.scalar.activation(sq[:, :, :], qk[:, :, :], ACT.Square).then_inc(squared, 1)
                act.wait_ge(summed, 1)
                link(nc.scalar.activation(r[:, :], r[:, :], ACT.Ln))
                nc.scalar.activation(r[:, :], r[:, :], ACT.Exp, scale=-0.5).then_inc(r_ready, 1)

            @block.vector
            def _(dve):
                link = Chain(dve, dc)
                dve.wait_ge(squared, 1)
                link(nc.vector.tensor_reduce(r[:, :], sq[:, :, :].rearrange("p t (g d) -> p (t g) d", d=HD), AX.X, ALU.add))
                nc.vector.tensor_scalar(r[:, :], r[:, :], 1e-12, None, ALU.max).then_inc(summed, 1)
                dve.wait_ge(r_ready, 1)
                q = r[:, :].rearrange("p (t h) -> p t h", h=2 * NH)[:, :, 0:NH]
                link(nc.vector.tensor_scalar(q, q, HD ** -0.5, None, ALU.mult))
                g = qk[:, :, :].rearrange("p t (g d) -> p (t g) d", d=HD)
                link(nc.vector.tensor_tensor(g, g, r[:, :].unsqueeze(2).broadcast_to([AT, NG, HD]), ALU.mult))
        with ExitStack() as c1:
            q = sbuf(nc, c1, "q", [AT, G, D])
            kx = sbuf(nc, c1, "kx", [AT, G, 2, D])
            sc = sbuf(nc, c1, "sc", [128, 2 * G, D])
            mx = sbuf(nc, c1, "mx", [128, 2 * G])
            sm = sbuf(nc, c1, "sm", [128, 2 * G])
            vs = sbuf(nc, c1, "vs", [128, 2 * G, S])
            ps = psum(nc, c1, "ps", [128, 2 * G, D])
            po = psum(nc, c1, "po", [128, 2, BANK])
            (q_staged, kx_ready, scored, centered, exped, a_ready, out_ready, out_kept, dc, act_passed, dve_passed, pe_passed) = c1.enter_context(
                stage(nc, "q_staged kx_ready scored centered exped a_ready out_ready out_kept dve_chain act_passed dve_passed pe_passed"))
            block = c1.enter_context(nc.Block())

            @block.scalar
            def _(act):
                hold = Hold(act, act_passed)
                free(act, out_kept)
                with act.Fori(0, NAT // G) as i:
                    hold(scored, i + 1)
                    nc.scalar.activation(q[:, :, :], qk[:, ds(i * G, G), 0:D], ACT.Copy).then_inc(q_staged, 1)
                    act.wait_ge(centered, i + 1)
                    nc.scalar.activation(sc[:, :, :], sc[:, :, :], ACT.Exp).then_inc(exped, 1)
                    hold(out_ready, i + 2)
                    nc.scalar.activation(halves(oT[:, ds(i * G * AT, G * AT)]), po[:, :, 0:GB * AT], ACT.Copy).then_inc(out_kept, 1)

            @block.tensor
            def _(pe):
                hold = Hold(pe, pe_passed)
                free(pe, scored, out_ready)
                with pe.Fori(0, NAT // G) as i:
                    pe.wait_ge(q_staged, i + 1)
                    pe.wait_ge(kx_ready, i + 1)
                    for t in range(G):
                        last = nc.tensor.matmul(ps[:, 2 * t:2 * t + 2, :], q[:, t, :], kx[:, t, :, :],
                                                start=True, stop=True)
                    last.then_inc(scored, 1)
                    hold(a_ready, i + 1)
                    pe.wait_ge(out_kept, i + 1)
                    for s in range(2 * G):
                        last = nc.tensor.matmul(po[:, s // (2 * GB), s % (2 * GB) * S:(s % (2 * GB) + 1) * S], sc[:, s, :], vs[:, s, :],
                                                start=True, stop=True)
                    last.then_inc(out_ready, 1)

            @block.vector
            def _(dve):
                hold = Hold(dve, dve_passed)
                link = Chain(dve, dc)
                with link.loop(NAT // G, 4) as i:
                    hold(scored, i + 1)
                    for s in range(2):
                        last = nc.vector.tensor_scalar(kx[:, :, s, :], qk[:, ds(i * G, G), D:2 * D], smask[:, s:s + 1], None, ALU.mult)
                    last.then_inc(kx_ready, 1)
                    hold(scored, i + 2)
                    dve.wait_ge(out_ready, i + 1)
                    link(nc.vector.tensor_tensor(sc[:, :, :], ps[:, :, :], hmask[:, :].unsqueeze(1).broadcast_to([128, 2 * G, D]), ALU.add))
                    link(nc.vector.tensor_reduce(mx[:, :], sc[:, :, :], AX.X, ALU.max))
                    nc.vector.tensor_tensor(sc[:, :, :], sc[:, :, :], mx[:, :].unsqueeze(2).broadcast_to([128, 2 * G, D]),
                                            ALU.subtract).then_inc(centered, 1)
                    dve.wait_ge(exped, i + 1)
                    link(nc.vector.tensor_reduce(sm[:, :], sc[:, :, :], AX.X, ALU.add))
                    link(nc.vector.reciprocal(sm[:, :], sm[:, :]))
                    nc.vector.tensor_tensor(vs[:, :, :], vT[:, ds(i * G * AT, G * AT)].rearrange("p (s n) -> p s n", n=S),
                                            sm[:, :].unsqueeze(2).broadcast_to([128, 2 * G, S]), ALU.mult).then_inc(a_ready, 1)
        project_features(nc, oT, hT, w[:, 3 * D:4 * D], cols[:, 1:2], residual=True)


def frame_attention(nc, cst, a, x, hT):
    with ExitStack() as ctx:
        def sb(name, shape, dt=F32):
            return sbuf(nc, ctx, name, shape, dt)

        w = sb("w", [128, 3 * D])
        bmask = sb("bmask", [AT, AT])
        qT = sb("qT", [128, NT])
        kT = sb("kT", [128, NT])
        v = sb("v", [AT, NAT, D])
        load(nc, (w[:, :], a["fa_w"]), (bmask[:, :], a["c_blockmask"]))
        project_features(nc, x, qT, w[:, 0:D], None)
        project_features(nc, x, kT, w[:, D:2 * D], None)
        project_tokens(nc, x, AT, w[:, 2 * D:3 * D], v, None)
        with ExitStack() as c1:
            q = sbuf(nc, c1, "q", [128, G, AT])
            vs = sbuf(nc, c1, "vs", [AT, G, D])
            sc = sbuf(nc, c1, "sc", [AT, G, AT])
            zr = sbuf(nc, c1, "zr", [AT, G, AT])
            pT = sbuf(nc, c1, "pT", [AT, G, AT])
            mx = sbuf(nc, c1, "mx", [AT, G])
            sm = sbuf(nc, c1, "sm", [AT, G])
            ps = psum(nc, c1, "ps", [AT, 2, BANK])
            pt = psum(nc, c1, "pt", [AT, 2, BANK])
            po = psum(nc, c1, "po", [128, 2, BANK])
            (staged, scored, centered, exped, p_ready, turned, pT_ready, out_ready, out_added, dc, act_passed, pe_passed) = c1.enter_context(
                stage(nc, "staged scored centered exped p_ready turned pT_ready out_ready out_added dve_chain act_passed pe_passed"))
            block = c1.enter_context(nc.Block())

            def tile(p, t):
                return p[:, t // GB, t % GB * AT:(t % GB + 1) * AT]

            def banks(t):
                return t.rearrange("p (h g) n -> p h (g n)", h=2)

            @block.scalar
            def _(act):
                hold = Hold(act, act_passed)
                with act.Fori(0, NAT // G) as i:
                    hold(out_ready, i + 1)
                    nc.scalar.activation(vs[:, :, :], v[:, ds(i * G, G), :], ACT.Copy)
                    nc.scalar.activation(q[:, :, :].rearrange("p g n -> p (g n)"), qT[:, ds(i * G * AT, G * AT)],
                                         ACT.Copy).then_inc(staged, 1)
                    act.wait_ge(centered, i + 1)
                    nc.scalar.activation(sc[:, :, :], sc[:, :, :], ACT.Exp).then_inc(exped, 1)
                    act.wait_ge(turned, i + 2)
                    nc.scalar.activation(banks(pT[:, :, :]), pt[:, :, 0:GB * AT], ACT.Copy).then_inc(pT_ready, 1)

            @block.tensor
            def _(pe):
                hold = Hold(pe, pe_passed)
                free(pe, out_ready, turned)
                with pe.Fori(0, NAT // G) as i:
                    hold(staged, i + 1)
                    for t in range(G):
                        last = nc.tensor.matmul(tile(ps, t), q[:, t, :], kT[:, ds((i * G + t) * AT, AT)],
                                                start=True, stop=True)
                    last.then_inc(scored, 1)
                    pe.wait_ge(p_ready, i + 1)
                    for t in range(G):
                        last = nc.tensor.transpose(tile(pt, t), sc[:, t, :], cst["ident"][0:AT, 0:AT])
                    last.then_inc(turned, 1)
                    pe.wait_ge(pT_ready, i + 1)
                    pe.wait_ge(out_added, i + 1)
                    for t in range(G):
                        last = nc.tensor.matmul(tile(po, t), vs[:, t, :], pT[:, t, :], start=True, stop=True)
                    last.then_inc(out_ready, 1)

            @block.vector
            def _(dve):
                link = Chain(dve, dc)
                free(dve, out_added)
                with link.loop(NAT // G, 7) as i:
                    dve.wait_ge(scored, i + 1)
                    dve.wait_ge(turned, i + 1)
                    link(nc.vector.tensor_scalar(banks(sc[:, :, :]), ps[:, :, 0:GB * AT], D ** -0.5, None, ALU.mult))
                    link(nc.vector.tensor_scalar(zr[:, :, :], sc[:, :, :], 0.0, 1e-10, ALU.is_equal, ALU.mult))
                    link(nc.vector.tensor_tensor(sc[:, :, :], sc[:, :, :], zr[:, :, :], ALU.add))
                    link(nc.vector.tensor_tensor(sc[:, :, :], sc[:, :, :], bmask[:, :].unsqueeze(1).broadcast_to([AT, G, AT]), ALU.add))
                    link(nc.vector.tensor_reduce(mx[:, :], sc[:, :, :], AX.X, ALU.max))
                    nc.vector.tensor_tensor(sc[:, :, :], sc[:, :, :], mx[:, :].unsqueeze(2).broadcast_to([AT, G, AT]),
                                            ALU.subtract).then_inc(centered, 1)
                    dve.wait_ge(exped, i + 1)
                    link(nc.vector.tensor_reduce(sm[:, :], sc[:, :, :], AX.X, ALU.add))
                    link(nc.vector.reciprocal(sm[:, :], sm[:, :]))
                    nc.vector.tensor_tensor(sc[:, :, :], sc[:, :, :], sm[:, :].unsqueeze(2).broadcast_to([AT, G, AT]),
                                            ALU.mult).then_inc(p_ready, 1)
                    dve.wait_ge(out_ready, i + 2)
                    o = hT[:, ds(i * G * AT, G * AT)]
                    nc.vector.tensor_tensor(halves(o), po[:, :, 0:GB * AT], halves(o), ALU.add).then_inc(out_added, 1)


NST = 64


class Taps:

    def __init__(self, nc, ctx):
        def sb(name, shape, dt=F32):
            return sbuf(nc, ctx, name, shape, dt)

        self.p = sb("p", [128, 7 * NST + 2])
        self.fc = sb("fc", [128, 3, NST])
        self.e = sb("e", [128, 2, NST])
        self.qd = sb("qd", [128, NST])
        self.st = sb("st", [128, NST])
        self.prod = sb("prod", [128, 4, NST])
        self.sums = sb("sums", [128, 3, NST // 2])
        self.dots = sb("dots", [128, S, 3])
        self.chain, self.done, self.passed = ctx.enter_context(stage(nc, "taps_chain taps_done taps_passed"))

    def prepare(self, nc, ctx, a):
        p, fc, e, qd, st, prod = self.p, self.fc, self.e, self.qd, self.st, self.prod
        L, Pl, Pr = p[:, 0:NST], p[:, NST:3 * NST].rearrange("p (k n) -> p k n", k=2), p[:, 3 * NST:5 * NST].rearrange("p (k n) -> p k n", k=2)
        B, C = p[:, 5 * NST:6 * NST], p[:, 6 * NST:7 * NST]
        log_dt = p[:, 7 * NST:7 * NST + 1]
        def sb(name, shape, dt=F32):
            return sbuf(nc, ctx, name, shape, dt)

        e2 = sb("e2", [128, 2, NST])
        di = sb("di", [128, NST])
        bd = sb("bd", [128, NST])
        g = sb("g", [128, 4])
        kc = sb("kc", [128, 4])
        t1 = sb("t1", [128, 2])
        dt = sb("dt", [128, 1])
        (loaded, exped, dc) = ctx.enter_context(stage(nc, "loaded exped dve_chain"))

        def attach(block):
            @block.sync
            def _(sp):
                sp.dma_start(p[:, :], a["ss_w"]).then_inc(loaded, 16)

            @block.scalar
            def _(act):
                act.wait_ge(loaded, 16)
                nc.scalar.activation(dt[:, :], log_dt, ACT.Exp)
                nc.scalar.activation(L, L, ACT.Exp).then_inc(exped, 1)

            @block.vector
            def _(dve):
                link = Chain(dve, dc)
                v = nc.vector
                dve.wait_ge(loaded, 16)
                dve.wait_ge(exped, 1)
                b2 = [128, 2, NST]
                link(v.tensor_scalar(di[:, :], L, dt[:, :], 0.5, ALU.mult, ALU.mult))
                link(v.tensor_scalar(di[:, :], di[:, :], 1.0, None, ALU.add))
                link(v.reciprocal(di[:, :], di[:, :]))
                link(v.tensor_scalar(Pl, Pl, dt[:, :], 0.5, ALU.mult, ALU.mult))
                link(v.tensor_tensor(e2[:, :, :], Pl, di[:, :].unsqueeze(1).broadcast_to(b2), ALU.mult))
                link(v.tensor_tensor(fc[:, 0:2, :], Pr, di[:, :].unsqueeze(1).broadcast_to(b2), ALU.mult))
                link(v.tensor_copy(fc[:, 2, :], C))
                for i in range(2):
                    link(v.tensor_tensor(prod[:, 2 * i:2 * i + 2, :], fc[:, i:i + 1, :].broadcast_to(b2), Pl, ALU.mult))
                link(v.tensor_reduce(g[:, :], prod[:, :, :], AX.X, ALU.add))
                link(v.tensor_scalar(kc[:, 0:1], g[:, 3:4], -1.0, 1.0, ALU.mult, ALU.add))
                link(v.tensor_scalar(kc[:, 3:4], g[:, 0:1], -1.0, 1.0, ALU.mult, ALU.add))
                link(v.tensor_copy(kc[:, 1:3], g[:, 1:3]))
                link(v.tensor_tensor(t1[:, 0:1], kc[:, 0:1], kc[:, 3:4], ALU.mult))
                link(v.tensor_tensor(t1[:, 1:2], kc[:, 1:2], kc[:, 2:3], ALU.mult))
                link(v.tensor_tensor(t1[:, 0:1], t1[:, 0:1], t1[:, 1:2], ALU.subtract))
                link(v.reciprocal(t1[:, 0:1], t1[:, 0:1]))
                link(v.tensor_scalar(kc[:, :], kc[:, :], t1[:, 0:1], None, ALU.mult))
                for j in range(2):
                    link(v.tensor_scalar(e[:, j, :], e2[:, 0, :], kc[:, j:j + 1], None, ALU.mult))
                    link(v.scalar_tensor_tensor(out=e[:, j, :], in0=e2[:, 1, :], scalar=kc[:, 2 + j:3 + j], in1=e[:, j, :],
                                                op0=ALU.mult, op1=ALU.add))

                link(v.tensor_scalar(bd[:, :], B, dt[:, :], None, ALU.mult))
                link(v.tensor_tensor(prod[:, 0:3, :], fc[:, :, :], bd[:, :].unsqueeze(1).broadcast_to([128, 3, NST]), ALU.mult))
                link(v.tensor_reduce(kc[:, 0:3], prod[:, 0:3, :], AX.X, ALU.add))
                link(v.tensor_tensor(st[:, :], bd[:, :], di[:, :], ALU.mult))
                for j in range(2):
                    link(v.scalar_tensor_tensor(out=st[:, :], in0=e[:, j, :], scalar=kc[:, j:j + 1], in1=st[:, :],
                                                op0=ALU.mult, op1=ALU.add))
                link(v.tensor_scalar(qd[:, :], di[:, :], 2.0, -1.0, ALU.mult, ALU.add))
                link(v.tensor_scalar(e[:, :, :], e[:, :, :], 2.0, None, ALU.mult))

        return attach

    def recur(self, nc, pool):
        fc, e, qd, st, prod, sums, dots = self.fc, self.e, self.qd, self.st, self.prod, self.sums, self.dots
        link = Chain(pool, self.chain)
        g = nc.gpsimd
        steps = []
        n = NST // 2
        while n > 1:
            steps.append(n)
            n //= 2
        with link.loop(S, 6 + len(steps)) as t:
            link(g.tensor_tensor(prod[:, 0:3, :], fc[:, :, :], st[:, :].unsqueeze(1).broadcast_to([128, 3, NST]), ALU.mult))
            src = prod[:, 0:3, :]
            for n in steps:
                link(g.tensor_tensor(sums[:, :, 0:n], src[:, :, 0:n], src[:, :, n:2 * n], ALU.add))
                src = sums
            d = dots[:, ds(t, 1), :].rearrange("p o n -> p (o n)")
            pool.sem_inc(self.passed, 1)
            link(g.tensor_tensor(d, sums[:, :, 0:1].rearrange("p a n -> p (a n)"), sums[:, :, 1:2].rearrange("p a n -> p (a n)"), ALU.add))
            link(g.tensor_tensor(st[:, :], st[:, :], qd[:, :], ALU.mult))
            pool.sem_inc(self.passed, 1)
            link(g.tensor_tensor(prod[:, 0:2, :], e[:, :, :], d[:, 0:2].unsqueeze(2).broadcast_to([128, 2, NST]), ALU.mult))
            for j in range(2):
                link(g.tensor_tensor(st[:, :], st[:, :], prod[:, j, :], ALU.add))
        g.tensor_tensor(dots[:, 0, 2:3], dots[:, 0, 2:3], self.p[:, 7 * NST + 1:7 * NST + 2], ALU.add).then_inc(self.done, 1)


PE_TAPS = 9


def state_space(nc, cst, taps, x, hT):
    with ExitStack() as ctx:
        diag = sbuf(nc, ctx, "diag", [128, PE_TAPS, 128])
        y = sbuf(nc, ctx, "y", [128, NT])
        py = psum(nc, ctx, "py", [128, 8, BANK])
        (diag_ready, summed, dc) = ctx.enter_context(stage(nc, "diag_ready summed dve_chain"))
        block = ctx.enter_context(nc.Block())
        xb = x[:, :].rearrange("p (b s) -> p b s", s=S)
        yb = y[:, :].rearrange("p (b s) -> p b s", s=S)

        @block.scalar
        def _(act):
            for t in range(PE_TAPS):
                nc.scalar.activation(diag[:, t, :], cst["ident"], ACT.Copy, scale=taps.dots[:, t, 2:3]).then_inc(diag_ready, 1)

        @block.tensor
        def _(pe):
            for t in range(PE_TAPS):
                pe.wait_ge(diag_ready, t + 1)
                for q in range(8):
                    o = py[:, q, 0:HB].rearrange("p (b s) -> p b s", s=S)[:, :, t:S]
                    last = nc.tensor.matmul(o, diag[:, t, :], xb[:, 8 * q:8 * q + 8, 0:S - t], start=(t == 0), stop=True,
                                            skip_group_check=True)
            last.then_inc(summed, 1)

        @block.vector
        def _(dve):
            link = Chain(dve, dc)
            v = nc.vector
            link(v.tensor_copy(y[:, :], hT[:, :]))
            for t in range(PE_TAPS, S):
                link(v.scalar_tensor_tensor(out=yb[:, :, t:S], in0=xb[:, :, 0:S - t], scalar=taps.dots[:, t, 2:3],
                                            in1=yb[:, :, t:S], op0=ALU.mult, op1=ALU.add))
            dve.wait_ge(summed, 1)
            v.tensor_tensor(hT[:, :].rearrange("p (q n) -> p q n", q=8), y[:, :].rearrange("p (q n) -> p q n", q=8),
                            py[:, :, 0:HB], ALU.add)


BIG = 1024.0


def route(nc, iota, l, E, K, oh, gate, prob):
    with ExitStack() as ctx:
        cand = sbuf(nc, ctx, "cand", [TT, NTT, E])
        left = sbuf(nc, ctx, "left", [TT, NTT, E])
        mx = sbuf(nc, ctx, "mx", [TT, 2, NTT])
        first = sbuf(nc, ctx, "first", [TT, NTT])
        (dc, ready, exped) = ctx.enter_context(stage(nc, "dve_chain ready exped"))
        block = ctx.enter_context(nc.Block())
        full = [TT, NTT, E]

        def over(t):
            return t.unsqueeze(2).broadcast_to(full)

        @block.vector
        def _(dve):
            link = Chain(dve, dc)
            v = nc.vector
            io = iota[:, 0:E].unsqueeze(1).broadcast_to(full)
            src = l
            for k in range(K):
                link(v.tensor_reduce(mx[:, k, :], src[:, :, :], AX.X, ALU.max))
                link(v.tensor_tensor(cand[:, :, :], src[:, :, :], over(mx[:, k, :]), ALU.is_equal))
                link(v.tensor_scalar(cand[:, :, :], cand[:, :, :], -BIG, BIG, ALU.mult, ALU.add))
                link(v.tensor_tensor(cand[:, :, :], cand[:, :, :], io, ALU.add))
                link(v.tensor_reduce(first[:, :], cand[:, :, :], AX.X, ALU.min))
                link(v.tensor_tensor(oh[k][:, :, :], io, over(first[:, :]), ALU.is_equal))
                if k + 1 < K:
                    link(v.tensor_scalar(left[:, :, :], oh[k][:, :, :], -1e30, None, ALU.mult))
                    link(v.tensor_tensor(left[:, :, :], left[:, :, :], l[:, :, :], ALU.add))
                    src = left
            if prob:
                v.tensor_tensor(cand[:, :, :], l[:, :, :], over(mx[:, 0, :]), ALU.subtract).then_inc(ready, 1)
                dve.wait_ge(exped, 1)
                link(v.tensor_reduce(first[:, :], cand[:, :, :], AX.X, ALU.add))
                link(v.reciprocal(gate[0][:, :], first[:, :]))
            else:
                v.tensor_tensor(gate[1][:, :], mx[:, 1, :], mx[:, 0, :], ALU.subtract).then_inc(ready, 1)
                dve.wait_ge(exped, 1)
                link(v.tensor_scalar(first[:, :], gate[1][:, :], 1.0, None, ALU.add))
                link(v.reciprocal(gate[0][:, :], first[:, :]))
                link(v.tensor_tensor(gate[1][:, :], gate[1][:, :], gate[0][:, :], ALU.mult))

        @block.scalar
        def _(act):
            act.wait_ge(ready, 1)
            t = cand[:, :, :] if prob else gate[1][:, :]
            nc.scalar.activation(t, t, ACT.Exp).then_inc(exped, 1)


def token_rows(nc, cst, x, out):
    with ExitStack() as ctx:
        xt = sbuf(nc, ctx, "xt", [D, 2, TT])
        ps = psum(nc, ctx, "ps", [TT, 2, BANK])
        (st0, st1, t0, t1, kp0, kp1, act_passed, dve_passed) = ctx.enter_context(
            stage(nc, "staged0 staged1 turned0 turned1 kept0 kept1 act_passed dve_passed"))
        staged, turned, kept = (st0, st1), (t0, t1), (kp0, kp1)
        block = ctx.enter_context(nc.Block())

        @block.scalar
        def _(act):
            hold = Hold(act, act_passed)
            with act.Fori(0, NTT // 2) as i:
                for j in range(2):
                    hold(turned[j], i + 1)
                    nc.scalar.activation(xt[:, j, :], x[:, ds((2 * i + j) * TT, TT)], ACT.Copy).then_inc(staged[j], 1)

        @block.tensor
        def _(pe):
            free(pe, *turned)
            with pe.Fori(0, NTT // 2) as i:
                for j in range(2):
                    pe.wait_ge(kept[j], i + 1)
                    pe.wait_ge(staged[j], i + 1)
                    nc.tensor.transpose(ps[:, j, 0:D], xt[:, j, :], cst["ident"]).then_inc(turned[j], 1)

        @block.vector
        def _(dve):
            hold = Hold(dve, dve_passed)
            free(dve, *kept)
            with dve.Fori(0, NTT // 2) as i:
                for j in range(2):
                    hold(turned[j], i + 2)
                    nc.vector.tensor_copy(out[:, ds(2 * i + j, 1), :].rearrange("p o n -> p (o n)"), ps[:, j, 0:D]).then_inc(kept[j], 1)


ST = 128


def mixture(nc, cst, a, key, x, logits, out, E, K, F, act_fn, prob, capacity=None, beside=None,
            beside_scatter=None):
    NTILE = (K * NT + E * (ST - 1)) // ST
    UN = 8
    NTILE = -(-NTILE // UN) * UN
    NSLOT = NTILE * ST
    W1, W2, B1 = (F, F, F // 128) if F else (D, 0, 0)
    WE = W1 + W2 + B1
    FC = F // 128
    w_dram, b_dram = a[key + "_w"], a[key + "_b"]
    xs = nc.dram_tensor(unique(nc, "slots_in"), [NSLOT, D], F32, kind="Internal").ap()
    ys = nc.dram_tensor(unique(nc, "slots_out"), [NSLOT, D], F32, kind="Internal").ap()
    with ExitStack() as ctx:
        def sb(name, shape, dt=F32):
            return sbuf(nc, ctx, name, shape, dt)

        oh = [sb(f"oh{k}", [TT, NTT, E]) for k in range(K)]
        gate = [sb(f"gate{k}", [TT, NTT]) for k in range(K)]
        keepg = sb("keepg", [TT, 2, NTT])
        slot = [sb(f"slot{k}", [TT, NTT], I32) for k in range(K)]
        eid = sb("eid", [1, NTILE], I32)
        rows = sb("rows", [TT, NTT, D])
        iota = sb("iota", [TT, 128])
        index = sb("index", [TT, 1])
        assert NTILE <= TT
        tri = sb("tri", [TT, TT])
        keep_t = sb("keep_t", [TT, E, NTT])
        load(nc, (iota[:, :], a["c_iota"]), (index[:, :], a["c_index"]), (tri[:, :], a["c_tri"]),
             (keep_t[:, :, :], a["c_carry"][:, 0:E * NTT].rearrange("p (e t) -> p e t", e=E)))
        zero = sb("zero", [128, D])
        (zeroed, cleared) = ctx.enter_context(stage(nc, "zeroed cleared"))
        with nc.Block() as block:
            @block.vector
            def _(dve):
                nc.vector.memset(zero[:, :], 0.0).then_inc(zeroed, 1)

            @block.scalar
            def _(act):
                act.wait_ge(zeroed, 1)
                act.dma_start(xs.rearrange("(p r) d -> p r d", p=128),
                             zero[:, :].unsqueeze(1).broadcast_to([128, NTILE, D])).then_inc(cleared, 16)
        route(nc, iota, logits, E, K, oh, gate, prob)
        token_rows(nc, cst, x, rows)

        with ExitStack() as c1:
            NBK = -(-NTT * E // BANK)
            comb = sbuf(nc, c1, "comb", [TT, NTT * E])
            rank = sbuf(nc, c1, "rank", [TT, NTT, E])
            tot = sbuf(nc, c1, "tot", [TT, E, NTT])
            incl = sbuf(nc, c1, "incl", [TT, E, NTT])
            ones = sbuf(nc, c1, "ones", [TT, TT])
            tf = sbuf(nc, c1, "tf", [TT, 4, E])
            ti = sbuf(nc, c1, "ti", [TT, E], I32)
            ended = sbuf(nc, c1, "ended", [TT, E])
            ef = sbuf(nc, c1, "ef", [TT, 1])
            sf = sbuf(nc, c1, "sf", [TT, NTT])
            pr = psum(nc, c1, "pr", [TT, NBK * BANK])
            pt = psum(nc, c1, "pt", [TT, NBK * BANK])
            pe_row = psum(nc, c1, "pe_row", [1, TT])
            (dc, combined, counted, e_ready, e_turned) = c1.enter_context(
                stage(nc, "dve_chain combined counted e_ready e_turned"))
            block = c1.enter_context(nc.Block())

            @block.tensor
            def _(pe):
                pe.wait_ge(combined, 1)
                for lhs, o in ((tri, pr), (ones, pt)):
                    for q in range(NBK):
                        n = min(BANK, NTT * E - q * BANK)
                        last = nc.tensor.matmul(o[:, q * BANK:q * BANK + n], lhs[:, :], comb[:, q * BANK:q * BANK + n],
                                                start=True, stop=True)
                last.then_inc(counted, 1)
                pe.wait_ge(e_ready, 1)
                nc.tensor.transpose(pe_row[:, :], ef[:, :], cst["ident"][0:TT, 0:TT]).then_inc(e_turned, 1)

            @block.vector
            def _(dve):
                link = Chain(dve, dc)
                v = nc.vector
                cb = comb[:, :].rearrange("p (t e) -> p t e", e=E)
                link(v.memset(ones[:, :], 1.0))
                if K == 2:
                    v.tensor_tensor(cb, oh[0][:, :, :], oh[1][:, :, :], ALU.add).then_inc(combined, 1)
                else:
                    v.tensor_copy(cb, oh[0][:, :, :]).then_inc(combined, 1)
                dve.wait_ge(counted, 1)
                link(v.tensor_copy(tot[:, :, :], pt[:, 0:NTT * E].rearrange("p (t e) -> p e t", e=E)))
                flat = "p e t -> p (e t)"
                link(v.tensor_tensor_scan(incl[:, :, :].rearrange(flat), keep_t[:, :, :].rearrange(flat),
                                          tot[:, :, :].rearrange(flat), 0.0, ALU.mult, ALU.add))
                link(v.tensor_tensor(tot[:, :, :], incl[:, :, :], tot[:, :, :], ALU.subtract))
                link(v.tensor_tensor(rank[:, :, :], pr[:, 0:NTT * E].rearrange("p (t e) -> p t e", e=E),
                                     tot[:, :, :].rearrange("p e t -> p t e"), ALU.add))
                n_e = incl[:, :, NTT - 1]
                link(v.tensor_scalar(ti[:, :], n_e, float(ST - 1), None, ALU.add))
                link(v.tensor_scalar(ti[:, :], ti[:, :], ST.bit_length() - 1, None, ALU.logical_shift_right))
                link(v.tensor_copy(tf[:, 0, :], ti[:, :]))
                link(v.memset(tf[:, 1, :], 1.0))
                link(v.tensor_tensor_scan(tf[:, 2, :], tf[:, 1, :], tf[:, 0, :], 0.0, ALU.mult, ALU.add))
                link(v.tensor_tensor(tf[:, 3, :], tf[:, 2, :], tf[:, 0, :], ALU.subtract))
                if capacity is not None:
                    link(v.tensor_tensor(cb, rank[:, :, :], oh[0][:, :, :], ALU.mult))
                    link(v.tensor_reduce(sf[:, :], cb, AX.X, ALU.add))
                    link(v.tensor_scalar(sf[:, :], sf[:, :], float(capacity), None, ALU.is_le))
                    link(v.tensor_tensor(keepg[:, 0, :], sf[:, :], gate[0][:, :], ALU.mult))
                    link(v.tensor_tensor(keepg[:, 1, :], gate[0][:, :], keepg[:, 0, :], ALU.subtract))
                link(v.tensor_scalar(tf[:, 1, :], tf[:, 3, :], float(ST), -1.0, ALU.mult, ALU.add))
                link(v.tensor_tensor(rank[:, :, :], rank[:, :, :], tf[:, 1:2, :].broadcast_to([TT, NTT, E]), ALU.add))
                for k in range(K):
                    link(v.tensor_tensor(cb, rank[:, :, :], oh[k][:, :, :], ALU.mult))
                    link(v.tensor_reduce(sf[:, :], cb, AX.X, ALU.add))
                    link(v.tensor_copy(slot[k][:, :], sf[:, :]))
                link(v.tensor_scalar(ended[:, :], tf[:, 2, :], index[:, :], None, ALU.is_le))
                link(v.tensor_reduce(ef[:, :], ended[:, :], AX.X, ALU.add))
                v.tensor_scalar(ef[:, :], ef[:, :], float(E - 1), None, ALU.min).then_inc(e_ready, 1)
                dve.wait_ge(e_turned, 1)
                link(v.tensor_copy(eid[:, :], pe_row[:, 0:NTILE]))

        with ExitStack() as c1:
            scattered, all_scattered = cst["scattered"].sem, cst["scattered"].add(16 * K * NTT)
            attach = beside_scatter(c1) if beside_scatter is not None else None
            block = c1.enter_context(nc.Block())
            if attach is not None:
                attach(block)

            @block.gpsimd
            def _(pool):
                pool.wait_ge(cleared, 16)
                for k in range(K):
                    for t in range(NTT):
                        pool.indirect_dma_start(xs, bass.IndirectOffsetOnAxis(ap=slot[k][:, t:t + 1], axis=0),
                                                rows[:, t, :], None).then_inc(scattered, 16)
                pool.wait_ge(scattered, all_scattered)

        with ExitStack() as c1:
            IT = NTILE // UN
            wb = sbuf(nc, c1, "wb", [128, UN, WE])
            bb = sbuf(nc, c1, "bb", [1, UN, D])
            xi = sbuf(nc, c1, "xi", [ST, UN, D])
            xT = sbuf(nc, c1, "xT", [D, UN, ST])
            eh = sbuf(nc, c1, "eh", [128, 2, max(FC, 1), ST])
            yo = sbuf(nc, c1, "yo", [ST, UN, D])
            one = sbuf(nc, c1, "one", [1, ST])
            px = psum(nc, c1, "px", [D, 2, BANK])
            ph = psum(nc, c1, "ph", [128, 2, BANK])
            po = psum(nc, c1, "po", [ST, 2, BANK])
            (one_ready, turned, xT_ready, up, h_ready, down, y_ready, sp_passed) = c1.enter_context(
                stage(nc, "one_ready turned xT_ready up h_ready down y_ready sp_passed"))
            per_buffer = c1.enter_context(stage(nc, " ".join(f"{n}{j}" for n in ("w_loaded", "x_loaded", "stored") for j in range(UN))))
            w_loaded, x_loaded, stored = [per_buffer[UN * k:UN * k + UN] for k in range(3)]
            FREE = UN
            block = c1.enter_context(nc.Block())

            def unrolled(eng, body):
                with eng.Fori(0, IT - 1) as i:
                    for j in range(UN):
                        body(i, j, False)
                for j in range(UN):
                    body(IT - 1, j, True)

            @block.sync
            def _(sp):
                hold = Hold(sp, sp_passed)
                with sp.Fori(0, IT) as i:
                    for j in range(UN):
                        e = sp.value_load(eid[0:1, ds(UN * i + j, 1)], min_val=0, max_val=E - 1)
                        hold(down, UN * i + j + 1)
                        sp.dma_start(wb[:, j, :], w_dram[ds(e, 1), :, :].rearrange("o p n -> p (o n)")).then_inc(w_loaded[j], 16)
                        sp.dma_start(bb[:, j, :], b_dram[ds(e, 1), :]).then_inc(w_loaded[j], 16)

            @block.tensor
            def _(pe):
                pe.sem_inc(down, FREE)
                pe.wait_ge(one_ready, 1)

                def turn(i, j):
                    i, j = i + j // UN, j % UN
                    pe.wait_ge(x_loaded[j], 16 * (i + 1))
                    nc.tensor.transpose(px[:, j % 2, 0:ST], xi[:, j, :], cst["ident"]).then_inc(turned, 1)

                def first_layer(i, j):
                    pe.wait_ge(xT_ready, UN * i + j + 1)
                    i, j = i + j // UN, j % UN
                    pe.wait_ge(w_loaded[j], 32 * (i + 1))
                    for f in range(FC):
                        last = nc.tensor.matmul(ph[:, j % 2, f * ST:(f + 1) * ST], wb[:, j, f * 128:(f + 1) * 128],
                                                xT[:, j, :], start=True, stop=True)
                    last.then_inc(up, 1)

                def second_layer(i, j):
                    t = UN * i + j
                    pe.wait_ge(y_ready, t + 1)
                    if F:
                        pe.wait_ge(h_ready, t + 1)
                        for f in range(FC):
                            nc.tensor.matmul(po[:, j % 2, 0:D], eh[:, j % 2, f, :], wb[:, j, F + f * D:F + (f + 1) * D],
                                             start=(f == 0), stop=False)
                    else:
                        pe.wait_ge(w_loaded[j], 32 * (i + 1))
                        nc.tensor.matmul(po[:, j % 2, 0:D], xT[:, j, :], wb[:, j, 0:D], start=True, stop=False)
                    nc.tensor.matmul(po[:, j % 2, 0:D], one[:, :], bb[:, j, :], start=False, stop=True).then_inc(down, 1)

                turn(0, 0)
                turn(0, 1)
                if F:
                    first_layer(0, 0)

                def body(i, j, last):
                    if not last or j + 2 < UN:
                        pe.wait_ge(xT_ready, UN * i + j + 1)
                        turn(i, j + 2)
                    elif not F:
                        pe.wait_ge(xT_ready, UN * i + j + 1)
                    if F and (not last or j + 1 < UN):
                        first_layer(i, j + 1)
                    second_layer(i, j)

                unrolled(pe, body)

            if beside is not None:
                @block.gpsimd
                def _(pool):
                    beside(nc, pool)

            @block.vector
            def _(dve):
                def turn(i, j):
                    t = UN * i + j
                    dve.wait_ge(turned, t + 1)
                    dve.wait_ge(down, t + 1)
                    nc.vector.tensor_copy(xT[:, j % UN, :], px[:, j % 2, 0:ST]).then_inc(xT_ready, 1)

                dve.sem_inc(y_ready, 2)
                nc.vector.memset(one[:, :], 1.0).then_inc(one_ready, 1)
                turn(0, 0)
                turn(0, 1)

                def body(i, j, last):
                    if not last or j + 2 < UN:
                        turn(i, j + 2)
                    dve.wait_ge(down, UN * i + j + 1 + FREE)
                    dve.wait_ge(stored[j], 16 * (i + 1))
                    nc.vector.tensor_copy(yo[:, j, :], po[:, j % 2, 0:D]).then_inc(y_ready, 1)

                unrolled(dve, body)

            @block.scalar
            def _(act):
                def hidden(i, j):
                    t = UN * i + j
                    act.wait_ge(up, t + 1)
                    act.wait_ge(down, t + FREE - 1)
                    j = j % UN
                    for f in range(FC):
                        last = nc.scalar.activation(eh[:, j % 2, f, :], ph[:, j % 2, f * ST:(f + 1) * ST], act_fn,
                                                    bias=wb[:, j, W1 + W2 + f:W1 + W2 + f + 1])
                    last.then_inc(h_ready, 1)

                if F:
                    nc.scalar.preload_act_table_set("silu_and_others" if act_fn == ACT.Silu else "gelu_and_others")

                def body(i, j, last):
                    if F and (not last or j + 1 < UN):
                        hidden(i, j + 1)
                    act.wait_ge(y_ready, UN * i + j + 3)
                    act.dma_start(ys[ds((UN * i + j) * ST, ST), :], yo[:, j, :]).then_inc(stored[j], 16)
                    if not last:
                        act.dma_start(xi[:, j, :], xs[ds((UN * (i + 1) + j) * ST, ST), :]).then_inc(x_loaded[j], 16)

                for j in range(UN):
                    act.sem_inc(stored[j], 16)
                    act.dma_start(xi[:, j, :], xs[j * ST:(j + 1) * ST, :]).then_inc(x_loaded[j], 16)
                if F:
                    hidden(0, 0)

                unrolled(act, body)
                for j in range(UN):
                    act.wait_ge(stored[j], 16 * (IT + 1))

        with ExitStack() as c1:
            gk = [sbuf(nc, c1, f"g{k}", [TT, NTT, D]) for k in range(K)]
            pt = psum(nc, c1, "pt", [D, 2, BANK])
            gathered = [(g.sem, g.add(16 * K)) for g in cst["gathered"]]
            (weighed, turned, added, dc) = c1.enter_context(stage(nc, "weighed turned added dve_chain"))
            block = c1.enter_context(nc.Block())

            @block.gpsimd
            def _(pool):
                for t in range(NTT):
                    for k in range(K):
                        pool.indirect_dma_start(gk[k][:, t, :], None, ys,
                                                bass.IndirectOffsetOnAxis(ap=slot[k][:, t:t + 1], axis=0)).then_inc(gathered[t][0], 16)

            @block.vector
            def _(dve):
                link = Chain(dve, dc)
                v = nc.vector

                def weigh(t):
                    dve.wait_ge(*gathered[t])
                    r = gk[0][:, t, :]
                    if capacity is not None:
                        link(v.tensor_scalar(r, r, keepg[:, 0, t:t + 1], None, ALU.mult))
                        v.scalar_tensor_tensor(out=r, in0=rows[:, t, :], scalar=keepg[:, 1, t:t + 1], in1=r,
                                               op0=ALU.mult, op1=ALU.add).then_inc(weighed, 1)
                    elif K == 1:
                        v.tensor_scalar(r, r, gate[0][:, t:t + 1], None, ALU.mult).then_inc(weighed, 1)
                    else:
                        link(v.tensor_scalar(r, r, gate[0][:, t:t + 1], None, ALU.mult))
                        v.scalar_tensor_tensor(out=r, in0=gk[1][:, t, :], scalar=gate[1][:, t:t + 1], in1=r,
                                               op0=ALU.mult, op1=ALU.add).then_inc(weighed, 1)

                def add(t):
                    dve.wait_ge(turned, t + 1)
                    o = out[:, t * TT:(t + 1) * TT]
                    v.tensor_tensor(o, pt[:, t % 2, 0:TT], o, ALU.add).then_inc(added, 1)

                weigh(0)
                for t in range(NTT):
                    if t + 1 < NTT:
                        weigh(t + 1)
                    add(t)

            @block.tensor
            def _(pe):
                for t in range(NTT):
                    if t >= 2:
                        pe.wait_ge(added, t - 1)
                    pe.wait_ge(weighed, t + 1)
                    nc.tensor.transpose(pt[:, t % 2, 0:TT], gk[0][:, t, :], cst["ident"][0:TT, 0:TT]).then_inc(turned, 1)


def switch_ffn(nc, cst, a, x, hT, taps):
    E = 16
    with ExitStack() as ctx:
        w = sbuf(nc, ctx, "w", [128, E])
        b = sbuf(nc, ctx, "b", [TT, E])
        l = sbuf(nc, ctx, "l", [TT, NTT, E])
        load(nc, (w[:, :], a["sw_r"]), (b[:, :], a["sw_rb"]))
        project_tokens(nc, x, TT, w[:, :], l, b[:, :])
        mixture(nc, cst, a, "sw", x, l, hT, E, 1, 0, None, True, capacity=int(1.2 * NT / E),
                beside_scatter=lambda c: taps.prepare(nc, c, a))


def gelu_ffn(nc, cst, a, x, hT, beside_scatter):
    E = 8
    with ExitStack() as ctx:
        w = sbuf(nc, ctx, "w", [128, E])
        b = sbuf(nc, ctx, "b", [TT, E])
        l = sbuf(nc, ctx, "l", [TT, NTT, E])
        load(nc, (w[:, :], a["gf_r"]), (b[:, :], a["gf_rb"]))
        project_tokens(nc, x, TT, w[:, :], l, b[:, :])
        mixture(nc, cst, a, "gf", x, l, hT, E, 1, 512, ACT.Gelu, True, beside_scatter=beside_scatter)


def two_layer_parts(nc, ctx, x, w1, b1, w2, b2, out, F, add):
    FC = F // 128
    hid = sbuf(nc, ctx, "hid", [128, 2, FC, HB])
    ph = psum(nc, ctx, "ph", [128, FC, BANK])
    po = psum(nc, ctx, "po", [128, 2, BANK])
    (up, h_ready, down, kept) = ctx.enter_context(stage(nc, "up h_ready down kept"))

    def attach(block):
        n = 2 * NCH

        @block.tensor
        def _(pe):
            def second(c):
                pe.wait_ge(h_ready, c + 1)
                if c >= 2:
                    pe.wait_ge(kept, c - 1)
                for f in range(FC):
                    last = nc.tensor.matmul(po[:, c % 2, 0:HB], w2[:, f * D:(f + 1) * D], hid[:, c % 2, f, :],
                                            start=(f == 0), stop=(f == FC - 1))
                last.then_inc(down, 1)

            for c in range(n):
                if c >= 1:
                    pe.wait_ge(h_ready, c)
                for f in range(FC):
                    last = nc.tensor.matmul(ph[:, f, 0:HB], w1[:, f * 128:(f + 1) * 128], x[:, c * HB:(c + 1) * HB],
                                            start=True, stop=True)
                last.then_inc(up, 1)
                if c >= 1:
                    second(c - 1)
            second(n - 1)

        @block.scalar
        def _(act):
            nc.scalar.preload_act_table_set("silu_and_others")
            for c in range(n):
                act.wait_ge(up, c + 1)
                if c >= 2:
                    act.wait_ge(down, c - 1)
                for f in range(FC):
                    last = nc.scalar.activation(hid[:, c % 2, f, :], ph[:, f, 0:HB], ACT.Silu, bias=b1[:, f:f + 1])
                last.then_inc(h_ready, 1)

        @block.vector
        def _(dve):
            for c in range(n):
                dve.wait_ge(down, c + 1)
                o = out[:, c * HB:(c + 1) * HB]
                if add:
                    nc.vector.scalar_tensor_tensor(out=o, in0=po[:, c % 2, 0:HB], scalar=b2, in1=o,
                                                   op0=ALU.add, op1=ALU.add).then_inc(kept, 1)
                else:
                    nc.vector.tensor_scalar(o, po[:, c % 2, 0:HB], b2, SHARED_SCALE, ALU.add, ALU.mult).then_inc(kept, 1)

    return attach


def two_layer(nc, *args):
    with ExitStack() as ctx:
        attach = two_layer_parts(nc, ctx, *args)
        attach(ctx.enter_context(nc.Block()))


SHARED_SCALE = 0.25
TEMP = 0.7


def silu_ffn(nc, cst, a, x, hT, taps):
    E, DR, DFF, DSH = 64, 64, 512, 256
    with ExitStack() as ctx:
        c = sbuf(nc, ctx, "c", [128, 12])
        moe = sbuf(nc, ctx, "moe", [128, NT])
        h = sbuf(nc, ctx, "h", [128, NT])
        load(nc, (c[:, :], a["sf_cols"]))
        layernorm(nc, cst, x, h, c[:, 0:1], c[:, 1:2])
        with ExitStack() as c1:
            ws = sbuf(nc, c1, "ws", [128, 2 * DSH])
            w = sbuf(nc, c1, "w", [128, DR])
            cb = sbuf(nc, c1, "cb", [DR, E])
            r = sbuf(nc, c1, "r", [DR, NT])
            l = sbuf(nc, c1, "l", [TT, NTT, E])
            load(nc, (ws[:, :], a["sf_ws"]), (w[:, :], a["sf_wr"]), (cb[:, :], a["sf_code"]))
            project_features(nc, h, r, w[:, :], None, rows=DR)
            project_tokens(nc, r, TT, cb[:, :], l, None)
            with ExitStack() as c2:
                (scaled,) = c2.enter_context(stage(nc, "scaled"))
                block = c2.enter_context(nc.Block())

                @block.vector
                def _(dve):
                    nc.vector.tensor_scalar(l[:, :, :], l[:, :, :], 1.0 / TEMP, None, ALU.mult).then_inc(scaled, 1)
            mixture(nc, cst, a, "sf", h, l, moe, E, 2, DFF, ACT.Silu, False, beside=taps.recur,
                    beside_scatter=lambda c2: two_layer_parts(nc, c2, h, ws[:, 0:DSH], c[:, 4:6], ws[:, DSH:2 * DSH], c[:, 6:7],
                                                              moe, DSH, False))
        layernorm(nc, cst, moe, h, c[:, 2:3], c[:, 3:4])
        with ExitStack() as c1:
            w = sbuf(nc, c1, "w", [128, 2 * DFF])
            load(nc, (w[:, :], a["sf_wf"]))
            two_layer(nc, h, w[:, 0:DFF], c[:, 7:11], w[:, DFF:2 * DFF], c[:, 11:12], hT, DFF, True)
        with ExitStack() as c1:
            (dc,) = c1.enter_context(stage(nc, "dve_chain"))
            block = c1.enter_context(nc.Block())

            @block.vector
            def _(dve):
                link = Chain(dve, dc)
                link(nc.vector.tensor_tensor(hT[:, :], hT[:, :], moe[:, :], ALU.add))
                link(nc.vector.tensor_tensor(hT[:, :], hT[:, :], x[:, :], ALU.add))



LE, LK, TS, BT = 8, 2, NB, S
EK = LE * LK
HE = LE // 2
CB = LK * BT
PERB = BANK // CB
GO = (0, 1, 3, 2)


def lstm_experts(nc, cst, a, weights, x, hT):
    with ExitStack() as ctx:
        def sb(name, shape, dt=F32):
            return sbuf(nc, ctx, name, shape, dt)

        mb = sb("mb", [128, EK, NT], F16)
        rwb = sb("rwb", [128, LK, NT])
        wT = sb("wT", [EK, NT])
        bsp = sb("bsp", [3 * LE, 4 * D], BF16)
        bsel = sb("bsel", [3 * LE, LE, CB], BF16)
        bo = sb("bo", [EK, D])
        wo = sb("wo", [128, LE, D])
        wi, wh, scale = weights
        xs = sb("xs", [128, 2, NT], F16)
        with ExitStack() as c1:
            w = sbuf(nc, c1, "w", [128, LE])
            b = sbuf(nc, c1, "b", [TT, LE])
            l = sbuf(nc, c1, "l", [TT, NTT, LE])
            oh = [sbuf(nc, c1, f"oh{k}", [TT, NTT, LE]) for k in range(LK)]
            gate = [sbuf(nc, c1, f"gate{k}", [TT, NTT]) for k in range(LK)]
            iota = sbuf(nc, c1, "iota", [TT, 128])
            load(nc, (iota[:, :], a["c_iota"]), (w[:, :], a["le_r"]), (b[:, :], a["le_rb"]), (bo[:, :], a["le_bo"]),
                 (wo[:, :, :], a["le_wo"].rearrange("p (e n) -> p e n", e=LE)))
            project_tokens(nc, x, TT, w[:, :], l, b[:, :])
            route(nc, iota, l, LE, LK, oh, gate, False)
            expand_routes(nc, cst, a, oh, gate, mb, rwb, wT)
        split_bias(nc, a, x, xs, bsp, bsel, scale)
        UN = 8
        GR = 4
        HC = HE * CB
        xm = sb("xm", [128, GR, 2, EK, BT], F16)
        z = sb("z", [128, 2, 5, HC])
        prod = sb("prod", [128, 2, 2, HC])
        tc = sb("tc", [128, 2, HC])
        h = sb("h", [128, 2, HC])
        hs = sb("hs", [128, 2, 2, HC], F16)
        hm = sb("hm", [128, 2, HE, LK, BT])
        hw = sb("hw", [128, UN, LE, BT])
        pg = [psum(nc, ctx, f"pg{q}", [128, 3, BANK]) for q in range(2)]
        py = psum(nc, ctx, "py", [128, BANK])
        names = "gates_ready activated c_ready tc_ready h_ready high_ready parts_ready hw_ready"
        s16 = ctx.enter_context(stage(nc, " ".join(f"{n}{q}" for n in names.split() for q in range(2))))
        gates_ready, activated, c_ready, tc_ready, h_ready, high_ready, parts_ready, hw_ready = [s16[2 * i:2 * i + 2] for i in range(8)]
        (cleared, x_ready, y_ready, y_added, dc, pc, pe_passed, dve_passed, pool_passed) = ctx.enter_context(
            stage(nc, "cleared x_ready y_ready y_added dve_chain pool_chain pe_passed dve_passed pool_passed"))
        block = ctx.enter_context(nc.Block())
        IT = TS // UN

        def tokens(t, n=1):
            return ds(t * BT, n * BT)

        def col(g, e):
            m = g * HE + e
            return m // PERB, (m % PERB) * CB

        @block.tensor
        def _(pe):
            hold = Hold(pe, pe_passed)
            pe.wait_ge(cleared, 1)

            def gates(q, t, j):
                p = pg[q]
                pe.wait_ge(activated[q], t + 1)
                pe.wait_ge(x_ready, t + 1)
                seen = set()
                for g in range(4):
                    e = 0
                    while e < HE:
                        bank, c = col(g, e)
                        n = 1
                        while e + n < HE and col(g, e + n)[0] == bank:
                            n += 1
                        nc.tensor.matmul(p[:, bank, c:c + n * CB], bsp[:, GO[g] * D:(GO[g] + 1) * D],
                                         bsel[:, q * HE + e:q * HE + e + n, :].rearrange("p e c -> p (e c)"),
                                         start=bank not in seen, stop=False, skip_group_check=True)
                        seen.add(bank)
                        e += n
                for u in range(2):
                    if u:
                        pe.wait_ge(parts_ready[q], t + 1)
                    for g in range(4):
                        for e in range(HE):
                            bank, c = col(g, e)
                            ee = q * HE + e
                            if u:
                                rhs = [hs[:, q, part, e * CB:(e + 1) * CB] for part in range(2)]
                            else:
                                rhs = [xm[:, j % GR, part, ee * LK:(ee + 1) * LK, :].rearrange("p k b -> p (k b)") for part in range(2)]
                            for wp, rp in ((0, 0), (0, 1), (1, 0)):
                                last = nc.tensor.matmul(p[:, bank, c:c + CB], (wh if u else wi)[:, wp, ee, GO[g] * D:(GO[g] + 1) * D],
                                                        rhs[rp], start=False, stop=u == 1 and wp == 1, skip_group_check=True)
                last.then_inc(gates_ready[q], 1)

            pe.sem_inc(y_ready, 2)

            def output(g, slot):
                for q in range(2):
                    hold(hw_ready[q], GR * g + (GR + 1))
                hold(y_added, g + 1)
                for e in range(LE):
                    nc.tensor.matmul(py[:, 0:GR * BT], wo[:, e, :], hw[:, slot:slot + GR, e, :], start=(e == 0), stop=False)
                nc.tensor.matmul(py[:, 0:GR * BT], bo[:, :], wT[:, tokens(GR * g, GR)], start=False, stop=True).then_inc(y_ready, 1)

            def body(i, first):
                for j in range(UN):
                    t = UN * i + j
                    gates(0, t, j)
                    if j % GR == 1 and not (first and j == 1):
                        output(i * (UN // GR) + (j // GR - 1), UN - GR - j // GR * GR)
                    gates(1, t, j)

            body(0, True)
            with pe.Fori(1, IT) as i:
                body(i, False)
            output(TS // GR - 1, UN - GR)

        @block.scalar
        def _(act):
            def body(i):
                for j in range(UN):
                    t = UN * i + j
                    for q in range(2):
                        act.wait_ge(gates_ready[q], t + 1)
                        flat = z[:, q, :, :].rearrange("p g n -> p (g n)")
                        for f, lo, hi in ((ACT.Sigmoid, 0, 3 * HE), (ACT.Tanh, 3 * HE, 4 * HE)):
                            while lo < hi:
                                bank = lo // PERB
                                n = min(hi, (bank + 1) * PERB) - lo
                                c = (lo % PERB) * CB
                                last = nc.scalar.activation(flat[:, lo * CB:(lo + n) * CB], pg[q][:, bank, c:c + n * CB], f,
                                                            scale=scale[:, 1:2])
                                lo += n
                        last.then_inc(activated[q], 1)
                        act.wait_ge(c_ready[q], t + 1)
                        nc.scalar.activation(tc[:, q, :], z[:, q, 4, :], ACT.Tanh).then_inc(tc_ready[q], 1)

            nc.scalar.preload_act_table_set("sigmoid_and_others")
            free(act, *activated)
            with act.Fori(0, IT) as i:
                body(i)

        @block.vector
        def _(dve):
            link = Chain(dve, dc)
            hold = Hold(dve, dve_passed)
            v = nc.vector
            v.memset(hs[:, :, :, :], 0.0)
            v.memset(z[:, :, 4, :], 0.0).then_inc(cleared, 1)

            free(dve, y_added, *parts_ready)

            def add(g):
                hold(y_ready, g + 3)
                o = hT[:, tokens(GR * g, GR)]
                v.tensor_tensor(o, py[:, 0:GR * BT], o, ALU.add).then_inc(y_added, 1)

            def body(i, first):
                for j in range(UN):
                    t = UN * i + j
                    for q in range(2):
                        dve.wait_ge(activated[q], t + 2)
                        link(v.tensor_tensor(prod[:, q, :, :], z[:, q, 0:2, :], z[:, q, 3:5, :], ALU.mult))
                        v.tensor_tensor(z[:, q, 4, :], prod[:, q, 0, :], prod[:, q, 1, :], ALU.add).then_inc(c_ready[q], 1)
                        dve.wait_ge(tc_ready[q], t + 1)
                        dve.wait_ge(hw_ready[q], t + 1)
                        v.tensor_tensor(h[:, q, :], z[:, q, 2, :], tc[:, q, :], ALU.mult).then_inc(h_ready[q], 1)
                        v.tensor_tensor(hs[:, q, 0, :], z[:, q, 2, :], tc[:, q, :], ALU.mult).then_inc(high_ready[q], 1)
                        dve.wait_ge(high_ready[q], t + 1)
                        v.tensor_tensor(hs[:, q, 1, :], h[:, q, :], hs[:, q, 0, :], ALU.subtract).then_inc(parts_ready[q], 1)
                    if j % GR == 2 and not (first and j == 2):
                        add(i * (UN // GR) + (j // GR - 1))

            dve.wait_ge(cleared, 1)
            body(0, True)
            with link.loop(IT - 1, 2 * UN) as i:
                body(i + 1, False)
            add(TS // GR - 1)

        @block.gpsimd
        def _(pool):
            link = Chain(pool, pc)
            hold = Hold(pool, pool_passed)
            g = nc.gpsimd

            def mask_x(t, j):
                for part in range(2):
                    last = g.tensor_tensor(xm[:, j % GR, part, :, :], xs[:, part, tokens(t)].unsqueeze(1).broadcast_to([128, EK, BT]),
                                           mb[:, :, tokens(t)], ALU.mult)
                last.then_inc(x_ready, 1)

            def weigh(t, j, i):
                for q in range(2):
                    hold(h_ready[q], t + 1)
                    if j % GR == 0:
                        hold(y_ready, i * (UN // GR) + (j // GR + 1))
                    hold(hw_ready[q], t + 1)
                    link(g.tensor_tensor(hm[:, q, :, :, :].rearrange("p e k b -> p (e k) b"),
                                         h[:, q, :].rearrange("p (m b) -> p m b", b=BT),
                                         mb[:, q * HE * LK:(q + 1) * HE * LK, tokens(t)], ALU.mult))
                    pool.sem_inc(pool_passed, 1)
                    link(g.tensor_tensor(hm[:, q, :, :, :], hm[:, q, :, :, :],
                                         rwb[:, :, tokens(t)].unsqueeze(1).broadcast_to([128, HE, LK, BT]), ALU.mult))
                    g.tensor_tensor(hw[:, j, q * HE:(q + 1) * HE, :], hm[:, q, :, 0, :], hm[:, q, :, 1, :],
                                    ALU.add).then_inc(hw_ready[q], 1)

            free(pool, *hw_ready)
            for j in range(GR):
                mask_x(j, j)
            with link.loop(IT - 1, 4 * UN) as i:
                for j in range(UN):
                    weigh(UN * i + j, j, i)
                    mask_x(UN * i + j + GR, j)
            for j in range(UN):
                weigh(TS - UN + j, j, IT - 1)
                if j + GR < UN:
                    mask_x(TS - UN + j + GR, j)


def split_weights(nc, ctx, cst, a, wi, wh, scale):
    wf = [sbuf(nc, ctx, f"wf{k}", [128, LE * 4 * D]) for k in range(2)]
    mx = sbuf(nc, ctx, "mx", [128, 3])
    row = sbuf(nc, ctx, "row", [1, 130])
    k = sbuf(nc, ctx, "k", [128, 3], I32)
    kf = sbuf(nc, ctx, "kf", [128, 3])
    ps = psum(nc, ctx, "ps", [128, BANK])
    pb = psum(nc, ctx, "pb", [128, BANK])
    (reduced, turned, largest, spread, dc, scale_known, scaled0, scaled1, highs, wl0, wl1) = ctx.enter_context(
        stage(nc, "reduced turned largest spread dve_chain scale_known scaled0 scaled1 highs w_loaded0 w_loaded1"))

    def attach(block):
        @block.sync
        def _(sp):
            sp.dma_start(wf[0][:, :], a["le_wi"]).then_inc(wl0, 16)
            sp.dma_start(wf[1][:, :], a["le_wh"]).then_inc(wl1, 16)

        @block.tensor
        def _(pe):
            pe.wait_ge(reduced, 1)
            nc.tensor.transpose(ps[0:1, 0:128], mx[:, 2:3], cst["ident"]).then_inc(turned, 1)
            pe.wait_ge(largest, 1)
            nc.tensor.matmul(pb[:, 0:1], row[0:1, 2:130], row[0:1, 0:1], start=True, stop=True).then_inc(spread, 1)

        @block.scalar
        def _(act):
            act.wait_ge(scale_known, 1)
            nc.scalar.activation(wf[1][:, :], wf[1][:, :], ACT.Copy, scale=scale[:, 0:1]).then_inc(scaled1, 1)
            for n in range(2):
                act.wait_ge((scaled0, scaled1)[n], 1)
                w = (wi, wh)[n]
                nc.scalar.activation(w[:, 0, :, :].rearrange("p e n -> p (e n)"), wf[n][:, :], ACT.Copy).then_inc(highs, 1)

        @block.vector
        def _(dve):
            link = Chain(dve, dc)
            v = nc.vector
            link(v.memset(row[:, :], 1.0))
            for n in range(2):
                dve.wait_ge((wl0, wl1)[n], 16)
                link(v.tensor_reduce(mx[:, n:n + 1], wf[n][:, :], AX.X, ALU.max, apply_absolute_value=True))
            v.tensor_tensor(mx[:, 2:3], mx[:, 0:1], mx[:, 1:2], ALU.max).then_inc(reduced, 1)
            dve.wait_ge(turned, 1)
            v.tensor_reduce(row[:, 0:1], ps[0:1, 0:128], AX.X, ALU.max).then_inc(largest, 1)
            dve.wait_ge(spread, 1)
            link(v.tensor_scalar(kf[:, 0:1], pb[:, 0:1], 2.0 ** -60, None, ALU.max))
            link(v.tensor_scalar(k[:, 0:1], kf[:, 0:1].bitcast(I32), 23, None, ALU.logical_shift_right))
            link(v.tensor_scalar(k[:, 1:2], k[:, 0:1], -1.0, 127.0 + 127.0 + 13.0, ALU.mult, ALU.add))
            link(v.tensor_scalar(k[:, 2:3], k[:, 0:1], -13.0, None, ALU.add))
            v.tensor_scalar(scale[:, :].bitcast(I32), k[:, 1:3], 23, None, ALU.logical_shift_left).then_inc(scale_known, 1)
            dve.wait_ge(scale_known, 1)
            v.tensor_scalar(wf[0][:, :], wf[0][:, :], scale[:, 0:1], None, ALU.mult).then_inc(scaled0, 1)
            for n in range(2):
                dve.wait_ge(highs, n + 1)
                w = (wi, wh)[n]
                link(v.tensor_tensor(w[:, 1, :, :].rearrange("p e n -> p (e n)"), wf[n][:, :],
                                     w[:, 0, :, :].rearrange("p e n -> p (e n)"), ALU.subtract))

    return attach


def expand_routes(nc, cst, a, oh, gate, mb, rwb, wT):
    with ExitStack() as ctx:
        ek = sbuf(nc, ctx, "ek", [TT, NTT, 2 * EK + LK])
        mT = sbuf(nc, ctx, "mT", [EK, NT], BF16)
        gT = sbuf(nc, ctx, "gT", [LK, NT])
        sel = sbuf(nc, ctx, "sel", [LK, LK, 128])
        selb = sbuf(nc, ctx, "selb", [EK, EK, 128], BF16)
        pt = psum(nc, ctx, "pt", [EK, 2, BANK])
        pbc = psum(nc, ctx, "pbc", [128, 3, 2, BANK])
        (placed, turned, kept, spread, read_a, read_b, dc) = ctx.enter_context(
            stage(nc, "placed turned kept spread spread_kept_act spread_kept_dve dve_chain"))
        block = ctx.enter_context(nc.Block())
        PB = BANK // TT
        parts = [(0, EK, mT), (EK, EK, wT), (2 * EK, LK, gT)]
        groups = [(p, q) for p in range(3) for q in range(-(-NTT // PB))]

        @block.vector
        def _(dve):
            link = Chain(dve, dc)
            v = nc.vector
            v.tensor_copy(selb[:, :, :], cst["ident"][0:EK, 0:EK].unsqueeze(2).broadcast_to([EK, EK, 128]))
            link(v.tensor_copy(sel[:, :, :], cst["ident"][0:LK, 0:LK].unsqueeze(2).broadcast_to([LK, LK, 128])))
            for k in range(LK):
                m = ek[:, :, 0:EK].rearrange("p t (e k) -> p t e k", k=LK)[:, :, :, k]
                w = ek[:, :, EK:2 * EK].rearrange("p t (e k) -> p t e k", k=LK)[:, :, :, k]
                v.tensor_copy(m, oh[k][:, :, :])
                v.tensor_copy(ek[:, :, 2 * EK + k], gate[k][:, :])
                link(v.tensor_tensor(w, oh[k][:, :, :], gate[k][:, :].unsqueeze(2).broadcast_to([TT, NTT, LE]), ALU.mult))
            v.tensor_copy(ek[0:1, 0, 0:1], ek[0:1, 0, 0:1]).then_inc(placed, 1)
            for n, (p, q) in enumerate(groups):
                at, rows, dst = parts[p]
                dve.wait_ge(turned, n + 1)
                m = min(PB, NTT - q * PB) * TT
                v.tensor_copy(dst[:, q * PB * TT:q * PB * TT + m], pt[0:rows, n % 2, 0:m]).then_inc(kept, 1)
            for n in range(1, (EK + LK) * NCH, 2):
                dve.wait_ge(spread, n + 1)
                r, c = n // NCH, n % NCH
                o = mb[:, r, c * CH:(c + 1) * CH] if r < EK else rwb[:, r - EK, c * CH:(c + 1) * CH]
                v.tensor_copy(halves(o), pbc[:, n % 3, :, 0:HB]).then_inc(read_b, 1)

        @block.scalar
        def _(act):
            for n in range(0, (EK + LK) * NCH, 2):
                act.wait_ge(spread, n + 1)
                r, c = n // NCH, n % NCH
                o = mb[:, r, c * CH:(c + 1) * CH] if r < EK else rwb[:, r - EK, c * CH:(c + 1) * CH]
                nc.scalar.activation(halves(o), pbc[:, n % 3, :, 0:HB], ACT.Copy).then_inc(read_a, 1)

        @block.tensor
        def _(pe):
            pe.wait_ge(placed, 1)
            for n, (p, q) in enumerate(groups):
                at, rows, dst = parts[p]
                if n >= 2:
                    pe.wait_ge(kept, n - 1)
                for t in range(q * PB, min(NTT, (q + 1) * PB)):
                    last = nc.tensor.transpose(pt[0:rows, n % 2, (t - q * PB) * TT:(t - q * PB + 1) * TT],
                                               ek[:, t, at:at + rows], cst["ident"][0:TT, 0:TT])
                last.then_inc(turned, 1)
            pe.wait_ge(kept, len(groups))
            for n in range((EK + LK) * NCH):
                r, c = n // NCH, n % NCH
                if n >= 3:
                    pe.wait_ge((read_a, read_b)[(n - 3) % 2], (n - 3) // 2 + 1)
                for k in range(2):
                    a0 = c * CH + k * HB
                    if r < EK:
                        last = nc.tensor.matmul(pbc[:, n % 3, k, 0:HB], selb[:, r, :], mT[:, a0:a0 + HB], start=True, stop=True)
                    else:
                        last = nc.tensor.matmul(pbc[:, n % 3, k, 0:HB], sel[:, r - EK, :], gT[:, a0:a0 + HB], start=True, stop=True)
                last.then_inc(spread, 1)


def split_bias(nc, a, x, xs, bsp, bsel, scale):
    with ExitStack() as ctx:
        P = 3 * LE
        b = sbuf(nc, ctx, "b", [P, 4 * D])
        r = sbuf(nc, ctx, "r", [P, 4 * D])
        part = sbuf(nc, ctx, "part", [P, 3, 4 * D], BF16)
        pick = sbuf(nc, ctx, "pick", [P, 3])
        bs = sbuf(nc, ctx, "bs", [P, LE])
        load(nc, (b[:, :], a["le_b"]), (pick[:, :], a["c_part"]), (bs[:, :], a["c_expert"]))
        (dc,) = ctx.enter_context(stage(nc, "dve_chain"))
        block = ctx.enter_context(nc.Block())

        @block.vector
        def _(dve):
            link = Chain(dve, dc)
            v = nc.vector
            link(v.tensor_copy(xs[:, 0, :], x[:, :]))
            v.tensor_tensor(xs[:, 1, :], x[:, :], xs[:, 0, :], ALU.subtract)
            link(v.tensor_scalar(b[:, :], b[:, :], scale[0:P, 0:1], None, ALU.mult))
            link(v.tensor_copy(part[:, 0, :], b[:, :]))
            link(v.tensor_tensor(r[:, :], b[:, :], part[:, 0, :], ALU.subtract))
            link(v.tensor_copy(part[:, 1, :], r[:, :]))
            link(v.tensor_tensor(r[:, :], r[:, :], part[:, 1, :], ALU.subtract))
            link(v.tensor_copy(part[:, 2, :], r[:, :]))
            link(v.tensor_scalar(bsp[:, :], part[:, 0, :], pick[:, 0:1], None, ALU.mult))
            for k in range(1, 3):
                link(v.scalar_tensor_tensor(out=bsp[:, :], in0=part[:, k, :], scalar=pick[:, k:k + 1], in1=bsp[:, :],
                                            op0=ALU.mult, op1=ALU.add))
            link(v.tensor_copy(bsel[:, :, :], bs[:, :].unsqueeze(2).broadcast_to([P, LE, CB])))


def masks():
    c = {}
    h = np.full((128, 128), -1e30, np.float32)
    for i in range(NH):
        h[HD * i:HD * i + HD, HD * i:HD * i + HD] = 0
    c["headmask"] = h
    s = np.zeros((AT, 2), np.float32)
    s[0:S, 0] = 1
    s[S:, 1] = 1
    c["seqmask"] = s
    b = np.full((AT, AT), -1e30, np.float32)
    b[0:S, 0:S] = 0
    b[S:, S:] = 0
    c["blockmask"] = b
    c["iota"] = np.tile(np.arange(128, dtype=np.float32)[None], (TT, 1))
    c["index"] = np.arange(TT, dtype=np.float32)[:, None]
    c["tri"] = np.triu(np.ones((TT, TT), np.float32))
    carry = np.ones((64, NTT), np.float32)
    carry[:, 0] = 0
    c["carry"] = np.tile(carry.reshape(1, -1), (TT, 1))
    part, expert = np.zeros((3 * LE, 3), np.float32), np.zeros((3 * LE, LE), np.float32)
    for i in range(3 * LE):
        part[i, i // LE] = 1
        expert[i, i % LE] = 1
    c["part"], c["expert"] = part, expert
    return c


def rest(nc, ctx, cst, a, hT, xn):
    taps = Taps(nc, ctx)
    layernorm(nc, cst, hT, xn)
    switch_ffn(nc, cst, a, xn, hT, taps)
    layernorm(nc, cst, hT, xn)
    channel_attention(nc, cst, a, xn, hT)
    layernorm(nc, cst, hT, xn)
    silu_ffn(nc, cst, a, xn, hT, taps)
    layernorm(nc, cst, hT, xn)
    state_space(nc, cst, taps, xn, hT)
    weights = (sbuf(nc, ctx, "wi", [128, 2, LE, 4 * D], F16), sbuf(nc, ctx, "wh", [128, 2, LE, 4 * D], F16),
               sbuf(nc, ctx, "scale", [128, 2]))
    layernorm(nc, cst, hT, xn)
    gelu_ffn(nc, cst, a, xn, hT, lambda c: split_weights(nc, c, cst, a, *weights))
    layernorm(nc, cst, hT, xn)
    frame_attention(nc, cst, a, xn, hT)
    layernorm(nc, cst, hT, xn)
    lstm_experts(nc, cst, a, weights, xn, hT)


def lay_out_rest(I, f):
    f["ca_w"] = np.concatenate([I["L1_attn_w_qkv"], I["L1_attn_w_proj"]], 1)
    f["ca_bqk"] = np.tile(I["L1_attn_b_qkv"][None, 0:2 * D], (AT, 1))
    f["ca_b"] = np.stack([I["L1_attn_b_qkv"][2 * D:], I["L1_attn_b_proj"]], 1)
    f["fa_w"] = np.concatenate([I["L3_attn_W" + c].T for c in "qkv"], 1)
    f["ss_w"] = np.concatenate([I["L2_attn_L_param"], I["L2_attn_P_left"].transpose(0, 2, 1).reshape(D, -1),
                                I["L2_attn_P_right"].reshape(D, -1), I["L2_attn_B"], I["L2_attn_C"],
                                I["L2_attn_log_dt"], I["L2_attn_D"][:, None]], 1)
    f["sw_r"] = I["L0_ffn_switch_w"].T
    f["sw_rb"] = np.tile(I["L0_ffn_switch_b"][None], (TT, 1))
    f["sw_w"] = I["L0_ffn_expert_w"].transpose(0, 2, 1)
    f["sw_b"] = I["L0_ffn_expert_b"]

    def experts(w1, b1, w2):
        E, _, F = w1.shape
        return np.concatenate([w1, w2.reshape(E, F // 128, 128, D).transpose(0, 2, 1, 3).reshape(E, 128, -1),
                               b1.reshape(E, F // 128, 128).transpose(0, 2, 1)], 2)

    g = lambda n: I["L2_ffn_" + n]
    f["gf_r"], f["gf_rb"] = g("Ws"), np.tile(g("bs")[None], (TT, 1))
    f["gf_w"], f["gf_b"] = experts(g("W1"), g("b1"), g("W2")), g("b2")
    g = lambda n: I["L1_ffn_" + n]
    f["sf_w"], f["sf_b"] = experts(g("W1"), g("b1"), g("W2")), g("b2")
    f["sf_cols"] = np.concatenate([g("ln1_g")[:, None], g("ln1_b")[:, None], g("ffln_g")[:, None], g("ffln_b")[:, None],
                                   g("bs1").reshape(2, 128).T, g("bs2")[:, None], g("bf1").reshape(4, 128).T, g("bf2")[:, None]], 1)
    f["sf_ws"] = np.concatenate([g("Ws1"), g("Ws2").reshape(2, 128, D).transpose(1, 0, 2).reshape(128, -1)], 1)
    f["sf_wf"] = np.concatenate([g("Wf1"), g("Wf2").reshape(4, 128, D).transpose(1, 0, 2).reshape(128, -1)], 1)
    f["sf_wr"], f["sf_code"] = g("Wr"), g("codebook").T
    g = lambda n: I["L3_ffn_" + n]
    f["le_r"], f["le_rb"] = g("router_w"), np.tile(g("router_b")[None], (TT, 1))
    for n in ("Wi", "Wh", "Wo"):
        f["le_" + n.lower()] = g(n).transpose(1, 0, 2).reshape(128, -1)
    f["le_b"] = np.tile(g("b"), (3, 1))
    f["le_bo"] = np.repeat(g("bo"), LK, 0)
    f.update({"c_" + k: v for k, v in masks().items()})


def mdct_constant():
    L = 2 * D
    n = np.arange(L, dtype=np.float32) + np.float32(0.5)
    k = np.float32(np.pi / D) * n[:D]
    z = np.sqrt(np.float32(2.0 / D * 2.0))
    wm = z * np.cos((n + np.float32(D / 2))[:, None] * k[None, :]).astype(np.float32)
    win = np.sin(np.float32(np.pi) * n / np.float32(L)).astype(np.float32)
    return np.ascontiguousarray((win[:, None] * wm).astype(np.float32).reshape(2, D, D).transpose(1, 0, 2))


def constants():
    c = {}
    c["ident"] = np.eye(128, dtype=np.float32)
    c["avg"] = np.full((128, 128), 1.0 / 128, np.float32)
    c["mdct"] = mdct_constant().reshape(128, 256)
    c["row"] = np.concatenate([np.zeros((32, 32)), np.tile(np.eye(32), (3, 1))]).astype(np.float32)
    c["eps"] = np.full((128, 1), EPS, np.float32)
    return c


def build(nc, a):
    with ExitStack() as ctx:
        hT = sbuf(nc, ctx, "hT", [128, NT], F32)
        xn = sbuf(nc, ctx, "xn", [128, NT], F32)
        cst, dims = {}, {"mdct": "p (k n) -> p k n"}
        with ExitStack() as c1:
            tiles = {}
            for name in ("ident", "avg", "eps"):
                tiles[name] = sbuf(nc, ctx, name, list(a["c_" + name].shape))
                cst[name] = tiles[name][:, :]
            (loaded,) = c1.enter_context(stage(nc, "constants_loaded"))
            block = c1.enter_context(nc.Block())

            @block.sync
            def _(sp):
                n = 0
                for name, t in tiles.items():
                    sp.dma_start(t[:, :], a["c_" + name]).then_inc(loaded, 16)
                    n += 16
                sp.wait_ge(loaded, n)

        def load_const(c1, name):
            t = sbuf(nc, c1, name, list(a["c_" + name].shape))
            with ExitStack() as c2:
                (loaded,) = c2.enter_context(stage(nc, "constants_loaded"))
                block = c2.enter_context(nc.Block())

                @block.sync
                def _(sp):
                    sp.dma_start(t[:, :], a["c_" + name]).then_inc(loaded, 16)
                    sp.wait_ge(loaded, 16)
            return t

        cst["gathered"] = [Counted(ctx.enter_context(nc.semaphore(f"gathered{t}"))) for t in range(NTT)]
        cst["scattered"] = Counted(ctx.enter_context(nc.semaphore("scattered")))

        with ExitStack() as c1:
            t = load_const(c1, "mdct")
            cst["mdct"] = t[:, :].rearrange("p (k n) -> p k n", k=2)
            tokenize(nc, cst, a["frames"], hT)
        with ExitStack() as c1:
            m = sbuf(nc, c1, "m", [128, NT], F32)
            layernorm(nc, cst, hT, xn)
            with ExitStack() as c2:
                (copied,) = c2.enter_context(stage(nc, "copied"))
                block = c2.enter_context(nc.Block())

                @block.vector
                def _(dve):
                    nc.vector.tensor_copy(m[:, :], xn[:, :]).then_inc(copied, 1)
            with ExitStack() as c2:
                row = sbuf(nc, c2, "row", [128, 32, 128], BF16)
                t = load_const(c2, "row")
                with ExitStack() as c3:
                    (widened,) = c3.enter_context(stage(nc, "widened"))
                    block = c3.enter_context(nc.Block())

                    @block.vector
                    def _(dve):
                        nc.vector.tensor_copy(row[:, :, :], t[:, :].unsqueeze(2).broadcast_to([128, 32, 128])).then_inc(widened, 1)
                cst["row"] = row
                with nc.Fori(0, NL) as layer:
                    mamba_layer(nc, cst, layer, a["mamba_w"], m)
            lstm_fusion(nc, cst, (a["lstm_ih"].rearrange("p (g n) -> p g n", g=4),
                                  a["lstm_hh"].rearrange("d p (g n) -> d p g n", g=4),
                                  a["lstm_b"], a["fus_w"].rearrange("p (k n) -> p k n", k=3), a["fus_b"]), xn, m, hT)
        rest(nc, ctx, cst, a, hT, xn)
        with ExitStack() as c1:
            (stored,) = c1.enter_context(stage(nc, "stored"))
            block = c1.enter_context(nc.Block())

            @block.sync
            def _(sp):
                sp.dma_start(a["out"], hT[:, :]).then_inc(stored, 16)
                sp.wait_ge(stored, 16)


def lay_out(inp):
    I = {k: np.asarray(v) for k, v in inp.items()}
    f = {}
    x = np.zeros((NB, (S + 1) * D), np.float32)
    x[:, D:D + I["x"].shape[1]] = I["x"]
    f["frames"] = x.reshape(NB, S + 1, D).transpose(2, 0, 1).reshape(D, NB * (S + 1))
    w = np.zeros((NL, 128, MWID), np.float32)

    def put(name, v):
        at, width = MW[name]
        w[:, 0:v.shape[1], at:at + width] = v
    g = lambda n: I["L0_attn_" + n]
    put("wi", g("in_proj_w").transpose(0, 2, 1))
    put("cw", g("conv_w").reshape(NL, 2, 128, DCV).transpose(0, 2, 1, 3).reshape(NL, 128, -1))
    put("cb", g("conv_b").reshape(NL, 2, 128).transpose(0, 2, 1))
    xp = g("x_proj_w")
    xp = np.concatenate([xp[:, 0:DTR]] + [xp[:, DTR:]] * 3, 1)
    put("xp", xp.reshape(NL, 128, 2, 128).transpose(0, 3, 2, 1).reshape(NL, 128, -1))
    put("dw", g("dt_proj_w").transpose(0, 2, 1))
    put("db", g("dt_proj_b").reshape(NL, 2, 128).transpose(0, 2, 1))
    put("alog", g("A_log").reshape(NL, 2, 128, DST).transpose(0, 2, 1, 3).reshape(NL, 128, -1))
    put("dp", g("D_param").reshape(NL, 2, 128).transpose(0, 2, 1))
    put("wo", g("out_proj_w").reshape(NL, D, 2, 128).transpose(0, 3, 2, 1).reshape(NL, 128, -1))
    put("g", g("ln_g")[:, :, None])
    put("b", g("ln_b")[:, :, None])
    f["mamba_w"] = w
    order = [0, 1, 3, 2]
    f["lstm_ih"] = g("lstm_w_ih").reshape(2, 4, H2, D)[:, order].transpose(3, 1, 0, 2).reshape(D, -1)
    f["lstm_hh"] = g("lstm_w_hh").reshape(2, 4, H2, H2)[:, order].transpose(0, 3, 1, 2).reshape(2, H2, -1)
    b = [g(n).reshape(2, 4, H2)[:, order].transpose(0, 2, 1).reshape(128, 4) for n in ("lstm_b_ih", "lstm_b_hh")]
    f["lstm_b"] = np.stack(b)
    fw = np.zeros((128, 3, D), np.float32)
    fw[:, 0] = g("fusion_w").T[0:128]
    fw[0:H2, 1] = g("fusion_w").T[128:128 + H2]
    fw[H2:128, 2] = g("fusion_w").T[128 + H2:256]
    f["fus_w"] = fw.reshape(128, 3 * D)
    f["fus_b"] = g("fusion_b")[:, None]
    lay_out_rest(I, f)
    f.update({"c_" + k: v for k, v in constants().items()})
    return {k: np.ascontiguousarray(v) for k, v in f.items()}


def kernel(**inputs):
    import concourse.bacc as bacc
    from concourse.bass_utils import run_bass_kernel_spmd

    nc = bacc.Bacc("TRN2", target_bir_lowering=False, num_devices=1)
    arrays = lay_out(inputs)
    args = {k: nc.dram_tensor(k, list(v.shape), mybir.dt.from_np(v.dtype), kind="ExternalInput").ap()
            for k, v in arrays.items()}
    args["out"] = nc.dram_tensor("out", [128, NT], F32, kind="ExternalOutput").ap()
    build(nc, args)
    r = run_bass_kernel_spmd(nc, [arrays], core_ids=[0])
    return r.results[0]["out"].reshape(D, NB, S).transpose(1, 2, 0)
```
